# Optimizing a Trainium2 kernel written in Bass

```python
import numpy as np
import jax
import jax.numpy as jnp

def _softmax(x, axis=-1):
    return jax.nn.softmax(x, axis=axis)

def _gelu(x):
    return jax.nn.gelu(x, approximate=True)

def _silu(x):
    return jax.nn.silu(x)

def _sigmoid(x):
    return jax.nn.sigmoid(x)

def _layernorm(x, axis=-1, eps=1e-05):
    m = jnp.mean(x, axis=axis, keepdims=True)
    v = jnp.var(x, axis=axis, keepdims=True)
    return (x - m) / jnp.sqrt(v + eps)

def _scatter_add(tgt, idx, src, axis=0):
    return tgt.at[idx].add(src)

def _segment_sum(src, seg, n):
    return jax.ops.segment_sum(src, seg, n)
kernel_name = 'mk_lm_tower_d4_tok_ids256_r4_e888bd'

def setup_inputs(seed: int=0):
    np.random.seed(seed)
    _w = jnp.asarray

    def _rec_inputs():
        import jax
        import jax.numpy as jnp
        _rk = jax.random.key(seed)
        x = jax.random.randint(jax.random.fold_in(_rk, 1), (64, 256), 0, 12564, jnp.int32)
        return x
    x = _rec_inputs()

    def _L0_tok_setup():
        import jax, jax.numpy as jnp
        import numpy as np
        VOCAB, N_TURNS, OUT_DIM, POLY_DEG = (50257, 4, 64, 4)
        key = jax.random.key(seed)
        k1, k2, k3 = jax.random.split(key, 3)
        token_ids = jax.random.randint(k1, (16, 1024), 0, VOCAB)
        turns = jax.random.normal(k2, (VOCAB, N_TURNS), dtype=jnp.float32) * 3.0
        poly_coeffs = jax.random.normal(k3, (N_TURNS, POLY_DEG + 1, OUT_DIM), dtype=jnp.float32) * 0.01
        return {'token_ids': token_ids, 'turns': turns, 'poly_coeffs': poly_coeffs}
    _L0_tok_all = _L0_tok_setup()
    _L0_tok_in = {k: v for k, v in _L0_tok_all.items() if k in ('turns', 'poly_coeffs')}
    del _L0_tok_all

    def _L0_attn_setup():
        import jax, jax.numpy as jnp
        import numpy as np
        SEQ_LEN = 512
        EMBED_DIM = 64
        BATCH = 8
        LN_EPS = 1e-05

        def _layernorm(x, g, b):
            mu = jnp.mean(x, axis=-1, keepdims=True)
            var = jnp.mean(jnp.square(x - mu), axis=-1, keepdims=True)
            return (x - mu) * jax.lax.rsqrt(var + LN_EPS) * g + b
        key = jax.random.key(seed)
        ks = jax.random.split(key, 8)
        C = EMBED_DIM
        x = jax.random.normal(ks[0], (BATCH, SEQ_LEN, C), dtype=jnp.float32)
        qkv_w = jax.random.normal(ks[1], (C, 3 * C), dtype=jnp.float32) * 0.02
        qkv_b = jnp.zeros((3 * C,), dtype=jnp.float32)
        proj_w = jax.random.normal(ks[2], (C, C), dtype=jnp.float32) * 0.02
        proj_b = jnp.zeros((C,), dtype=jnp.float32)
        ln1_g = jnp.ones((C,), dtype=jnp.float32)
        ln1_b = jnp.zeros((C,), dtype=jnp.float32)
        ln2_g = jnp.ones((C,), dtype=jnp.float32)
        ln2_b = jnp.zeros((C,), dtype=jnp.float32)
        bias_table = jax.random.truncated_normal(ks[3], -2.0, 2.0, (2 * SEQ_LEN - 1,), dtype=jnp.float32) * 0.02
        scale = jnp.asarray(1.0 / np.sqrt(C), dtype=jnp.float32)
        return {'x': x, 'ln1_g': ln1_g, 'ln1_b': ln1_b, 'qkv_w': qkv_w, 'qkv_b': qkv_b, 'bias_table': bias_table, 'scale': scale, 'proj_w': proj_w, 'proj_b': proj_b, 'ln2_g': ln2_g, 'ln2_b': ln2_b}
    _L0_attn_all = _L0_attn_setup()
    _L0_attn_in = {k: v for k, v in _L0_attn_all.items() if k in ('ln1_g', 'ln1_b', 'qkv_w', 'qkv_b', 'bias_table', 'scale', 'proj_w', 'proj_b', 'ln2_g', 'ln2_b')}
    del _L0_attn_all

    def _L0_ffn_setup():
        import jax, jax.numpy as jnp
        import numpy as np
        B, S, H, F, E, K = (8, 1024, 64, 128, 16, 2)
        EPS = 1e-05
        key = jax.random.key(seed)
        ks = jax.random.split(key, 9)
        sc = 0.02
        return {'x': jax.random.normal(ks[0], (B, S, H), dtype=jnp.float32), 'gate_w': jax.random.normal(ks[1], (H, E), dtype=jnp.float32) * sc, 'gate_b': jnp.zeros((E,), dtype=jnp.float32), 'w1': jax.random.normal(ks[2], (E, H, F), dtype=jnp.float32) * sc, 'b1': jnp.zeros((E, F), dtype=jnp.float32), 'w2': jax.random.normal(ks[3], (E, F, H), dtype=jnp.float32) * sc, 'b2': jnp.zeros((E, H), dtype=jnp.float32), 'gamma': jnp.ones((H,), dtype=jnp.float32), 'beta': jnp.zeros((H,), dtype=jnp.float32)}
    _L0_ffn_all = _L0_ffn_setup()
    _L0_ffn_in = {k: v for k, v in _L0_ffn_all.items() if k in ('gate_w', 'gate_b', 'w1', 'b1', 'w2', 'b2', 'gamma', 'beta')}
    del _L0_ffn_all

    def _L1_attn_setup():
        import jax, jax.numpy as jnp
        import numpy as np
        key = jax.random.key(seed)
        ks = jax.random.split(key, 5)
        b, t, e, h = (8, 256, 64, 8)
        w = lambda k, shape: jax.random.normal(k, shape, dtype=jnp.float32) * 0.02
        return {'x': jax.random.normal(ks[0], (b, t, e), dtype=jnp.float32), 'Wq': w(ks[1], (e, e * h)), 'bq': jnp.zeros((e * h,), jnp.float32), 'Wk': w(ks[2], (e, e * h)), 'bk': jnp.zeros((e * h,), jnp.float32), 'Wv': w(ks[3], (e, e * h)), 'bv': jnp.zeros((e * h,), jnp.float32), 'Wu': w(ks[4], (e * h, e)), 'bu': jnp.zeros((e,), jnp.float32)}
    _L1_attn_all = _L1_attn_setup()
    _L1_attn_in = {k: v for k, v in _L1_attn_all.items() if k in ('Wq', 'bq', 'Wk', 'bk', 'Wv', 'bv', 'Wu', 'bu')}
    del _L1_attn_all

    def _L1_ffn_setup():
        import jax, jax.numpy as jnp
        import numpy as np
        B, S, H, NH, NE = (4, 256, 64, 4, 4)
        D = H // NH
        EPS = 1e-08

        def layernorm(x, g, b):
            m = jnp.mean(x, axis=-1, keepdims=True)
            v = jnp.mean((x - m) ** 2, axis=-1, keepdims=True)
            return (x - m) / jnp.sqrt(v + EPS) * g + b
        key = jax.random.key(seed)
        ks = jax.random.split(key, 18)
        sc = 0.05
        return {'x': jax.random.normal(ks[0], (B, S, H), jnp.float32), 'hl_w': jax.random.normal(ks[1], (NH, D, H), jnp.float32) * sc, 'hl_b': jax.random.normal(ks[2], (NH, D), jnp.float32) * sc, 'wq': jax.random.normal(ks[3], (NH, NE, D, D), jnp.float32) * sc, 'wk': jax.random.normal(ks[4], (NH, D, D), jnp.float32) * sc, 'wv': jax.random.normal(ks[5], (NH, D, D), jnp.float32) * sc, 'gate_w': jax.random.normal(ks[6], (NH, NE, NE * D), jnp.float32) * sc, 'gate_b': jax.random.normal(ks[7], (NH, NE), jnp.float32) * sc, 'ln_g': jnp.ones((D,), jnp.float32), 'ln_b': jnp.zeros((D,), jnp.float32), 'fc1_w': jax.random.normal(ks[8], (D, D), jnp.float32) * sc, 'fc1_b': jax.random.normal(ks[9], (D,), jnp.float32) * sc, 'fc2_w': jax.random.normal(ks[10], (D, D), jnp.float32) * sc, 'fc2_b': jax.random.normal(ks[11], (D,), jnp.float32) * sc, 'fnorm_g': jnp.ones((D,), jnp.float32), 'fnorm_b': jnp.zeros((D,), jnp.float32), 'fgate_w': jax.random.normal(ks[12], (NH, H), jnp.float32) * sc}
    _L1_ffn_all = _L1_ffn_setup()
    _L1_ffn_in = {k: v for k, v in _L1_ffn_all.items() if k in ('hl_w', 'hl_b', 'wq', 'wk', 'wv', 'gate_w', 'gate_b', 'ln_g', 'ln_b', 'fc1_w', 'fc1_b', 'fc2_w', 'fc2_b', 'fnorm_g', 'fnorm_b', 'fgate_w')}
    del _L1_ffn_all

    def _L2_attn_setup():
        import jax, jax.numpy as jnp
        import numpy as np
        N_HEADS, D_MODEL, D_HEAD = (8, 64, 32)
        BATCH, SEQ = (2, 512)
        INIT_RANGE = 0.02

        def _odd_causal_mask(S):
            i = jnp.arange(S)[:, None]
            j = jnp.arange(S)[None, :]
            allowed = (j < i) & (j % 2 == 1) | (i == j)
            return allowed
        key = jax.random.key(seed)
        ks = jax.random.split(key, 6)
        x = jax.random.normal(ks[0], (BATCH, SEQ, D_MODEL), dtype=jnp.float32)
        W_Q = INIT_RANGE * jax.random.normal(ks[1], (N_HEADS, D_MODEL, D_HEAD), dtype=jnp.float32)
        W_K = INIT_RANGE * jax.random.normal(ks[2], (N_HEADS, D_MODEL, D_HEAD), dtype=jnp.float32)
        W_V = INIT_RANGE * jax.random.normal(ks[3], (N_HEADS, D_MODEL, D_HEAD), dtype=jnp.float32)
        W_O = INIT_RANGE * jax.random.normal(ks[4], (N_HEADS, D_HEAD, D_MODEL), dtype=jnp.float32)
        b_Q = jnp.zeros((N_HEADS, D_HEAD), dtype=jnp.float32)
        b_K = jnp.zeros((N_HEADS, D_HEAD), dtype=jnp.float32)
        b_V = jnp.zeros((N_HEADS, D_HEAD), dtype=jnp.float32)
        b_O = jnp.zeros((D_MODEL,), dtype=jnp.float32)
        return {'normalized_resid_pre': x, 'W_Q': W_Q, 'W_K': W_K, 'W_V': W_V, 'W_O': W_O, 'b_Q': b_Q, 'b_K': b_K, 'b_V': b_V, 'b_O': b_O}
    _L2_attn_all = _L2_attn_setup()
    _L2_attn_in = {k: v for k, v in _L2_attn_all.items() if k in ('W_Q', 'W_K', 'W_V', 'W_O', 'b_Q', 'b_K', 'b_V', 'b_O')}
    del _L2_attn_all

    def _L2_ffn_setup():
        import jax, jax.numpy as jnp
        import numpy as np
        B, T, C = (64, 96, 64)
        NH, NKV = (4, 2)
        HD = C // NH
        NREP = NH // NKV
        NE, TOPK = (8, 2)
        HID = int(8 / 3 * C)
        EPS_RMS = 1e-06

        def _rope_tables(t_len):
            inv_freq = 1.0 / 10000.0 ** (np.arange(0, HD, 2, dtype=np.float32) / HD)
            t = np.arange(t_len, dtype=np.float32)
            freqs = np.outer(t, inv_freq)
            emb = np.concatenate([freqs, freqs], axis=-1)
            return (jnp.asarray(np.cos(emb)), jnp.asarray(np.sin(emb)))

        def _rotate_half(x):
            h = x.shape[-1] // 2
            return jnp.concatenate([-x[..., h:], x[..., :h]], axis=-1)

        def _rmsnorm(v, w):
            return v * jax.lax.rsqrt(jnp.mean(v * v, axis=-1, keepdims=True) + EPS_RMS) * w
        key = jax.random.key(seed)
        ks = jax.random.split(key, 10)
        s = lambda k, shape: jax.random.normal(k, shape, jnp.float32) * 0.02
        return {'x': jax.random.normal(ks[0], (B, T, C), jnp.float32), 'ln1_w': jnp.ones((C,), jnp.float32), 'ln2_w': jnp.ones((C,), jnp.float32), 'wq': s(ks[1], (NH * HD, C)), 'wk': s(ks[2], (NKV * HD, C)), 'wv': s(ks[3], (NKV * HD, C)), 'wo': s(ks[4], (C, C)), 'router_w': s(ks[5], (NE, C)), 'w1': s(ks[6], (NE, HID, C)), 'w2': s(ks[7], (NE, C, HID)), 'w3': s(ks[8], (NE, HID, C))}
    _L2_ffn_all = _L2_ffn_setup()
    _L2_ffn_in = {k: v for k, v in _L2_ffn_all.items() if k in ('ln1_w', 'ln2_w', 'wq', 'wk', 'wv', 'wo', 'router_w', 'w1', 'w2', 'w3')}
    del _L2_ffn_all

    def _L3_attn_setup():
        import jax, jax.numpy as jnp
        import numpy as np
        import math
        B, N, D = (4, 1024, 64)
        key = jax.random.key(seed)
        k0, k1, k2, k3 = jax.random.split(key, 4)
        bound = math.sqrt(6.0 / D)
        return {'x': jax.random.normal(k0, (B, N, D), dtype=jnp.float32), 'Wq': jax.random.uniform(k1, (D, D), dtype=jnp.float32, minval=-bound, maxval=bound), 'Wk': jax.random.uniform(k2, (D, D), dtype=jnp.float32, minval=-bound, maxval=bound), 'Wv': jax.random.uniform(k3, (D, D), dtype=jnp.float32, minval=-bound, maxval=bound)}
    _L3_attn_all = _L3_attn_setup()
    _L3_attn_in = {k: v for k, v in _L3_attn_all.items() if k in ('Wq', 'Wk', 'Wv')}
    del _L3_attn_all

    def _L3_ffn_setup():
        import math
        import jax, jax.numpy as jnp
        import numpy as np
        CAPACITY_FACTOR = 1.25
        key = jax.random.key(seed)
        ks = jax.random.split(key, 5)
        B, L, D, F, E = (8, 2048, 64, 256, 8)
        h = jax.random.normal(ks[0], (B, L, D), dtype=jnp.float32)
        gate_w = jax.random.normal(ks[1], (D, E), dtype=jnp.float32) * 0.02
        gate_b = jnp.zeros((E,), dtype=jnp.float32)
        w1 = jax.random.normal(ks[2], (E, D, F), dtype=jnp.float32) * (1.0 / math.sqrt(D))
        b1 = jnp.zeros((E, F), dtype=jnp.float32)
        w2 = jax.random.normal(ks[3], (E, F, D), dtype=jnp.float32) * (1.0 / math.sqrt(F))
        b2 = jnp.zeros((E, D), dtype=jnp.float32)
        return {'h': h, 'gate_w': gate_w, 'gate_b': gate_b, 'w1': w1, 'b1': b1, 'w2': w2, 'b2': b2}
    _L3_ffn_all = _L3_ffn_setup()
    _L3_ffn_in = {k: v for k, v in _L3_ffn_all.items() if k in ('gate_w', 'gate_b', 'w1', 'b1', 'w2', 'b2')}
    del _L3_ffn_all
    return {'x': x, 'L0_tok_turns': _L0_tok_in['turns'], 'L0_tok_poly_coeffs': _L0_tok_in['poly_coeffs'], 'L0_attn_ln1_g': _L0_attn_in['ln1_g'], 'L0_attn_ln1_b': _L0_attn_in['ln1_b'], 'L0_attn_qkv_w': _L0_attn_in['qkv_w'], 'L0_attn_qkv_b': _L0_attn_in['qkv_b'], 'L0_attn_bias_table': _L0_attn_in['bias_table'], 'L0_attn_scale': _L0_attn_in['scale'], 'L0_attn_proj_w': _L0_attn_in['proj_w'], 'L0_attn_proj_b': _L0_attn_in['proj_b'], 'L0_attn_ln2_g': _L0_attn_in['ln2_g'], 'L0_attn_ln2_b': _L0_attn_in['ln2_b'], 'L0_ffn_gate_w': _L0_ffn_in['gate_w'], 'L0_ffn_gate_b': _L0_ffn_in['gate_b'], 'L0_ffn_w1': _L0_ffn_in['w1'], 'L0_ffn_b1': _L0_ffn_in['b1'], 'L0_ffn_w2': _L0_ffn_in['w2'], 'L0_ffn_b2': _L0_ffn_in['b2'], 'L0_ffn_gamma': _L0_ffn_in['gamma'], 'L0_ffn_beta': _L0_ffn_in['beta'], 'L1_attn_Wq': _L1_attn_in['Wq'], 'L1_attn_bq': _L1_attn_in['bq'], 'L1_attn_Wk': _L1_attn_in['Wk'], 'L1_attn_bk': _L1_attn_in['bk'], 'L1_attn_Wv': _L1_attn_in['Wv'], 'L1_attn_bv': _L1_attn_in['bv'], 'L1_attn_Wu': _L1_attn_in['Wu'], 'L1_attn_bu': _L1_attn_in['bu'], 'L1_ffn_hl_w': _L1_ffn_in['hl_w'], 'L1_ffn_hl_b': _L1_ffn_in['hl_b'], 'L1_ffn_wq': _L1_ffn_in['wq'], 'L1_ffn_wk': _L1_ffn_in['wk'], 'L1_ffn_wv': _L1_ffn_in['wv'], 'L1_ffn_gate_w': _L1_ffn_in['gate_w'], 'L1_ffn_gate_b': _L1_ffn_in['gate_b'], 'L1_ffn_ln_g': _L1_ffn_in['ln_g'], 'L1_ffn_ln_b': _L1_ffn_in['ln_b'], 'L1_ffn_fc1_w': _L1_ffn_in['fc1_w'], 'L1_ffn_fc1_b': _L1_ffn_in['fc1_b'], 'L1_ffn_fc2_w': _L1_ffn_in['fc2_w'], 'L1_ffn_fc2_b': _L1_ffn_in['fc2_b'], 'L1_ffn_fnorm_g': _L1_ffn_in['fnorm_g'], 'L1_ffn_fnorm_b': _L1_ffn_in['fnorm_b'], 'L1_ffn_fgate_w': _L1_ffn_in['fgate_w'], 'L2_attn_W_Q': _L2_attn_in['W_Q'], 'L2_attn_W_K': _L2_attn_in['W_K'], 'L2_attn_W_V': _L2_attn_in['W_V'], 'L2_attn_W_O': _L2_attn_in['W_O'], 'L2_attn_b_Q': _L2_attn_in['b_Q'], 'L2_attn_b_K': _L2_attn_in['b_K'], 'L2_attn_b_V': _L2_attn_in['b_V'], 'L2_attn_b_O': _L2_attn_in['b_O'], 'L2_ffn_ln1_w': _L2_ffn_in['ln1_w'], 'L2_ffn_ln2_w': _L2_ffn_in['ln2_w'], 'L2_ffn_wq': _L2_ffn_in['wq'], 'L2_ffn_wk': _L2_ffn_in['wk'], 'L2_ffn_wv': _L2_ffn_in['wv'], 'L2_ffn_wo': _L2_ffn_in['wo'], 'L2_ffn_router_w': _L2_ffn_in['router_w'], 'L2_ffn_w1': _L2_ffn_in['w1'], 'L2_ffn_w2': _L2_ffn_in['w2'], 'L2_ffn_w3': _L2_ffn_in['w3'], 'L3_attn_Wq': _L3_attn_in['Wq'], 'L3_attn_Wk': _L3_attn_in['Wk'], 'L3_attn_Wv': _L3_attn_in['Wv'], 'L3_ffn_gate_w': _L3_ffn_in['gate_w'], 'L3_ffn_gate_b': _L3_ffn_in['gate_b'], 'L3_ffn_w1': _L3_ffn_in['w1'], 'L3_ffn_b1': _L3_ffn_in['b1'], 'L3_ffn_w2': _L3_ffn_in['w2'], 'L3_ffn_b2': _L3_ffn_in['b2']}

def reference(x, L0_tok_turns, L0_tok_poly_coeffs, L0_attn_ln1_g, L0_attn_ln1_b, L0_attn_qkv_w, L0_attn_qkv_b, L0_attn_bias_table, L0_attn_scale, L0_attn_proj_w, L0_attn_proj_b, L0_attn_ln2_g, L0_attn_ln2_b, L0_ffn_gate_w, L0_ffn_gate_b, L0_ffn_w1, L0_ffn_b1, L0_ffn_w2, L0_ffn_b2, L0_ffn_gamma, L0_ffn_beta, L1_attn_Wq, L1_attn_bq, L1_attn_Wk, L1_attn_bk, L1_attn_Wv, L1_attn_bv, L1_attn_Wu, L1_attn_bu, L1_ffn_hl_w, L1_ffn_hl_b, L1_ffn_wq, L1_ffn_wk, L1_ffn_wv, L1_ffn_gate_w, L1_ffn_gate_b, L1_ffn_ln_g, L1_ffn_ln_b, L1_ffn_fc1_w, L1_ffn_fc1_b, L1_ffn_fc2_w, L1_ffn_fc2_b, L1_ffn_fnorm_g, L1_ffn_fnorm_b, L1_ffn_fgate_w, L2_attn_W_Q, L2_attn_W_K, L2_attn_W_V, L2_attn_W_O, L2_attn_b_Q, L2_attn_b_K, L2_attn_b_V, L2_attn_b_O, L2_ffn_ln1_w, L2_ffn_ln2_w, L2_ffn_wq, L2_ffn_wk, L2_ffn_wv, L2_ffn_wo, L2_ffn_router_w, L2_ffn_w1, L2_ffn_w2, L2_ffn_w3, L3_attn_Wq, L3_attn_Wk, L3_attn_Wv, L3_ffn_gate_w, L3_ffn_gate_b, L3_ffn_w1, L3_ffn_b1, L3_ffn_w2, L3_ffn_b2):
    import jax
    import jax.numpy as jnp

    def _L0_tok_ref(token_ids, turns, poly_coeffs):
        import jax, jax.numpy as jnp
        import numpy as np
        VOCAB, N_TURNS, OUT_DIM, POLY_DEG = (50257, 4, 64, 4)
        base_turns = turns[token_ids]
        x = jax.lax.stop_gradient(jnp.trunc(base_turns)).astype(jnp.float32)
        degs = jnp.arange(POLY_DEG + 1, dtype=jnp.float32)
        xp = x[..., None] ** degs
        emb = jnp.einsum('bstd,tdo->bso', xp, poly_coeffs)
        return emb

    def _L0_attn_ref(x, ln1_g, ln1_b, qkv_w, qkv_b, bias_table, scale, proj_w, proj_b, ln2_g, ln2_b):
        import jax, jax.numpy as jnp
        import numpy as np
        SEQ_LEN = 512
        EMBED_DIM = 64
        BATCH = 8
        LN_EPS = 1e-05

        def _layernorm(x, g, b):
            mu = jnp.mean(x, axis=-1, keepdims=True)
            var = jnp.mean(jnp.square(x - mu), axis=-1, keepdims=True)
            return (x - mu) * jax.lax.rsqrt(var + LN_EPS) * g + b
        B, N, C = x.shape
        h = _layernorm(x, ln1_g, ln1_b)
        qkv = h @ qkv_w + qkv_b
        q, k, v = jnp.split(qkv, 3, axis=-1)
        coords = jnp.arange(N)
        rel_idx = coords[None, :] - coords[:, None] + (N - 1)
        rel_bias = bias_table[rel_idx]
        attn = jnp.einsum('bnc,bmc->bnm', q, k) + rel_bias
        attn = jax.nn.softmax(attn, axis=-1) * scale
        out = jnp.einsum('bnm,bmc->bnc', attn, v)
        out = out @ proj_w + proj_b
        out = _layernorm(out, ln2_g, ln2_b)
        return out

    def _L0_ffn_ref(x, gate_w, gate_b, w1, b1, w2, b2, gamma, beta):
        import jax, jax.numpy as jnp
        import numpy as np
        B, S, H, F, E, K = (8, 1024, 64, 128, 16, 2)
        EPS = 1e-05
        gate_logits = x @ gate_w + gate_b
        topk_vals, topk_idx = jax.lax.top_k(gate_logits, K)
        topk_w = jax.nn.softmax(topk_vals, axis=-1)
        h = jax.nn.relu(jnp.einsum('bsh,ehf->bsef', x, w1) + b1)
        expert_out = jnp.einsum('bsef,efh->bseh', h, w2) + b2
        sel = jnp.take_along_axis(expert_out, topk_idx[:, :, :, None], axis=2)
        moe = jnp.sum(topk_w[..., None] * sel, axis=2)
        y = x + moe
        mu = jnp.mean(y, axis=-1, keepdims=True)
        var = jnp.var(y, axis=-1, keepdims=True)
        return (y - mu) / jnp.sqrt(var + EPS) * gamma + beta

    def _L1_attn_ref(x, Wq, bq, Wk, bk, Wv, bv, Wu, bu):
        import jax, jax.numpy as jnp
        import numpy as np
        b, t, e = x.shape
        h = Wq.shape[1] // e
        q = (x @ Wq + bq).reshape(b, t, h, e)
        k = (x @ Wk + bk).reshape(b, t, h, e)
        v = (x @ Wv + bv).reshape(b, t, h, e)
        scores = jnp.einsum('bihe,bjhe->bhij', q, k) / jnp.sqrt(jnp.asarray(e, jnp.float32))
        i = jnp.arange(t)[:, None]
        j = jnp.arange(t)[None, :]
        scores = jnp.where(j >= i, -jnp.inf, scores)
        scores = jnp.where(i == 0, 0.0, scores)
        att = jax.nn.softmax(scores, axis=-1)
        att = jnp.where(i == 0, 0.0, att)
        out = jnp.einsum('bhij,bjhe->bihe', att, v).reshape(b, t, h * e)
        return out @ Wu + bu

    def _L1_ffn_ref(x, hl_w, hl_b, wq, wk, wv, gate_w, gate_b, ln_g, ln_b, fc1_w, fc1_b, fc2_w, fc2_b, fnorm_g, fnorm_b, fgate_w):
        import jax, jax.numpy as jnp
        import numpy as np
        B, S, H, NH, NE = (4, 256, 64, 4, 4)
        D = H // NH
        EPS = 1e-08

        def layernorm(x, g, b):
            m = jnp.mean(x, axis=-1, keepdims=True)
            v = jnp.mean((x - m) ** 2, axis=-1, keepdims=True)
            return (x - m) / jnp.sqrt(v + EPS) * g + b
        b, s, h = x.shape
        nh, d, _ = wk.shape
        ne = wq.shape[1]
        sx = jnp.einsum('bsh,ndh->bnsd', x, hl_w) + hl_b[None, :, None, :]
        pad = sx == 0
        q = jnp.einsum('bnsd,neod->bneso', sx, wq)
        k = jnp.einsum('bnsd,nod->bnso', sx, wk)
        v = jnp.einsum('bnsd,nod->bnso', sx, wv)
        causal = jnp.where(jnp.tril(jnp.ones((s, s), bool)), 0.0, -jnp.inf).astype(x.dtype)
        scores = jnp.einsum('bnesd,bntd->bnest', q, k) * d ** 0.5 + causal
        att = jax.nn.softmax(scores, axis=-1)
        qkv = jnp.einsum('bnest,bntd->bnesd', att, v)
        qkv = jnp.where(pad[:, :, None], 0.0, qkv)
        out = jnp.transpose(qkv, (0, 1, 3, 2, 4)).reshape(b, nh, s, ne * d)
        gs = jax.nn.softmax(jnp.einsum('bnsf,nef->bnse', out, gate_w) + gate_b[None, :, None, :], axis=-1)
        mixed = jnp.einsum('bnsed,bnse->bnsd', out.reshape(b, nh, s, ne, d), gs)
        resid = sx[jnp.arange(nh), jnp.arange(nh)]
        hn = layernorm(mixed + resid, ln_g, ln_b)
        f_n = jnp.transpose(hn, (0, 2, 1, 3)).reshape(b, s, h)
        fx = f_n.reshape(b, s, nh, d)
        pm = fx == 0
        hx = jnp.where(pm, 0.0, fx @ fc1_w.T + fc1_b)
        hx = jax.nn.relu(hx)
        hx = jnp.where(pm, 0.0, hx @ fc2_w.T + fc2_b)
        hx = layernorm(hx + fx, fnorm_g, fnorm_b)
        fout = hx.reshape(b, s, h)
        fg = jax.nn.softmax(fout @ fgate_w.T, axis=-1)
        return (fout.reshape(b, s, nh, d) * fg[..., None]).reshape(b, s, h)

    def _L2_attn_ref(normalized_resid_pre, W_Q, W_K, W_V, W_O, b_Q, b_K, b_V, b_O):
        import jax, jax.numpy as jnp
        import numpy as np
        N_HEADS, D_MODEL, D_HEAD = (8, 64, 32)
        BATCH, SEQ = (2, 512)
        INIT_RANGE = 0.02

        def _odd_causal_mask(S):
            i = jnp.arange(S)[:, None]
            j = jnp.arange(S)[None, :]
            allowed = (j < i) & (j % 2 == 1) | (i == j)
            return allowed
        x = normalized_resid_pre
        q = jnp.einsum('bsm,hmd->bshd', x, W_Q) + b_Q
        k = jnp.einsum('bsm,hmd->bshd', x, W_K) + b_K
        v = jnp.einsum('bsm,hmd->bshd', x, W_V) + b_V
        scale = 1.0 / jnp.sqrt(jnp.float32(D_HEAD))
        scores = jnp.einsum('bqhd,bkhd->bhqk', q, k) * scale
        allowed = _odd_causal_mask(scores.shape[-1])
        scores = jnp.where(allowed, scores, -jnp.inf)
        pattern = jax.nn.softmax(scores, axis=-1)
        z = jnp.einsum('bkhd,bhqk->bqhd', v, pattern)
        return jnp.einsum('bqhd,hdm->bqm', z, W_O) + b_O

    def _L2_ffn_ref(x, ln1_w, ln2_w, wq, wk, wv, wo, router_w, w1, w2, w3):
        import jax, jax.numpy as jnp
        import numpy as np
        B, T, C = (64, 96, 64)
        NH, NKV = (4, 2)
        HD = C // NH
        NREP = NH // NKV
        NE, TOPK = (8, 2)
        HID = int(8 / 3 * C)
        EPS_RMS = 1e-06

        def _rope_tables(t_len):
            inv_freq = 1.0 / 10000.0 ** (np.arange(0, HD, 2, dtype=np.float32) / HD)
            t = np.arange(t_len, dtype=np.float32)
            freqs = np.outer(t, inv_freq)
            emb = np.concatenate([freqs, freqs], axis=-1)
            return (jnp.asarray(np.cos(emb)), jnp.asarray(np.sin(emb)))

        def _rotate_half(x):
            h = x.shape[-1] // 2
            return jnp.concatenate([-x[..., h:], x[..., :h]], axis=-1)

        def _rmsnorm(v, w):
            return v * jax.lax.rsqrt(jnp.mean(v * v, axis=-1, keepdims=True) + EPS_RMS) * w
        Bx, Tx, Cx = x.shape
        h = _rmsnorm(x, ln1_w)
        q = (h @ wq.T).reshape(Bx, Tx, NH, HD).transpose(0, 2, 1, 3)
        k = (h @ wk.T).reshape(Bx, Tx, NKV, HD).transpose(0, 2, 1, 3)
        v = (h @ wv.T).reshape(Bx, Tx, NKV, HD).transpose(0, 2, 1, 3)
        cos, sin = _rope_tables(Tx)
        cos, sin = (cos[None, None], sin[None, None])
        q = q * cos + _rotate_half(q) * sin
        k = k * cos + _rotate_half(k) * sin
        k = jnp.repeat(k, NREP, axis=1)
        v = jnp.repeat(v, NREP, axis=1)
        scores = jnp.einsum('bhtd,bhsd->bhts', q, k) / jnp.sqrt(jnp.float32(HD))
        causal = jnp.tril(jnp.ones((Tx, Tx), dtype=bool))
        scores = jnp.where(causal[None, None], scores, jnp.float32(-1e+30))
        att = jax.nn.softmax(scores, axis=-1)
        y = jnp.einsum('bhts,bhsd->bhtd', att, v).transpose(0, 2, 1, 3).reshape(Bx, Tx, Cx)
        x = x + y @ wo.T
        flat = _rmsnorm(x, ln2_w).reshape(-1, Cx)
        probs = jax.nn.softmax(flat @ router_w.T, axis=-1)
        tp, ti = jax.lax.top_k(probs, TOPK)
        tp = tp / (jnp.sum(tp, axis=-1, keepdims=True) + 1e-09)
        weights = jnp.sum(tp[..., None] * jax.nn.one_hot(ti, NE, dtype=flat.dtype), axis=1)
        out = jnp.zeros_like(flat)
        for e in range(NE):
            hh = jax.nn.silu(flat @ w1[e].T) * (flat @ w3[e].T)
            out = out + weights[:, e:e + 1] * (hh @ w2[e].T)
        return x + out.reshape(Bx, Tx, Cx)

    def _L3_attn_ref(x, Wq, Wk, Wv):
        import jax, jax.numpy as jnp
        import numpy as np
        import math
        B, N, D = (4, 1024, 64)
        q = x @ Wq.T
        k = x @ Wk.T
        v = x @ Wv.T
        n = x.shape[1]
        d_k = x.shape[2]
        mask = jnp.triu(jnp.ones((n, n), dtype=x.dtype), k=1)
        scale = jnp.asarray(1.0 / math.sqrt(d_k), dtype=x.dtype)
        s = (jnp.einsum('bnd,bmd->bnm', q, k) - (1.0 - mask) * 10000000000.0) * scale
        s = jax.nn.softmax(s, axis=1)
        return jnp.einsum('bnm,bmd->bnd', s, v)

    def _L3_ffn_ref(h, gate_w, gate_b, w1, b1, w2, b2):
        import math
        import jax, jax.numpy as jnp
        import numpy as np
        CAPACITY_FACTOR = 1.25
        B, L, D = h.shape
        E = gate_w.shape[1]
        T = B * L
        C = max(1, math.ceil(CAPACITY_FACTOR * T / E))
        x = h.reshape(T, D)
        logits = x @ gate_w + gate_b
        probs = jax.nn.softmax(logits, axis=-1)
        idx = jnp.argmax(probs, axis=-1)
        prb = jnp.take_along_axis(probs, idx[:, None], axis=1)[:, 0]
        one_hot = jax.nn.one_hot(idx, E, dtype=jnp.float32)
        pos = (jnp.cumsum(one_hot, axis=0) * one_hot).sum(-1).astype(jnp.int32) - 1
        kept = pos < C
        pos_safe = jnp.where(kept, pos, C)
        buf = jnp.zeros((E, C, D), dtype=h.dtype).at[idx, pos_safe].set(x, mode='drop')
        hmid = jax.nn.relu(jnp.einsum('ecd,edf->ecf', buf, w1) + b1[:, None, :])
        ybuf = jnp.einsum('ecf,efd->ecd', hmid, w2) + b2[:, None, :]
        pos_g = jnp.minimum(pos, C - 1)
        y_tok = ybuf[idx, pos_g] * (prb * kept)[:, None]
        y = y_tok.reshape(B, L, D)
        y = jnp.nan_to_num(y, nan=0.0, posinf=10000.0, neginf=-10000.0)
        return y
    h = _L0_tok_ref(x, L0_tok_turns, L0_tok_poly_coeffs)
    h = h + _L0_attn_ref(_layernorm(h, axis=-1), L0_attn_ln1_g, L0_attn_ln1_b, L0_attn_qkv_w, L0_attn_qkv_b, L0_attn_bias_table, L0_attn_scale, L0_attn_proj_w, L0_attn_proj_b, L0_attn_ln2_g, L0_attn_ln2_b)
    h = h + _L0_ffn_ref(_layernorm(h, axis=-1), L0_ffn_gate_w, L0_ffn_gate_b, L0_ffn_w1, L0_ffn_b1, L0_ffn_w2, L0_ffn_b2, L0_ffn_gamma, L0_ffn_beta)
    h = h + _L1_attn_ref(_layernorm(h, axis=-1), L1_attn_Wq, L1_attn_bq, L1_attn_Wk, L1_attn_bk, L1_attn_Wv, L1_attn_bv, L1_attn_Wu, L1_attn_bu)
    h = h + _L1_ffn_ref(_layernorm(h, axis=-1), L1_ffn_hl_w, L1_ffn_hl_b, L1_ffn_wq, L1_ffn_wk, L1_ffn_wv, L1_ffn_gate_w, L1_ffn_gate_b, L1_ffn_ln_g, L1_ffn_ln_b, L1_ffn_fc1_w, L1_ffn_fc1_b, L1_ffn_fc2_w, L1_ffn_fc2_b, L1_ffn_fnorm_g, L1_ffn_fnorm_b, L1_ffn_fgate_w)
    h = h + _L2_attn_ref(_layernorm(h, axis=-1), L2_attn_W_Q, L2_attn_W_K, L2_attn_W_V, L2_attn_W_O, L2_attn_b_Q, L2_attn_b_K, L2_attn_b_V, L2_attn_b_O)
    h = h + _L2_ffn_ref(_layernorm(h, axis=-1), L2_ffn_ln1_w, L2_ffn_ln2_w, L2_ffn_wq, L2_ffn_wk, L2_ffn_wv, L2_ffn_wo, L2_ffn_router_w, L2_ffn_w1, L2_ffn_w2, L2_ffn_w3)
    h = h + _L3_attn_ref(_layernorm(h, axis=-1), L3_attn_Wq, L3_attn_Wk, L3_attn_Wv)
    h = h + _L3_ffn_ref(_layernorm(h, axis=-1), L3_ffn_gate_w, L3_ffn_gate_b, L3_ffn_w1, L3_ffn_b1, L3_ffn_w2, L3_ffn_b2)
    return h

_drawn_inputs = setup_inputs


def setup_inputs(seed=0):
    import zlib

    import numpy as np

    out = dict(_drawn_inputs(seed))
    spreads = {'L0_attn_ln1_g': (1.0, 0.6),
     'L0_attn_ln1_b': (0.0, 0.8),
     'L0_attn_qkv_b': (0.0, 0.8),
     'L0_attn_proj_b': (0.0, 0.1),
     'L0_attn_ln2_g': (1.0, 0.2),
     'L0_attn_ln2_b': (0.0, 0.402),
     'L0_ffn_gate_b': (0.0, 0.8),
     'L0_ffn_b1': (0.0, 0.8),
     'L0_ffn_b2': (0.0, 0.8),
     'L0_ffn_gamma': (1.0, 0.599),
     'L0_ffn_beta': (0.0, 0.602),
     'L1_attn_bq': (0.0, 0.8),
     'L1_attn_bk': (0.0, 2.0),
     'L1_attn_bv': (0.0, 0.8),
     'L1_attn_bu': (0.0, 0.643),
     'L1_ffn_ln_g': (1.0, 0.6),
     'L1_ffn_ln_b': (0.0, 0.8),
     'L1_ffn_fnorm_g': (1.0, 0.6),
     'L1_ffn_fnorm_b': (0.0, 0.8),
     'L2_attn_b_Q': (0.0, 0.8),
     'L2_attn_b_K': (0.0, 2.0),
     'L2_attn_b_V': (0.0, 0.8),
     'L2_attn_b_O': (0.0, 0.599),
     'L2_ffn_ln1_w': (1.0, 0.6),
     'L2_ffn_ln2_w': (1.0, 0.6),
     'L3_ffn_gate_b': (0.0, 0.8),
     'L3_ffn_b1': (0.0, 0.8),
     'L3_ffn_b2': (0.0, 2.0)}
    factors = {'L0_attn_qkv_w': 8.0,
     'L0_attn_bias_table': 8.0,
     'L0_attn_proj_w': 8.0,
     'L0_ffn_gate_w': 7.228,
     'L0_ffn_w1': 8.0,
     'L0_ffn_w2': 8.0,
     'L1_attn_Wq': 8.0,
     'L1_attn_Wk': 8.0,
     'L1_attn_Wv': 8.0,
     'L1_attn_Wu': 8.0,
     'L1_ffn_hl_b': 8.0,
     'L1_ffn_wq': 8.0,
     'L1_ffn_wk': 8.0,
     'L1_ffn_wv': 8.0,
     'L1_ffn_gate_w': 8.0,
     'L1_ffn_gate_b': 8.0,
     'L1_ffn_fc1_w': 8.0,
     'L1_ffn_fc1_b': 8.0,
     'L1_ffn_fc2_w': 8.0,
     'L1_ffn_fc2_b': 8.0,
     'L1_ffn_fgate_w': 6.889,
     'L2_attn_W_Q': 8.0,
     'L2_attn_W_K': 8.0,
     'L2_attn_W_V': 8.0,
     'L2_attn_W_O': 8.0,
     'L2_ffn_wq': 8.0,
     'L2_ffn_wk': 8.0,
     'L2_ffn_wv': 8.0,
     'L2_ffn_wo': 8.0,
     'L2_ffn_router_w': 8.0,
     'L2_ffn_w1': 8.0,
     'L2_ffn_w2': 8.0,
     'L2_ffn_w3': 8.0,
     'L3_ffn_gate_w': 8.0,
     'L3_ffn_w1': 8.0,
     'L3_ffn_w2': 8.0}
    for name, (base, spread) in spreads.items():
        noise = np.random.default_rng([zlib.crc32(name.encode()), seed]).standard_normal(out[name].shape)
        drawn = base * np.exp(spread * noise) if base else spread * noise
        out[name] = jnp.asarray(drawn.astype(out[name].dtype))
    for name, factor in factors.items():
        out[name] = (out[name] * factor).astype(out[name].dtype)
    return out
```

```python
from contextlib import ExitStack

import numpy as np
import concourse.bass as bass
from concourse import mybir

F32 = mybir.dt.float32
BF16 = mybir.dt.bfloat16
I32 = mybir.dt.int32
U32 = mybir.dt.uint32
ALU = mybir.AluOpType
ACT = mybir.ActivationFunctionType
AX = mybir.AxisListType

P = 128
SEQS, SEQ, C = 64, 256, 64
TILES = SEQS * SEQ // P
GT = 4
GROUPS = TILES // GT
NTOK = GT * P
BIG = 3.0e38
MASKED = -1.0e30
VOCAB, TURNS, DEG = 50257, 4, 5
E0, F0 = 16, 128
E2, F2, F2C = 8, 170, 85
E3, F3 = 8, 256
CAP3 = -(-5 * SEQS * SEQ // (4 * E3))

IMAGE = [
    ("ident", P, 0), ("coef", 4 * C, 0), ("rank", 16, 0),
    ("a0_qk", 128, 0), ("a0_v", C, 0), ("a0_lnw", 2, 0), ("a0_qkb", 2, 0), ("a0_vb", C, 0), ("a0_bias", 4 * P, 0),
    ("a0_scale", 1, 0), ("a0_o", C, 0), ("a0_ob", C, 0), ("a0_g2", C, 0), ("a0_b2", C, 0),
    ("f0_gw", E0, 1), ("f0_gb", E0, 1), ("f0_w1", E0 // 2 * F0, 1), ("f0_b1", E0, 1), ("f0_w2", E0 * C, 1),
    ("f0_b2", GT * C, 1), ("f0_g", C, 1), ("f0_b", C, 1),
    ("a1_q", 512, 2), ("a1_k", 512, 2), ("a1_v", 512, 2), ("a1_o", 4 * C, 2), ("a1_qb", 4, 2), ("a1_kb", 4, 2),
    ("a1_vb", 512, 2), ("a1_ob", C, 2), ("row0", 2, 2),
    ("f1_hl", C, 3), ("f1_hlb", 1, 3), ("f1_hlbr", C, 3), ("f1_q", 4 * P, 3), ("f1_k", P, 3), ("f1_v", C, 3),
    ("f1_g", 32, 3), ("f1_gb", 16, 3), ("f1_lg", 16, 3), ("f1_lb", 16, 3), ("f1_1", C, 3), ("f1_1b", 1, 3),
    ("f1_2", C, 3), ("f1_2b", 16, 3), ("f1_ng", 16, 3), ("f1_nb", 16, 3), ("f1_fg", 4, 3),
    ("a2_q", 256, 4), ("a2_k", 256, 4), ("a2_v", 256, 4), ("a2_qb", 2, 4), ("a2_kb", 2, 4), ("a2_vb", 256, 4),
    ("a2_o", 2 * C, 4), ("a2_ob", C, 4),
    ("r2_ln", 1, 5), ("r2_q", P, 5), ("r2_qp", P, 5), ("r2_k", P, 5), ("r2_kp", P, 5), ("r2_v", 32, 5), ("r2_o", C, 5),
    ("r2_cq", SEQ, 5), ("r2_sq", SEQ, 5), ("r2_ck", SEQ, 5), ("r2_sk", SEQ, 5),
    ("f2_ln", 1, 6), ("f2_gw", E2, 6), ("f2_w1", E2 * F2C, 6), ("f2_w3", E2 * F2C, 6), ("f2_w2", 2 * E2 * C, 6),
    ("a3_q", C, 7), ("a3_k", C, 7), ("a3_v", C, 7), ("a3_mask", 4 * P, 7),
    ("f3_gw", E3, 8), ("f3_gb", E3, 8), ("f3_w1", E3 * P, 8), ("f3_b1", 2 * E3, 8), ("f3_w2", 2 * E3 * C, 8),
    ("f3_b2", GT * C, 8), ("tri", P, 8), ("ones", P, 8),
]
LOADS = 9


LATE = LOADS - 1


def image_offsets():
    at, out, starts, dram = 0, {}, [], 0
    for k in range(LOADS):
        if k == LATE:
            total, at = at, starts[1][0]
        cols = sum(c for _, c, g in IMAGE if g == k)
        starts.append((at, dram, cols))
        dram += cols
        for name, cols, group in IMAGE:
            if group == k:
                out[name] = (at, cols)
                at += cols
    assert at <= starts[3][0]
    return out, total, starts


class Count:

    def __init__(self, sem):
        self.sem, self.base, self.per, self.credit = sem, 0, 0, 0

    def stage(self, per, credit=0):
        self.per, self.credit = per, credit

    def after(self, i, n=0):
        return i * self.per + (self.base + self.credit + n)

    def close(self, groups):
        self.base += self.credit + groups * self.per
        self.per = self.credit = 0


def rows(ap, n, inner):
    return ap.rearrange("p (a c) -> p a c", a=1).to_broadcast([P, n, inner])


class Core:

    def __init__(self, nc, ctx):
        self.nc, self.ctx = nc, ctx
        self.off, total, self.starts = image_offsets()
        self.h = ctx.enter_context(nc.sbuf_tensor("h", [P, TILES + GT, C], F32))
        self.w = ctx.enter_context(nc.sbuf_tensor("weights", [P, total], F32))
        self.wb = ctx.enter_context(nc.sbuf_tensor("masks", [P, 18, P], BF16))
        self.xn = ctx.enter_context(nc.sbuf_tensor("xn", [P, GT, 2, C], F32))
        self.xU = ctx.enter_context(nc.sbuf_tensor("xT_upper", [P, NTOK], F32))
        self.xL = ctx.enter_context(nc.sbuf_tensor("xT_lower", [P, NTOK], F32))
        self.bnst = ctx.enter_context(nc.sbuf_tensor("bnst", [P, GT, 6], F32))
        self.mv = ctx.enter_context(nc.sbuf_tensor("mv", [P, GT, 2], F32))
        self.rstd = ctx.enter_context(nc.sbuf_tensor("rstd", [P, GT], F32))
        self.rwork = ctx.enter_context(nc.sbuf_tensor("rwork", [P, 4, 16], F32))
        self.half = ctx.enter_context(nc.sbuf_tensor("minus_half", [P, 16], F32))
        self.bank = [ctx.enter_context(nc.psum_tensor(f"bank{b}", [P, 512], F32)) for b in range(8)]
        self.counts = {}
        self.carrier = ctx.enter_context(nc.semaphore("wait_carrier"))
        self.loaded = [ctx.enter_context(nc.semaphore(f"loaded{k}")) for k in range(LOADS)]

    def count(self, name):
        if name not in self.counts:
            self.counts[name] = Count(self.ctx.enter_context(self.nc.semaphore(name)))
        return self.counts[name]

    def W(self, name, p0=0, p1=P):
        at, cols = self.off[name]
        return self.w[p0:p1, at:at + cols]

    def settle(self, eng):
        eng.sem_inc(self.carrier, 1)

    def hgroup(self, i):
        return self.h[:, bass.ds(i * GT, GT), :]


def link(eng, cnt, i, step, K=None):
    def then(ins, wait=True, settle=False):
        step[0] += 1
        ins.then_inc(cnt.sem, 1)
        if wait:
            eng.wait_ge(cnt.sem, cnt.after(i, step[0]))
        if settle:
            K.settle(eng)
    return then


class Front:

    def __init__(self, K, kind, eps, dup=False, scale=None, bias=None, src=None, kept=None):
        self.K, self.kind, self.eps, self.dup = K, kind, eps, dup
        self.scale, self.bias, self.src, self.kept = scale, bias, K.h if src is None else src, kept
        self.vec, self.stats, self.rs = K.count("front_vec"), K.count("stats_ready"), K.count("rstd_ready")
        self.pool, self.xn_r = K.count("front_pool"), K.count("xn_ready")
        self.xt_ps, self.xt_r = K.count("xT_in_psum"), K.count("xT_ready")
        self.passes = len(eps)
        self.vec.stage({"ln": 1, "lnln": 3, "rms": 2, "lnrms": 4}[kind])
        self.stats.stage(self.passes)
        self.rs.stage(self.passes)
        self.pool.stage(self.passes)
        self.xn_r.stage(1)
        self.xt_ps.stage(1, 1)
        self.xt_r.stage(1)

    def close(self, groups=GROUPS + 1):
        for c in (self.vec, self.stats, self.rs, self.pool, self.xn_r, self.xt_ps, self.xt_r):
            c.close(groups)

    def open_pe(self, pe):
        pe.sem_inc(self.xt_ps.sem, 1)

    def mean_var(self, v, src, lk):
        K = self.K
        for j in range(GT):
            ins = v.bn_stats(K.bnst[:, j, :], src(j))
        lk(ins, settle=True)
        for j in range(GT):
            ins = v.bn_aggr(K.mv[:, j, :], K.bnst[:, j, :])
        ins.then_inc(self.stats.sem, 1)

    def mean_square(self, v, src, lk):
        K = self.K
        lk(v.tensor_tensor(K.xn[:, :, 0, :], src, src, ALU.mult))
        lk(v.tensor_reduce(K.mv[:, :, 0], K.xn[:, :, 0, :], AX.X, ALU.add))
        v.tensor_scalar(K.mv[:, :, 1], K.mv[:, :, 0], 1.0 / C, None, ALU.mult).then_inc(self.stats.sem, 1)

    def statistics(self, v, i):
        self.lk = link(v, self.vec, i, [0], self.K)
        if self.kind == "rms":
            v.wait_ge(self.xt_ps.sem, self.xt_ps.after(i, 0))
            self.mean_square(v, self.src[:, bass.ds(i * GT, GT), :], self.lk)
        else:
            self.mean_var(v, lambda j: self.src[:, bass.ds(i * GT + j, 1), :], self.lk)

    def rstds(self, g, i):
        K = self.K
        for n, eps in enumerate(self.eps):
            g.wait_ge(self.stats.sem, self.stats.after(i, n + 1))
            K.settle(g)
            g.tensor_scalar(K.rwork[:, 0, 0:GT], K.mv[:, :, 1], eps, None, ALU.add).then_inc(self.pool.sem, 1)
            g.wait_ge(self.pool.sem, self.pool.after(i, n + 1))
            g.tensor_tensor(K.rstd[:, :], K.rwork[:, 0, 0:GT], K.half[:, 0:GT], ALU.pow).then_inc(self.rs.sem, 1)

    def normalise(self, v, i):
        K = self.K
        v.wait_ge(self.rs.sem, self.rs.after(i, 1))
        v.wait_ge(self.xt_ps.sem, self.xt_ps.after(i, 0))
        centred = (lambda dst, src, j: v.tensor_scalar(dst, src, K.mv[:, j, 0:1], K.rstd[:, j:j + 1], ALU.subtract, ALU.mult))
        scaled = (lambda dst, src, j: v.tensor_scalar(dst, src, K.rstd[:, j:j + 1], None, ALU.mult))
        tile = (lambda j: self.src[:, bass.ds(i * GT + j, 1), :])
        last = centred
        if self.kind == "lnln":
            for j in range(GT):
                ins = centred(K.xn[:, j, 0, :], tile(j), j)
            self.lk(ins)
            self.mean_var(v, lambda j: K.xn[:, j, 0, :], self.lk)
            tile = (lambda j: K.xn[:, j, 0, :])
        elif self.kind == "lnrms":
            for j in range(GT):
                ins = centred(self.kept[:, bass.ds(i * GT + j, 1), :], tile(j), j)
            self.lk(ins)
            self.mean_square(v, self.kept[:, bass.ds(i * GT, GT), :], self.lk)
            tile = (lambda j: self.kept[:, bass.ds(i * GT + j, 1), :])
        if self.passes == 2:
            v.wait_ge(self.rs.sem, self.rs.after(i, 2))
        if "rms" in self.kind:
            last = scaled
        for j in range(GT):
            for d in range(2 if self.dup else 1):
                ins = last(K.xn[:, j, d, :], tile(j), j)
        ins.then_inc(self.xn_r.sem, 1)

    def transpose(self, pe, i, bank):
        K = self.K
        pe.wait_ge(self.xn_r.sem, self.xn_r.after(i, 1))
        K.settle(pe)
        for j in range(GT):
            if self.dup:
                ins = pe.transpose(K.bank[bank][:, j * P:(j + 1) * P], K.xn[:, j, :, :].rearrange("p a c -> p (a c)"), K.W("ident"))
            else:
                ins = pe.transpose(K.bank[bank][0:C, j * P:(j + 1) * P], K.xn[:, j, 0, :], K.W("ident"))
        ins.then_inc(self.xt_ps.sem, 1)

    def move(self, a, i, bank):
        K = self.K
        a.wait_ge(self.xt_ps.sem, self.xt_ps.after(i, 1))
        for dst, p0 in ((K.xU, 0), (K.xL, C))[:2 if self.dup else 1]:
            r = slice(p0, p0 + C)
            if self.scale is None:
                ins = a.activation(dst[r, :], K.bank[bank][r, :], ACT.Copy)
            elif self.bias is None:
                ins = a.activation(dst[r, :], K.bank[bank][r, :], ACT.Copy, scale=self.scale[r, :])
            else:
                ins = a.activation(dst[r, :], K.bank[bank][r, :], ACT.Identity, scale=self.scale[r, :], bias=self.bias[r, :])
        ins.then_inc(self.xt_r.sem, 1)


def embed_stage(K, x, turns, image, masks):
    nc = K.nc
    HALF = 4
    CT = TILES // HALF
    feat_r, ft_ps, ft_sb, emb_ps, emb_r = (K.count(n) for n in ("features_ready", "featT_in_psum", "featT_ready",
                                                                "emb_in_psum", "emb_ready"))
    with ExitStack() as ctx:
        def sb(n, s, d=F32):
            return ctx.enter_context(nc.sbuf_tensor(n, s, d))
        ids = sb("ids", [P, TILES], I32)
        rowsT = sb("turn_rows", [P, TILES * TURNS])
        absT = sb("turn_abs", [P, TILES * TURNS])
        intT = sb("turn_int", [P, TILES * TURNS], I32)
        feat = sb("features", [P, TILES, 32])
        fstage = sb("feature_stage", [P, 2, P])
        featT = sb("featT", [P, 2, P])
        masks_in = sb("masks_in", [P, 18, P])
        masks_loaded = K.count("masks_loaded")
        ids_in, gathered = K.count("ids_in"), [K.count(f"gathered{c}") for c in range(HALF)]
        vec, zeroed, staged = K.count("embed_vec"), K.count("zeroed"), K.count("feature_staged")
        for c in (feat_r, ft_ps, ft_sb, emb_ps, emb_r, staged):
            c.stage(1)
        block = ctx.enter_context(nc.Block())

        @block.sync
        def _(sp):
            sp.dma_start(ids[:, :], x).then_inc(ids_in.sem, 16)
            sp.dma_start(masks_in[:, :, :], masks).then_inc(masks_loaded.sem, 16)
            for k in range(LATE):
                at, src, cols = K.starts[k]
                sp.dma_start(K.w[:, at:at + cols], image[:, src:src + cols]).then_inc(K.loaded[k], 16)

        @block.gpsimd
        def _(g):
            g.memset(K.half[:, :], -0.5)
            g.memset(K.h[:, TILES:TILES + GT, :], 0.0)
            g.memset(feat[:, :, TURNS * DEG:32], 0.0)
            g.memset(feat[:, :, 0:TURNS], 1.0).then_inc(zeroed.sem, 1)
            g.wait_ge(ids_in.sem, 16)
            for c in range(HALF):
                for j in range(c * CT, (c + 1) * CT):
                    g.indirect_dma_start(rowsT[:, j * TURNS:(j + 1) * TURNS], None, turns,
                                         bass.IndirectOffsetOnAxis(ids[:, j:j + 1].bitcast(U32), 0)).then_inc(gathered[c].sem, 16)

        per_chunk = GROUPS // HALF

        @block.scalar
        def _(a):
            a.preload_act_table(ACT.Exp)
            for c in range(HALF):
                a.wait_ge(feat_r.sem, c + 1)
                with a.Fori(c * per_chunk // 2, (c + 1) * per_chunk // 2) as i0:
                    for u in range(2):
                        i = i0 * 2 + u
                        a.wait_ge(emb_ps.sem, i + 1)
                        a.activation(fstage[:, u, :], feat[:, bass.ds(i * GT, GT), :], ACT.Copy).then_inc(staged.sem, 1)
                        a.wait_ge(ft_ps.sem, i + 1)
                        a.activation(featT[:, u, :], K.bank[u][:, 0:P], ACT.Copy).then_inc(ft_sb.sem, 1)

        @block.tensor
        def _(pe):
            pe.wait_ge(K.loaded[0], 16)
            pe.sem_inc(emb_ps.sem, 1)
            with pe.Fori(0, GROUPS // 2) as i0:
                for u in range(2):
                    i = i0 * 2 + u
                    pe.wait_ge(staged.sem, i + 1)
                    pe.transpose(K.bank[u][:, 0:P], fstage[:, u, :], K.W("ident")).then_inc(ft_ps.sem, 1)
                    pe.wait_ge(ft_sb.sem, i + 1)
                    pe.wait_ge(emb_r.sem, i0 * 2 + 1)
                    pe.matmul(K.bank[2 + u][:, 0:GT * C], featT[:, u, :], K.W("coef"), start=True, stop=True)\
                        .then_inc(emb_ps.sem, 1)

        @block.vector
        def _(v):
            n = 0
            v.memset(K.xU[C:P, :], 0.0)
            v.memset(K.xL[0:C, :], 0.0)
            v.wait_ge(masks_loaded.sem, 16)
            v.tensor_copy(K.wb[:, :, :], masks_in[:, :, :])
            v.wait_ge(zeroed.sem, 1)

            def lk(ins):
                nonlocal n
                n += 1
                ins.then_inc(vec.sem, 1)
                v.wait_ge(vec.sem, n)
            for c in range(HALF):
                v.wait_ge(gathered[c].sem, 16 * CT)
                s = slice(c * CT * TURNS, (c + 1) * CT * TURNS)
                t, a, k = rowsT[:, s], absT[:, s], intT[:, s]
                lk(v.scalar_tensor_tensor(a, t, -1.0, t, ALU.mult, ALU.max))
                lk(v.tensor_copy(k, a))
                f1 = feat[:, c * CT:(c + 1) * CT, TURNS:2 * TURNS]
                a3 = a.rearrange("p (j d) -> p j d", d=TURNS)
                t3 = t.rearrange("p (j d) -> p j d", d=TURNS)
                lk(v.tensor_copy(f1, k.rearrange("p (j d) -> p j d", d=TURNS)))
                lk(v.tensor_tensor(a3, f1, a3, ALU.is_gt))
                lk(v.tensor_tensor(f1, f1, a3, ALU.subtract))
                lk(v.tensor_scalar(a, t, 0.0, 2.0, ALU.is_ge, ALU.mult))
                lk(v.tensor_scalar(a, a, -1.0, None, ALU.add))
                lk(v.tensor_tensor(f1, f1, a3, ALU.mult))
                for d in range(2, DEG):
                    prev = feat[:, c * CT:(c + 1) * CT, (d - 1) * TURNS:d * TURNS]
                    cur = feat[:, c * CT:(c + 1) * CT, d * TURNS:(d + 1) * TURNS]
                    ins = v.tensor_tensor(cur, prev, f1, ALU.mult)
                    if d < DEG - 1:
                        lk(ins)
                ins.then_inc(feat_r.sem, 1)
            v.sem_inc(emb_r.sem, 1)
            with v.Fori(0, GROUPS // 2) as i0:
                for u in range(2):
                    i = i0 * 2 + u
                    v.wait_ge(emb_ps.sem, i + 2)
                    v.tensor_copy(K.hgroup(i), K.bank[2 + u][:, 0:GT * C].rearrange("p (j c) -> p j c", j=GT))\
                        .then_inc(emb_r.sem, 1)


def late_weights(K, image):
    with K.nc.Block() as block:
        @block.sync
        def _(sp):
            at, src, cols = K.starts[LATE]
            sp.dma_start(K.w[:, at:at + cols], image[:, src:src + cols]).then_inc(K.loaded[LATE], 16)


def store_stage(K, out):
    nc = K.nc
    done = K.count("stored")
    with nc.Block() as block:
        @block.sync
        def _(sp):
            o = out.rearrange("b (a p) c -> p (b a) c", p=P)
            for k in range(8):
                n = TILES // 8
                sp.dma_start(o[:, k * n:(k + 1) * n, :], K.h[:, k * n:(k + 1) * n, :]).then_inc(done.sem, 16)
            sp.wait_ge(done.sem, 128)


class Unit:

    def __init__(self, scores, masks, softs, outs, vw, dest):
        self.scores, self.masks, self.softs, self.outs, self.vw, self.dest = scores, masks, softs, outs, vw, dest
        self.cols = max(c + r * w for c, r, w in softs)
        self.rows = sum(r for _, r, _ in softs)


SB = (0, 1, 2)
TB = (3, 4)
OB = (5, 6)
RP = 3


class Units:

    def __init__(self, K, ctx, units, bias=None, rownorm=None):
        nc = K.nc
        self.K, self.units, self.bias, self.rownorm = K, units, bias, rownorm
        self.N = len(units)
        self.p = ctx.enter_context(nc.sbuf_tensor(f"probs_{nc.next_id()}", [P, RP, 512], F32))
        self.pT = ctx.enter_context(nc.sbuf_tensor(f"probsT_{nc.next_id()}", [P, 2, 512], F32))
        self.nm = ctx.enter_context(nc.sbuf_tensor(f"negmax_{nc.next_id()}", [P, 4, 4], F32))
        self.rd = ctx.enter_context(nc.sbuf_tensor(f"rden_{nc.next_id()}", [P, 2, 4], F32))
        if bias is not None:
            self.sb = ctx.enter_context(nc.sbuf_tensor(f"biased_{nc.next_id()}", [P, 4, 512], F32))
        names = ("scores_ready", "max_ready", "probs_ready", "probsT_in_psum", "probsT_ready", "values_summed", "normalised")
        self.sc, self.mx, self.ex, self.tp, self.tr, self.pv, self.no = (K.count(n) for n in names)
        self.vec = K.count("unit_vec")
        for c, credit in ((self.sc, 0), (self.mx, 0), (self.ex, 4), (self.tp, RP), (self.tr, 2), (self.pv, 2), (self.no, 2)):
            c.stage(self.N, credit)
        self.vec.stage(self.N * (1 + (bias is not None) + (rownorm is not None)))

    def close(self):
        for c in (self.sc, self.mx, self.ex, self.tp, self.tr, self.pv, self.no, self.vec):
            c.close(GROUPS)

    def open_pe(self, pe):
        pe.sem_inc(self.tp.sem, RP)
        pe.sem_inc(self.pv.sem, 2)

    def open_act(self, a):
        a.sem_inc(self.ex.sem, 4)
        a.sem_inc(self.tr.sem, 2)

    def open_vec(self, v):
        v.sem_inc(self.no.sem, 2)

    def tensor(self, pe, i, splice):
        K = self.K
        for s in range(self.N + 3):
            if s < self.N:
                u, b = self.units[s], K.bank[SB[s % 3]]
                pe.wait_ge(self.ex.sem, self.ex.after(i, s - 2))
                for n, (c, w, lhsT, rhs) in enumerate(u.scores):
                    ins = pe.matmul(b[:, c:c + w], lhsT, rhs, start=n == 0 or not u.masks, stop=not u.masks, skip_group_check=True)
                for n, (c, w, m) in enumerate(u.masks):
                    ins = pe.matmul(b[:, c:c + w], K.wb[:, 0, :], m, start=False, stop=True, skip_group_check=True)
                ins.then_inc(self.sc.sem, 1)
            if s in splice:
                splice[s](pe)
            if 0 <= s - 2 < self.N:
                t = s - 2
                pe.wait_ge(self.ex.sem, self.ex.after(i, t + 1))
                pe.wait_ge(self.tr.sem, self.tr.after(i, t - 1))
                for c in range(0, self.units[t].cols, P):
                    ins = pe.transpose(K.bank[TB[t % 2]][:, c:c + P], self.p[:, t % RP, c:c + P], K.W("ident"))
                ins.then_inc(self.tp.sem, 1)
            if 0 <= s - 3:
                t = s - 3
                u = self.units[t]
                pe.wait_ge(self.tr.sem, self.tr.after(i, t + 1))
                pe.wait_ge(self.no.sem, self.no.after(i, t - 1))
                for n, terms in enumerate(u.outs):
                    for m, (blk, val) in enumerate(terms):
                        ins = pe.matmul(K.bank[OB[t % 2]][:, n * u.vw:(n + 1) * u.vw], self.pT[:, t % 2, blk * P:(blk + 1) * P], val,
                                        start=m == 0, stop=m == len(terms) - 1, skip_group_check=True)
                ins.then_inc(self.pv.sem, 1)

    def vector(self, v, i, splice):
        K = self.K
        st = [0]
        lk = link(v, self.vec, i, st, K)
        for s in range(self.N + 4):
            if s < self.N:
                u, b = self.units[s], K.bank[SB[s % 3]]
                v.wait_ge(self.sc.sem, self.sc.after(i, s + 1))
                v.wait_ge(self.ex.sem, self.ex.after(i, s - 3))
                src = b
                if self.bias is not None:
                    lk(v.tensor_tensor(self.sb[:, s % 4, :], b[:, :], self.bias, ALU.add))
                    src = self.sb[:, s % 4, :]
                r = 0
                for n, (c, k, w) in enumerate(u.softs):
                    ins = v.tensor_reduce(self.nm[:, s % 4, r:r + k], src[:, c:c + k * w].rearrange("p (a b) -> p a b", a=k),
                                          AX.X, ALU.max, negate=True)
                    r += k
                ins.then_inc(self.mx.sem, 1)
            if s in splice:
                splice[s](v)
            if s >= 4:
                t = s - 4
                u = self.units[t]
                o = K.bank[OB[t % 2]][:, 0:len(u.outs) * u.vw].rearrange("p (a c) -> p a c", c=u.vw)
                n = len(u.outs)
                v.wait_ge(self.pv.sem, self.pv.after(i, t + 1))
                lk(v.reciprocal(self.rd[:, t % 2, 0:n].rearrange("p (a c) -> p a c", c=1), o[:, :, u.vw - 1:u.vw]))
                if self.rownorm is not None:
                    lk(v.tensor_tensor(self.rd[:, t % 2, 0:n], self.rd[:, t % 2, 0:n], self.rownorm(t, n), ALU.mult))
                v.tensor_tensor(u.dest, o[:, :, 0:u.vw - 1],
                                self.rd[:, t % 2, 0:n].rearrange("p (a c) -> p a c", c=1).to_broadcast([P, n, u.vw - 1]), ALU.mult)\
                    .then_inc(self.no.sem, 1)

    def scalar(self, a, i, splice):
        K = self.K
        for s in range(self.N + 2):
            if s < self.N:
                u = self.units[s]
                a.wait_ge(self.mx.sem, self.mx.after(i, s + 1))
                a.wait_ge(self.tp.sem, self.tp.after(i, s - RP + 1))
                src = K.bank[SB[s % 3]] if self.bias is None else self.sb[:, s % 4, :]
                r = 0
                for c, k, w in u.softs:
                    for m in range(k):
                        ins = a.activation(self.p[:, s % RP, c + m * w:c + (m + 1) * w], src[:, c + m * w:c + (m + 1) * w],
                                           ACT.Exp, bias=self.nm[:, s % 4, r:r + 1])
                        r += 1
                ins.then_inc(self.ex.sem, 1)
            if s in splice:
                splice[s](a)
            if s >= 2:
                t = s - 2
                a.wait_ge(self.tp.sem, self.tp.after(i, t + 1))
                a.wait_ge(self.pv.sem, self.pv.after(i, t - 1))
                n = self.units[t].cols
                a.activation(self.pT[:, t % 2, 0:n], K.bank[TB[t % 2]][:, 0:n], ACT.Copy).then_inc(self.tr.sem, 1)


PB = (0, 1, 2, 7)


class Projections:

    def __init__(self, K, jobs):
        self.K, self.jobs = K, jobs
        self.ready, self.by = K.count("projection_ready"), {"act": K.count("projection_moved_act"), "vec": K.count("projection_moved_vec")}
        self.ready.stage(len(jobs))
        self.idx = []
        seen = {"act": 0, "vec": 0}
        for who, *_ in jobs:
            seen[who] += 1
            self.idx.append(seen[who])
        for who in seen:
            self.by[who].stage(seen[who])
        self.seen = seen

    def close(self):
        for c in (self.ready, *self.by.values()):
            c.close(GROUPS + 1)

    def tensor(self, pe, i):
        for j, (who, mm, _) in enumerate(self.jobs):
            if j >= len(PB):
                w = self.jobs[j - len(PB)][0]
                pe.wait_ge(self.by[w].sem, self.by[w].after(i, self.idx[j - len(PB)]))
            elif j == 0:
                for w, n in self.seen.items():
                    if n:
                        pe.wait_ge(self.by[w].sem, self.by[w].after(i, 0))
            self.K.settle(pe)
            mm(pe, self.K.bank[PB[j % 4]], i).then_inc(self.ready.sem, 1)

    def move(self, eng, who, i):
        for j, (w, _, mv) in enumerate(self.jobs):
            if w == who:
                eng.wait_ge(self.ready.sem, self.ready.after(i, j + 1))
                mv(eng, self.K.bank[PB[j % 4]], i).then_inc(self.by[who].sem, 1)

    def wait_moved(self, pe, i):
        for w, n in self.seen.items():
            if n:
                pe.wait_ge(self.by[w].sem, self.by[w].after(i, n))


def attention_stage(K, name, load, front, make):
    nc = K.nc
    with ExitStack() as ctx:
        units, proj, tail = make(ctx)
        block = ctx.enter_context(nc.Block())
        tail.stage()
        A0, A1, A2 = 0, min(2, units.N), min(4, units.N + 1)

        @block.tensor
        def _(pe):
            pe.wait_ge(K.loaded[load], 16)
            front.open_pe(pe)
            units.open_pe(pe)
            front.transpose(pe, 0, 7)
            pe.wait_ge(front.xt_r.sem, front.xt_r.after(0, 1))
            proj.tensor(pe, 0)
            with pe.Fori(0, GROUPS) as i:
                proj.wait_moved(pe, i)
                units.tensor(pe, i, {1: lambda e: tail.wait_free(e, i), A2: lambda e: front.transpose(e, i + 1, 7)})
                pe.wait_ge(front.xt_r.sem, front.xt_r.after(i + 1, 1))
                proj.tensor(pe, i + 1)
                tail.tensor(pe, i)

        @block.vector
        def _(v):
            v.wait_ge(K.loaded[load], 16)
            units.open_vec(v)
            tail.open_vec(v)
            front.statistics(v, 0)
            front.normalise(v, 0)
            proj.move(v, "vec", 0)
            with v.Fori(0, GROUPS) as i:
                units.vector(v, i, {A0: lambda e: front.statistics(e, i + 1), 1: lambda e: tail.early(e, i),
                                   A1: lambda e: front.normalise(e, i + 1)})
                proj.move(v, "vec", i + 1)
                tail.vector(v, i)

        @block.scalar
        def _(a):
            a.wait_ge(K.loaded[load], 16)
            units.open_act(a)
            front.move(a, 0, 7)
            proj.move(a, "act", 0)
            with a.Fori(0, GROUPS) as i:
                def move(e):
                    e.wait_ge(proj.ready.sem, proj.ready.after(i, len(proj.jobs)))
                    front.move(e, i + 1, 7)
                units.scalar(a, i, {min(A2, units.N + 1): move})
                proj.move(a, "act", i + 1)
                tail.scalar(a, i)

        @block.gpsimd
        def _(g):
            front.rstds(g, 0)
            with g.Fori(0, GROUPS) as i:
                front.rstds(g, i + 1)
                tail.gpsimd(g, i)
        units.close()
        proj.close()
        front.close()
        tail.close()


class OutTail:

    def __init__(self, K, ctx, osb, wo, bias, post_norm=None, onto=None):
        nc = K.nc
        self.onto = K.h if onto is None else onto
        self.K, self.osb, self.wo, self.bias, self.post_norm = K, osb, wo, bias, post_norm
        self.width = osb.shape[2]
        self.nch = -(-self.width // P)
        self.k = min(P, self.width)
        self.oT = ctx.enter_context(nc.sbuf_tensor(f"outT_{nc.next_id()}", [P, self.nch, NTOK], F32))
        self.y = ctx.enter_context(nc.sbuf_tensor(f"out_{nc.next_id()}", [P, GT, C], F32))
        names = ("outT_in_psum", "outT_ready", "out_in_psum", "out_moved", "tail_vec", "tail_stats", "tail_pool", "tail_rstd")
        self.tps, self.tr, self.ops, self.mvd, self.vec, self.st, self.pool, self.rs = (K.count(n) for n in names)
        self.units, self.more = None, []

    def stage(self):
        for c, per in ((self.tps, self.nch), (self.tr, self.nch), (self.ops, 1), (self.mvd, 1),
                       (self.vec, 4 if self.post_norm else 0), (self.st, 1), (self.pool, 1), (self.rs, 1)):
            if self.post_norm or c not in (self.st, self.pool, self.rs):
                c.stage(per, int(c is self.mvd))

    def close(self):
        for c in (self.tps, self.tr, self.ops, self.mvd, self.vec, self.st, self.pool, self.rs):
            c.close(GROUPS)
        for c, groups in self.more:
            c.close(groups)

    def open_vec(self, v):
        v.sem_inc(self.mvd.sem, 1)

    def early(self, v, i):
        pass

    def wait_free(self, pe, i):
        pe.wait_ge(self.mvd.sem, self.mvd.after(i, 0))

    def tensor(self, pe, i):
        K = self.K
        pe.wait_ge(self.units.no.sem, self.units.no.after(i, self.units.N))
        K.settle(pe)
        for c in range(self.nch):
            for j in range(GT):
                ins = pe.transpose(K.bank[3 + c][0:self.k, j * P:(j + 1) * P], self.osb[:, j, c * P:c * P + self.k], K.W("ident"))
            ins.then_inc(self.tps.sem, 1)
        pe.wait_ge(self.tr.sem, self.tr.after(i, self.nch))
        K.settle(pe)
        for j in range(GT):
            for c in range(self.nch):
                ins = pe.matmul(K.bank[3][:, j * C:(j + 1) * C], self.oT[0:self.k, c, j * P:(j + 1) * P],
                                self.wo[0:self.k, c * C:(c + 1) * C], start=c == 0, stop=c == self.nch - 1, skip_group_check=True)
        ins.then_inc(self.ops.sem, 1)

    def scalar(self, a, i):
        for c in range(self.nch):
            a.wait_ge(self.tps.sem, self.tps.after(i, c + 1))
            a.activation(self.oT[0:self.k, c, :], self.K.bank[3 + c][0:self.k, :], ACT.Copy).then_inc(self.tr.sem, 1)

    def vector(self, v, i):
        K, y = self.K, self.y
        lk = link(v, self.vec, i, [0], self.K)
        v.wait_ge(self.ops.sem, self.ops.after(i, 1))
        o = K.bank[3][:, 0:GT * C].rearrange("p (j c) -> p j c", j=GT)
        dest = self.onto[:, bass.ds(i * GT, GT), :]
        if self.bias is None:
            v.tensor_tensor(dest, dest, o, ALU.add).then_inc(self.mvd.sem, 1)
            return
        v.tensor_tensor(y[:, :, :], o, rows(self.bias, GT, C), ALU.add).then_inc(self.mvd.sem, 1)
        v.wait_ge(self.mvd.sem, self.mvd.after(i, 1))
        if self.post_norm:
            eps, g, b, bnst, mv, rstd, _ = self.post_norm
            for j in range(GT):
                ins = v.bn_stats(bnst[:, j, :], y[:, j, :])
            lk(ins, settle=True)
            for j in range(GT):
                ins = v.bn_aggr(mv[:, j, :], bnst[:, j, :])
            ins.then_inc(self.st.sem, 1)
            v.wait_ge(self.rs.sem, self.rs.after(i, 1))
            for j in range(GT):
                ins = v.tensor_scalar(y[:, j, :], y[:, j, :], mv[:, j, 0:1], rstd[:, j:j + 1], ALU.subtract, ALU.mult)
            lk(ins)
            lk(v.tensor_tensor(y[:, :, :], y[:, :, :], rows(g, GT, C), ALU.mult))
            lk(v.tensor_tensor(y[:, :, :], y[:, :, :], rows(b, GT, C), ALU.add))
        v.tensor_tensor(dest, dest, y[:, :, :], ALU.add)

    def gpsimd(self, g, i):
        if self.post_norm:
            eps, _, _, _, mv, rstd, work = self.post_norm
            g.wait_ge(self.st.sem, self.st.after(i, 1))
            self.K.settle(g)
            g.tensor_scalar(work, mv[:, :, 1], eps, None, ALU.add).then_inc(self.pool.sem, 1)
            g.wait_ge(self.pool.sem, self.pool.after(i, 1))
            g.tensor_tensor(rstd, work, self.K.half[:, 0:GT], ALU.pow).then_inc(self.rs.sem, 1)


def values(ctx, nc, heads, d):
    return ctx.enter_context(nc.sbuf_tensor(f"values_{nc.next_id()}", [P, GT, heads, d + 1], F32))


def prepare(K, ones=(), zeros=()):
    with K.nc.Block() as block:
        @block.vector
        def _(v):
            for t in ones:
                v.memset(t, 1.0)
            for t in zeros:
                v.memset(t, 0.0)


def first_attention(K):
    nc = K.nc
    front = Front(K, "lnln", (1e-5, 1e-5), scale=K.W("a0_lnw")[:, 0:1], bias=K.W("a0_lnw")[:, 1:2])

    def make(ctx):
        qT = ctx.enter_context(nc.sbuf_tensor("a0_qT", [P, NTOK], F32))
        kT = ctx.enter_context(nc.sbuf_tensor("a0_kT", [P, NTOK], F32))
        vt = values(ctx, nc, 1, C)
        osb = ctx.enter_context(nc.sbuf_tensor("a0_o_sb", [P, GT, C], F32))
        post = (1e-5, K.W("a0_g2"), K.W("a0_b2"), ctx.enter_context(nc.sbuf_tensor("a0_bn", [P, GT, 6], F32)),
                ctx.enter_context(nc.sbuf_tensor("a0_mv", [P, GT, 2], F32)),
                ctx.enter_context(nc.sbuf_tensor("a0_rstd", [P, GT], F32))[:, :], 
                ctx.enter_context(nc.sbuf_tensor("a0_work", [P, GT], F32))[:, :])
        prepare(K, [vt[:, :, :, C:C + 1]], [qT[C:P, :], kT[C:P, :]])
        x = K.xU[:, :]
        jobs = [
            ("act", lambda pe, b, i: pe.matmul(b[0:C, :], K.W("a0_qk")[:, 0:C], x, start=True, stop=True),
             lambda a, b, i: a.activation(qT[0:C, :], b[0:C, :], ACT.Identity, bias=K.W("a0_qkb", 0, C)[:, 0:1])),
            ("vec", lambda pe, b, i: pe.matmul(b[0:C, :], K.W("a0_qk")[:, C:2 * C], x, start=True, stop=True),
             lambda v, b, i: v.tensor_scalar(kT[0:C, :], b[0:C, :], K.W("a0_qkb", 0, C)[:, 1:2], None, ALU.add)),
            ("vec", lambda pe, b, i: [pe.matmul(b[:, j * C:(j + 1) * C], K.xU[:, j * P:(j + 1) * P], K.W("a0_v"),
                                                start=True, stop=True) for j in range(GT)][-1],
             lambda v, b, i: v.tensor_tensor(vt[:, :, 0, 0:C], b[:, 0:GT * C].rearrange("p (j c) -> p j c", j=GT),
                                             rows(K.W("a0_vb"), GT, C), ALU.add)),
        ]
        us = []
        for s in range(2):
            us.append(Unit([(qb * SEQ, SEQ, qT[:, s * SEQ + qb * P:s * SEQ + (qb + 1) * P], kT[:, s * SEQ:(s + 1) * SEQ])
                            for qb in range(2)], [], [(0, 2, SEQ)],
                           [[(2 * qb + kb, vt[:, 2 * s + kb, 0, :]) for kb in range(2)] for qb in range(2)],
                           C + 1, osb[:, 2 * s:2 * s + 2, :]))
        units = Units(K, ctx, us, bias=K.W("a0_bias"), rownorm=lambda t, n: K.W("a0_scale").to_broadcast([P, n]))
        tail = OutTail(K, ctx, osb, K.W("a0_o"), K.W("a0_ob"), post)
        tail.units = units
        return units, Projections(K, jobs), tail
    attention_stage(K, "a0", 0, front, make)


def second_attention(K):
    nc = K.nc
    front = Front(K, "ln", (1e-5,))

    def make(ctx):
        H = 8
        qT = ctx.enter_context(nc.sbuf_tensor("a1_qT", [P, 4, NTOK], F32))
        kT = ctx.enter_context(nc.sbuf_tensor("a1_kT", [P, 2, 4, NTOK], F32))
        vt = values(ctx, nc, H, C)
        osb = ctx.enter_context(nc.sbuf_tensor("a1_o_sb", [P, GT, H * C], F32))
        prepare(K, [vt[:, :, :, C:C + 1]], [kT[C:P, 0, :, :], kT[0:C, 1, :, :]])
        x = K.xU[:, :]

        def qjob(c):
            return ("vec", lambda pe, b, i: pe.matmul(b[:, :], K.W("a1_q")[:, c * P:(c + 1) * P], x, start=True, stop=True),
                    lambda v, b, i: v.tensor_scalar(qT[:, c, :], b[:, :], K.W("a1_qb")[:, c:c + 1], 0.125, ALU.add, ALU.mult))

        def kjob(c):
            return ("act", lambda pe, b, i: pe.matmul(b[:, :], K.W("a1_k")[:, c * P:(c + 1) * P], x, start=True, stop=True),
                    lambda a, b, i: [a.activation(kT[r, p, c, :], b[r, :], ACT.Identity, bias=K.W("a1_kb")[r, c:c + 1])
                                     for p, r in enumerate((slice(0, C), slice(C, P)))][-1])

        def vjob(j):
            return ("vec", lambda pe, b, i: pe.matmul(b[:, :], K.xU[:, j * P:(j + 1) * P], K.W("a1_v"), start=True, stop=True),
                    lambda v, b, i: v.tensor_tensor(vt[:, j, :, 0:C], b[:, :].rearrange("p (h c) -> p h c", h=H),
                                                    K.W("a1_vb").rearrange("p (h c) -> p h c", h=H), ALU.add))
        jobs = [f(c) for c in range(4) for f in (qjob, kjob, vjob)]
        o5 = osb[:, :, :].rearrange("p j (m a c) -> p j m a c", m=4, a=2)
        us, q0 = [], []
        strict4 = K.wb[:, 1:5, :].rearrange("p a c -> p (a c)")
        strict = K.wb[:, 1, :]
        for s in range(2):
            t0 = s * SEQ
            for p in range(2):
                us.append(Unit([(P * m, P, qT[:, m, t0:t0 + P], kT[:, p, m, t0:t0 + P]) for m in range(4)], [(0, 512, strict4)],
                               [(0, 4, P)], [[(m, vt[:, 2 * s, 2 * m + p, :])] for m in range(4)], C + 1, o5[:, 2 * s, :, p, :]))
                q0.append(0)
                for mp in range(2):
                    us.append(Unit([(SEQ * a, SEQ, qT[:, 2 * mp + a, t0 + P:t0 + SEQ], kT[:, p, 2 * mp + a, t0:t0 + SEQ]) for a in range(2)],
                                   [(SEQ * a + P, P, strict) for a in range(2)], [(0, 2, SEQ)],
                                   [[(2 * a + kb, vt[:, 2 * s + kb, 2 * (2 * mp + a) + p, :]) for kb in range(2)] for a in range(2)],
                                   C + 1, o5[:, 2 * s + 1, 2 * mp:2 * mp + 2, p, :]))
                    q0.append(1)
        units = Units(K, ctx, us, rownorm=lambda t, n: K.W("row0")[:, q0[t]:q0[t] + 1].to_broadcast([P, n]))
        tail = OutTail(K, ctx, osb, K.W("a1_o"), K.W("a1_ob"))
        tail.units = units
        return units, Projections(K, jobs), tail
    attention_stage(K, "a1", 2, front, make)


def second_routed_attention(K, x1):
    nc = K.nc
    front = Front(K, "lnrms", (1e-5, 1e-6), scale=K.W("r2_ln"), kept=x1)

    def make(ctx):
        H, HK, D = 4, 2, 16
        qT = ctx.enter_context(nc.sbuf_tensor("r2_qT", [P, NTOK], F32))
        kT = ctx.enter_context(nc.sbuf_tensor("r2_kT", [P, 4, NTOK], F32))
        t1 = ctx.enter_context(nc.sbuf_tensor("r2_t1", [P, NTOK], F32))
        t2 = ctx.enter_context(nc.sbuf_tensor("r2_t2", [P, NTOK], F32))
        vt = values(ctx, nc, HK, D)
        osb = ctx.enter_context(nc.sbuf_tensor("r2_o_sb", [P, GT, C], F32))
        prepare(K, [vt[:, :, :, D:D + 1]], [kT[:, :, :]])
        rope = K.count("rotary_part")
        rope.stage(2)

        def pair(ap):
            return ap.rearrange("p (s t) -> p s t", s=2)

        def table(name):
            return K.W(name).rearrange("p (s t) -> p s t", s=1).to_broadcast([P, 2, SEQ])

        moved = K.count("projection_moved_vec")

        def plain(w, tab, before):
            def mv(v, b, i):
                if before:
                    v.wait_ge(moved.sem, moved.after(i, before))
                return v.tensor_tensor(pair(t1[:, :]), pair(b[:, :]), table(tab), ALU.mult)
            return ("vec", lambda pe, b, i: pe.matmul(b[:, :], K.W(w), K.xU[:, :], start=True, stop=True), mv)

        def turned(w, tab, dst, n):
            def mv(v, b, i):
                v.tensor_tensor(pair(t2[:, :]), pair(b[:, :]), table(tab), ALU.mult).then_inc(rope.sem, 1)
                v.wait_ge(rope.sem, rope.after(i, n))
                for out, r in dst:
                    ins = v.tensor_tensor(out, t1[r, :], t2[r, :], ALU.add)
                return ins
            return ("vec", lambda pe, b, i: pe.matmul(b[:, :], K.W(w), K.xU[:, :], start=True, stop=True), mv)
        jobs = [plain("r2_q", "r2_cq", 0), turned("r2_qp", "r2_sq", [(qT[:, :], slice(0, P))], 1),
                plain("r2_k", "r2_ck", 2), turned("r2_kp", "r2_sk", [(kT[32 * n:32 * n + 32, n, :], slice(32 * n, 32 * n + 32)) for n in range(H)], 2),
                ("act", lambda pe, b, i: [pe.matmul(b[:, j * 32:(j + 1) * 32], K.xU[:, j * P:(j + 1) * P], K.W("r2_v"),
                                                    start=True, stop=True) for j in range(GT)][-1],
                 lambda a, b, i: a.activation(vt[:, :, :, 0:D], b[:, 0:GT * 32].rearrange("p (j h c) -> p j h c", j=GT, h=HK), ACT.Copy))]
        us = []
        causal = K.wb[:, 5, :]
        for s in range(2):
            t0 = s * SEQ
            for n in range(H):
                g = n // (H // HK)
                us.append(Unit([(0, P, qT[:, t0:t0 + P], kT[:, n, t0:t0 + P]), (P, SEQ, qT[:, t0 + P:t0 + SEQ], kT[:, n, t0:t0 + SEQ])],
                               [(0, P, causal), (SEQ, P, causal)], [(0, 1, P), (P, 1, SEQ)],
                               [[(0, vt[:, 2 * s, g, :])], [(1, vt[:, 2 * s, g, :]), (2, vt[:, 2 * s + 1, g, :])]],
                               D + 1, osb[:, 2 * s:2 * s + 2, n * D:(n + 1) * D]))
        units = Units(K, ctx, us)
        tail = OutTail(K, ctx, osb, K.W("r2_o"), None, onto=x1)
        tail.units = units
        tail.more = [(rope, GROUPS + 1)]
        return units, Projections(K, jobs), tail
    attention_stage(K, "r2", 5, front, make)


class GateTail(OutTail):

    def __init__(self, K, ctx, qo, sx, mixed):
        super().__init__(K, ctx, qo.rearrange("p j n e d -> p j (n e d)"), K.W("f1_g"), K.W("f1_gb"))
        nc = K.nc
        self.qo, self.sx, self.mixed = qo, sx, mixed
        self.padm = ctx.enter_context(nc.sbuf_tensor("f1_not_padded", [P, GT * C], F32))
        self.lg = ctx.enter_context(nc.sbuf_tensor("f1_gate", [P, GT * 16], F32))
        self.m = ctx.enter_context(nc.sbuf_tensor("f1_gate_work", [P, GT * 4], F32))
        self.masked, self.shifted, self.exps = K.count("pads_zeroed"), K.count("gate_shifted"), K.count("gate_exps")

    def stage(self):
        for c, per in ((self.tps, self.nch), (self.tr, self.nch), (self.ops, 1), (self.mvd, 1), (self.vec, 6),
                       (self.masked, 1), (self.shifted, 1), (self.exps, 1)):
            c.stage(per, int(c is self.mvd))
        self.more = [(c, GROUPS) for c in (self.masked, self.shifted, self.exps)]

    def tensor(self, pe, i):
        K = self.K
        pe.wait_ge(self.masked.sem, self.masked.after(i, 1))
        K.settle(pe)
        for c in range(self.nch):
            for j in range(GT):
                ins = pe.transpose(K.bank[3 + c][:, j * P:(j + 1) * P], self.osb[:, j, c * P:(c + 1) * P], K.W("ident"))
            ins.then_inc(self.tps.sem, 1)
        pe.wait_ge(self.tr.sem, self.tr.after(i, self.nch))
        K.settle(pe)
        for j in range(GT):
            for c in range(self.nch):
                ins = pe.matmul(K.bank[3][:, j * 16:(j + 1) * 16], self.oT[:, c, j * P:(j + 1) * P],
                                self.wo[:, c * 16:(c + 1) * 16], start=c == 0, stop=c == self.nch - 1, skip_group_check=True)
        ins.then_inc(self.ops.sem, 1)

    def scalar(self, a, i):
        super().scalar(a, i)
        a.wait_ge(self.shifted.sem, self.shifted.after(i, 1))
        a.activation(self.lg[:, :], self.lg[:, :], ACT.Exp).then_inc(self.exps.sem, 1)

    def vector(self, v, i):
        K, qo = self.K, self.qo
        lk = link(v, self.vec, i, [0], K)
        over = (lambda t, e: t.rearrange("p (a c) -> p a c", c=1).to_broadcast([P, t.shape[1], e]))
        four = (lambda t: t.rearrange("p (a c) -> p a c", c=4))
        K.proj.wait_moved(v, i + 1)
        lk(v.tensor_scalar(self.padm[:, :].rearrange("p (j c) -> p j c", j=GT), self.sx[:, bass.ds(i * GT, GT), :], 0.0, None,
                           ALU.not_equal))
        q4 = qo[:, :, :, :, :].rearrange("p j n e d -> p (j n) e d")
        v.tensor_tensor(q4, q4, self.padm[:, :].rearrange("p (a b d) -> p a b d", b=1, d=16).to_broadcast([P, GT * 4, 4, 16]), ALU.mult)\
            .then_inc(self.masked.sem, 1)
        v.wait_ge(self.ops.sem, self.ops.after(i, 1))
        v.tensor_tensor(self.lg[:, :].rearrange("p (j c) -> p j c", j=GT), K.bank[3][:, 0:GT * 16].rearrange("p (j c) -> p j c", j=GT),
                        rows(K.W("f1_gb"), GT, 16), ALU.add).then_inc(self.mvd.sem, 1)
        v.wait_ge(self.mvd.sem, self.mvd.after(i, 1))
        lk(v.tensor_reduce(self.m[:, :], four(self.lg[:, :]), AX.X, ALU.max))
        v.tensor_tensor(four(self.lg[:, :]), four(self.lg[:, :]), over(self.m[:, :], 4), ALU.subtract).then_inc(self.shifted.sem, 1)
        v.wait_ge(self.exps.sem, self.exps.after(i, 1))
        K.settle(v)
        lk(v.tensor_reduce(self.m[:, :], four(self.lg[:, :]), AX.X, ALU.add))
        lk(v.reciprocal(self.m[:, :], self.m[:, :]))
        lk(v.tensor_tensor(four(self.lg[:, :]), four(self.lg[:, :]), over(self.m[:, :], 4), ALU.mult))
        qe = qo[:, :, :, :, :].rearrange("p j n e d -> p (j n e) d")
        lk(v.tensor_tensor(qe, qe, over(self.lg[:, :], 16), ALU.mult))
        v.tensor_reduce(self.mixed[:, bass.ds(i * GT, GT), :].rearrange("p j (n d) -> p (j n) d", n=4),
                        qo[:, :, :, :, :].rearrange("p j n e d -> p (j n) d e"), AX.X, ALU.add)


def expert_heads(K):
    nc = K.nc
    with ExitStack() as ctx:
        sx = ctx.enter_context(nc.sbuf_tensor("head_features", [P, TILES + GT, C], F32))
        mixed = ctx.enter_context(nc.sbuf_tensor("mixed", [P, TILES, C], F32))
        expert_attention(K, sx, mixed)
        head_feed_forward(K, sx, mixed)


def expert_attention(K, sx, mixed):
    nc = K.nc
    front = Front(K, "ln", (1e-5,))

    def make(ctx):
        H, D, E = 4, 16, 4
        sxT = ctx.enter_context(nc.sbuf_tensor("f1_sxT", [P, NTOK], F32))
        qT = ctx.enter_context(nc.sbuf_tensor("f1_qT", [P, E, NTOK], F32))
        kT = ctx.enter_context(nc.sbuf_tensor("f1_kT", [P, H, NTOK], F32))
        vt = values(ctx, nc, H, D)
        qo = ctx.enter_context(nc.sbuf_tensor("f1_qo", [P, GT, H, E, D], F32))
        prepare(K, [vt[:, :, :, D:D + 1]], [sxT[C:P, :], kT[:, :, :]])
        moved = K.count("projection_moved_act")

        def heads(pe, b, i):
            pe.wait_ge(moved.sem, moved.after(i, 1))
            K.settle(pe)
            return b

        def qjob(e):
            def mm(pe, b, i):
                return pe.matmul(heads(pe, b, i)[:, :], K.W("f1_q")[:, e * P:(e + 1) * P], sxT[:, :], start=True, stop=True)
            if e % 2:
                return ("act", mm, lambda a, b, i: a.activation(qT[:, e, :], b[:, :], ACT.Copy, scale=4.0))
            return ("vec", mm, lambda v, b, i: v.tensor_scalar(qT[:, e, :], b[:, :], 4.0, None, ALU.mult))
        jobs = [
            ("act", lambda pe, b, i: pe.matmul(b[0:C, :], K.W("f1_hl"), K.xU[:, :], start=True, stop=True),
             lambda a, b, i: a.activation(sxT[0:C, :], b[0:C, :], ACT.Identity, bias=K.W("f1_hlb", 0, C))),
            ("vec", lambda pe, b, i: [pe.matmul(b[:, j * C:(j + 1) * C], K.xU[:, j * P:(j + 1) * P], K.W("f1_hl"),
                                                start=True, stop=True) for j in range(GT)][-1],
             lambda v, b, i: v.tensor_tensor(sx[:, bass.ds(i * GT, GT), :], b[:, 0:GT * C].rearrange("p (j c) -> p j c", j=GT),
                                             rows(K.W("f1_hlbr"), GT, C), ALU.add)),
            *[qjob(e) for e in range(E)],
            ("act", lambda pe, b, i: pe.matmul(b[:, :], K.W("f1_k"), sxT[:, :], start=True, stop=True),
             lambda a, b, i: [a.activation(kT[32 * n:32 * n + 32, n, :], b[32 * n:32 * n + 32, :], ACT.Copy) for n in range(H)][-1]),
            ("vec", lambda pe, b, i: [pe.matmul(b[:, j * C:(j + 1) * C], sxT[:, j * P:(j + 1) * P], K.W("f1_v"),
                                                start=True, stop=True) for j in range(GT)][-1],
             lambda v, b, i: v.tensor_copy(vt[:, :, :, 0:D], b[:, 0:GT * C].rearrange("p (j h c) -> p j h c", j=GT, h=H))),
        ]
        causal4 = K.wb[:, 5:9, :].rearrange("p a c -> p (a c)")
        causal = K.wb[:, 5, :]
        us = []
        for s in range(2):
            t0 = s * SEQ
            for n in range(H):
                us.append(Unit([(e * P, P, qT[:, e, t0:t0 + P], kT[:, n, t0:t0 + P]) for e in range(E)], [(0, 512, causal4)],
                               [(0, E, P)], [[(e, vt[:, 2 * s, n, :])] for e in range(E)], D + 1, qo[:, 2 * s, n, :, :]))
                for p in range(2):
                    us.append(Unit([(a * SEQ, SEQ, qT[:, 2 * p + a, t0 + P:t0 + SEQ], kT[:, n, t0:t0 + SEQ]) for a in range(2)],
                                   [(a * SEQ + P, P, causal) for a in range(2)], [(0, 2, SEQ)],
                                   [[(2 * a + kb, vt[:, 2 * s + kb, n, :]) for kb in range(2)] for a in range(2)],
                                   D + 1, qo[:, 2 * s + 1, n, 2 * p:2 * p + 2, :]))
        units = Units(K, ctx, us)
        tail = GateTail(K, ctx, qo, sx, mixed)
        tail.units = units
        K.proj = Projections(K, jobs)
        return units, K.proj, tail
    attention_stage(K, "f1", 3, front, make)


def head_feed_forward(K, sx, mixed):
    nc = K.nc
    H, D, FT = 4, 16, 8
    STEPS, N, R = TILES // FT, FT * C, FT * 4
    with ExitStack() as ctx:
        def sb(n, s):
            return ctx.enter_context(nc.sbuf_tensor(f"ff_{n}", s, F32))
        fx, y, sq, npm = (sb(n, [P, N]) for n in ("fx", "y", "square", "not_zero"))
        fxT, h1, npmT = (sb(n, [C, FT * P]) for n in ("fxT", "hidden", "not_zeroT"))
        resid = sb("resid", [P, 2, C])
        mean, var, work, rstd, fg, m = (sb(n, [P, R]) for n in ("mean", "var", "work", "rstd", "gate", "gate_work"))
        half = sb("minus_half", [P, R])
        names = ("ff_vec", "norm_stats", "norm_pool", "norm_rstd", "fx_ready", "fxT_in_psum", "fxT_ready", "not_zeroT", "hidden1_in_psum",
                 "hidden1_moved", "hidden1_ready", "layers_in_psum", "fout_ready", "foutT_in_psum", "foutT_ready", "head_gate_in_psum",
                 "head_gate_shifted", "head_gate_exps", "halves_set")
        counts = [K.count(n) for n in names]
        (vec, st, pl, rs, fr, ftp, ftr, nzt, h1p, h1m, h1r, zp, fo, fop, fot, gp, gsh, gex, hs) = counts
        VEC = 24
        for c, per in zip(counts, (VEC, 2, 2, 2, 1, 1, 1, 1, 2, 2, 1, 1, 1, 1, 1, 1, 1, 1, 0)):
            c.stage(per, 0)
        block = ctx.enter_context(nc.Block())
        r3 = (lambda t: t.rearrange("p (a d) -> p a d", d=D))
        over = (lambda t, n: t.rearrange("p (a c) -> p a c", c=1).to_broadcast([P, t.shape[1], n]))
        row16 = (lambda name: rows(K.W(name), R, D))

        @block.vector
        def _(v):
            v.wait_ge(hs.sem, hs.base + 1)
            for n in range(H):
                ins = v.tensor_copy(resid[:, :, n * D:(n + 1) * D], sx[:, 2 * n:2 * n + 2, n * D:(n + 1) * D])
            ins.then_inc(hs.sem, 1)
            v.wait_ge(hs.sem, hs.base + 2)
            with v.Fori(0, STEPS) as i:
                lk = link(v, vec, i, [0], K)

                def norm(t, dst, g, b, k):
                    lk(v.tensor_reduce(mean[:, :], r3(t[:, :]), AX.X, ALU.add))
                    lk(v.tensor_scalar(mean[:, :], mean[:, :], 1.0 / D, None, ALU.mult))
                    lk(v.tensor_tensor(r3(t[:, :]), r3(t[:, :]), over(mean[:, :], D), ALU.subtract))
                    lk(v.tensor_tensor(sq[:, :], t[:, :], t[:, :], ALU.mult))
                    lk(v.tensor_reduce(var[:, :], r3(sq[:, :]), AX.X, ALU.add))
                    v.tensor_scalar(var[:, :], var[:, :], 1.0 / D, None, ALU.mult).then_inc(st.sem, 1)
                    v.wait_ge(rs.sem, rs.after(i, k))
                    lk(v.tensor_tensor(r3(t[:, :]), r3(t[:, :]), over(rstd[:, :], D), ALU.mult))
                    lk(v.tensor_tensor(r3(t[:, :]), r3(t[:, :]), row16(g), ALU.mult))
                    return v.tensor_tensor(r3(dst[:, :]), r3(t[:, :]), row16(b), ALU.add)
                lk(v.tensor_tensor(fx[:, :].rearrange("p (s t c) -> p s (t c)", t=2, c=C),
                                   mixed[:, bass.ds(i * FT, FT), :].rearrange("p (s t) c -> p s (t c)", t=2),
                                   resid[:, :, :].rearrange("p (s t) c -> p s (t c)", s=1).to_broadcast([P, FT // 2, 2 * C]), ALU.add))
                norm(fx, fx, "f1_lg", "f1_lb", 1).then_inc(fr.sem, 1)
                v.wait_ge(fr.sem, fr.after(i, 1))
                lk(v.tensor_scalar(npm[:, :], fx[:, :], 0.0, None, ALU.not_equal))
                v.wait_ge(ftr.sem, ftr.after(i, 1))
                v.tensor_scalar(npmT[:, :], fxT[:, :], 0.0, None, ALU.not_equal).then_inc(nzt.sem, 1)
                v.wait_ge(nzt.sem, nzt.after(i, 1))
                v.wait_ge(h1m.sem, h1m.after(i, 2))
                v.tensor_tensor(h1[:, :], h1[:, :], npmT[:, :], ALU.mult).then_inc(h1r.sem, 1)
                v.wait_ge(zp.sem, zp.after(i, 1))
                lk(v.tensor_tensor(r3(y[:, :]), r3(K.bank[4][:, :]), row16("f1_2b"), ALU.add))
                lk(v.tensor_tensor(y[:, :], y[:, :], npm[:, :], ALU.mult))
                lk(v.tensor_tensor(y[:, :], y[:, :], fx[:, :], ALU.add))
                norm(y, y, "f1_ng", "f1_nb", 2).then_inc(fo.sem, 1)
                v.wait_ge(gp.sem, gp.after(i, 1))
                four = (lambda t: t.rearrange("p (a c) -> p a c", c=H))
                lk(v.tensor_reduce(m[:, 0:FT], four(K.bank[5][:, 0:R]), AX.X, ALU.max))
                v.tensor_tensor(four(fg[:, :]), four(K.bank[5][:, 0:R]), over(m[:, 0:FT], H), ALU.subtract).then_inc(gsh.sem, 1)
                v.wait_ge(gex.sem, gex.after(i, 1))
                K.settle(v)
                lk(v.tensor_reduce(m[:, 0:FT], four(fg[:, :]), AX.X, ALU.add))
                lk(v.reciprocal(m[:, 0:FT], m[:, 0:FT]))
                lk(v.tensor_tensor(four(fg[:, :]), four(fg[:, :]), over(m[:, 0:FT], H), ALU.mult))
                lk(v.tensor_tensor(r3(y[:, :]), r3(y[:, :]), over(fg[:, :], D), ALU.mult))
                dest = K.h[:, bass.ds(i * FT, FT), :]
                v.tensor_tensor(dest, dest, y[:, :].rearrange("p (j c) -> p j c", j=FT), ALU.add)

        @block.gpsimd
        def _(g):
            g.memset(half[:, :], -0.5).then_inc(hs.sem, 1)
            with g.Fori(0, STEPS) as i:
                for k in range(2):
                    g.wait_ge(st.sem, st.after(i, k + 1))
                    K.settle(g)
                    g.tensor_scalar(work[:, :], var[:, :], 1e-8, None, ALU.add).then_inc(pl.sem, 1)
                    g.wait_ge(pl.sem, pl.after(i, k + 1))
                    g.tensor_tensor(rstd[:, :], work[:, :], half[:, :], ALU.pow).then_inc(rs.sem, 1)

        @block.tensor
        def _(pe):
            with pe.Fori(0, STEPS) as i:
                def turn(src, ready, out):
                    pe.wait_ge(ready.sem, ready.after(i, 1))
                    K.settle(pe)
                    for j in range(FT):
                        ins = pe.transpose(K.bank[j // 4][0:C, (j % 4) * P:(j % 4 + 1) * P], src[:, j * C:(j + 1) * C], K.W("ident"))
                    ins.then_inc(out.sem, 1)
                turn(fx, fr, ftp)
                pe.wait_ge(ftr.sem, ftr.after(i, 1))
                K.settle(pe)
                for b in range(2):
                    pe.matmul(K.bank[2 + b][0:C, :], K.W("f1_1", 0, C), fxT[:, b * NTOK:(b + 1) * NTOK], start=True, stop=True)\
                        .then_inc(h1p.sem, 1)
                pe.wait_ge(h1r.sem, h1r.after(i, 1))
                K.settle(pe)
                for j in range(FT):
                    ins = pe.matmul(K.bank[4][:, j * C:(j + 1) * C], h1[:, j * P:(j + 1) * P], K.W("f1_2", 0, C), start=True, stop=True,
                                    skip_group_check=True)
                ins.then_inc(zp.sem, 1)
                turn(y, fo, fop)
                pe.wait_ge(fot.sem, fot.after(i, 1))
                K.settle(pe)
                for j in range(FT):
                    ins = pe.matmul(K.bank[5][:, j * H:(j + 1) * H], fxT[:, j * P:(j + 1) * P], K.W("f1_fg", 0, C), start=True, stop=True,
                                    skip_group_check=True)
                ins.then_inc(gp.sem, 1)

        @block.scalar
        def _(a):
            with a.Fori(0, STEPS) as i:
                def out(ready, done):
                    a.wait_ge(ready.sem, ready.after(i, 1))
                    for b in range(2):
                        ins = a.activation(fxT[:, b * NTOK:(b + 1) * NTOK], K.bank[b][0:C, :], ACT.Copy)
                    ins.then_inc(done.sem, 1)
                out(ftp, ftr)
                for b in range(2):
                    a.wait_ge(h1p.sem, h1p.after(i, b + 1))
                    a.activation(h1[:, b * NTOK:(b + 1) * NTOK], K.bank[2 + b][0:C, :], ACT.Relu, bias=K.W("f1_1b", 0, C)).then_inc(h1m.sem, 1)
                out(fop, fot)
                a.wait_ge(gsh.sem, gsh.after(i, 1))
                a.activation(fg[:, :], fg[:, :], ACT.Exp).then_inc(gex.sem, 1)
        for c in counts:
            c.close(STEPS)


def third_attention(K):
    nc = K.nc
    front = Front(K, "ln", (1e-5,))

    def make(ctx):
        H, D = 8, 32
        scale = float(np.float32(1.0) / np.sqrt(np.float32(D)))
        qT = ctx.enter_context(nc.sbuf_tensor("a2_qT", [P, 2, NTOK], F32))
        kT = ctx.enter_context(nc.sbuf_tensor("a2_kT", [P, 4, 2, NTOK], F32))
        vt = values(ctx, nc, H, D)
        osb = ctx.enter_context(nc.sbuf_tensor("a2_o_sb", [P, GT, H * D], F32))
        prepare(K, [vt[:, :, :, D:D + 1]], [kT[:, n, :, :] for n in range(4)])
        x = K.xU[:, :]

        def qjob(c):
            return ("vec", lambda pe, b, i: pe.matmul(b[:, :], K.W("a2_q")[:, c * P:(c + 1) * P], x, start=True, stop=True),
                    lambda v, b, i: v.tensor_scalar(qT[:, c, :], b[:, :], K.W("a2_qb")[:, c:c + 1], scale, ALU.add, ALU.mult))

        def kjob(c):
            return ("act", lambda pe, b, i: pe.matmul(b[:, :], K.W("a2_k")[:, c * P:(c + 1) * P], x, start=True, stop=True),
                    lambda a, b, i: [a.activation(kT[r, n, c, :], b[r, :], ACT.Identity, bias=K.W("a2_kb")[r, c:c + 1])
                                     for n, r in enumerate(slice(32 * n, 32 * n + 32) for n in range(4))][-1])

        def vjob(c):
            def mm(pe, b, i):
                for n in range(2):
                    j = 2 * c + n
                    ins = pe.matmul(b[:, n * SEQ:(n + 1) * SEQ], K.xU[:, j * P:(j + 1) * P], K.W("a2_v"), start=True, stop=True)
                return ins
            return ("vec", mm, lambda v, b, i: v.tensor_tensor(
                vt[:, 2 * c:2 * c + 2, :, 0:D], b[:, :].rearrange("p (j h c) -> p j h c", j=2, h=H),
                K.W("a2_vb").rearrange("p (j h c) -> p j h c", j=1, h=H).to_broadcast([P, 2, H, D]), ALU.add))
        jobs = [f(c) for c in range(2) for f in (qjob, kjob, vjob)]
        o5 = osb[:, :, :].rearrange("p j (m n c) -> p j m n c", m=2, n=4)
        us = []
        m0 = K.wb[:, 9:11, :].rearrange("p a c -> p (a c)")
        m1 = K.wb[:, 11:15, :].rearrange("p a c -> p (a c)")
        for s in range(2):
            t0 = s * SEQ
            for n in range(4):
                us.append(Unit([(P * m, P, qT[:, m, t0:t0 + P], kT[:, n, m, t0:t0 + P]) for m in range(2)], [(0, 2 * P, m0)],
                               [(0, 2, P)], [[(m, vt[:, 2 * s, 4 * m + n, :])] for m in range(2)], D + 1, o5[:, 2 * s, :, n, :]))
                us.append(Unit([(SEQ * m, SEQ, qT[:, m, t0 + P:t0 + SEQ], kT[:, n, m, t0:t0 + SEQ]) for m in range(2)], [(0, 512, m1)],
                               [(0, 2, SEQ)], [[(2 * m + kb, vt[:, 2 * s + kb, 4 * m + n, :]) for kb in range(2)] for m in range(2)],
                               D + 1, o5[:, 2 * s + 1, :, n, :]))
        units = Units(K, ctx, us)
        tail = OutTail(K, ctx, osb, K.W("a2_o"), K.W("a2_ob"))
        tail.units = units
        return units, Projections(K, jobs), tail
    attention_stage(K, "a2", 4, front, make)


def pick_first_max(v, lk, src, top, eq, one):
    n, e = src.shape[1], src.shape[2]
    b = (lambda t: t.rearrange("p (a c) -> p a c", c=1).to_broadcast([P, n, e]))
    lk(v.tensor_reduce(top, src, AX.X, ALU.max))
    lk(v.tensor_tensor(eq, src, b(top), ALU.is_equal))
    lk(v.tensor_tensor(eq, eq, pick_first_max.rank(n, e), ALU.mult))
    lk(v.tensor_reduce(pick_first_max.work, eq, AX.X, ALU.max))
    lk(v.tensor_tensor(one, eq, b(pick_first_max.work), ALU.is_equal))


class Mixture:

    def __init__(self, K, kind, load, front, E, CH, M, w1, w2, b1=None, w3=None, gw=None, gb=None, b2=None, kept=None):
        self.K, self.kind, self.load, self.front, self.kept = K, kind, load, front, kept
        self.E, self.CH, self.M, self.w1, self.w2, self.b1, self.w3, self.gw, self.gb, self.b2 = E, CH, M, w1, w2, b1, w3, gw, gb, b2
        self.NC = E * CH

    def run(self):
        K, nc, E, CH, NC, M = self.K, self.K.nc, self.E, self.CH, self.NC, self.M
        kind, front, kept = self.kind, self.front, self.kept
        gated = self.w3 is not None
        R = 8
        lag = 4 if gated else 6
        with ExitStack() as ctx:
            def sb(n, s, d=F32):
                return ctx.enter_context(nc.sbuf_tensor(f"{kind}_{n}", s, d))
            hT = sb("hidden", [P, R, NTOK])
            ug = sb("gate_part", [P, 2, NTOK]) if gated else None
            prod = sb("weighted", [P, 2, GT * C])
            acc = sb("sum", [P, GT, C])
            bsum = sb("bias_sum", [P, GT, C])
            g = sb("weights", [P, GT, 32])
            gT = sb("weightsT", [P, P])
            lg, ex, eq, o1, o2, l2 = (sb(n, [P, GT, E]) for n in ("logits", "exps", "equal", "first", "second", "rest"))
            m1, m2, wk, sm = (sb(n, [P, GT]) for n in ("top1", "top2", "work", "sums"))
            run = sb("run", [P, GT + 1, E])
            bnst, mv, rstd, wk4 = sb("bn", [P, GT, 6]), sb("mv", [P, GT, 2]), sb("rstd", [P, GT]), sb("wk4", [P, GT])
            mask = sb("mask", [P, GT * C], I32) if kind == "f3" else None
            limits = sb("limits", [P, 3, GT * C]) if kind == "f3" else None
            names = ("logits_ready", "choice_vec", "shifted", "exps_ready", "weights_ready", "weightsT_in_psum", "weightsT_ready",
                     "bias_in_psum", "sum_started", "hidden_in_psum", "hidden_ready", "gate_ready", "expert_out", "weighted_ready",
                     "summed", "mixture_stats", "mixture_pool", "mixture_rstd", "counts_in_psum", "counted", "cleared", "bias_moved")
            counts = [K.count(n) for n in names]
            (lgr, vec, shf, exr, wr, gtp, gtr, bps, acs, hps, hr, gtd, eo, pr, sd, mst, mpl, mrs, cps, cntd, clr, bmv) = counts
            steps = {"f0": 22, "f2": 21, "f3": 25}[kind]
            for c, per, cr in ((lgr, 1, 0), (vec, steps, 0), (shf, 1, 0), (exr, 1, 0), (wr, 1, 0), (gtp, self.b2 is not None, 0),
                               (gtr, self.b2 is not None, 0), (bps, self.b2 is not None, 0), (acs, 1, 0), (hps, NC, 0), (hr, NC, R),
                               (gtd, NC if gated else 0, 0), (eo, E, 2 * R), (pr, E, 2), (sd, E, 2), (mst, kind == "f0", 0),
                               (mpl, kind == "f0", 0), (mrs, kind == "f0", 0), (cps, kind == "f3", 0), (cntd, kind == "f3", 0), (clr, 0, 1),
                               (bmv, self.b2 is not None, self.b2 is not None)):
                c.stage(int(per), int(cr))
            block = ctx.enter_context(nc.Block())
            B7 = K.bank[7]
            flat = (lambda t: t.rearrange("p a c -> p (a c)"))
            b3 = (lambda t: t.rearrange("p (a c) -> p a c", c=1).to_broadcast([P, GT, E]))
            rank = K.W("rank")[:, 0:E].rearrange("p (a c) -> p a c", a=1).to_broadcast([P, GT, E])

            def hbank(c):
                return (K.bank[2 * (c % 2)], K.bank[2 * (c % 2) + 1]) if gated else (K.bank[c % 4], None)
            nbanks = 2 if gated else 4

            @block.tensor
            def _(pe):
                pe.wait_ge(K.loaded[self.load], 16)
                pe.wait_ge(clr.sem, clr.base + 1)
                front.open_pe(pe)
                pe.sem_inc(eo.sem, 2 * R)
                front.transpose(pe, 0, 6)
                with pe.Fori(0, GROUPS) as i:
                    pe.wait_ge(bmv.sem, bmv.after(i if self.b2 is not None else 0, 0))
                    pe.wait_ge(front.xt_r.sem, front.xt_r.after(i, 1))
                    K.settle(pe)
                    for j in range(GT):
                        ins = pe.matmul(B7[:, j * E:(j + 1) * E], K.xU[:, j * P:(j + 1) * P], self.gw[:, :], start=True, stop=True,
                                        skip_group_check=True)
                    ins.then_inc(lgr.sem, 1)

                    def outputs(e):
                        pe.wait_ge(hr.sem, hr.after(i, (e + 1) * CH))
                        pe.wait_ge(pr.sem, pr.after(i, e - 1))
                        for j in range(GT):
                            for n in range(CH):
                                c = e * CH + n
                                ins = pe.matmul(K.bank[4 + e % 2][:, j * C:(j + 1) * C], hT[0:M, c % R, j * P:(j + 1) * P],
                                                self.w2[0:M, c * C:(c + 1) * C], start=n == 0, stop=n == CH - 1, skip_group_check=True)
                        ins.then_inc(eo.sem, 1)

                    done = 0
                    for c in range(NC):
                        z, z3 = hbank(c)
                        x = K.xL if c % 2 else K.xU
                        pe.wait_ge(hr.sem, hr.after(i, c - nbanks + 1))
                        ins = pe.matmul(z[0:M, :], self.w1[:, (c // 2) * M:(c // 2 + 1) * M], x[:, :], start=True, stop=True)
                        if gated:
                            ins = pe.matmul(z3[0:M, :], self.w3[:, (c // 2) * M:(c // 2 + 1) * M], x[:, :], start=True, stop=True)
                        ins.then_inc(hps.sem, 1)
                        if kind == "f3" and c == 5:
                            pe.wait_ge(cntd.sem, cntd.after(i, 1))
                            pe.matmul(B7[:, 64:64 + GT * E], K.W("tri"), flat(o1[:, :, :]), start=True, stop=False, skip_group_check=True)
                            pe.matmul(B7[:, 64:64 + GT * E], K.W("ones"), flat(run[:, 0:GT, :]), start=False, stop=True,
                                      skip_group_check=True).then_inc(cps.sem, 1)
                        if self.b2 is not None and c == NC - 4:
                            pe.wait_ge(wr.sem, wr.after(i, 1))
                            pe.transpose(B7[:, P:2 * P], flat(g[:, :, :]), K.W("ident")).then_inc(gtp.sem, 1)
                        if self.b2 is not None and c == NC - 2:
                            pe.wait_ge(gtr.sem, gtr.after(i, 1))
                            pe.matmul(B7[:, 2 * P:4 * P], gT[:, :], self.b2, start=True, stop=True, skip_group_check=True).then_inc(bps.sem, 1)
                        while (done + 1) * CH - 1 <= c - lag:
                            outputs(done)
                            done += 1
                    front.transpose(pe, i + 1, 6)
                    while done < E:
                        outputs(done)
                        done += 1

            @block.scalar
            def _(a):
                a.wait_ge(K.loaded[self.load], 16)
                if not gated:
                    a.sem_inc(hr.sem, R)
                front.move(a, 0, 6)
                with a.Fori(0, GROUPS) as i:
                    for c in range(NC):
                        if c == 2:
                            a.wait_ge(shf.sem, shf.after(i, 1))
                            a.activation(ex[:, :, :], ex[:, :, :], ACT.Exp).then_inc(exr.sem, 1)
                        z, _ = hbank(c)
                        a.wait_ge(hps.sem, hps.after(i, c + 1))
                        if gated:
                            a.wait_ge(hr.sem, hr.after(i, c - 1))
                            a.activation(ug[0:M, c % 2, :], z[0:M, :], ACT.Silu).then_inc(gtd.sem, 1)
                        else:
                            a.wait_ge(eo.sem, eo.after(i, (c - R) // CH + 1))
                            a.activation(hT[0:M, c % R, :], z[0:M, :], ACT.Relu, bias=self.b1[0:M, c:c + 1]).then_inc(hr.sem, 1)
                        if self.b2 is not None and c == NC - 4:
                            a.wait_ge(gtp.sem, gtp.after(i, 1))
                            a.activation(gT[:, :], B7[:, P:2 * P], ACT.Copy).then_inc(gtr.sem, 1)
                    front.move(a, i + 1, 6)

            @block.gpsimd
            def _(p):
                if kind == "f3":
                    for n, x in enumerate((0.0, 1.0e4, -1.0e4)):
                        p.memset(limits[:, n, :], x)
                p.memset(run[:, :, :], 0.0)
                p.memset(g[:, :, :], 0.0).then_inc(clr.sem, 1)
                p.sem_inc(sd.sem, 2)
                front.rstds(p, 0)
                with p.Fori(0, GROUPS) as i:
                    for e in range(E):
                        if e == (2 if gated else 3):
                            front.rstds(p, i + 1)
                        p.wait_ge(pr.sem, pr.after(i, e + 1))
                        if e == 0:
                            p.wait_ge(acs.sem, acs.after(i, 1))
                        else:
                            p.wait_ge(sd.sem, sd.after(i, e))
                        p.tensor_tensor(flat(acc[:, :, :]), flat(acc[:, :, :]), prod[:, e % 2, :], ALU.add).then_inc(sd.sem, 1)
                    if kind == "f0":
                        p.wait_ge(mst.sem, mst.after(i, 1))
                        K.settle(p)
                        p.tensor_scalar(wk4[:, :], mv[:, :, 1], 1e-5, None, ALU.add).then_inc(mpl.sem, 1)
                        p.wait_ge(mpl.sem, mpl.after(i, 1))
                        p.tensor_tensor(rstd[:, :], wk4[:, :], K.half[:, 0:GT], ALU.pow).then_inc(mrs.sem, 1)

            @block.vector
            def _(v):
                v.wait_ge(K.loaded[self.load], 16)
                v.wait_ge(clr.sem, clr.base + 1)
                v.sem_inc(pr.sem, 2)
                if self.b2 is not None:
                    v.sem_inc(bmv.sem, 1)
                if gated:
                    v.sem_inc(hr.sem, R)
                front.statistics(v, 0)
                front.normalise(v, 0)
                with v.Fori(0, GROUPS) as i:
                    st = [0]
                    lk = link(v, vec, i, st, K)

                    def pick(src, top, one):
                        lk(v.tensor_reduce(top[:, :], src[:, :, :], AX.X, ALU.max))
                        lk(v.tensor_tensor(eq[:, :, :], src[:, :, :], b3(top[:, :]), ALU.is_equal))
                        lk(v.tensor_tensor(eq[:, :, :], eq[:, :, :], rank, ALU.mult))
                        lk(v.tensor_reduce(wk[:, :], eq[:, :, :], AX.X, ALU.max))
                        lk(v.tensor_tensor(one[:, :, :], eq[:, :, :], b3(wk[:, :]), ALU.is_equal))

                    def both(src):
                        pick(src, m1, o1)
                        hook()
                        lk(v.scalar_tensor_tensor(flat(l2[:, :, :]), flat(o1[:, :, :]), -BIG, flat(src[:, :, :]), ALU.mult, ALU.add))
                        pick(l2, m2, o2)
                        hook()
                        lk(v.tensor_tensor(o1[:, :, :], o1[:, :, :], o2[:, :, :], ALU.add))

                    def logits():
                        src = B7[:, 0:GT * E].rearrange("p (j e) -> p j e", j=GT)
                        v.wait_ge(lgr.sem, lgr.after(i, 1))
                        if self.gb is not None:
                            lk(v.tensor_tensor(lg[:, :, :], src, rows(self.gb, GT, E), ALU.add))
                        else:
                            lk(v.tensor_copy(lg[:, :, :], src))
                        lk(v.tensor_reduce(m1[:, :], lg[:, :, :], AX.X, ALU.max))
                        v.tensor_tensor(ex[:, :, :], lg[:, :, :], b3(m1[:, :]), ALU.subtract).then_inc(shf.sem, 1)
                        v.wait_ge(shf.sem, shf.after(i, 1))

                    def choose():
                        if kind == "f0":
                            both(lg)
                            v.wait_ge(exr.sem, exr.after(i, 1))
                            lk(v.tensor_tensor(o1[:, :, :], o1[:, :, :], ex[:, :, :], ALU.mult))
                            lk(v.tensor_reduce(sm[:, :], o1[:, :, :], AX.X, ALU.add))
                            lk(v.reciprocal(sm[:, :], sm[:, :]))
                            v.tensor_tensor(g[:, :, 0:E], o1[:, :, :], b3(sm[:, :]), ALU.mult).then_inc(wr.sem, 1)
                            return
                        v.wait_ge(exr.sem, exr.after(i, 1))
                        K.settle(v)
                        lk(v.tensor_reduce(sm[:, :], ex[:, :, :], AX.X, ALU.add))
                        lk(v.reciprocal(sm[:, :], sm[:, :]))
                        lk(v.tensor_tensor(lg[:, :, :], ex[:, :, :], b3(sm[:, :]), ALU.mult))
                        if kind == "f2":
                            both(lg)
                            lk(v.tensor_tensor(o1[:, :, :], o1[:, :, :], lg[:, :, :], ALU.mult))
                            lk(v.tensor_reduce(sm[:, :], o1[:, :, :], AX.X, ALU.add))
                            lk(v.tensor_scalar(sm[:, :], sm[:, :], 1e-9, None, ALU.add))
                            lk(v.reciprocal(sm[:, :], sm[:, :]))
                            v.tensor_tensor(g[:, :, 0:E], o1[:, :, :], b3(sm[:, :]), ALU.mult).then_inc(wr.sem, 1)
                            return
                        pick(lg, m1, o1)
                        for j in range(GT):
                            ins = v.tensor_tensor(run[:, j + 1, :], run[:, j, :], o1[:, j, :], ALU.add)
                            if j < GT - 1:
                                lk(ins)
                        ins.then_inc(cntd.sem, 1)
                        v.wait_ge(cps.sem, cps.after(i, 1))
                        lk(v.tensor_copy(run[:, 0, :], run[:, GT, :]))
                        lk(v.tensor_tensor(l2[:, :, :], B7[:, 64:64 + GT * E].rearrange("p (j e) -> p j e", j=GT), o1[:, :, :], ALU.mult))
                        lk(v.tensor_reduce(sm[:, :], l2[:, :, :], AX.X, ALU.add))
                        lk(v.tensor_scalar(sm[:, :], sm[:, :], float(CAP3), None, ALU.is_le))
                        lk(v.tensor_tensor(sm[:, :], sm[:, :], m1[:, :], ALU.mult))
                        v.tensor_tensor(g[:, :, 0:E], o1[:, :, :], b3(sm[:, :]), ALU.mult).then_inc(wr.sem, 1)

                    def weigh(e):
                        v.wait_ge(eo.sem, eo.after(i, e + 1))
                        v.wait_ge(sd.sem, sd.after(i, e - 1))
                        v.tensor_tensor(prod[:, e % 2, :].rearrange("p (j c) -> p j c", j=GT),
                                        K.bank[4 + e % 2][:, 0:GT * C].rearrange("p (j c) -> p j c", j=GT),
                                        g[:, :, e:e + 1].to_broadcast([P, GT, C]), ALU.mult).then_inc(pr.sem, 1)

                    gates = [0]

                    def gate():
                        c = gates[0]
                        gates[0] += 1
                        v.wait_ge(gtd.sem, gtd.after(i, c + 1))
                        v.wait_ge(eo.sem, eo.after(i, (c - R) // CH + 1))
                        v.tensor_tensor(hT[0:M, c % R, :], ug[0:M, c % 2, :], hbank(c)[1][0:M, :], ALU.mult).then_inc(hr.sem, 1)
                        return c

                    hook = gate if gated else (lambda: None)
                    logits()
                    hook()
                    hook()
                    choose()
                    v.wait_ge(wr.sem, wr.after(i, 1))
                    if kind == "f0":
                        v.tensor_copy(acc[:, :, :], K.xn[:, :, 0, :]).then_inc(acs.sem, 1)
                    elif kind == "f2":
                        v.tensor_copy(acc[:, :, :], kept[:, bass.ds(i * GT, GT), :]).then_inc(acs.sem, 1)
                    else:
                        v.memset(acc[:, :, :], 0.0).then_inc(acs.sem, 1)
                    if gated:
                        e = 0
                        while gates[0] < NC:
                            c = gate()
                            if c == 4:
                                front.statistics(v, i + 1)
                            if c == 10:
                                front.normalise(v, i + 1)
                            if c - lag >= 1 and (c - lag) % CH == CH - 1:
                                weigh(e)
                                e += 1
                        for e in range(e, E):
                            weigh(e)
                    else:
                        for e in range(E):
                            weigh(e)
                            if e == E - 3:
                                v.wait_ge(bps.sem, bps.after(i, 1))
                                v.tensor_copy(bsum[:, :, :], B7[:, 2 * P:4 * P].rearrange("p (j c) -> p j c", j=GT)).then_inc(bmv.sem, 1)
                            if e == 1:
                                front.statistics(v, i + 1)
                            if e == E // 2 - 1:
                                front.normalise(v, i + 1)
                    v.wait_ge(sd.sem, sd.after(i, E))
                    if self.b2 is not None:
                        v.wait_ge(bmv.sem, bmv.after(i, 1))
                        lk(v.tensor_tensor(acc[:, :, :], acc[:, :, :], bsum[:, :, :], ALU.add))
                    if kind == "f0":
                        for j in range(GT):
                            ins = v.bn_stats(bnst[:, j, :], acc[:, j, :])
                        lk(ins, settle=True)
                        for j in range(GT):
                            ins = v.bn_aggr(mv[:, j, :], bnst[:, j, :])
                        ins.then_inc(mst.sem, 1)
                        v.wait_ge(mrs.sem, mrs.after(i, 1))
                        for j in range(GT):
                            ins = v.tensor_scalar(acc[:, j, :], acc[:, j, :], mv[:, j, 0:1], rstd[:, j:j + 1], ALU.subtract, ALU.mult)
                        lk(ins)
                        lk(v.tensor_tensor(acc[:, :, :], acc[:, :, :], rows(K.W("f0_g"), GT, C), ALU.mult))
                        lk(v.tensor_tensor(acc[:, :, :], acc[:, :, :], rows(K.W("f0_b"), GT, C), ALU.add))
                    if kind == "f3":
                        y = flat(acc[:, :, :])
                        lk(v.tensor_tensor(mask[:, :], y, y, ALU.not_equal), settle=True)
                        lk(v.copy_predicated(y, mask[:, :], limits[:, 0, :]))
                        lk(v.tensor_scalar(mask[:, :], y, 3.4028234e38, None, ALU.is_gt), settle=True)
                        lk(v.copy_predicated(y, mask[:, :], limits[:, 1, :]))
                        lk(v.tensor_scalar(mask[:, :], y, -3.4028234e38, None, ALU.is_lt), settle=True)
                        lk(v.copy_predicated(y, mask[:, :], limits[:, 2, :]))
                    v.tensor_tensor(K.hgroup(i), K.hgroup(i), acc[:, :, :], ALU.add)
                    assert st[0] == steps, (kind, st[0])
            for c in counts:
                c.close(GROUPS)
            front.close()


def first_mixture(K):
    Mixture(K, "f0", 1, Front(K, "ln", (1e-5,), dup=True), E0, 1, F0, K.W("f0_w1"), K.W("f0_w2"), b1=K.W("f0_b1"),
            gw=K.W("f0_gw"), gb=K.W("f0_gb"), b2=K.W("f0_b2")).run()


def second_mixture(K, x1):
    Mixture(K, "f2", 6, Front(K, "rms", (1e-6,), dup=True, scale=K.W("f2_ln"), src=x1), E2, 2, F2C, K.W("f2_w1"), K.W("f2_w2"),
            w3=K.W("f2_w3"), gw=K.W("f2_gw"), kept=x1).run()


def third_mixture(K):
    Mixture(K, "f3", 8, Front(K, "ln", (1e-5,), dup=True), E3, 2, P, K.W("f3_w1"), K.W("f3_w2"), b1=K.W("f3_b1"),
            gw=K.W("f3_gw"), gb=K.W("f3_gb"), b2=K.W("f3_b2")).run()


def third_layer_block(K, which=(0, 1)):
    with K.nc.sbuf_tensor("x1", [P, TILES + GT, C], F32) as x1:
        with K.nc.Block() as block:
            @block.vector
            def _(v):
                v.memset(x1[:, TILES:TILES + GT, :], 0.0)
        second_routed_attention(K, x1)
        second_mixture(K, x1)


class KeySoftmaxUnits:

    N = 2

    def __init__(self, K, ctx, qT, kT, vt, scale, mask):
        nc = K.nc
        self.K, self.qT, self.kT, self.vt, self.scale, self.mask = K, qT, kT, vt, scale, mask
        self.sb = ctx.enter_context(nc.sbuf_tensor("a3_masked", [P, 2, 2 * SEQ], F32))
        self.p = ctx.enter_context(nc.sbuf_tensor("a3_probs", [P, 2, 2 * SEQ], F32))
        self.vs = ctx.enter_context(nc.sbuf_tensor("a3_values_over_sum", [P, 2, 2, C], F32))
        self.nm = ctx.enter_context(nc.sbuf_tensor("a3_negmax", [P, 2, 4], F32))
        self.rd = ctx.enter_context(nc.sbuf_tensor("a3_rden", [P, 2, 2], F32))
        names = ("scores_ready", "max_ready", "probs_ready", "values_over_sum", "values_summed", "normalised", "unit_vec")
        self.sc, self.mx, self.ex, self.vo, self.pv, self.no, self.vec = self.all = [K.count(n) for n in names]
        for c, credit in ((self.sc, 0), (self.mx, 0), (self.ex, 2), (self.vo, 0), (self.pv, 2), (self.no, 2)):
            c.stage(2, credit)
        self.vec.stage(8)

    def close(self):
        for c in self.all:
            c.close(GROUPS)

    def open_pe(self, pe):
        pe.sem_inc(self.pv.sem, 2)

    def open_act(self, a):
        a.sem_inc(self.ex.sem, 2)

    def open_vec(self, v):
        v.sem_inc(self.no.sem, 2)

    def tensor(self, pe, i, splice):
        K = self.K
        for s in range(2):
            for m in range(2):
                k0 = s * SEQ + m * P
                ins = pe.matmul(K.bank[s][:, m * SEQ:(m + 1) * SEQ], self.kT[:, k0:k0 + P], self.qT[:, s * SEQ:(s + 1) * SEQ],
                                start=True, stop=True)
            ins.then_inc(self.sc.sem, 1)
        for s in range(2):
            pe.wait_ge(self.vo.sem, self.vo.after(i, s + 1))
            pe.wait_ge(self.no.sem, self.no.after(i, s - 1))
            for n in range(2):
                for m in range(2):
                    ins = pe.matmul(K.bank[OB[s]][:, n * C:(n + 1) * C], self.p[:, s, m * SEQ + n * P:m * SEQ + (n + 1) * P],
                                    self.vs[:, s, m, :], start=m == 0, stop=m == 1, skip_group_check=True)
            ins.then_inc(self.pv.sem, 1)
        for k in sorted(splice):
            splice[k](pe)

    def vector(self, v, i, splice):
        K = self.K
        lk = link(v, self.vec, i, [0], K)
        steps = [splice[k] for k in sorted(splice)]
        for s in range(2):
            v.wait_ge(self.sc.sem, self.sc.after(i, s + 1))
            v.wait_ge(self.ex.sem, self.ex.after(i, s - 1))
            lk(v.tensor_tensor(self.sb[:, s, :], K.bank[s][:, :], self.mask, ALU.add))
            lk(v.tensor_reduce(self.nm[:, s, 2:4], self.sb[:, s, :].rearrange("p (a b) -> p a b", a=2), AX.X, ALU.max, negate=True))
            v.tensor_scalar(self.nm[:, s, 0:2], self.nm[:, s, 2:4], self.scale, None, ALU.mult).then_inc(self.mx.sem, 1)
        steps[0](v)
        K.proj.wait_moved(v, i)
        for s in range(2):
            v.wait_ge(self.ex.sem, self.ex.after(i, s + 1))
            lk(v.tensor_reduce(self.rd[:, s, :], self.p[:, s, :].rearrange("p (a b) -> p a b", a=2), AX.X, ALU.add))
            lk(v.reciprocal(self.rd[:, s, :], self.rd[:, s, :]))
            v.wait_ge(self.pv.sem, self.pv.after(i, s - 1))
            v.tensor_tensor(self.vs[:, s, :, :], self.vt[:, 2 * s:2 * s + 2, :],
                            self.rd[:, s, :].rearrange("p (a c) -> p a c", c=1).to_broadcast([P, 2, C]), ALU.mult).then_inc(self.vo.sem, 1)
        for f in steps[1:]:
            f(v)
        for s in range(2):
            v.wait_ge(self.pv.sem, self.pv.after(i, s + 1))
            dest = K.h[:, bass.ds(i * GT + 2 * s, 2), :]
            v.tensor_tensor(dest, dest, K.bank[OB[s]][:, 0:2 * C].rearrange("p (j c) -> p j c", j=2), ALU.add).then_inc(self.no.sem, 1)

    def scalar(self, a, i, splice):
        K = self.K
        for s in range(2):
            a.wait_ge(self.mx.sem, self.mx.after(i, s + 1))
            a.wait_ge(self.pv.sem, self.pv.after(i, s - 1))
            for m in range(2):
                r = slice(m * SEQ, (m + 1) * SEQ)
                ins = a.activation(self.p[:, s, r], self.sb[:, s, r], ACT.Exp, bias=self.nm[:, s, m:m + 1], scale=self.scale)
            ins.then_inc(self.ex.sem, 1)
        for k in sorted(splice):
            splice[k](a)


class NoTail:

    def stage(self):
        pass

    close = stage

    def open_vec(self, v):
        pass

    def early(self, e, i):
        pass

    wait_free = tensor = vector = scalar = gpsimd = early


def last_attention(K):
    nc = K.nc
    front = Front(K, "ln", (1e-5,))

    def make(ctx):
        qT = ctx.enter_context(nc.sbuf_tensor("a3_qT", [P, NTOK], F32))
        kT = ctx.enter_context(nc.sbuf_tensor("a3_kT", [P, NTOK], F32))
        prepare(K, [], [qT[C:P, :], kT[C:P, :]])
        vt = ctx.enter_context(nc.sbuf_tensor("a3_v_sb", [P, GT, C], F32))
        x = K.xU[:, :]
        jobs = [
            ("act", lambda pe, b, i: pe.matmul(b[0:C, :], K.W("a3_q"), x, start=True, stop=True),
             lambda a, b, i: a.activation(qT[0:C, :], b[0:C, :], ACT.Copy)),
            ("vec", lambda pe, b, i: pe.matmul(b[0:C, :], K.W("a3_k"), x, start=True, stop=True),
             lambda v, b, i: v.tensor_copy(kT[0:C, :], b[0:C, :])),
            ("act", lambda pe, b, i: [pe.matmul(b[:, j * C:(j + 1) * C], K.xU[:, j * P:(j + 1) * P], K.W("a3_v"),
                                                start=True, stop=True) for j in range(GT)][-1],
             lambda a, b, i: a.activation(vt[:, :, :], b[:, 0:GT * C].rearrange("p (j c) -> p j c", j=GT), ACT.Copy)),
        ]
        units = KeySoftmaxUnits(K, ctx, qT, kT, vt, 0.125, K.W("a3_mask"))
        K.proj = Projections(K, jobs)
        return units, K.proj, NoTail()
    attention_stage(K, "a3", 7, front, make)


STAGES = [first_attention, first_mixture, second_attention, expert_heads, third_attention, third_layer_block, last_attention, third_mixture]


def tower(nc, x, turns, image, masks, out, stages=None, h_in=None):
    with ExitStack() as ctx:
        K = Core(nc, ctx)
        embed_stage(K, x, turns, image, masks)
        if h_in is not None:
            hin = K.count("h_in")
            with nc.Block() as block:
                @block.sync
                def _(sp):
                    sp.dma_start(K.h[:, 0:TILES, :], h_in.rearrange("b (a p) c -> p (b a) c", p=P)).then_inc(hin.sem, 16)
                    sp.wait_ge(hin.sem, 16)
        for k, st in enumerate(STAGES):
            if stages is None or k in stages:
                st(K)
            if k == 2:
                late_weights(K, image)
        store_stage(K, out)


def lay_out(a):
    out = {}
    f = lambda n: np.asarray(a[n], np.float32) if np.asarray(a[n]).dtype != np.float32 else np.asarray(a[n])

    def put(name, parts, cols=None):
        w = dict((n, c) for n, c, _ in IMAGE)[name]
        t = np.zeros((P, w), np.float32)
        for (r0, c0, m) in parts:
            m = np.atleast_2d(m)
            t[r0:r0 + m.shape[0], c0:c0 + m.shape[1]] = m
        out[name] = t

    def col(name, *vs):
        put(name, [(0, k, v.reshape(-1, 1)) for k, v in enumerate(vs)])

    def row(name, v):
        put(name, [(0, 0, np.broadcast_to(v.reshape(1, -1), (P, v.size)))])

    put("ident", [(0, 0, np.eye(P, dtype=np.float32))])
    co = f("L0_tok_poly_coeffs").transpose(1, 0, 2).reshape(TURNS * DEG, C)
    put("coef", [(32 * j, j * C, co) for j in range(GT)])
    qkv, qb = f("L0_attn_qkv_w"), f("L0_attn_qkv_b")
    put("a0_qk", [(0, 0, qkv[:, :128])])
    put("a0_v", [(0, 0, qkv[:, 128:])])
    col("a0_lnw", f("L0_attn_ln1_g"), f("L0_attn_ln1_b"))
    col("a0_qkb", qb[:C], qb[C:2 * C])
    row("a0_vb", qb[128:])
    t = f("L0_attn_bias_table")
    q, k = np.arange(SEQ)[:, None], np.arange(SEQ)[None, :]
    rel = t[k - q + SEQ - 1]
    put("a0_bias", [(0, SEQ * b, rel[b * P:(b + 1) * P]) for b in range(2)])
    row("a0_scale", f("L0_attn_scale").reshape(1))
    put("a0_o", [(0, 0, f("L0_attn_proj_w"))])
    row("a0_ob", f("L0_attn_proj_b"))
    row("a0_g2", f("L0_attn_ln2_g"))
    row("a0_b2", f("L0_attn_ln2_b"))
    put("a1_q", [(0, 0, f("L1_attn_Wq"))])
    put("a1_k", [(0, 0, f("L1_attn_Wk"))])
    put("a1_v", [(0, 0, f("L1_attn_Wv"))])
    put("a1_o", [(0, c * C, f("L1_attn_Wu")[c * P:(c + 1) * P]) for c in range(4)])
    put("a1_qb", [(0, 0, f("L1_attn_bq").reshape(4, P).T)])
    put("a1_kb", [(0, 0, f("L1_attn_bk").reshape(4, P).T)])
    row("a1_vb", f("L1_attn_bv"))
    row("a1_ob", f("L1_attn_bu"))
    r0 = np.ones((P, 2), np.float32)
    r0[0, 0] = 0
    put("row0", [(0, 0, r0)])

    put("rank", [(0, 0, np.broadcast_to(16.0 - np.arange(16, dtype=np.float32), (P, 16)))])

    def halves(w, m):
        return [(C * (c % 2), (c // 2) * m, w[c]) for c in range(len(w))]

    def block_bias(b2, e):
        t = np.zeros((P, GT * C), np.float32)
        for j in range(GT):
            t[32 * j:32 * j + e, j * C:(j + 1) * C] = b2
        return [(0, 0, t)]
    put("f0_gw", [(0, 0, f("L0_ffn_gate_w"))])
    row("f0_gb", f("L0_ffn_gate_b"))
    put("f0_w1", halves(f("L0_ffn_w1"), F0))
    put("f0_b1", [(0, 0, f("L0_ffn_b1").T)])
    put("f0_w2", [(0, e * C, f("L0_ffn_w2")[e]) for e in range(E0)])
    put("f0_b2", block_bias(f("L0_ffn_b2"), E0))
    row("f0_g", f("L0_ffn_gamma"))
    row("f0_b", f("L0_ffn_beta"))
    put("a2_q", [(0, 0, f("L2_attn_W_Q").transpose(1, 0, 2).reshape(C, 256))])
    put("a2_k", [(0, 0, f("L2_attn_W_K").transpose(1, 0, 2).reshape(C, 256))])
    put("a2_v", [(0, 0, f("L2_attn_W_V").transpose(1, 0, 2).reshape(C, 256))])
    put("a2_qb", [(0, 0, f("L2_attn_b_Q").reshape(2, P).T)])
    put("a2_kb", [(0, 0, f("L2_attn_b_K").reshape(2, P).T)])
    row("a2_vb", f("L2_attn_b_V"))
    put("a2_o", [(0, c * C, f("L2_attn_W_O").reshape(256, C)[c * P:(c + 1) * P]) for c in range(2)])
    row("a2_ob", f("L2_attn_b_O"))
    col("r2_ln", f("L2_ffn_ln1_w"))
    wq, wk = f("L2_ffn_wq"), f("L2_ffn_wk")
    turn = np.concatenate([np.arange(8, 16), np.arange(0, 8)])
    put("r2_q", [(0, 32 * n, wq[16 * n:16 * n + 16].T) for n in range(4)])
    put("r2_qp", [(0, 32 * n, wq[16 * n:16 * n + 16][turn].T) for n in range(4)])
    put("r2_k", [(0, 32 * n, wk[16 * (n // 2):16 * (n // 2) + 16].T) for n in range(4)])
    put("r2_kp", [(0, 32 * n, wk[16 * (n // 2):16 * (n // 2) + 16][turn].T) for n in range(4)])
    put("r2_v", [(0, 0, f("L2_ffn_wv").T)])
    put("r2_o", [(0, 0, f("L2_ffn_wo").T)])
    inv = 1.0 / 10000.0 ** (np.arange(0, 16, 2, dtype=np.float32) / 16)
    fr = np.outer(np.arange(SEQ, dtype=np.float32), inv)
    emb = np.concatenate([fr, fr], axis=-1).astype(np.float32)
    cos, sin = np.cos(emb).T, np.sin(emb).T.copy()
    sin[0:8] *= -1.0
    for name, tab, sc in (("r2_cq", cos, 0.25), ("r2_sq", sin, 0.25), ("r2_ck", cos, 1.0), ("r2_sk", sin, 1.0)):
        put(name, [(32 * n, 0, (tab * sc).astype(np.float32)) for n in range(4)])
    put("f2_ln", [(0, 0, np.concatenate([f("L2_ffn_ln2_w")] * 2).reshape(P, 1))])
    put("f2_gw", [(0, 0, f("L2_ffn_router_w").T)])
    put("f2_w1", halves(f("L2_ffn_w1").reshape(16, F2C, C).transpose(0, 2, 1), F2C))
    put("f2_w3", halves(f("L2_ffn_w3").reshape(16, F2C, C).transpose(0, 2, 1), F2C))
    w2 = f("L2_ffn_w2").transpose(0, 2, 1).reshape(16, F2C, C)
    put("f2_w2", [(0, c * C, w2[c]) for c in range(16)])
    put("f3_gw", [(0, 0, f("L3_ffn_gate_w"))])
    row("f3_gb", f("L3_ffn_gate_b"))
    w1 = f("L3_ffn_w1").reshape(E3, C, 2, P).transpose(0, 2, 1, 3).reshape(16, C, P)
    put("f3_w1", halves(w1, P))
    put("f3_b1", [(0, 0, f("L3_ffn_b1").reshape(16, P).T)])
    w2 = f("L3_ffn_w2").reshape(16, P, C)
    put("f3_w2", [(0, c * C, w2[c]) for c in range(16)])
    put("f3_b2", block_bias(f("L3_ffn_b2"), E3))
    put("tri", [(0, 0, np.triu(np.ones((P, P), np.float32)))])
    put("ones", [(0, 0, np.ones((P, P), np.float32))])
    put("a3_q", [(0, 0, f("L3_attn_Wq").T)])
    put("a3_k", [(0, 0, f("L3_attn_Wk").T)])
    put("a3_v", [(0, 0, f("L3_attn_Wv").T)])
    n, k = np.arange(SEQ)[None, :], np.arange(P)[:, None]
    put("a3_mask", [(0, b * SEQ, np.where(n < k + b * P, 0, -1.0e10).astype(np.float32)) for b in range(2)])
    hl = f("L1_ffn_hl_w").reshape(C, C)
    put("f1_hl", [(0, 0, hl.T)])
    put("f1_hlb", [(0, 0, f("L1_ffn_hl_b").reshape(C, 1))])
    row("f1_hlbr", f("L1_ffn_hl_b").reshape(C))
    wq, wk, wv, gw = f("L1_ffn_wq"), f("L1_ffn_wk"), f("L1_ffn_wv"), f("L1_ffn_gate_w")
    put("f1_q", [(16 * n, e * P + 32 * n, wq[n, e].T) for n in range(4) for e in range(4)])
    put("f1_k", [(16 * n, 32 * n, wk[n].T) for n in range(4)])
    put("f1_v", [(16 * n, 16 * n, wv[n].T) for n in range(4)])
    put("f1_g", [(64 * (n % 2), 16 * (n // 2) + 4 * n, gw[n].T) for n in range(4)])
    row("f1_gb", f("L1_ffn_gate_b").reshape(16))
    for name, key in (("f1_lg", "ln_g"), ("f1_lb", "ln_b"), ("f1_2b", "fc2_b"), ("f1_ng", "fnorm_g"), ("f1_nb", "fnorm_b")):
        row(name, f("L1_ffn_" + key))
    put("f1_1", [(16 * n, 16 * n, f("L1_ffn_fc1_w").T) for n in range(4)])
    put("f1_2", [(16 * n, 16 * n, f("L1_ffn_fc2_w").T) for n in range(4)])
    put("f1_1b", [(16 * n, 0, f("L1_ffn_fc1_b").reshape(16, 1)) for n in range(4)])
    put("f1_fg", [(0, 0, f("L1_ffn_fgate_w").T)])
    image = np.concatenate([out[n] if n in out else np.zeros((P, c), np.float32) for n, c, _ in IMAGE], axis=1)
    m = np.zeros((P, 18, P), np.float32)
    q, k = np.arange(P)[:, None], np.arange(P)[None, :]
    m[:, 0] = np.eye(P)
    for n in range(4):
        m[:, 1 + n] = np.where(k >= q, MASKED, 0)
        m[:, 5 + n] = np.where(k > q, MASKED, 0)
    for n in range(2):
        odd0 = np.where(((k < q) & (k % 2 == 1)) | (k == q), 0, MASKED)
        m[:, 9 + n] = odd0
        m[:, 11 + 2 * n] = np.where((k % 2 == 1) & (q >= 0), 0, MASKED)
        m[:, 12 + 2 * n] = odd0
    ids = np.ascontiguousarray(np.asarray(a["x"]).astype(np.int32).reshape(TILES, P).T)
    return {"x": ids, "turns": f("L0_tok_turns"), "image": np.ascontiguousarray(image), "masks": m}


def kernel(**inputs):
    import concourse.bacc as bacc
    from concourse.bass_utils import run_bass_kernel_spmd
    arrays = lay_out(inputs)
    nc = bacc.Bacc("TRN2", target_bir_lowering=False, num_devices=1)
    args, feeds = {}, {}
    for name, v in arrays.items():
        feeds[f"in_{name}"] = v
        args[name] = nc.dram_tensor(f"in_{name}", v.shape, mybir.dt.from_np(v.dtype), kind="ExternalInput").ap()
    out = nc.dram_tensor("out", (SEQS, SEQ, C), F32, kind="ExternalOutput").ap()
    tower(nc, args["x"], args["turns"], args["image"], args["masks"], out)
    r = run_bass_kernel_spmd(nc, [feeds], core_ids=[0])
    return r.results[0]["out"]
```

```python
from contextlib import ExitStack

import numpy as np
import concourse.bass as bass
from concourse import mybir

F32 = mybir.dt.float32
BF16 = mybir.dt.bfloat16
I32 = mybir.dt.int32
U32 = mybir.dt.uint32
ALU = mybir.AluOpType
ACT = mybir.ActivationFunctionType
AX = mybir.AxisListType

P = 128
SEQS, SEQ, C = 64, 256, 64
TILES = SEQS * SEQ // P
GT = 4
GROUPS = TILES // GT
NTOK = GT * P
BIG = 3.0e38
MASKED = -1.0e30
VOCAB, TURNS, DEG = 50257, 4, 5
E0, F0 = 16, 128
E2, F2, F2C = 8, 170, 85
E3, F3 = 8, 256
CAP3 = -(-5 * SEQS * SEQ // (4 * E3))

IMAGE = [
    ("ident", P, 0), ("coef", 4 * C, 0), ("rank", 16, 0),
    ("a0_qk", 128, 0), ("a0_v", C, 0), ("a0_lnw", 2, 0), ("a0_qkb", 2, 0), ("a0_vb", C, 0), ("a0_bias", 4 * P, 0),
    ("a0_scale", 1, 0), ("a0_o", C, 0), ("a0_ob", C, 0), ("a0_g2", C, 0), ("a0_b2", C, 0),
    ("f0_gw", E0, 1), ("f0_gb", E0, 1), ("f0_w1", E0 // 2 * F0, 1), ("f0_b1", E0, 1), ("f0_w2", E0 * C, 1),
    ("f0_b2", GT * C, 1), ("f0_g", C, 1), ("f0_b", C, 1),
    ("a1_q", 512, 2), ("a1_k", 512, 2), ("a1_v", 512, 2), ("a1_o", 4 * C, 2), ("a1_qb", 4, 2), ("a1_kb", 4, 2),
    ("a1_vb", 512, 2), ("a1_ob", C, 2), ("row0", 2, 2),
    ("f1_hl", C, 3), ("f1_hlb", 1, 3), ("f1_hlbr", C, 3), ("f1_q", 4 * P, 3), ("f1_k", P, 3), ("f1_v", C, 3),
    ("f1_g", 32, 3), ("f1_gb", 16, 3), ("f1_lg", 16, 3), ("f1_lb", 16, 3), ("f1_1", C, 3), ("f1_1b", 1, 3),
    ("f1_2", C, 3), ("f1_2b", 16, 3), ("f1_ng", 16, 3), ("f1_nb", 16, 3), ("f1_fg", 4, 3),
    ("a2_q", 256, 4), ("a2_k", 256, 4), ("a2_v", 256, 4), ("a2_qb", 2, 4), ("a2_kb", 2, 4), ("a2_vb", 256, 4),
    ("a2_o", 2 * C, 4), ("a2_ob", C, 4),
    ("r2_ln", 1, 5), ("r2_q", P, 5), ("r2_qp", P, 5), ("r2_k", P, 5), ("r2_kp", P, 5), ("r2_v", 32, 5), ("r2_o", C, 5),
    ("r2_cq", SEQ, 5), ("r2_sq", SEQ, 5), ("r2_ck", SEQ, 5), ("r2_sk", SEQ, 5),
    ("f2_ln", 1, 6), ("f2_gw", E2, 6), ("f2_w1", E2 * F2C, 6), ("f2_w3", E2 * F2C, 6), ("f2_w2", 2 * E2 * C, 6),
    ("a3_q", C, 7), ("a3_k", C, 7), ("a3_v", C, 7), ("a3_mask", 4 * P, 7),
    ("f3_gw", E3, 8), ("f3_gb", E3, 8), ("f3_w1", E3 * P, 8), ("f3_b1", 2 * E3, 8), ("f3_w2", 2 * E3 * C, 8),
    ("f3_b2", GT * C, 8), ("tri", P, 8), ("ones", P, 8),
]
LOADS = 9


LATE = (4, 5, 8)


def image_offsets():
    at, out, starts, dram = 0, {}, {}, {}
    size = [sum(c for _, c, g in IMAGE if g == k) for k in range(LOADS)]
    for k in [k for k in range(LOADS) if k not in LATE] + list(LATE):
        if k == LATE[0]:
            total, at = at, out["a0_qk"][0]
        starts[k] = (at, sum(size[:k]), size[k])
        for name, cols, group in IMAGE:
            if group == k:
                out[name] = (at, cols)
                at += cols
    assert at <= starts[3][0]
    return out, total, starts


class Count:

    def __init__(self, sem):
        self.sem, self.base, self.per, self.credit = sem, 0, 0, 0

    def stage(self, per, credit=0):
        self.per, self.credit = per, credit

    def after(self, i, n=0):
        return i * self.per + (self.base + self.credit + n)

    def close(self, groups, extra=0):
        self.base += self.credit + groups * self.per + extra
        self.per = self.credit = 0


def rows(ap, n, inner):
    return ap.rearrange("p (a c) -> p a c", a=1).to_broadcast([P, n, inner])


class Core:

    def __init__(self, nc, ctx):
        self.nc, self.ctx = nc, ctx
        self.off, total, self.starts = image_offsets()
        self.h = ctx.enter_context(nc.sbuf_tensor("h", [P, TILES + GT, C], F32))
        self.w = ctx.enter_context(nc.sbuf_tensor("weights", [P, total], F32))
        self.wb = ctx.enter_context(nc.sbuf_tensor("masks", [P, 18, P], BF16))
        self.xn = ctx.enter_context(nc.sbuf_tensor("xn", [P, GT, 2, C], F32))
        self.xU = ctx.enter_context(nc.sbuf_tensor("xT_upper", [P, NTOK], F32))
        self.xL = ctx.enter_context(nc.sbuf_tensor("xT_lower", [P, NTOK], F32))
        self.bnst = ctx.enter_context(nc.sbuf_tensor("bnst", [P, GT, 6], F32))
        self.mv = ctx.enter_context(nc.sbuf_tensor("mv", [P, GT, 2], F32))
        self.rstd = ctx.enter_context(nc.sbuf_tensor("rstd", [P, GT], F32))
        self.rwork = ctx.enter_context(nc.sbuf_tensor("rwork", [P, 4, 16], F32))
        self.half = ctx.enter_context(nc.sbuf_tensor("minus_half", [P, 16], F32))
        self.bank = [ctx.enter_context(nc.psum_tensor(f"bank{b}", [P, 512], F32)) for b in range(8)]
        self.counts = {}
        self.carrier = ctx.enter_context(nc.semaphore("wait_carrier"))
        self.loaded = [ctx.enter_context(nc.semaphore(f"loaded{k}")) for k in range(LOADS)]

    def count(self, name):
        if name not in self.counts:
            self.counts[name] = Count(self.ctx.enter_context(self.nc.semaphore(name)))
        return self.counts[name]

    def W(self, name, p0=0, p1=P):
        at, cols = self.off[name]
        return self.w[p0:p1, at:at + cols]

    def settle(self, eng):
        eng.sem_inc(self.carrier, 1)

    def hgroup(self, i):
        return self.h[:, bass.ds(i * GT, GT), :]


def link(eng, cnt, i, step, K=None):
    def then(ins, wait=True, settle=False):
        step[0] += 1
        ins.then_inc(cnt.sem, 1)
        if wait:
            eng.wait_ge(cnt.sem, cnt.after(i, step[0]))
        if settle:
            K.settle(eng)
    return then


class Front:

    def __init__(self, K, kind, eps, dup=False, scale=None, bias=None, src=None, kept=None):
        self.K, self.kind, self.eps, self.dup = K, kind, eps, dup
        self.scale, self.bias, self.src, self.kept = scale, bias, K.h if src is None else src, kept
        self.vec, self.stats, self.rs = K.count("front_vec"), K.count("stats_ready"), K.count("rstd_ready")
        self.pool, self.xn_r = K.count("front_pool"), K.count("xn_ready")
        self.xt_ps, self.xt_r = K.count("xT_in_psum"), K.count("xT_ready")
        self.passes = len(eps)
        self.vec.stage({"ln": 1, "lnln": 3, "rms": 2, "lnrms": 4}[kind])
        self.stats.stage(self.passes)
        self.rs.stage(self.passes)
        self.pool.stage(self.passes)
        self.xn_r.stage(1)
        self.xt_ps.stage(1, 1)
        self.xt_r.stage(1)

    def close(self, groups=GROUPS + 1):
        for c in (self.vec, self.stats, self.rs, self.pool, self.xn_r, self.xt_ps, self.xt_r):
            c.close(groups)

    def open_pe(self, pe):
        pe.sem_inc(self.xt_ps.sem, 1)

    def mean_var(self, v, src, lk):
        K = self.K
        for j in range(GT):
            ins = v.bn_stats(K.bnst[:, j, :], src(j))
        lk(ins, settle=True)
        for j in range(GT):
            ins = v.bn_aggr(K.mv[:, j, :], K.bnst[:, j, :])
        ins.then_inc(self.stats.sem, 1)

    def mean_square(self, v, src, lk):
        K = self.K
        lk(v.tensor_tensor(K.xn[:, :, 0, :], src, src, ALU.mult))
        lk(v.tensor_reduce(K.mv[:, :, 0], K.xn[:, :, 0, :], AX.X, ALU.add))
        v.tensor_scalar(K.mv[:, :, 1], K.mv[:, :, 0], 1.0 / C, None, ALU.mult).then_inc(self.stats.sem, 1)

    def statistics(self, v, i):
        self.lk = link(v, self.vec, i, [0], self.K)
        if self.kind == "rms":
            v.wait_ge(self.xt_ps.sem, self.xt_ps.after(i, 0))
            self.mean_square(v, self.src[:, bass.ds(i * GT, GT), :], self.lk)
        else:
            self.mean_var(v, lambda j: self.src[:, bass.ds(i * GT + j, 1), :], self.lk)

    def rstds(self, g, i):
        K = self.K
        for n, eps in enumerate(self.eps):
            g.wait_ge(self.stats.sem, self.stats.after(i, n + 1))
            K.settle(g)
            g.tensor_scalar(K.rwork[:, 0, 0:GT], K.mv[:, :, 1], eps, None, ALU.add).then_inc(self.pool.sem, 1)
            g.wait_ge(self.pool.sem, self.pool.after(i, n + 1))
            g.tensor_tensor(K.rstd[:, :], K.rwork[:, 0, 0:GT], K.half[:, 0:GT], ALU.pow).then_inc(self.rs.sem, 1)

    def normalise(self, v, i):
        K = self.K
        v.wait_ge(self.rs.sem, self.rs.after(i, 1))
        v.wait_ge(self.xt_ps.sem, self.xt_ps.after(i, 0))
        centred = (lambda dst, src, j: v.tensor_scalar(dst, src, K.mv[:, j, 0:1], K.rstd[:, j:j + 1], ALU.subtract, ALU.mult))
        scaled = (lambda dst, src, j: v.tensor_scalar(dst, src, K.rstd[:, j:j + 1], None, ALU.mult))
        tile = (lambda j: self.src[:, bass.ds(i * GT + j, 1), :])
        last = centred
        if self.kind == "lnln":
            for j in range(GT):
                ins = centred(K.xn[:, j, 0, :], tile(j), j)
            self.lk(ins)
            self.mean_var(v, lambda j: K.xn[:, j, 0, :], self.lk)
            tile = (lambda j: K.xn[:, j, 0, :])
        elif self.kind == "lnrms":
            for j in range(GT):
                ins = centred(self.kept[:, bass.ds(i * GT + j, 1), :], tile(j), j)
            self.lk(ins)
            self.mean_square(v, self.kept[:, bass.ds(i * GT, GT), :], self.lk)
            tile = (lambda j: self.kept[:, bass.ds(i * GT + j, 1), :])
        if self.passes == 2:
            v.wait_ge(self.rs.sem, self.rs.after(i, 2))
        if "rms" in self.kind:
            last = scaled
        for j in range(GT):
            for d in range(2 if self.dup else 1):
                ins = last(K.xn[:, j, d, :], tile(j), j)
        ins.then_inc(self.xn_r.sem, 1)

    def transpose(self, pe, i, bank):
        K = self.K
        pe.wait_ge(self.xn_r.sem, self.xn_r.after(i, 1))
        K.settle(pe)
        for j in range(GT):
            if self.dup:
                ins = pe.transpose(K.bank[bank][:, j * P:(j + 1) * P], K.xn[:, j, :, :].rearrange("p a c -> p (a c)"), K.W("ident"))
            else:
                ins = pe.transpose(K.bank[bank][0:C, j * P:(j + 1) * P], K.xn[:, j, 0, :], K.W("ident"))
        ins.then_inc(self.xt_ps.sem, 1)

    def move(self, a, i, bank, to=None):
        K = self.K
        a.wait_ge(self.xt_ps.sem, self.xt_ps.after(i, 1))
        for dst, p0 in zip(to or (K.xU, K.xL), (0, C) if self.dup else (0,)):
            r = slice(p0, p0 + C)
            if self.scale is None:
                ins = a.activation(dst[r, :], K.bank[bank][r, :], ACT.Copy)
            elif self.bias is None:
                ins = a.activation(dst[r, :], K.bank[bank][r, :], ACT.Copy, scale=self.scale[r, :])
            else:
                ins = a.activation(dst[r, :], K.bank[bank][r, :], ACT.Identity, scale=self.scale[r, :], bias=self.bias[r, :])
        ins.then_inc(self.xt_r.sem, 1)


def embed_stage(K, x, turns, image, masks):
    nc = K.nc
    HALF = 4
    CT = TILES // HALF
    feat_r, ft_ps, ft_sb, emb_ps, emb_r = (K.count(n) for n in ("features_ready", "featT_in_psum", "featT_ready",
                                                                "emb_in_psum", "emb_ready"))
    with ExitStack() as ctx:
        def sb(n, s, d=F32):
            return ctx.enter_context(nc.sbuf_tensor(n, s, d))
        ids = sb("ids", [P, TILES], I32)
        rowsT = sb("turn_rows", [P, TILES * TURNS])
        absT = sb("turn_abs", [P, TILES * TURNS])
        intT = sb("turn_int", [P, TILES * TURNS], I32)
        feat = sb("features", [P, TILES, 32])
        fstage = sb("feature_stage", [P, 2, P])
        featT = sb("featT", [P, 2, P])
        masks_in = sb("masks_in", [P, 18, P])
        masks_loaded = K.count("masks_loaded")
        ids_in, gathered = K.count("ids_in"), [K.count(f"gathered{c}") for c in range(HALF)]
        vec, zeroed, staged = K.count("embed_vec"), K.count("zeroed"), K.count("feature_staged")
        for c in (feat_r, ft_ps, ft_sb, emb_ps, emb_r, staged):
            c.stage(1)
        block = ctx.enter_context(nc.Block())

        @block.sync
        def _(sp):
            sp.dma_start(ids[:, :], x).then_inc(ids_in.sem, 16)
            sp.dma_start(masks_in[:, :, :], masks).then_inc(masks_loaded.sem, 16)
            for k in [k for k in range(LOADS) if k not in LATE]:
                at, src, cols = K.starts[k]
                sp.dma_start(K.w[:, at:at + cols], image[:, src:src + cols]).then_inc(K.loaded[k], 16)

        @block.gpsimd
        def _(g):
            g.memset(K.half[:, :], -0.5)
            g.memset(K.h[:, TILES:TILES + GT, :], 0.0)
            g.memset(feat[:, :, TURNS * DEG:32], 0.0)
            g.memset(feat[:, :, 0:TURNS], 1.0).then_inc(zeroed.sem, 1)
            g.wait_ge(ids_in.sem, 16)
            for c in range(HALF):
                for j in range(c * CT, (c + 1) * CT):
                    g.indirect_dma_start(rowsT[:, j * TURNS:(j + 1) * TURNS], None, turns,
                                         bass.IndirectOffsetOnAxis(ids[:, j:j + 1].bitcast(U32), 0)).then_inc(gathered[c].sem, 16)

        per_chunk = GROUPS // HALF

        @block.scalar
        def _(a):
            a.preload_act_table(ACT.Exp)
            for c in range(HALF):
                a.wait_ge(feat_r.sem, c + 1)
                with a.Fori(c * per_chunk // 2, (c + 1) * per_chunk // 2) as i0:
                    for u in range(2):
                        i = i0 * 2 + u
                        a.wait_ge(emb_ps.sem, i + 1)
                        a.activation(fstage[:, u, :], feat[:, bass.ds(i * GT, GT), :], ACT.Copy).then_inc(staged.sem, 1)
                        a.wait_ge(ft_ps.sem, i + 1)
                        a.activation(featT[:, u, :], K.bank[u][:, 0:P], ACT.Copy).then_inc(ft_sb.sem, 1)

        @block.tensor
        def _(pe):
            pe.wait_ge(K.loaded[0], 16)
            pe.sem_inc(emb_ps.sem, 1)
            with pe.Fori(0, GROUPS // 2) as i0:
                for u in range(2):
                    i = i0 * 2 + u
                    pe.wait_ge(staged.sem, i + 1)
                    pe.transpose(K.bank[u][:, 0:P], fstage[:, u, :], K.W("ident")).then_inc(ft_ps.sem, 1)
                    pe.wait_ge(ft_sb.sem, i + 1)
                    pe.wait_ge(emb_r.sem, i0 * 2 + 1)
                    pe.matmul(K.bank[2 + u][:, 0:GT * C], featT[:, u, :], K.W("coef"), start=True, stop=True)\
                        .then_inc(emb_ps.sem, 1)

        @block.vector
        def _(v):
            n = 0
            v.memset(K.xU[C:P, :], 0.0)
            v.memset(K.xL[0:C, :], 0.0)
            v.wait_ge(masks_loaded.sem, 16)
            v.tensor_copy(K.wb[:, :, :], masks_in[:, :, :])
            v.wait_ge(zeroed.sem, 1)

            def lk(ins):
                nonlocal n
                n += 1
                ins.then_inc(vec.sem, 1)
                v.wait_ge(vec.sem, n)
            for c in range(HALF):
                v.wait_ge(gathered[c].sem, 16 * CT)
                s = slice(c * CT * TURNS, (c + 1) * CT * TURNS)
                t, a, k = rowsT[:, s], absT[:, s], intT[:, s]
                lk(v.scalar_tensor_tensor(a, t, -1.0, t, ALU.mult, ALU.max))
                lk(v.tensor_copy(k, a))
                f1 = feat[:, c * CT:(c + 1) * CT, TURNS:2 * TURNS]
                a3 = a.rearrange("p (j d) -> p j d", d=TURNS)
                t3 = t.rearrange("p (j d) -> p j d", d=TURNS)
                lk(v.tensor_copy(f1, k.rearrange("p (j d) -> p j d", d=TURNS)))
                lk(v.tensor_tensor(a3, f1, a3, ALU.is_gt))
                lk(v.tensor_tensor(f1, f1, a3, ALU.subtract))
                lk(v.tensor_scalar(a, t, 0.0, 2.0, ALU.is_ge, ALU.mult))
                lk(v.tensor_scalar(a, a, -1.0, None, ALU.add))
                lk(v.tensor_tensor(f1, f1, a3, ALU.mult))
                for d in range(2, DEG):
                    prev = feat[:, c * CT:(c + 1) * CT, (d - 1) * TURNS:d * TURNS]
                    cur = feat[:, c * CT:(c + 1) * CT, d * TURNS:(d + 1) * TURNS]
                    ins = v.tensor_tensor(cur, prev, f1, ALU.mult)
                    if d < DEG - 1:
                        lk(ins)
                ins.then_inc(feat_r.sem, 1)
            v.sem_inc(emb_r.sem, 1)
            with v.Fori(0, GROUPS // 2) as i0:
                for u in range(2):
                    i = i0 * 2 + u
                    v.wait_ge(emb_ps.sem, i + 2)
                    v.tensor_copy(K.hgroup(i), K.bank[2 + u][:, 0:GT * C].rearrange("p (j c) -> p j c", j=GT))\
                        .then_inc(emb_r.sem, 1)


def late_weights(K, image):
    with K.nc.Block() as block:
        @block.sync
        def _(sp):
            for k in LATE:
                at, src, cols = K.starts[k]
                sp.dma_start(K.w[:, at:at + cols], image[:, src:src + cols]).then_inc(K.loaded[k], 16)


def store_stage(K, out):
    nc = K.nc
    done = K.count("stored")
    with nc.Block() as block:
        @block.sync
        def _(sp):
            o = out.rearrange("b (a p) c -> p (b a) c", p=P)
            for k in range(8):
                n = TILES // 8
                sp.dma_start(o[:, k * n:(k + 1) * n, :], K.h[:, k * n:(k + 1) * n, :]).then_inc(done.sem, 16)
            sp.wait_ge(done.sem, 128)


class Unit:

    def __init__(self, scores, masks, softs, outs, vw, dest):
        self.scores, self.masks, self.softs, self.outs, self.vw, self.dest = scores, masks, softs, outs, vw, dest
        self.cols = max(c + r * w for c, r, w in softs)
        self.rows = sum(r for _, r, _ in softs)


TB = (3, 4)
OB = (5, 6)
JB = (2, 7)


class Units:

    def __init__(self, K, ctx, units, bias=None, rownorm=None, piped=False):
        nc = K.nc
        self.K, self.sets, self.bias, self.rownorm, self.piped = K, units, bias, rownorm, piped
        self.N = len(units[0])
        self.SB, self.RP = ((0, 1), 2) if piped else ((0, 1, 2), 3)
        self.p = ctx.enter_context(nc.sbuf_tensor(f"probs_{nc.next_id()}", [P, self.RP, 512], F32))
        self.pT = ctx.enter_context(nc.sbuf_tensor(f"probsT_{nc.next_id()}", [P, 2, 512], F32))
        self.nm = ctx.enter_context(nc.sbuf_tensor(f"negmax_{nc.next_id()}", [P, 4, 4], F32))
        self.rd = ctx.enter_context(nc.sbuf_tensor(f"rden_{nc.next_id()}", [P, 2, 4], F32))
        if bias is not None:
            self.sb = ctx.enter_context(nc.sbuf_tensor(f"biased_{nc.next_id()}", [P, 4, 512], F32))
        names = ("scores_ready", "max_ready", "probs_ready", "probsT_in_psum", "probsT_ready", "values_summed", "normalised")
        self.sc, self.mx, self.ex, self.tp, self.tr, self.pv, self.no = (K.count(n) for n in names)
        self.vec = K.count("unit_vec")
        for c, credit in ((self.sc, 0), (self.mx, 0), (self.ex, 4), (self.tp, self.RP), (self.tr, 2), (self.pv, 2), (self.no, 2)):
            c.stage(self.N, credit)
        self.links = 1 + (bias is not None) + (rownorm is not None)
        self.vec.stage(self.N * self.links)

    def close(self, steps=0):
        for c, behind in ((self.sc, 0), (self.mx, 0), (self.ex, 0), (self.tp, 2), (self.tr, 2), (self.pv, 3), (self.no, 4)):
            c.close(GROUPS, max(0, steps - behind))
        self.vec.close(GROUPS)

    def open_pe(self, pe):
        pe.sem_inc(self.tp.sem, self.RP)
        pe.sem_inc(self.pv.sem, 2)

    def open_act(self, a):
        a.sem_inc(self.ex.sem, 4)
        a.sem_inc(self.tr.sem, 2)

    def open_vec(self, v):
        v.sem_inc(self.no.sem, 2)

    def unit(self, u, t):
        return self.sets[u % len(self.sets)][t] if t >= 0 else self.sets[(u + 1) % len(self.sets)][t]

    def pe_scores(self, pe, i, u, s):
        K, unit, nb = self.K, self.unit(u, s), len(self.SB)
        b = K.bank[self.SB[s % nb]]
        pe.wait_ge(self.ex.sem, self.ex.after(i, s - nb + 1))
        for n, (c, w, lhsT, rhs) in enumerate(unit.scores):
            ins = pe.matmul(b[:, c:c + w], lhsT, rhs, start=n == 0 or not unit.masks, stop=not unit.masks, skip_group_check=True)
        for n, (c, w, m) in enumerate(unit.masks):
            ins = pe.matmul(b[:, c:c + w], K.wb[:, 0, :], m, start=False, stop=True, skip_group_check=True)
        ins.then_inc(self.sc.sem, 1)

    def pe_turn(self, pe, i, u, t):
        K = self.K
        pe.wait_ge(self.ex.sem, self.ex.after(i, t + 1))
        pe.wait_ge(self.tr.sem, self.tr.after(i, t - 1))
        for c in range(0, self.unit(u, t).cols, P):
            ins = pe.transpose(K.bank[TB[t % 2]][:, c:c + P], self.p[:, t % self.RP, c:c + P], K.W("ident"))
        ins.then_inc(self.tp.sem, 1)

    def pe_values(self, pe, i, u, t):
        K, unit = self.K, self.unit(u, t)
        pe.wait_ge(self.tr.sem, self.tr.after(i, t + 1))
        pe.wait_ge(self.no.sem, self.no.after(i, t - 1))
        for n, terms in enumerate(unit.outs):
            for m, (blk, val) in enumerate(terms):
                ins = pe.matmul(K.bank[OB[t % 2]][:, n * unit.vw:(n + 1) * unit.vw], self.pT[:, t % 2, blk * P:(blk + 1) * P], val,
                                start=m == 0, stop=m == len(terms) - 1, skip_group_check=True)
        ins.then_inc(self.pv.sem, 1)

    def vec_max(self, v, i, u, s, lk):
        K, unit = self.K, self.unit(u, s)
        b = K.bank[self.SB[s % len(self.SB)]]
        v.wait_ge(self.sc.sem, self.sc.after(i, s + 1))
        v.wait_ge(self.ex.sem, self.ex.after(i, s - 3))
        src = b
        if self.bias is not None:
            lk(v.tensor_tensor(self.sb[:, s % 4, :], b[:, :], self.bias, ALU.add))
            src = self.sb[:, s % 4, :]
        r = 0
        for n, (c, k, w) in enumerate(unit.softs):
            ins = v.tensor_reduce(self.nm[:, s % 4, r:r + k], src[:, c:c + k * w].rearrange("p (a b) -> p a b", a=k),
                                  AX.X, ALU.max, negate=True)
            r += k
        ins.then_inc(self.mx.sem, 1)

    def vec_norm(self, v, i, u, t, lk):
        K, unit = self.K, self.unit(u, t)
        n = len(unit.outs)
        o = K.bank[OB[t % 2]][:, 0:n * unit.vw].rearrange("p (a c) -> p a c", c=unit.vw)
        v.wait_ge(self.pv.sem, self.pv.after(i, t + 1))
        lk(v.reciprocal(self.rd[:, t % 2, 0:n].rearrange("p (a c) -> p a c", c=1), o[:, :, unit.vw - 1:unit.vw]))
        if self.rownorm is not None:
            lk(v.tensor_tensor(self.rd[:, t % 2, 0:n], self.rd[:, t % 2, 0:n], self.rownorm(t % self.N, n), ALU.mult))
        v.tensor_tensor(unit.dest, o[:, :, 0:unit.vw - 1],
                        self.rd[:, t % 2, 0:n].rearrange("p (a c) -> p a c", c=1).to_broadcast([P, n, unit.vw - 1]), ALU.mult)\
            .then_inc(self.no.sem, 1)

    def act_exp(self, a, i, u, s):
        unit = self.unit(u, s)
        a.wait_ge(self.mx.sem, self.mx.after(i, s + 1))
        a.wait_ge(self.tp.sem, self.tp.after(i, s - self.RP + 1))
        src = self.K.bank[self.SB[s % len(self.SB)]] if self.bias is None else self.sb[:, s % 4, :]
        r = 0
        for c, k, w in unit.softs:
            for m in range(k):
                ins = a.activation(self.p[:, s % self.RP, c + m * w:c + (m + 1) * w], src[:, c + m * w:c + (m + 1) * w],
                                   ACT.Exp, bias=self.nm[:, s % 4, r:r + 1])
                r += 1
        ins.then_inc(self.ex.sem, 1)

    def act_move(self, a, i, u, t):
        a.wait_ge(self.tp.sem, self.tp.after(i, t + 1))
        a.wait_ge(self.pv.sem, self.pv.after(i, t - 1))
        n = self.unit(u, t).cols
        a.activation(self.pT[:, t % 2, 0:n], self.K.bank[TB[t % 2]][:, 0:n], ACT.Copy).then_inc(self.tr.sem, 1)

    def tensor(self, pe, i, splice):
        for s in range(self.N + 3):
            if s < self.N:
                self.pe_scores(pe, i, 0, s)
            if s in splice:
                splice[s](pe)
            if 0 <= s - 2 < self.N:
                self.pe_turn(pe, i, 0, s - 2)
            if 0 <= s - 3:
                self.pe_values(pe, i, 0, s - 3)

    def vector(self, v, i, splice):
        lk = link(v, self.vec, i, [0], self.K)
        for s in range(self.N + 4):
            if s < self.N:
                self.vec_max(v, i, 0, s, lk)
            if s in splice:
                splice[s](v)
            if s >= 4:
                self.vec_norm(v, i, 0, s - 4, lk)

    def scalar(self, a, i, splice):
        for s in range(self.N + 2):
            if s < self.N:
                self.act_exp(a, i, 0, s)
            if s in splice:
                splice[s](a)
            if s >= 2:
                self.act_move(a, i, 0, s - 2)


class Jobs:

    def __init__(self, K, front, proj, tail):
        self.K, self.front, self.np, self.nt = K, front, len(proj[0]), len(tail[0])
        self.jobs = [proj[u] + tail[u] for u in range(2)]
        self.ready = K.count("projection_ready")
        self.by = {"act": K.count("projection_moved_act"), "vec": K.count("projection_moved_vec")}
        who = [w for w, *_ in self.jobs[0]]
        self.who = who
        self.idx = [who[:k + 1].count(w) for k, w in enumerate(who)]
        self.early = {w: who[self.np:].count(w) for w in self.by}
        self.ready.stage(len(who), len(who))
        for w in self.by:
            self.by[w].stage(who.count(w), who.count(w))

    def close(self):
        for c in (self.ready, *self.by.values()):
            c.close(GROUPS)

    def value(self, cnt, b, n, early):
        return cnt.base + early + n if isinstance(b, int) else cnt.after(b, n)

    def open(self, eng, who):
        cnt, n = (self.ready, self.nt) if who == "pe" else (self.by[who], self.early[who])
        if n:
            eng.sem_inc(cnt.sem, n)

    def wait_moved(self, eng, b, k):
        w = self.who[k]
        eng.wait_ge(self.by[w].sem, self.value(self.by[w], b, self.idx[k], self.early[w]))

    def wait_proj(self, eng, b):
        for w in self.by:
            n = self.who[:self.np].count(w)
            if n:
                eng.wait_ge(self.by[w].sem, self.value(self.by[w], b, n, self.early[w]))

    def bank(self, k):
        return JB[(k + 1) % 2]

    def free(self, pe, b, k):
        nj = len(self.who)
        prev = k - 2
        if prev == -1:
            return
        if prev >= 0:
            self.wait_moved(pe, b, prev)
            return
        if isinstance(b, int):
            return
        last = [j for j in range(-1, nj) if self.bank(j) == self.bank(k)][-1]
        w = self.who[last]
        pe.wait_ge(self.by[w].sem, self.by[w].after(b, self.idx[last] - self.by[w].per))

    def tensor(self, pe, b, u, k):
        if k == -1:
            self.free(pe, b, k)
            self.front.transpose(pe, b + 1, self.bank(k))
            return
        if k == 0:
            pe.wait_ge(self.front.xt_r.sem, self.front.xt_r.after(b + 1, 1))
        self.free(pe, b, k)
        self.K.settle(pe)
        g, u = (b + 1, 1 - u) if k < self.np else (b, u)
        self.jobs[u][k][1](pe, self.K.bank[self.bank(k)], g).then_inc(self.ready.sem, 1)

    def move(self, eng, who, b, u, k):
        if k == -1:
            if who == "act":
                self.front.move(eng, b + 1, self.bank(k))
            return
        if self.who[k] == who:
            eng.wait_ge(self.ready.sem, self.value(self.ready, b, k + 1, self.nt))
            g, u = (b + 1, 1 - u) if k < self.np else (b, u)
            self.jobs[u][k][2](eng, self.K.bank[self.bank(k)], g).then_inc(self.by[who].sem, 1)


def piped_stage(K, load, front, r, make, first=2):
    nc = K.nc
    with ExitStack() as ctx:
        units, jobs, tail = make(ctx)
        N = units.N
        links = (r - 4) * units.links
        units.vec.stage(N * units.links, links)
        place = {}
        slots = [(s, n) for s in range(r + 1, N) for n in range(3)][first + 1:]
        place[(r + 1, first)] = [-1]
        for k in range(jobs.np):
            place.setdefault(slots[k * len(slots) // jobs.np], []).append(k)
        for k in range(jobs.nt):
            n = k + 1 + (k == jobs.nt - 1 and jobs.nt > 2)
            assert 4 + n // 3 < r
            place[(4 + n // 3, n % 3)] = [jobs.np + k]

        def body(step, b, u):
            for s in range(r, N):
                step(b, u, s, b, u)
            for s in range(r):
                step(b + 1, 1 - u, s, b, u)

        def run(eng, step, begin):
            begin()
            for s in range(r):
                step(0, 0, s, None, None)
            with eng.Fori(0, GROUPS // 2) as i0:
                body(step, i0 * 2, 0)
                body(step, i0 * 2 + 1, 1)

        block = ctx.enter_context(nc.Block())

        @block.tensor
        def _(pe):
            def job(b, u, s, n):
                for k in place.get((s, n), ()) if b is not None else ():
                    jobs.tensor(pe, b, u, k)

            def step(g, u, s, b, bu):
                if s == 0:
                    jobs.wait_proj(pe, -1 if b is None else b)
                units.pe_scores(pe, g, u, s)
                job(b, bu, s, 0)
                if b is not None or s >= 2:
                    units.pe_turn(pe, g, u, s - 2)
                job(b, bu, s, 1)
                if b is not None or s >= 3:
                    units.pe_values(pe, g, u, s - 3)
                job(b, bu, s, 2)

            def begin():
                pe.wait_ge(K.loaded[load], 16)
                front.open_pe(pe)
                units.open_pe(pe)
                jobs.open(pe, "pe")
                for k in range(-1, jobs.np):
                    jobs.tensor(pe, -1, 1, k)
            run(pe, step, begin)

        @block.vector
        def _(v):
            lk = [None]

            def step(g, u, s, b, bu):
                if b is None:
                    if s == 0:
                        lk[0] = link(v, units.vec, 0, [-links], K)
                elif s == r:
                    lk[0] = link(v, units.vec, b, [0], K)
                    front.statistics(v, b + 1)
                elif s == r + 1:
                    front.normalise(v, b + 1)
                elif s < r and s in tail.vec_hooks:
                    tail.vec_hooks[s](v, b, bu)
                units.vec_max(v, g, u, s, lk[0])
                for n in range(3):
                    for k in place.get((s, n), ()) if b is not None else ():
                        jobs.move(v, "vec", b, bu, k)
                    if n == 0 and (b is not None or s >= 4):
                        units.vec_norm(v, g, u, s - 4, lk[0])

            def begin():
                v.wait_ge(K.loaded[load], 16)
                units.open_vec(v)
                jobs.open(v, "vec")
                front.statistics(v, 0)
                front.normalise(v, 0)
                for k in range(jobs.np):
                    jobs.move(v, "vec", -1, 1, k)
            run(v, step, begin)

        @block.scalar
        def _(a):
            def step(g, u, s, b, bu):
                if b is not None and s < r and s in tail.act_hooks:
                    tail.act_hooks[s](a, b, bu)
                units.act_exp(a, g, u, s)
                for n in range(3):
                    for k in place.get((s, n), ()) if b is not None else ():
                        jobs.move(a, "act", b, bu, k)
                    if n == 0 and (b is not None or s >= 2):
                        units.act_move(a, g, u, s - 2)

            def begin():
                a.wait_ge(K.loaded[load], 16)
                units.open_act(a)
                jobs.open(a, "act")
                for k in range(-1, jobs.np):
                    jobs.move(a, "act", -1, 1, k)
            run(a, step, begin)

        @block.gpsimd
        def _(g):
            front.rstds(g, 0)
            with g.Fori(0, GROUPS) as i:
                front.rstds(g, i + 1)
        units.close(r)
        units.vec.base += 0
        jobs.close()
        front.close()
        for c, per in tail.counts:
            c.close(GROUPS + per)


class PipedTail:

    def __init__(self, K, ctx, osb, wo, bias, units, onto=None):
        nc = K.nc
        self.K, self.osb, self.wo, self.bias, self.units = K, osb, wo, bias, units
        self.onto = K.h if onto is None else onto
        self.width = osb[0].shape[2]
        self.nch, self.k = -(-self.width // P), min(P, self.width)
        self.oT = ctx.enter_context(nc.sbuf_tensor(f"outT_{nc.next_id()}", [P, self.nch, NTOK], F32))
        self.y = ctx.enter_context(nc.sbuf_tensor(f"out_{nc.next_id()}", [P, GT, C], F32)) if bias is not None else None
        self.vec = K.count("tail_vec")
        self.vec.stage(1 if bias is not None else 0)
        self.counts = [(self.vec, 0)]
        self.vec_hooks, self.act_hooks = {}, {}
        self.jobs = None

    def heads_ready(self, pe, g):
        pe.wait_ge(self.units.no.sem, self.units.no.after(g, self.units.N))

    def cols(self, j, width):
        return slice(j * width, (j + 1) * width)

    def list(self, u, width=C):
        def turn(c):
            def mm(pe, b, g):
                if c == 0:
                    self.heads_ready(pe, g)
                    self.K.settle(pe)
                for j in range(GT):
                    ins = pe.transpose(b[0:self.k, j * P:(j + 1) * P], self.osb[u][:, j, c * P:c * P + self.k], self.K.W("ident"))
                return ins
            return ("act", mm, lambda a, b, g: a.activation(self.oT[0:self.k, c, :], b[0:self.k, :], ACT.Copy))

        def product(pe, b, g):
            self.jobs.wait_moved(pe, g, self.jobs.np + self.nch - 1)
            self.K.settle(pe)
            for j in range(GT):
                for c in range(self.nch):
                    ins = pe.matmul(b[:, self.cols(j, width)], self.oT[0:self.k, c, j * P:(j + 1) * P],
                                    self.wo[0:self.k, c * width:(c + 1) * width], start=c == 0, stop=c == self.nch - 1, skip_group_check=True)
            return ins
        return [turn(c) for c in range(self.nch)] + [("vec", product, self.add)]

    def add(self, v, b, g):
        dest = self.onto[:, bass.ds(g * GT, GT), :]
        o = b[:, 0:GT * C].rearrange("p (j c) -> p j c", j=GT)
        if self.bias is None:
            return v.tensor_tensor(dest, dest, o, ALU.add)
        v.tensor_tensor(self.y[:, :, :], o, rows(self.bias, GT, C), ALU.add).then_inc(self.vec.sem, 1)
        v.wait_ge(self.vec.sem, self.vec.after(g, 1))
        self.K.settle(v)
        return v.tensor_tensor(dest, dest, self.y[:, :, :], ALU.add)


PB = (0, 1, 2, 7)


class Projections:

    def __init__(self, K, jobs):
        self.K, self.jobs = K, jobs
        self.ready, self.by = K.count("projection_ready"), {"act": K.count("projection_moved_act"), "vec": K.count("projection_moved_vec")}
        self.ready.stage(len(jobs))
        self.idx = []
        seen = {"act": 0, "vec": 0}
        for who, *_ in jobs:
            seen[who] += 1
            self.idx.append(seen[who])
        for who in seen:
            self.by[who].stage(seen[who])
        self.seen = seen

    def close(self):
        for c in (self.ready, *self.by.values()):
            c.close(GROUPS + 1)

    def tensor(self, pe, i):
        for j, (who, mm, _) in enumerate(self.jobs):
            if j >= len(PB):
                w = self.jobs[j - len(PB)][0]
                pe.wait_ge(self.by[w].sem, self.by[w].after(i, self.idx[j - len(PB)]))
            elif j == 0:
                for w, n in self.seen.items():
                    if n:
                        pe.wait_ge(self.by[w].sem, self.by[w].after(i, 0))
            self.K.settle(pe)
            mm(pe, self.K.bank[PB[j % 4]], i).then_inc(self.ready.sem, 1)

    def move(self, eng, who, i):
        for j, (w, _, mv) in enumerate(self.jobs):
            if w == who:
                eng.wait_ge(self.ready.sem, self.ready.after(i, j + 1))
                mv(eng, self.K.bank[PB[j % 4]], i).then_inc(self.by[who].sem, 1)

    def wait_moved(self, pe, i):
        for w, n in self.seen.items():
            if n:
                pe.wait_ge(self.by[w].sem, self.by[w].after(i, n))


def attention_stage(K, name, load, front, make):
    nc = K.nc
    with ExitStack() as ctx:
        units, proj, tail = make(ctx)
        block = ctx.enter_context(nc.Block())
        tail.stage()
        A0, A1, A2 = 0, min(2, units.N), min(4, units.N + 1)

        @block.tensor
        def _(pe):
            pe.wait_ge(K.loaded[load], 16)
            front.open_pe(pe)
            units.open_pe(pe)
            front.transpose(pe, 0, 7)
            pe.wait_ge(front.xt_r.sem, front.xt_r.after(0, 1))
            proj.tensor(pe, 0)
            with pe.Fori(0, GROUPS) as i:
                proj.wait_moved(pe, i)
                units.tensor(pe, i, {1: lambda e: tail.wait_free(e, i), A2: lambda e: front.transpose(e, i + 1, 7)})
                pe.wait_ge(front.xt_r.sem, front.xt_r.after(i + 1, 1))
                proj.tensor(pe, i + 1)
                tail.tensor(pe, i)

        @block.vector
        def _(v):
            v.wait_ge(K.loaded[load], 16)
            units.open_vec(v)
            tail.open_vec(v)
            front.statistics(v, 0)
            front.normalise(v, 0)
            proj.move(v, "vec", 0)
            with v.Fori(0, GROUPS) as i:
                units.vector(v, i, {A0: lambda e: front.statistics(e, i + 1), 1: lambda e: tail.early(e, i),
                                   A1: lambda e: front.normalise(e, i + 1)})
                proj.move(v, "vec", i + 1)
                tail.vector(v, i)

        @block.scalar
        def _(a):
            a.wait_ge(K.loaded[load], 16)
            units.open_act(a)
            front.move(a, 0, 7)
            proj.move(a, "act", 0)
            with a.Fori(0, GROUPS) as i:
                def move(e):
                    e.wait_ge(proj.ready.sem, proj.ready.after(i, len(proj.jobs)))
                    front.move(e, i + 1, 7)
                units.scalar(a, i, {min(A2, units.N + 1): move})
                proj.move(a, "act", i + 1)
                tail.scalar(a, i)

        @block.gpsimd
        def _(g):
            front.rstds(g, 0)
            with g.Fori(0, GROUPS) as i:
                front.rstds(g, i + 1)
                tail.gpsimd(g, i)
        units.close()
        proj.close()
        front.close()
        tail.close()


class OutTail:

    def __init__(self, K, ctx, osb, wo, bias, post_norm=None, onto=None):
        nc = K.nc
        self.onto = K.h if onto is None else onto
        self.K, self.osb, self.wo, self.bias, self.post_norm = K, osb, wo, bias, post_norm
        self.width = osb.shape[2]
        self.nch = -(-self.width // P)
        self.k = min(P, self.width)
        self.oT = ctx.enter_context(nc.sbuf_tensor(f"outT_{nc.next_id()}", [P, self.nch, NTOK], F32))
        self.y = ctx.enter_context(nc.sbuf_tensor(f"out_{nc.next_id()}", [P, GT, C], F32))
        names = ("outT_in_psum", "outT_ready", "out_in_psum", "out_moved", "tail_vec", "tail_stats", "tail_pool", "tail_rstd")
        self.tps, self.tr, self.ops, self.mvd, self.vec, self.st, self.pool, self.rs = (K.count(n) for n in names)
        self.units, self.more = None, []

    def stage(self):
        for c, per in ((self.tps, self.nch), (self.tr, self.nch), (self.ops, 1), (self.mvd, 1),
                       (self.vec, 4 if self.post_norm else 0), (self.st, 1), (self.pool, 1), (self.rs, 1)):
            if self.post_norm or c not in (self.st, self.pool, self.rs):
                c.stage(per, int(c is self.mvd))

    def close(self):
        for c in (self.tps, self.tr, self.ops, self.mvd, self.vec, self.st, self.pool, self.rs):
            c.close(GROUPS)
        for c, groups in self.more:
            c.close(groups)

    def open_vec(self, v):
        v.sem_inc(self.mvd.sem, 1)

    def early(self, v, i):
        pass

    def wait_free(self, pe, i):
        pe.wait_ge(self.mvd.sem, self.mvd.after(i, 0))

    def tensor(self, pe, i):
        K = self.K
        pe.wait_ge(self.units.no.sem, self.units.no.after(i, self.units.N))
        K.settle(pe)
        for c in range(self.nch):
            for j in range(GT):
                ins = pe.transpose(K.bank[3 + c][0:self.k, j * P:(j + 1) * P], self.osb[:, j, c * P:c * P + self.k], K.W("ident"))
            ins.then_inc(self.tps.sem, 1)
        pe.wait_ge(self.tr.sem, self.tr.after(i, self.nch))
        K.settle(pe)
        for j in range(GT):
            for c in range(self.nch):
                ins = pe.matmul(K.bank[3][:, j * C:(j + 1) * C], self.oT[0:self.k, c, j * P:(j + 1) * P],
                                self.wo[0:self.k, c * C:(c + 1) * C], start=c == 0, stop=c == self.nch - 1, skip_group_check=True)
        ins.then_inc(self.ops.sem, 1)

    def scalar(self, a, i):
        for c in range(self.nch):
            a.wait_ge(self.tps.sem, self.tps.after(i, c + 1))
            a.activation(self.oT[0:self.k, c, :], self.K.bank[3 + c][0:self.k, :], ACT.Copy).then_inc(self.tr.sem, 1)

    def vector(self, v, i):
        K, y = self.K, self.y
        lk = link(v, self.vec, i, [0], self.K)
        v.wait_ge(self.ops.sem, self.ops.after(i, 1))
        o = K.bank[3][:, 0:GT * C].rearrange("p (j c) -> p j c", j=GT)
        dest = self.onto[:, bass.ds(i * GT, GT), :]
        if self.bias is None:
            v.tensor_tensor(dest, dest, o, ALU.add).then_inc(self.mvd.sem, 1)
            return
        v.tensor_tensor(y[:, :, :], o, rows(self.bias, GT, C), ALU.add).then_inc(self.mvd.sem, 1)
        v.wait_ge(self.mvd.sem, self.mvd.after(i, 1))
        if self.post_norm:
            eps, g, b, bnst, mv, rstd, _ = self.post_norm
            for j in range(GT):
                ins = v.bn_stats(bnst[:, j, :], y[:, j, :])
            lk(ins, settle=True)
            for j in range(GT):
                ins = v.bn_aggr(mv[:, j, :], bnst[:, j, :])
            ins.then_inc(self.st.sem, 1)
            v.wait_ge(self.rs.sem, self.rs.after(i, 1))
            for j in range(GT):
                ins = v.tensor_scalar(y[:, j, :], y[:, j, :], mv[:, j, 0:1], rstd[:, j:j + 1], ALU.subtract, ALU.mult)
            lk(ins)
            lk(v.tensor_tensor(y[:, :, :], y[:, :, :], rows(g, GT, C), ALU.mult))
            lk(v.tensor_tensor(y[:, :, :], y[:, :, :], rows(b, GT, C), ALU.add))
        v.tensor_tensor(dest, dest, y[:, :, :], ALU.add)

    def gpsimd(self, g, i):
        if self.post_norm:
            eps, _, _, _, mv, rstd, work = self.post_norm
            g.wait_ge(self.st.sem, self.st.after(i, 1))
            self.K.settle(g)
            g.tensor_scalar(work, mv[:, :, 1], eps, None, ALU.add).then_inc(self.pool.sem, 1)
            g.wait_ge(self.pool.sem, self.pool.after(i, 1))
            g.tensor_tensor(rstd, work, self.K.half[:, 0:GT], ALU.pow).then_inc(self.rs.sem, 1)


def values(ctx, nc, heads, d):
    return ctx.enter_context(nc.sbuf_tensor(f"values_{nc.next_id()}", [P, GT, heads, d + 1], F32))


def prepare(K, ones=(), zeros=()):
    with K.nc.Block() as block:
        @block.vector
        def _(v):
            for t in ones:
                v.memset(t, 1.0)
            for t in zeros:
                v.memset(t, 0.0)


def first_attention(K):
    nc = K.nc
    front = Front(K, "lnln", (1e-5, 1e-5), scale=K.W("a0_lnw")[:, 0:1], bias=K.W("a0_lnw")[:, 1:2])

    def make(ctx):
        qT = ctx.enter_context(nc.sbuf_tensor("a0_qT", [P, NTOK], F32))
        kT = ctx.enter_context(nc.sbuf_tensor("a0_kT", [P, NTOK], F32))
        vt = values(ctx, nc, 1, C)
        osb = ctx.enter_context(nc.sbuf_tensor("a0_o_sb", [P, GT, C], F32))
        post = (1e-5, K.W("a0_g2"), K.W("a0_b2"), ctx.enter_context(nc.sbuf_tensor("a0_bn", [P, GT, 6], F32)),
                ctx.enter_context(nc.sbuf_tensor("a0_mv", [P, GT, 2], F32)),
                ctx.enter_context(nc.sbuf_tensor("a0_rstd", [P, GT], F32))[:, :], 
                ctx.enter_context(nc.sbuf_tensor("a0_work", [P, GT], F32))[:, :])
        prepare(K, [vt[:, :, :, C:C + 1]], [qT[C:P, :], kT[C:P, :]])
        x = K.xU[:, :]
        jobs = [
            ("act", lambda pe, b, i: pe.matmul(b[0:C, :], K.W("a0_qk")[:, 0:C], x, start=True, stop=True),
             lambda a, b, i: a.activation(qT[0:C, :], b[0:C, :], ACT.Identity, bias=K.W("a0_qkb", 0, C)[:, 0:1])),
            ("vec", lambda pe, b, i: pe.matmul(b[0:C, :], K.W("a0_qk")[:, C:2 * C], x, start=True, stop=True),
             lambda v, b, i: v.tensor_scalar(kT[0:C, :], b[0:C, :], K.W("a0_qkb", 0, C)[:, 1:2], None, ALU.add)),
            ("vec", lambda pe, b, i: [pe.matmul(b[:, j * C:(j + 1) * C], K.xU[:, j * P:(j + 1) * P], K.W("a0_v"),
                                                start=True, stop=True) for j in range(GT)][-1],
             lambda v, b, i: v.tensor_tensor(vt[:, :, 0, 0:C], b[:, 0:GT * C].rearrange("p (j c) -> p j c", j=GT),
                                             rows(K.W("a0_vb"), GT, C), ALU.add)),
        ]
        us = []
        for s in range(2):
            us.append(Unit([(qb * SEQ, SEQ, qT[:, s * SEQ + qb * P:s * SEQ + (qb + 1) * P], kT[:, s * SEQ:(s + 1) * SEQ])
                            for qb in range(2)], [], [(0, 2, SEQ)],
                           [[(2 * qb + kb, vt[:, 2 * s + kb, 0, :]) for kb in range(2)] for qb in range(2)],
                           C + 1, osb[:, 2 * s:2 * s + 2, :]))
        units = Units(K, ctx, [us], bias=K.W("a0_bias"), rownorm=lambda t, n: K.W("a0_scale").to_broadcast([P, n]))
        tail = OutTail(K, ctx, osb, K.W("a0_o"), K.W("a0_ob"), post)
        tail.units = units
        return units, Projections(K, jobs), tail
    attention_stage(K, "a0", 0, front, make)


def second_attention(K):
    nc = K.nc
    front = Front(K, "ln", (1e-5,))

    def make(ctx):
        H = 8
        qT = ctx.enter_context(nc.sbuf_tensor("a1_qT", [P, 4, NTOK], F32))
        kT = ctx.enter_context(nc.sbuf_tensor("a1_kT", [P, 2, 4, NTOK], F32))
        vt = values(ctx, nc, H, C)
        osb = ctx.enter_context(nc.sbuf_tensor("a1_o_sb", [P, GT, H * C], F32))
        prepare(K, [vt[:, :, :, C:C + 1]], [kT[C:P, 0, :, :], kT[0:C, 1, :, :]])
        x = K.xU[:, :]

        def qjob(c):
            return ("vec", lambda pe, b, i: pe.matmul(b[:, :], K.W("a1_q")[:, c * P:(c + 1) * P], x, start=True, stop=True),
                    lambda v, b, i: v.tensor_scalar(qT[:, c, :], b[:, :], K.W("a1_qb")[:, c:c + 1], 0.125, ALU.add, ALU.mult))

        def kjob(c):
            return ("act", lambda pe, b, i: pe.matmul(b[:, :], K.W("a1_k")[:, c * P:(c + 1) * P], x, start=True, stop=True),
                    lambda a, b, i: [a.activation(kT[r, p, c, :], b[r, :], ACT.Identity, bias=K.W("a1_kb")[r, c:c + 1])
                                     for p, r in enumerate((slice(0, C), slice(C, P)))][-1])

        def vjob(j):
            return ("vec", lambda pe, b, i: pe.matmul(b[:, :], K.xU[:, j * P:(j + 1) * P], K.W("a1_v"), start=True, stop=True),
                    lambda v, b, i: v.tensor_tensor(vt[:, j, :, 0:C], b[:, :].rearrange("p (h c) -> p h c", h=H),
                                                    K.W("a1_vb").rearrange("p (h c) -> p h c", h=H), ALU.add))
        jobs = [f(c) for c in range(4) for f in (qjob, kjob, vjob)]
        o5 = osb[:, :, :].rearrange("p j (m a c) -> p j m a c", m=4, a=2)
        us, q0 = [], []
        strict4 = K.wb[:, 1:5, :].rearrange("p a c -> p (a c)")
        strict = K.wb[:, 1, :]
        for s in range(2):
            t0 = s * SEQ
            for p in range(2):
                us.append(Unit([(P * m, P, qT[:, m, t0:t0 + P], kT[:, p, m, t0:t0 + P]) for m in range(4)], [(0, 512, strict4)],
                               [(0, 4, P)], [[(m, vt[:, 2 * s, 2 * m + p, :])] for m in range(4)], C + 1, o5[:, 2 * s, :, p, :]))
                q0.append(0)
                for mp in range(2):
                    us.append(Unit([(SEQ * a, SEQ, qT[:, 2 * mp + a, t0 + P:t0 + SEQ], kT[:, p, 2 * mp + a, t0:t0 + SEQ]) for a in range(2)],
                                   [(SEQ * a + P, P, strict) for a in range(2)], [(0, 2, SEQ)],
                                   [[(2 * a + kb, vt[:, 2 * s + kb, 2 * (2 * mp + a) + p, :]) for kb in range(2)] for a in range(2)],
                                   C + 1, o5[:, 2 * s + 1, 2 * mp:2 * mp + 2, p, :]))
                    q0.append(1)
        units = Units(K, ctx, [us], rownorm=lambda t, n: K.W("row0")[:, q0[t]:q0[t] + 1].to_broadcast([P, n]))
        tail = OutTail(K, ctx, osb, K.W("a1_o"), K.W("a1_ob"))
        tail.units = units
        return units, Projections(K, jobs), tail
    attention_stage(K, "a1", 2, front, make)


def second_routed_attention(K, x1):
    nc = K.nc
    front = Front(K, "lnrms", (1e-5, 1e-6), scale=K.W("r2_ln"), kept=x1)

    def make(ctx):
        H, HK, D = 4, 2, 16
        qT = ctx.enter_context(nc.sbuf_tensor("r2_qT", [P, NTOK], F32))
        kT = ctx.enter_context(nc.sbuf_tensor("r2_kT", [P, 4, NTOK], F32))
        t1 = ctx.enter_context(nc.sbuf_tensor("r2_t1", [P, NTOK], F32))
        t2 = ctx.enter_context(nc.sbuf_tensor("r2_t2", [P, NTOK], F32))
        vt = values(ctx, nc, HK, D)
        osb = ctx.enter_context(nc.sbuf_tensor("r2_o_sb", [P, GT, C], F32))
        prepare(K, [vt[:, :, :, D:D + 1]], [kT[:, :, :]])
        rope = K.count("rotary_part")
        rope.stage(2)

        def pair(ap):
            return ap.rearrange("p (s t) -> p s t", s=2)

        def table(name):
            return K.W(name).rearrange("p (s t) -> p s t", s=1).to_broadcast([P, 2, SEQ])

        moved = K.count("projection_moved_vec")

        def plain(w, tab, before):
            def mv(v, b, i):
                if before:
                    v.wait_ge(moved.sem, moved.after(i, before))
                return v.tensor_tensor(pair(t1[:, :]), pair(b[:, :]), table(tab), ALU.mult)
            return ("vec", lambda pe, b, i: pe.matmul(b[:, :], K.W(w), K.xU[:, :], start=True, stop=True), mv)

        def turned(w, tab, dst, n):
            def mv(v, b, i):
                v.tensor_tensor(pair(t2[:, :]), pair(b[:, :]), table(tab), ALU.mult).then_inc(rope.sem, 1)
                v.wait_ge(rope.sem, rope.after(i, n))
                for out, r in dst:
                    ins = v.tensor_tensor(out, t1[r, :], t2[r, :], ALU.add)
                return ins
            return ("vec", lambda pe, b, i: pe.matmul(b[:, :], K.W(w), K.xU[:, :], start=True, stop=True), mv)
        jobs = [plain("r2_q", "r2_cq", 0), turned("r2_qp", "r2_sq", [(qT[:, :], slice(0, P))], 1),
                plain("r2_k", "r2_ck", 2), turned("r2_kp", "r2_sk", [(kT[32 * n:32 * n + 32, n, :], slice(32 * n, 32 * n + 32)) for n in range(H)], 2),
                ("act", lambda pe, b, i: [pe.matmul(b[:, j * 32:(j + 1) * 32], K.xU[:, j * P:(j + 1) * P], K.W("r2_v"),
                                                    start=True, stop=True) for j in range(GT)][-1],
                 lambda a, b, i: a.activation(vt[:, :, :, 0:D], b[:, 0:GT * 32].rearrange("p (j h c) -> p j h c", j=GT, h=HK), ACT.Copy))]
        us = []
        causal = K.wb[:, 5, :]
        for s in range(2):
            t0 = s * SEQ
            for n in range(H):
                g = n // (H // HK)
                us.append(Unit([(0, P, qT[:, t0:t0 + P], kT[:, n, t0:t0 + P]), (P, SEQ, qT[:, t0 + P:t0 + SEQ], kT[:, n, t0:t0 + SEQ])],
                               [(0, P, causal), (SEQ, P, causal)], [(0, 1, P), (P, 1, SEQ)],
                               [[(0, vt[:, 2 * s, g, :])], [(1, vt[:, 2 * s, g, :]), (2, vt[:, 2 * s + 1, g, :])]],
                               D + 1, osb[:, 2 * s:2 * s + 2, n * D:(n + 1) * D]))
        units = Units(K, ctx, [us])
        tail = OutTail(K, ctx, osb, K.W("r2_o"), None, onto=x1)
        tail.units = units
        tail.more = [(rope, GROUPS + 1)]
        return units, Projections(K, jobs), tail
    attention_stage(K, "r2", 5, front, make)


class GateTail(PipedTail):

    def __init__(self, K, ctx, qo, sx, mixed, units):
        super().__init__(K, ctx, [q.rearrange("p j n e d -> p j (n e d)") for q in qo], K.W("f1_g"), None, units)
        nc = K.nc
        self.qo, self.sx, self.mixed = qo, sx, mixed
        self.padm = ctx.enter_context(nc.sbuf_tensor("f1_not_padded", [P, GT * C], F32))
        self.lg = ctx.enter_context(nc.sbuf_tensor("f1_gate", [P, GT * 16], F32))
        self.m = ctx.enter_context(nc.sbuf_tensor("f1_gate_work", [P, GT * 4], F32))
        self.masked, self.shifted, self.exps = K.count("pads_zeroed"), K.count("gate_shifted"), K.count("gate_exps")
        self.vec.stage(6)
        for c in (self.masked, self.shifted, self.exps):
            c.stage(1)
            self.counts.append((c, 0))
        self.vec_hooks = {4: self.mask, 7: self.shift, 8: self.mix}
        self.act_hooks = {8: self.exp}

    def heads_ready(self, pe, g):
        pe.wait_ge(self.masked.sem, self.masked.after(g, 1))

    def link(self, v, g, done):
        return link(v, self.vec, g, [done], self.K)

    def over(self, t, e):
        return t.rearrange("p (a c) -> p a c", c=1).to_broadcast([P, t.shape[1], e])

    def four(self):
        return self.lg[:, :].rearrange("p (a c) -> p a c", c=4)

    def mask(self, v, g, u):
        lk = self.link(v, g, 0)
        self.jobs.wait_proj(v, g)
        v.wait_ge(self.units.no.sem, self.units.no.after(g, self.units.N))
        lk(v.tensor_scalar(self.padm[:, :].rearrange("p (j c) -> p j c", j=GT), self.sx[:, bass.ds(g * GT, GT), :], 0.0, None,
                           ALU.not_equal))
        q4 = self.qo[u][:, :, :, :, :].rearrange("p j n e d -> p (j n) e d")
        v.tensor_tensor(q4, q4, self.padm[:, :].rearrange("p (a b d) -> p a b d", b=1, d=16).to_broadcast([P, GT * 4, 4, 16]), ALU.mult)\
            .then_inc(self.masked.sem, 1)

    def add(self, v, b, g):
        return v.tensor_tensor(self.lg[:, :].rearrange("p (j c) -> p j c", j=GT), b[:, 0:GT * 16].rearrange("p (j c) -> p j c", j=GT),
                               rows(self.K.W("f1_gb"), GT, 16), ALU.add)

    def shift(self, v, g, u):
        lk = self.link(v, g, 1)
        self.jobs.wait_moved(v, g, self.jobs.np + self.nch)
        self.K.settle(v)
        lk(v.tensor_reduce(self.m[:, :], self.four(), AX.X, ALU.max))
        v.tensor_tensor(self.four(), self.four(), self.over(self.m[:, :], 4), ALU.subtract).then_inc(self.shifted.sem, 1)

    def exp(self, a, g, u):
        a.wait_ge(self.shifted.sem, self.shifted.after(g, 1))
        a.activation(self.lg[:, :], self.lg[:, :], ACT.Exp).then_inc(self.exps.sem, 1)

    def mix(self, v, g, u):
        lk = self.link(v, g, 2)
        v.wait_ge(self.exps.sem, self.exps.after(g, 1))
        self.K.settle(v)
        lk(v.tensor_reduce(self.m[:, :], self.four(), AX.X, ALU.add))
        lk(v.reciprocal(self.m[:, :], self.m[:, :]))
        lk(v.tensor_tensor(self.four(), self.four(), self.over(self.m[:, :], 4), ALU.mult))
        qe = self.qo[u][:, :, :, :, :].rearrange("p j n e d -> p (j n e) d")
        lk(v.tensor_tensor(qe, qe, self.over(self.lg[:, :], 16), ALU.mult))
        v.tensor_reduce(self.mixed[:, bass.ds(g * GT, GT), :].rearrange("p j (n d) -> p (j n) d", n=4),
                        self.qo[u][:, :, :, :, :].rearrange("p j n e d -> p (j n) d e"), AX.X, ALU.add)


def expert_heads(K):
    nc = K.nc
    with ExitStack() as ctx:
        sx = ctx.enter_context(nc.sbuf_tensor("head_features", [P, TILES + GT, C], F32))
        mixed = ctx.enter_context(nc.sbuf_tensor("mixed", [P, TILES, C], F32))
        expert_attention(K, sx, mixed)
        head_feed_forward(K, sx, mixed)


def expert_attention(K, sx, mixed):
    nc = K.nc
    front = Front(K, "ln", (1e-5,))

    def make(ctx):
        H, D, E = 4, 16, 4
        sxT = ctx.enter_context(nc.sbuf_tensor("f1_sxT", [P, NTOK], F32))
        qT, kT, vt, qo = [], [], [], []
        for u in range(2):
            qT.append(ctx.enter_context(nc.sbuf_tensor(f"f1_qT{u}", [P, E, NTOK], F32)))
            kT.append(ctx.enter_context(nc.sbuf_tensor(f"f1_kT{u}", [P, H, NTOK], F32)))
            vt.append(values(ctx, nc, H, D))
            qo.append(ctx.enter_context(nc.sbuf_tensor(f"f1_qo{u}", [P, GT, H, E, D], F32)))
        prepare(K, [vt[u][:, :, :, D:D + 1] for u in range(2)], [sxT[C:P, :]] + [kT[u][:, :, :] for u in range(2)])
        jobs = [None]

        def heads(pe, i):
            jobs[0].wait_moved(pe, i - 1, 0)
            K.settle(pe)

        def qjob(u, e):
            def mm(pe, b, i):
                heads(pe, i)
                return pe.matmul(b[:, :], K.W("f1_q")[:, e * P:(e + 1) * P], sxT[:, :], start=True, stop=True)
            if e % 2:
                return ("act", mm, lambda a, b, i: a.activation(qT[u][:, e, :], b[:, :], ACT.Copy, scale=4.0))
            return ("vec", mm, lambda v, b, i: v.tensor_scalar(qT[u][:, e, :], b[:, :], 4.0, None, ALU.mult))

        def kproduct(pe, b, i):
            heads(pe, i)
            return pe.matmul(b[:, :], K.W("f1_k"), sxT[:, :], start=True, stop=True)

        def vproduct(pe, b, i):
            heads(pe, i)
            return [pe.matmul(b[:, j * C:(j + 1) * C], sxT[:, j * P:(j + 1) * P], K.W("f1_v"), start=True, stop=True) for j in range(GT)][-1]

        def proj(u):
            return [
                ("act", lambda pe, b, i: pe.matmul(b[0:C, :], K.W("f1_hl"), K.xU[:, :], start=True, stop=True),
                 lambda a, b, i: a.activation(sxT[0:C, :], b[0:C, :], ACT.Identity, bias=K.W("f1_hlb", 0, C))),
                ("vec", lambda pe, b, i: [pe.matmul(b[:, j * C:(j + 1) * C], K.xU[:, j * P:(j + 1) * P], K.W("f1_hl"),
                                                    start=True, stop=True) for j in range(GT)][-1],
                 lambda v, b, i: v.tensor_tensor(sx[:, bass.ds(i * GT, GT), :], b[:, 0:GT * C].rearrange("p (j c) -> p j c", j=GT),
                                                 rows(K.W("f1_hlbr"), GT, C), ALU.add)),
                *[qjob(u, e) for e in range(E)],
                ("act", kproduct, lambda a, b, i: [a.activation(kT[u][32 * n:32 * n + 32, n, :], b[32 * n:32 * n + 32, :], ACT.Copy)
                                                   for n in range(H)][-1]),
                ("vec", vproduct, lambda v, b, i: v.tensor_copy(vt[u][:, :, :, 0:D], b[:, 0:GT * C].rearrange("p (j h c) -> p j h c", j=GT, h=H))),
            ]
        causal4 = K.wb[:, 5:9, :].rearrange("p a c -> p (a c)")
        causal = K.wb[:, 5, :]
        sets = [[], []]
        for u in range(2):
            q, k, v = qT[u], kT[u], vt[u]
            for s in range(2):
                t0 = s * SEQ
                for n in range(H):
                    sets[u].append(Unit([(e * P, P, q[:, e, t0:t0 + P], k[:, n, t0:t0 + P]) for e in range(E)], [(0, 512, causal4)],
                                        [(0, E, P)], [[(e, v[:, 2 * s, n, :])] for e in range(E)], D + 1, qo[u][:, 2 * s, n, :, :]))
                    for p in range(2):
                        sets[u].append(Unit([(a * SEQ, SEQ, q[:, 2 * p + a, t0 + P:t0 + SEQ], k[:, n, t0:t0 + SEQ]) for a in range(2)],
                                            [(a * SEQ + P, P, causal) for a in range(2)], [(0, 2, SEQ)],
                                            [[(2 * a + kb, v[:, 2 * s + kb, n, :]) for kb in range(2)] for a in range(2)],
                                            D + 1, qo[u][:, 2 * s + 1, n, 2 * p:2 * p + 2, :]))
        units = Units(K, ctx, sets, piped=True)
        tail = GateTail(K, ctx, qo, sx, mixed, units)
        jobs[0] = tail.jobs = Jobs(K, front, [proj(u) for u in range(2)], [tail.list(u, 16) for u in range(2)])
        return units, tail.jobs, tail
    piped_stage(K, 3, front, 9, make)


def head_feed_forward(K, sx, mixed):
    nc = K.nc
    H, D, FT = 4, 16, 8
    STEPS, N, R = TILES // FT, FT * C, FT * 4
    with ExitStack() as ctx:
        def sb(n, s):
            return ctx.enter_context(nc.sbuf_tensor(f"ff_{n}", s, F32))
        fx, y, sq, npm = (sb(n, [P, N]) for n in ("fx", "y", "square", "not_zero"))
        fxT, h1, npmT = (sb(n, [C, FT * P]) for n in ("fxT", "hidden", "not_zeroT"))
        resid = sb("resid", [P, 2, C])
        mean, var, work, rstd, fg, m = (sb(n, [P, R]) for n in ("mean", "var", "work", "rstd", "gate", "gate_work"))
        half = sb("minus_half", [P, R])
        names = ("ff_vec", "norm_stats", "norm_pool", "norm_rstd", "fx_ready", "fxT_in_psum", "fxT_ready", "not_zeroT", "hidden1_in_psum",
                 "hidden1_moved", "hidden1_ready", "layers_in_psum", "fout_ready", "foutT_in_psum", "foutT_ready", "head_gate_in_psum",
                 "head_gate_shifted", "head_gate_exps", "halves_set")
        counts = [K.count(n) for n in names]
        (vec, st, pl, rs, fr, ftp, ftr, nzt, h1p, h1m, h1r, zp, fo, fop, fot, gp, gsh, gex, hs) = counts
        VEC = 24
        for c, per in zip(counts, (VEC, 2, 2, 2, 1, 1, 1, 1, 2, 2, 1, 1, 1, 1, 1, 1, 1, 1, 0)):
            c.stage(per, 0)
        block = ctx.enter_context(nc.Block())
        r3 = (lambda t: t.rearrange("p (a d) -> p a d", d=D))
        over = (lambda t, n: t.rearrange("p (a c) -> p a c", c=1).to_broadcast([P, t.shape[1], n]))
        row16 = (lambda name: rows(K.W(name), R, D))

        @block.vector
        def _(v):
            v.wait_ge(hs.sem, hs.base + 1)
            for n in range(H):
                ins = v.tensor_copy(resid[:, :, n * D:(n + 1) * D], sx[:, 2 * n:2 * n + 2, n * D:(n + 1) * D])
            ins.then_inc(hs.sem, 1)
            v.wait_ge(hs.sem, hs.base + 2)
            with v.Fori(0, STEPS) as i:
                lk = link(v, vec, i, [0], K)

                def norm(t, dst, g, b, k):
                    lk(v.tensor_reduce(mean[:, :], r3(t[:, :]), AX.X, ALU.add))
                    lk(v.tensor_scalar(mean[:, :], mean[:, :], 1.0 / D, None, ALU.mult))
                    lk(v.tensor_tensor(r3(t[:, :]), r3(t[:, :]), over(mean[:, :], D), ALU.subtract))
                    lk(v.tensor_tensor(sq[:, :], t[:, :], t[:, :], ALU.mult))
                    lk(v.tensor_reduce(var[:, :], r3(sq[:, :]), AX.X, ALU.add))
                    v.tensor_scalar(var[:, :], var[:, :], 1.0 / D, None, ALU.mult).then_inc(st.sem, 1)
                    v.wait_ge(rs.sem, rs.after(i, k))
                    lk(v.tensor_tensor(r3(t[:, :]), r3(t[:, :]), over(rstd[:, :], D), ALU.mult))
                    lk(v.tensor_tensor(r3(t[:, :]), r3(t[:, :]), row16(g), ALU.mult))
                    return v.tensor_tensor(r3(dst[:, :]), r3(t[:, :]), row16(b), ALU.add)
                lk(v.tensor_tensor(fx[:, :].rearrange("p (s t c) -> p s (t c)", t=2, c=C),
                                   mixed[:, bass.ds(i * FT, FT), :].rearrange("p (s t) c -> p s (t c)", t=2),
                                   resid[:, :, :].rearrange("p (s t) c -> p s (t c)", s=1).to_broadcast([P, FT // 2, 2 * C]), ALU.add))
                norm(fx, fx, "f1_lg", "f1_lb", 1).then_inc(fr.sem, 1)
                v.wait_ge(fr.sem, fr.after(i, 1))
                lk(v.tensor_scalar(npm[:, :], fx[:, :], 0.0, None, ALU.not_equal))
                v.wait_ge(ftr.sem, ftr.after(i, 1))
                v.tensor_scalar(npmT[:, :], fxT[:, :], 0.0, None, ALU.not_equal).then_inc(nzt.sem, 1)
                v.wait_ge(nzt.sem, nzt.after(i, 1))
                v.wait_ge(h1m.sem, h1m.after(i, 2))
                v.tensor_tensor(h1[:, :], h1[:, :], npmT[:, :], ALU.mult).then_inc(h1r.sem, 1)
                v.wait_ge(zp.sem, zp.after(i, 1))
                lk(v.tensor_tensor(r3(y[:, :]), r3(K.bank[4][:, :]), row16("f1_2b"), ALU.add))
                lk(v.tensor_tensor(y[:, :], y[:, :], npm[:, :], ALU.mult))
                lk(v.tensor_tensor(y[:, :], y[:, :], fx[:, :], ALU.add))
                norm(y, y, "f1_ng", "f1_nb", 2).then_inc(fo.sem, 1)
                v.wait_ge(gp.sem, gp.after(i, 1))
                four = (lambda t: t.rearrange("p (a c) -> p a c", c=H))
                lk(v.tensor_reduce(m[:, 0:FT], four(K.bank[5][:, 0:R]), AX.X, ALU.max))
                v.tensor_tensor(four(fg[:, :]), four(K.bank[5][:, 0:R]), over(m[:, 0:FT], H), ALU.subtract).then_inc(gsh.sem, 1)
                v.wait_ge(gex.sem, gex.after(i, 1))
                K.settle(v)
                lk(v.tensor_reduce(m[:, 0:FT], four(fg[:, :]), AX.X, ALU.add))
                lk(v.reciprocal(m[:, 0:FT], m[:, 0:FT]))
                lk(v.tensor_tensor(four(fg[:, :]), four(fg[:, :]), over(m[:, 0:FT], H), ALU.mult))
                lk(v.tensor_tensor(r3(y[:, :]), r3(y[:, :]), over(fg[:, :], D), ALU.mult))
                dest = K.h[:, bass.ds(i * FT, FT), :]
                v.tensor_tensor(dest, dest, y[:, :].rearrange("p (j c) -> p j c", j=FT), ALU.add)

        @block.gpsimd
        def _(g):
            g.memset(half[:, :], -0.5).then_inc(hs.sem, 1)
            with g.Fori(0, STEPS) as i:
                for k in range(2):
                    g.wait_ge(st.sem, st.after(i, k + 1))
                    K.settle(g)
                    g.tensor_scalar(work[:, :], var[:, :], 1e-8, None, ALU.add).then_inc(pl.sem, 1)
                    g.wait_ge(pl.sem, pl.after(i, k + 1))
                    g.tensor_tensor(rstd[:, :], work[:, :], half[:, :], ALU.pow).then_inc(rs.sem, 1)

        @block.tensor
        def _(pe):
            with pe.Fori(0, STEPS) as i:
                def turn(src, ready, out):
                    pe.wait_ge(ready.sem, ready.after(i, 1))
                    K.settle(pe)
                    for j in range(FT):
                        ins = pe.transpose(K.bank[j // 4][0:C, (j % 4) * P:(j % 4 + 1) * P], src[:, j * C:(j + 1) * C], K.W("ident"))
                    ins.then_inc(out.sem, 1)
                turn(fx, fr, ftp)
                pe.wait_ge(ftr.sem, ftr.after(i, 1))
                K.settle(pe)
                for b in range(2):
                    pe.matmul(K.bank[2 + b][0:C, :], K.W("f1_1", 0, C), fxT[:, b * NTOK:(b + 1) * NTOK], start=True, stop=True)\
                        .then_inc(h1p.sem, 1)
                pe.wait_ge(h1r.sem, h1r.after(i, 1))
                K.settle(pe)
                for j in range(FT):
                    ins = pe.matmul(K.bank[4][:, j * C:(j + 1) * C], h1[:, j * P:(j + 1) * P], K.W("f1_2", 0, C), start=True, stop=True,
                                    skip_group_check=True)
                ins.then_inc(zp.sem, 1)
                turn(y, fo, fop)
                pe.wait_ge(fot.sem, fot.after(i, 1))
                K.settle(pe)
                for j in range(FT):
                    ins = pe.matmul(K.bank[5][:, j * H:(j + 1) * H], fxT[:, j * P:(j + 1) * P], K.W("f1_fg", 0, C), start=True, stop=True,
                                    skip_group_check=True)
                ins.then_inc(gp.sem, 1)

        @block.scalar
        def _(a):
            with a.Fori(0, STEPS) as i:
                def out(ready, done):
                    a.wait_ge(ready.sem, ready.after(i, 1))
                    for b in range(2):
                        ins = a.activation(fxT[:, b * NTOK:(b + 1) * NTOK], K.bank[b][0:C, :], ACT.Copy)
                    ins.then_inc(done.sem, 1)
                out(ftp, ftr)
                for b in range(2):
                    a.wait_ge(h1p.sem, h1p.after(i, b + 1))
                    a.activation(h1[:, b * NTOK:(b + 1) * NTOK], K.bank[2 + b][0:C, :], ACT.Relu, bias=K.W("f1_1b", 0, C)).then_inc(h1m.sem, 1)
                out(fop, fot)
                a.wait_ge(gsh.sem, gsh.after(i, 1))
                a.activation(fg[:, :], fg[:, :], ACT.Exp).then_inc(gex.sem, 1)
        for c in counts:
            c.close(STEPS)


def third_attention(K):
    nc = K.nc
    front = Front(K, "ln", (1e-5,))

    def make(ctx):
        H, D = 8, 32
        scale = float(np.float32(1.0) / np.sqrt(np.float32(D)))
        qT, kT, vt, osb = [], [], [], []
        for u in range(2):
            qT.append(ctx.enter_context(nc.sbuf_tensor(f"a2_qT{u}", [P, 2, NTOK], F32)))
            kT.append(ctx.enter_context(nc.sbuf_tensor(f"a2_kT{u}", [P, 4, 2, NTOK], F32)))
            vt.append(values(ctx, nc, H, D))
            osb.append(ctx.enter_context(nc.sbuf_tensor(f"a2_o_sb{u}", [P, GT, H * D], F32)))
        prepare(K, [vt[u][:, :, :, D:D + 1] for u in range(2)], [kT[u][:, n, :, :] for u in range(2) for n in range(4)])
        x = K.xU[:, :]

        def qjob(u, c):
            return ("vec", lambda pe, b, i: pe.matmul(b[:, :], K.W("a2_q")[:, c * P:(c + 1) * P], x, start=True, stop=True),
                    lambda v, b, i: v.tensor_scalar(qT[u][:, c, :], b[:, :], K.W("a2_qb")[:, c:c + 1], scale, ALU.add, ALU.mult))

        def kjob(u, c):
            return ("act", lambda pe, b, i: pe.matmul(b[:, :], K.W("a2_k")[:, c * P:(c + 1) * P], x, start=True, stop=True),
                    lambda a, b, i: [a.activation(kT[u][r, n, c, :], b[r, :], ACT.Identity, bias=K.W("a2_kb")[r, c:c + 1])
                                     for n, r in enumerate(slice(32 * n, 32 * n + 32) for n in range(4))][-1])

        def vjob(u, c):
            def mm(pe, b, i):
                for n in range(2):
                    j = 2 * c + n
                    ins = pe.matmul(b[:, n * SEQ:(n + 1) * SEQ], K.xU[:, j * P:(j + 1) * P], K.W("a2_v"), start=True, stop=True)
                return ins
            return ("vec", mm, lambda v, b, i: v.tensor_tensor(
                vt[u][:, 2 * c:2 * c + 2, :, 0:D], b[:, :].rearrange("p (j h c) -> p j h c", j=2, h=H),
                K.W("a2_vb").rearrange("p (j h c) -> p j h c", j=1, h=H).to_broadcast([P, 2, H, D]), ALU.add))
        proj = [[f(u, c) for c in range(2) for f in (qjob, kjob, vjob)] for u in range(2)]
        sets = [[], []]
        m0 = K.wb[:, 9:11, :].rearrange("p a c -> p (a c)")
        m1 = K.wb[:, 11:15, :].rearrange("p a c -> p (a c)")
        for u in range(2):
            q, k, v = qT[u], kT[u], vt[u]
            o5 = osb[u][:, :, :].rearrange("p j (m n c) -> p j m n c", m=2, n=4)
            for s in range(2):
                t0 = s * SEQ
                for n in range(4):
                    sets[u].append(Unit([(P * m, P, q[:, m, t0:t0 + P], k[:, n, m, t0:t0 + P]) for m in range(2)], [(0, 2 * P, m0)],
                                        [(0, 2, P)], [[(m, v[:, 2 * s, 4 * m + n, :])] for m in range(2)], D + 1, o5[:, 2 * s, :, n, :]))
                    sets[u].append(Unit([(SEQ * m, SEQ, q[:, m, t0 + P:t0 + SEQ], k[:, n, m, t0:t0 + SEQ]) for m in range(2)], [(0, 512, m1)],
                                        [(0, 2, SEQ)], [[(2 * m + kb, v[:, 2 * s + kb, 4 * m + n, :]) for kb in range(2)] for m in range(2)],
                                        D + 1, o5[:, 2 * s + 1, :, n, :]))
        units = Units(K, ctx, sets, piped=True)
        tail = PipedTail(K, ctx, osb, K.W("a2_o"), K.W("a2_ob"), units)
        tail.jobs = Jobs(K, front, proj, [tail.list(u) for u in range(2)])
        return units, tail.jobs, tail
    piped_stage(K, 4, front, 6, make)


def pick_first_max(v, lk, src, top, eq, one):
    n, e = src.shape[1], src.shape[2]
    b = (lambda t: t.rearrange("p (a c) -> p a c", c=1).to_broadcast([P, n, e]))
    lk(v.tensor_reduce(top, src, AX.X, ALU.max))
    lk(v.tensor_tensor(eq, src, b(top), ALU.is_equal))
    lk(v.tensor_tensor(eq, eq, pick_first_max.rank(n, e), ALU.mult))
    lk(v.tensor_reduce(pick_first_max.work, eq, AX.X, ALU.max))
    lk(v.tensor_tensor(one, eq, b(pick_first_max.work), ALU.is_equal))


class Mixture:

    def __init__(self, K, kind, load, front, E, CH, M, w1, w2, b1=None, w3=None, gw=None, gb=None, b2=None, kept=None):
        self.K, self.kind, self.load, self.front, self.kept = K, kind, load, front, kept
        self.E, self.CH, self.M, self.w1, self.w2, self.b1, self.w3, self.gw, self.gb, self.b2 = E, CH, M, w1, w2, b1, w3, gw, gb, b2
        self.NC = E * CH

    def run(self):
        K, nc, E, CH, NC, M = self.K, self.K.nc, self.E, self.CH, self.NC, self.M
        kind, front, kept, biased = self.kind, self.front, self.kept, self.b2 is not None
        gated = self.w3 is not None
        R = 8
        lag = 4 if gated else 6
        at_turn, at_router, at_exp = {"f0": (9, 11, 13), "f2": (6, 8, 9), "f3": (9, 11, 13)}[kind]
        with ExitStack() as ctx:
            def sb(n, s, d=F32):
                return ctx.enter_context(nc.sbuf_tensor(f"{kind}_{n}", s, d))
            xs = [(K.xU, K.xL), (sb("xT_upper", [P, NTOK]), sb("xT_lower", [P, NTOK]))]
            hT = sb("hidden", [P, R, NTOK])
            ug = sb("gate_part", [P, 2, NTOK]) if gated else None
            prod = sb("weighted", [P, 2, GT * C])
            acc = sb("sum", [P, GT, C])
            bsum = sb("bias_sum", [P, GT, C])
            g = sb("weights", [P, 2, GT, 32])
            gT = sb("weightsT", [P, P])
            lg, ex, eq, o1, o2, l2 = (sb(n, [P, GT, E]) for n in ("logits", "exps", "equal", "first", "second", "rest"))
            m1, m2, wk, sm = (sb(n, [P, GT]) for n in ("top1", "top2", "work", "sums"))
            run = sb("run", [P, GT + 1, E])
            bnst, mv, rstd, wk4 = sb("bn", [P, GT, 6]), sb("mv", [P, GT, 2]), sb("rstd", [P, GT]), sb("wk4", [P, GT])
            mask = sb("mask", [P, GT * C], I32) if kind == "f3" else None
            limits = sb("limits", [P, 3, GT * C]) if kind == "f3" else None
            names = ("logits_ready", "choice_vec", "shifted", "exps_ready", "weights_ready", "counts_in_psum", "counted",
                     "weightsT_in_psum", "weightsT_ready", "bias_in_psum", "sum_started", "hidden_in_psum", "hidden_ready", "gate_ready",
                     "expert_out", "weighted_ready", "summed", "mixture_stats", "mixture_pool", "mixture_rstd", "cleared", "bias_moved",
                     "mixture_vec")
            counts = [K.count(n) for n in names]
            (lgr, vec, shf, exr, wr, cps, cntd, gtp, gtr, bps, acs, hps, hr, gtd, eo, pr, sd, mst, mpl, mrs, clr, bmv, fin) = counts
            choice_steps, final_steps = {"f0": (17, 6), "f2": (21, 1), "f3": (18, 8)}[kind]
            for c, per, cr in ((lgr, 1, 0), (vec, choice_steps, 0), (shf, 1, 0), (exr, 1, 0), (wr, 1, 0), (cps, kind == "f3", 0),
                               (cntd, kind == "f3", 0), (gtp, biased, 0), (gtr, biased, 0), (bps, biased, 0), (acs, 1, 0), (hps, NC, 0),
                               (hr, NC, R), (gtd, NC if gated else 0, 0), (eo, E, 2 * R), (pr, E, 2), (sd, E, 2), (mst, kind == "f0", 0),
                               (mpl, kind == "f0", 0), (mrs, kind == "f0", 0), (clr, 0, 2), (bmv, biased, biased), (fin, final_steps, 0)):
                c.stage(int(per), int(cr))
            block = ctx.enter_context(nc.Block())
            B6, B7 = K.bank[6], K.bank[7]
            flat = (lambda t: t.rearrange("p a c -> p (a c)"))
            b3 = (lambda t: t.rearrange("p (a c) -> p a c", c=1).to_broadcast([P, GT, E]))
            rank = K.W("rank")[:, 0:E].rearrange("p (a c) -> p a c", a=1).to_broadcast([P, GT, E])

            def hbank(c):
                return (K.bank[2 * (c % 2)], K.bank[2 * (c % 2) + 1]) if gated else (K.bank[c % 4], None)
            nbanks = 2 if gated else 4

            @block.tensor
            def _(pe):
                def router(n, u):
                    pe.wait_ge(front.xt_r.sem, front.xt_r.after(n, 1))
                    K.settle(pe)
                    for j in range(GT):
                        ins = pe.matmul(B6[:, j * E:(j + 1) * E], xs[u][0][:, j * P:(j + 1) * P], self.gw[:, :], start=True, stop=True,
                                        skip_group_check=True)
                    ins.then_inc(lgr.sem, 1)

                def places(n):
                    pe.wait_ge(cntd.sem, cntd.after(n, 1))
                    K.settle(pe)
                    pe.matmul(B6[:, 64:64 + GT * E], K.W("tri"), flat(o1[:, :, :]), start=True, stop=False, skip_group_check=True)
                    pe.matmul(B6[:, 64:64 + GT * E], K.W("ones"), flat(run[:, 0:GT, :]), start=False, stop=True,
                              skip_group_check=True).then_inc(cps.sem, 1)

                def outputs(i, e):
                    pe.wait_ge(hr.sem, hr.after(i, (e + 1) * CH))
                    pe.wait_ge(pr.sem, pr.after(i, e - 1))
                    for j in range(GT):
                        for n in range(CH):
                            c = e * CH + n
                            ins = pe.matmul(K.bank[4 + e % 2][:, j * C:(j + 1) * C], hT[0:M, c % R, j * P:(j + 1) * P],
                                            self.w2[0:M, c * C:(c + 1) * C], start=n == 0, stop=n == CH - 1, skip_group_check=True)
                    ins.then_inc(eo.sem, 1)
                pe.wait_ge(K.loaded[self.load], 16)
                pe.wait_ge(clr.sem, clr.base + 2)
                front.open_pe(pe)
                pe.sem_inc(eo.sem, 2 * R)
                front.transpose(pe, 0, 6)
                router(0, 0)
                if kind == "f3":
                    places(0)
                with pe.Fori(0, GROUPS // 2) as i0:
                    for u in range(2):
                        i, done = i0 * 2 + u, 0
                        for c in range(NC):
                            z, z3 = hbank(c)
                            x = xs[u][c % 2]
                            pe.wait_ge(hr.sem, hr.after(i, c - nbanks + 1))
                            ins = pe.matmul(z[0:M, :], self.w1[:, (c // 2) * M:(c // 2 + 1) * M], x[:, :], start=True, stop=True)
                            if gated:
                                ins = pe.matmul(z3[0:M, :], self.w3[:, (c // 2) * M:(c // 2 + 1) * M], x[:, :], start=True, stop=True)
                            ins.then_inc(hps.sem, 1)
                            if c == at_turn:
                                front.transpose(pe, i + 1, 6)
                            if c == at_router:
                                router(i + 1, 1 - u)
                            if biased and c == NC - 4:
                                pe.wait_ge(bmv.sem, bmv.after(i, 0))
                                pe.wait_ge(wr.sem, wr.after(i, 1))
                                K.settle(pe)
                                pe.transpose(B7[:, P:2 * P], flat(g[:, u, :, :]), K.W("ident")).then_inc(gtp.sem, 1)
                            if biased and c == NC - 2:
                                pe.wait_ge(gtr.sem, gtr.after(i, 1))
                                pe.matmul(B7[:, 2 * P:4 * P], gT[:, :], self.b2, start=True, stop=True, skip_group_check=True).then_inc(bps.sem, 1)
                            while (done + 1) * CH - 1 <= c - lag:
                                outputs(i, done)
                                done += 1
                        while done < E:
                            outputs(i, done)
                            done += 1
                        if kind == "f3":
                            places(i + 1)

            @block.scalar
            def _(a):
                def exps(n):
                    a.wait_ge(shf.sem, shf.after(n, 1))
                    a.activation(ex[:, :, :], ex[:, :, :], ACT.Exp).then_inc(exr.sem, 1)
                a.wait_ge(K.loaded[self.load], 16)
                if not gated:
                    a.sem_inc(hr.sem, R)
                front.move(a, 0, 6, xs[0])
                exps(0)
                with a.Fori(0, GROUPS // 2) as i0:
                    for u in range(2):
                        i = i0 * 2 + u
                        for c in range(NC):
                            z, _ = hbank(c)
                            a.wait_ge(hps.sem, hps.after(i, c + 1))
                            if gated:
                                a.wait_ge(hr.sem, hr.after(i, c - 1))
                                a.activation(ug[0:M, c % 2, :], z[0:M, :], ACT.Silu).then_inc(gtd.sem, 1)
                            else:
                                a.wait_ge(eo.sem, eo.after(i, (c - R) // CH + 1))
                                a.activation(hT[0:M, c % R, :], z[0:M, :], ACT.Relu, bias=self.b1[0:M, c:c + 1]).then_inc(hr.sem, 1)
                            if c == at_turn:
                                front.move(a, i + 1, 6, xs[1 - u])
                            if c == at_exp:
                                exps(i + 1)
                            if biased and c == NC - 4:
                                a.wait_ge(gtp.sem, gtp.after(i, 1))
                                a.activation(gT[:, :], B7[:, P:2 * P], ACT.Copy).then_inc(gtr.sem, 1)

            @block.gpsimd
            def _(p):
                if kind == "f3":
                    for n, x in enumerate((0.0, 1.0e4, -1.0e4)):
                        p.memset(limits[:, n, :], x)
                p.memset(run[:, :, :], 0.0)
                p.memset(g[:, :, :, :], 0.0).then_inc(clr.sem, 1)
                p.sem_inc(sd.sem, 2)
                front.rstds(p, 0)
                with p.Fori(0, GROUPS) as i:
                    front.rstds(p, i + 1)
                    for e in range(E):
                        p.wait_ge(pr.sem, pr.after(i, e + 1))
                        if e == 0:
                            p.wait_ge(acs.sem, acs.after(i, 1))
                        else:
                            p.wait_ge(sd.sem, sd.after(i, e))
                        p.tensor_tensor(flat(acc[:, :, :]), flat(acc[:, :, :]), prod[:, e % 2, :], ALU.add).then_inc(sd.sem, 1)
                    if kind == "f0":
                        p.wait_ge(mst.sem, mst.after(i, 1))
                        K.settle(p)
                        p.tensor_scalar(wk4[:, :], mv[:, :, 1], 1e-5, None, ALU.add).then_inc(mpl.sem, 1)
                        p.wait_ge(mpl.sem, mpl.after(i, 1))
                        p.tensor_tensor(rstd[:, :], wk4[:, :], K.half[:, 0:GT], ALU.pow).then_inc(mrs.sem, 1)

            @block.vector
            def _(v):
                work = []

                def fill():
                    if work:
                        work.pop(0)()

                def choose(n, u, every):
                    st = [0]

                    def lk(ins, settle=False):
                        st[0] += 1
                        ins.then_inc(vec.sem, 1)
                        if st[0] > 3 and st[0] % every == 0:
                            fill()
                        v.wait_ge(vec.sem, vec.after(n, st[0]))
                        if settle:
                            K.settle(v)

                    def pick(src, top, one):
                        lk(v.tensor_reduce(top[:, :], src[:, :, :], AX.X, ALU.max))
                        lk(v.tensor_tensor(eq[:, :, :], src[:, :, :], b3(top[:, :]), ALU.is_equal))
                        lk(v.tensor_tensor(eq[:, :, :], eq[:, :, :], rank, ALU.mult))
                        lk(v.tensor_reduce(wk[:, :], eq[:, :, :], AX.X, ALU.max))
                        lk(v.tensor_tensor(one[:, :, :], eq[:, :, :], b3(wk[:, :]), ALU.is_equal))

                    def both(src):
                        pick(src, m1, o1)
                        lk(v.scalar_tensor_tensor(flat(l2[:, :, :]), flat(o1[:, :, :]), -BIG, flat(src[:, :, :]), ALU.mult, ALU.add))
                        pick(l2, m2, o2)
                        lk(v.tensor_tensor(o1[:, :, :], o1[:, :, :], o2[:, :, :], ALU.add))
                    weights = g[:, u, :, 0:E]
                    src = B6[:, 0:GT * E].rearrange("p (j e) -> p j e", j=GT)
                    v.wait_ge(lgr.sem, lgr.after(n, 1))
                    if self.gb is not None:
                        lk(v.tensor_tensor(lg[:, :, :], src, rows(self.gb, GT, E), ALU.add))
                    else:
                        lk(v.tensor_copy(lg[:, :, :], src))
                    lk(v.tensor_reduce(m1[:, :], lg[:, :, :], AX.X, ALU.max))
                    v.tensor_tensor(ex[:, :, :], lg[:, :, :], b3(m1[:, :]), ALU.subtract).then_inc(shf.sem, 1)
                    v.wait_ge(shf.sem, shf.after(n, 1))
                    if kind == "f0":
                        both(lg)
                        v.wait_ge(exr.sem, exr.after(n, 1))
                        K.settle(v)
                        lk(v.tensor_tensor(o1[:, :, :], o1[:, :, :], ex[:, :, :], ALU.mult))
                        lk(v.tensor_reduce(sm[:, :], o1[:, :, :], AX.X, ALU.add))
                        lk(v.reciprocal(sm[:, :], sm[:, :]))
                        v.tensor_tensor(weights, o1[:, :, :], b3(sm[:, :]), ALU.mult).then_inc(wr.sem, 1)
                        assert st[0] == choice_steps
                        return
                    v.wait_ge(exr.sem, exr.after(n, 1))
                    K.settle(v)
                    lk(v.tensor_reduce(sm[:, :], ex[:, :, :], AX.X, ALU.add))
                    lk(v.reciprocal(sm[:, :], sm[:, :]))
                    lk(v.tensor_tensor(lg[:, :, :], ex[:, :, :], b3(sm[:, :]), ALU.mult))
                    if kind == "f2":
                        both(lg)
                        lk(v.tensor_tensor(o1[:, :, :], o1[:, :, :], lg[:, :, :], ALU.mult))
                        lk(v.tensor_reduce(sm[:, :], o1[:, :, :], AX.X, ALU.add))
                        lk(v.tensor_scalar(sm[:, :], sm[:, :], 1e-9, None, ALU.add))
                        lk(v.reciprocal(sm[:, :], sm[:, :]))
                        v.tensor_tensor(weights, o1[:, :, :], b3(sm[:, :]), ALU.mult).then_inc(wr.sem, 1)
                        assert st[0] == choice_steps
                        return
                    pick(lg, m1, o1)
                    for j in range(GT):
                        ins = v.tensor_tensor(run[:, j + 1, :], run[:, j, :], o1[:, j, :], ALU.add)
                        if j < GT - 1:
                            lk(ins)
                    ins.then_inc(cntd.sem, 1)
                    while work:
                        fill()
                    v.wait_ge(cps.sem, cps.after(n, 1))
                    K.settle(v)
                    lk(v.tensor_copy(run[:, 0, :], run[:, GT, :]))
                    lk(v.tensor_tensor(l2[:, :, :], B6[:, 64:64 + GT * E].rearrange("p (j e) -> p j e", j=GT), o1[:, :, :], ALU.mult))
                    lk(v.tensor_reduce(sm[:, :], l2[:, :, :], AX.X, ALU.add))
                    lk(v.tensor_scalar(sm[:, :], sm[:, :], float(CAP3), None, ALU.is_le))
                    lk(v.tensor_tensor(sm[:, :], sm[:, :], m1[:, :], ALU.mult))
                    v.tensor_tensor(weights, o1[:, :, :], b3(sm[:, :]), ALU.mult).then_inc(wr.sem, 1)
                    assert st[0] == choice_steps

                def weigh(i, u, e):
                    v.wait_ge(eo.sem, eo.after(i, e + 1))
                    v.wait_ge(sd.sem, sd.after(i, e - 1))
                    v.tensor_tensor(prod[:, e % 2, :].rearrange("p (j c) -> p j c", j=GT),
                                    K.bank[4 + e % 2][:, 0:GT * C].rearrange("p (j c) -> p j c", j=GT),
                                    g[:, u, :, e:e + 1].to_broadcast([P, GT, C]), ALU.mult).then_inc(pr.sem, 1)

                def gate(i, c):
                    v.wait_ge(gtd.sem, gtd.after(i, c + 1))
                    v.wait_ge(eo.sem, eo.after(i, (c - R) // CH + 1))
                    v.tensor_tensor(hT[0:M, c % R, :], ug[0:M, c % 2, :], hbank(c)[1][0:M, :], ALU.mult).then_inc(hr.sem, 1)

                def move_bias(i):
                    v.wait_ge(bps.sem, bps.after(i, 1))
                    v.tensor_copy(bsum[:, :, :], B7[:, 2 * P:4 * P].rearrange("p (j c) -> p j c", j=GT)).then_inc(bmv.sem, 1)

                def group(i, u):
                    if kind == "f0":
                        v.wait_ge(wr.sem, wr.after(i, 1))
                        v.tensor_copy(acc[:, :, :], K.xn[:, :, 0, :]).then_inc(acs.sem, 1)
                    elif kind == "f2":
                        K.settle(v)
                        v.tensor_copy(acc[:, :, :], kept[:, bass.ds(i * GT, GT), :]).then_inc(acs.sem, 1)
                    else:
                        v.memset(acc[:, :, :], 0.0).then_inc(acs.sem, 1)
                    v.wait_ge(wr.sem, wr.after(i, 1))
                    front.statistics(v, i + 1)
                    e = 0
                    if gated:
                        for c in range(NC):
                            work.append(lambda c=c: gate(i, c))
                            if c - lag >= 1 and (c - lag) % CH == CH - 1:
                                work.append(lambda e=e: weigh(i, u, e))
                                e += 1
                    for e in range(e, E):
                        work.append(lambda e=e: weigh(i, u, e))
                        if biased and e == E - 3:
                            work.append(lambda: move_bias(i))
                    before_norm, before_choice, every = {"f0": (2, 3, 2), "f2": (3, 8, 1), "f3": (1, 2, 3)}[kind]
                    for _ in range(before_norm):
                        fill()
                    front.normalise(v, i + 1)
                    for _ in range(before_choice):
                        fill()
                    choose(i + 1, 1 - u, every)
                    while work:
                        fill()
                    v.wait_ge(sd.sem, sd.after(i, E))
                    st = [0]
                    lk = link(v, fin, i, st, K)
                    if biased:
                        v.wait_ge(bmv.sem, bmv.after(i, 1))
                        lk(v.tensor_tensor(acc[:, :, :], acc[:, :, :], bsum[:, :, :], ALU.add))
                    if kind == "f0":
                        for j in range(GT):
                            ins = v.bn_stats(bnst[:, j, :], acc[:, j, :])
                        lk(ins, settle=True)
                        for j in range(GT):
                            ins = v.bn_aggr(mv[:, j, :], bnst[:, j, :])
                        ins.then_inc(mst.sem, 1)
                        v.wait_ge(mrs.sem, mrs.after(i, 1))
                        for j in range(GT):
                            ins = v.tensor_scalar(acc[:, j, :], acc[:, j, :], mv[:, j, 0:1], rstd[:, j:j + 1], ALU.subtract, ALU.mult)
                        lk(ins)
                        lk(v.tensor_tensor(acc[:, :, :], acc[:, :, :], rows(K.W("f0_g"), GT, C), ALU.mult))
                        lk(v.tensor_tensor(acc[:, :, :], acc[:, :, :], rows(K.W("f0_b"), GT, C), ALU.add))
                    if kind == "f3":
                        y = flat(acc[:, :, :])
                        lk(v.tensor_tensor(mask[:, :], y, y, ALU.not_equal), settle=True)
                        lk(v.copy_predicated(y, mask[:, :], limits[:, 0, :]))
                        lk(v.tensor_scalar(mask[:, :], y, 3.4028234e38, None, ALU.is_gt), settle=True)
                        lk(v.copy_predicated(y, mask[:, :], limits[:, 1, :]))
                        lk(v.tensor_scalar(mask[:, :], y, -3.4028234e38, None, ALU.is_lt), settle=True)
                        lk(v.copy_predicated(y, mask[:, :], limits[:, 2, :]))
                    lk(v.tensor_tensor(K.hgroup(i), K.hgroup(i), acc[:, :, :], ALU.add))
                    assert st[0] == final_steps, (kind, st[0])

                v.memset(xs[1][0][C:P, :], 0.0)
                v.memset(xs[1][1][0:C, :], 0.0).then_inc(clr.sem, 1)
                v.wait_ge(K.loaded[self.load], 16)
                v.wait_ge(clr.sem, clr.base + 2)
                v.sem_inc(pr.sem, 2)
                if biased:
                    v.sem_inc(bmv.sem, 1)
                if gated:
                    v.sem_inc(hr.sem, R)
                front.statistics(v, 0)
                front.normalise(v, 0)
                choose(0, 0, 1)
                with v.Fori(0, GROUPS // 2) as i0:
                    for u in range(2):
                        group(i0 * 2 + u, u)
            for c in counts:
                c.close(GROUPS + (c in (lgr, vec, shf, exr, wr, cps, cntd)))
            front.close()


def first_mixture(K):
    Mixture(K, "f0", 1, Front(K, "ln", (1e-5,), dup=True), E0, 1, F0, K.W("f0_w1"), K.W("f0_w2"), b1=K.W("f0_b1"),
            gw=K.W("f0_gw"), gb=K.W("f0_gb"), b2=K.W("f0_b2")).run()


def second_mixture(K, x1):
    Mixture(K, "f2", 6, Front(K, "rms", (1e-6,), dup=True, scale=K.W("f2_ln"), src=x1), E2, 2, F2C, K.W("f2_w1"), K.W("f2_w2"),
            w3=K.W("f2_w3"), gw=K.W("f2_gw"), kept=x1).run()


def third_mixture(K):
    Mixture(K, "f3", 8, Front(K, "ln", (1e-5,), dup=True), E3, 2, P, K.W("f3_w1"), K.W("f3_w2"), b1=K.W("f3_b1"),
            gw=K.W("f3_gw"), gb=K.W("f3_gb"), b2=K.W("f3_b2")).run()


def third_layer_block(K, which=(0, 1)):
    with K.nc.sbuf_tensor("x1", [P, TILES + GT, C], F32) as x1:
        with K.nc.Block() as block:
            @block.vector
            def _(v):
                v.memset(x1[:, TILES:TILES + GT, :], 0.0)
        second_routed_attention(K, x1)
        second_mixture(K, x1)


class KeySoftmaxUnits:

    N = 2

    def __init__(self, K, ctx, qT, kT, vt, scale, mask):
        nc = K.nc
        self.K, self.qT, self.kT, self.vt, self.scale, self.mask = K, qT, kT, vt, scale, mask
        self.sb = ctx.enter_context(nc.sbuf_tensor("a3_masked", [P, 2, 2 * SEQ], F32))
        self.p = ctx.enter_context(nc.sbuf_tensor("a3_probs", [P, 2, 2 * SEQ], F32))
        self.vs = ctx.enter_context(nc.sbuf_tensor("a3_values_over_sum", [P, 2, 2, C], F32))
        self.nm = ctx.enter_context(nc.sbuf_tensor("a3_negmax", [P, 2, 4], F32))
        self.rd = ctx.enter_context(nc.sbuf_tensor("a3_rden", [P, 2, 2], F32))
        names = ("scores_ready", "max_ready", "probs_ready", "values_over_sum", "values_summed", "normalised", "unit_vec")
        self.sc, self.mx, self.ex, self.vo, self.pv, self.no, self.vec = self.all = [K.count(n) for n in names]
        for c, credit in ((self.sc, 0), (self.mx, 0), (self.ex, 2), (self.vo, 0), (self.pv, 2), (self.no, 2)):
            c.stage(2, credit)
        self.vec.stage(8)

    def close(self):
        for c in self.all:
            c.close(GROUPS)

    def open_pe(self, pe):
        pe.sem_inc(self.pv.sem, 2)

    def open_act(self, a):
        a.sem_inc(self.ex.sem, 2)

    def open_vec(self, v):
        v.sem_inc(self.no.sem, 2)

    def tensor(self, pe, i, splice):
        K = self.K
        for s in range(2):
            for m in range(2):
                k0 = s * SEQ + m * P
                ins = pe.matmul(K.bank[s][:, m * SEQ:(m + 1) * SEQ], self.kT[:, k0:k0 + P], self.qT[:, s * SEQ:(s + 1) * SEQ],
                                start=True, stop=True)
            ins.then_inc(self.sc.sem, 1)
        for s in range(2):
            pe.wait_ge(self.vo.sem, self.vo.after(i, s + 1))
            pe.wait_ge(self.no.sem, self.no.after(i, s - 1))
            for n in range(2):
                for m in range(2):
                    ins = pe.matmul(K.bank[OB[s]][:, n * C:(n + 1) * C], self.p[:, s, m * SEQ + n * P:m * SEQ + (n + 1) * P],
                                    self.vs[:, s, m, :], start=m == 0, stop=m == 1, skip_group_check=True)
            ins.then_inc(self.pv.sem, 1)
        for k in sorted(splice):
            splice[k](pe)

    def vector(self, v, i, splice):
        K = self.K
        lk = link(v, self.vec, i, [0], K)
        steps = [splice[k] for k in sorted(splice)]
        for s in range(2):
            v.wait_ge(self.sc.sem, self.sc.after(i, s + 1))
            v.wait_ge(self.ex.sem, self.ex.after(i, s - 1))
            lk(v.tensor_tensor(self.sb[:, s, :], K.bank[s][:, :], self.mask, ALU.add))
            lk(v.tensor_reduce(self.nm[:, s, 2:4], self.sb[:, s, :].rearrange("p (a b) -> p a b", a=2), AX.X, ALU.max, negate=True))
            v.tensor_scalar(self.nm[:, s, 0:2], self.nm[:, s, 2:4], self.scale, None, ALU.mult).then_inc(self.mx.sem, 1)
        steps[0](v)
        K.proj.wait_moved(v, i)
        for s in range(2):
            v.wait_ge(self.ex.sem, self.ex.after(i, s + 1))
            lk(v.tensor_reduce(self.rd[:, s, :], self.p[:, s, :].rearrange("p (a b) -> p a b", a=2), AX.X, ALU.add))
            lk(v.reciprocal(self.rd[:, s, :], self.rd[:, s, :]))
            v.wait_ge(self.pv.sem, self.pv.after(i, s - 1))
            v.tensor_tensor(self.vs[:, s, :, :], self.vt[:, 2 * s:2 * s + 2, :],
                            self.rd[:, s, :].rearrange("p (a c) -> p a c", c=1).to_broadcast([P, 2, C]), ALU.mult).then_inc(self.vo.sem, 1)
        for f in steps[1:]:
            f(v)
        for s in range(2):
            v.wait_ge(self.pv.sem, self.pv.after(i, s + 1))
            dest = K.h[:, bass.ds(i * GT + 2 * s, 2), :]
            v.tensor_tensor(dest, dest, K.bank[OB[s]][:, 0:2 * C].rearrange("p (j c) -> p j c", j=2), ALU.add).then_inc(self.no.sem, 1)

    def scalar(self, a, i, splice):
        K = self.K
        for s in range(2):
            a.wait_ge(self.mx.sem, self.mx.after(i, s + 1))
            a.wait_ge(self.pv.sem, self.pv.after(i, s - 1))
            for m in range(2):
                r = slice(m * SEQ, (m + 1) * SEQ)
                ins = a.activation(self.p[:, s, r], self.sb[:, s, r], ACT.Exp, bias=self.nm[:, s, m:m + 1], scale=self.scale)
            ins.then_inc(self.ex.sem, 1)
        for k in sorted(splice):
            splice[k](a)


class NoTail:

    def stage(self):
        pass

    close = stage

    def open_vec(self, v):
        pass

    def early(self, e, i):
        pass

    wait_free = tensor = vector = scalar = gpsimd = early


def last_attention(K):
    nc = K.nc
    front = Front(K, "ln", (1e-5,))

    def make(ctx):
        qT = ctx.enter_context(nc.sbuf_tensor("a3_qT", [P, NTOK], F32))
        kT = ctx.enter_context(nc.sbuf_tensor("a3_kT", [P, NTOK], F32))
        prepare(K, [], [qT[C:P, :], kT[C:P, :]])
        vt = ctx.enter_context(nc.sbuf_tensor("a3_v_sb", [P, GT, C], F32))
        x = K.xU[:, :]
        jobs = [
            ("act", lambda pe, b, i: pe.matmul(b[0:C, :], K.W("a3_q"), x, start=True, stop=True),
             lambda a, b, i: a.activation(qT[0:C, :], b[0:C, :], ACT.Copy)),
            ("vec", lambda pe, b, i: pe.matmul(b[0:C, :], K.W("a3_k"), x, start=True, stop=True),
             lambda v, b, i: v.tensor_copy(kT[0:C, :], b[0:C, :])),
            ("act", lambda pe, b, i: [pe.matmul(b[:, j * C:(j + 1) * C], K.xU[:, j * P:(j + 1) * P], K.W("a3_v"),
                                                start=True, stop=True) for j in range(GT)][-1],
             lambda a, b, i: a.activation(vt[:, :, :], b[:, 0:GT * C].rearrange("p (j c) -> p j c", j=GT), ACT.Copy)),
        ]
        units = KeySoftmaxUnits(K, ctx, qT, kT, vt, 0.125, K.W("a3_mask"))
        K.proj = Projections(K, jobs)
        return units, K.proj, NoTail()
    attention_stage(K, "a3", 7, front, make)


STAGES = [first_attention, first_mixture, second_attention, expert_heads, third_attention, third_layer_block, last_attention, third_mixture]


def tower(nc, x, turns, image, masks, out, stages=None, h_in=None):
    with ExitStack() as ctx:
        K = Core(nc, ctx)
        embed_stage(K, x, turns, image, masks)
        if h_in is not None:
            hin = K.count("h_in")
            with nc.Block() as block:
                @block.sync
                def _(sp):
                    sp.dma_start(K.h[:, 0:TILES, :], h_in.rearrange("b (a p) c -> p (b a) c", p=P)).then_inc(hin.sem, 16)
                    sp.wait_ge(hin.sem, 16)
        for k, st in enumerate(STAGES):
            if stages is None or k in stages:
                st(K)
            if k == 2:
                late_weights(K, image)
        store_stage(K, out)


def lay_out(a):
    out = {}
    f = lambda n: np.asarray(a[n], np.float32) if np.asarray(a[n]).dtype != np.float32 else np.asarray(a[n])

    def put(name, parts, cols=None):
        w = dict((n, c) for n, c, _ in IMAGE)[name]
        t = np.zeros((P, w), np.float32)
        for (r0, c0, m) in parts:
            m = np.atleast_2d(m)
            t[r0:r0 + m.shape[0], c0:c0 + m.shape[1]] = m
        out[name] = t

    def col(name, *vs):
        put(name, [(0, k, v.reshape(-1, 1)) for k, v in enumerate(vs)])

    def row(name, v):
        put(name, [(0, 0, np.broadcast_to(v.reshape(1, -1), (P, v.size)))])

    put("ident", [(0, 0, np.eye(P, dtype=np.float32))])
    co = f("L0_tok_poly_coeffs").transpose(1, 0, 2).reshape(TURNS * DEG, C)
    put("coef", [(32 * j, j * C, co) for j in range(GT)])
    qkv, qb = f("L0_attn_qkv_w"), f("L0_attn_qkv_b")
    put("a0_qk", [(0, 0, qkv[:, :128])])
    put("a0_v", [(0, 0, qkv[:, 128:])])
    col("a0_lnw", f("L0_attn_ln1_g"), f("L0_attn_ln1_b"))
    col("a0_qkb", qb[:C], qb[C:2 * C])
    row("a0_vb", qb[128:])
    t = f("L0_attn_bias_table")
    q, k = np.arange(SEQ)[:, None], np.arange(SEQ)[None, :]
    rel = t[k - q + SEQ - 1]
    put("a0_bias", [(0, SEQ * b, rel[b * P:(b + 1) * P]) for b in range(2)])
    row("a0_scale", f("L0_attn_scale").reshape(1))
    put("a0_o", [(0, 0, f("L0_attn_proj_w"))])
    row("a0_ob", f("L0_attn_proj_b"))
    row("a0_g2", f("L0_attn_ln2_g"))
    row("a0_b2", f("L0_attn_ln2_b"))
    put("a1_q", [(0, 0, f("L1_attn_Wq"))])
    put("a1_k", [(0, 0, f("L1_attn_Wk"))])
    put("a1_v", [(0, 0, f("L1_attn_Wv"))])
    put("a1_o", [(0, c * C, f("L1_attn_Wu")[c * P:(c + 1) * P]) for c in range(4)])
    put("a1_qb", [(0, 0, f("L1_attn_bq").reshape(4, P).T)])
    put("a1_kb", [(0, 0, f("L1_attn_bk").reshape(4, P).T)])
    row("a1_vb", f("L1_attn_bv"))
    row("a1_ob", f("L1_attn_bu"))
    r0 = np.ones((P, 2), np.float32)
    r0[0, 0] = 0
    put("row0", [(0, 0, r0)])

    put("rank", [(0, 0, np.broadcast_to(16.0 - np.arange(16, dtype=np.float32), (P, 16)))])

    def halves(w, m):
        return [(C * (c % 2), (c // 2) * m, w[c]) for c in range(len(w))]

    def block_bias(b2, e):
        t = np.zeros((P, GT * C), np.float32)
        for j in range(GT):
            t[32 * j:32 * j + e, j * C:(j + 1) * C] = b2
        return [(0, 0, t)]
    put("f0_gw", [(0, 0, f("L0_ffn_gate_w"))])
    row("f0_gb", f("L0_ffn_gate_b"))
    put("f0_w1", halves(f("L0_ffn_w1"), F0))
    put("f0_b1", [(0, 0, f("L0_ffn_b1").T)])
    put("f0_w2", [(0, e * C, f("L0_ffn_w2")[e]) for e in range(E0)])
    put("f0_b2", block_bias(f("L0_ffn_b2"), E0))
    row("f0_g", f("L0_ffn_gamma"))
    row("f0_b", f("L0_ffn_beta"))
    put("a2_q", [(0, 0, f("L2_attn_W_Q").transpose(1, 0, 2).reshape(C, 256))])
    put("a2_k", [(0, 0, f("L2_attn_W_K").transpose(1, 0, 2).reshape(C, 256))])
    put("a2_v", [(0, 0, f("L2_attn_W_V").transpose(1, 0, 2).reshape(C, 256))])
    put("a2_qb", [(0, 0, f("L2_attn_b_Q").reshape(2, P).T)])
    put("a2_kb", [(0, 0, f("L2_attn_b_K").reshape(2, P).T)])
    row("a2_vb", f("L2_attn_b_V"))
    put("a2_o", [(0, c * C, f("L2_attn_W_O").reshape(256, C)[c * P:(c + 1) * P]) for c in range(2)])
    row("a2_ob", f("L2_attn_b_O"))
    col("r2_ln", f("L2_ffn_ln1_w"))
    wq, wk = f("L2_ffn_wq"), f("L2_ffn_wk")
    turn = np.concatenate([np.arange(8, 16), np.arange(0, 8)])
    put("r2_q", [(0, 32 * n, wq[16 * n:16 * n + 16].T) for n in range(4)])
    put("r2_qp", [(0, 32 * n, wq[16 * n:16 * n + 16][turn].T) for n in range(4)])
    put("r2_k", [(0, 32 * n, wk[16 * (n // 2):16 * (n // 2) + 16].T) for n in range(4)])
    put("r2_kp", [(0, 32 * n, wk[16 * (n // 2):16 * (n // 2) + 16][turn].T) for n in range(4)])
    put("r2_v", [(0, 0, f("L2_ffn_wv").T)])
    put("r2_o", [(0, 0, f("L2_ffn_wo").T)])
    inv = 1.0 / 10000.0 ** (np.arange(0, 16, 2, dtype=np.float32) / 16)
    fr = np.outer(np.arange(SEQ, dtype=np.float32), inv)
    emb = np.concatenate([fr, fr], axis=-1).astype(np.float32)
    cos, sin = np.cos(emb).T, np.sin(emb).T.copy()
    sin[0:8] *= -1.0
    for name, tab, sc in (("r2_cq", cos, 0.25), ("r2_sq", sin, 0.25), ("r2_ck", cos, 1.0), ("r2_sk", sin, 1.0)):
        put(name, [(32 * n, 0, (tab * sc).astype(np.float32)) for n in range(4)])
    put("f2_ln", [(0, 0, np.concatenate([f("L2_ffn_ln2_w")] * 2).reshape(P, 1))])
    put("f2_gw", [(0, 0, f("L2_ffn_router_w").T)])
    put("f2_w1", halves(f("L2_ffn_w1").reshape(16, F2C, C).transpose(0, 2, 1), F2C))
    put("f2_w3", halves(f("L2_ffn_w3").reshape(16, F2C, C).transpose(0, 2, 1), F2C))
    w2 = f("L2_ffn_w2").transpose(0, 2, 1).reshape(16, F2C, C)
    put("f2_w2", [(0, c * C, w2[c]) for c in range(16)])
    put("f3_gw", [(0, 0, f("L3_ffn_gate_w"))])
    row("f3_gb", f("L3_ffn_gate_b"))
    w1 = f("L3_ffn_w1").reshape(E3, C, 2, P).transpose(0, 2, 1, 3).reshape(16, C, P)
    put("f3_w1", halves(w1, P))
    put("f3_b1", [(0, 0, f("L3_ffn_b1").reshape(16, P).T)])
    w2 = f("L3_ffn_w2").reshape(16, P, C)
    put("f3_w2", [(0, c * C, w2[c]) for c in range(16)])
    put("f3_b2", block_bias(f("L3_ffn_b2"), E3))
    put("tri", [(0, 0, np.triu(np.ones((P, P), np.float32)))])
    put("ones", [(0, 0, np.ones((P, P), np.float32))])
    put("a3_q", [(0, 0, f("L3_attn_Wq").T)])
    put("a3_k", [(0, 0, f("L3_attn_Wk").T)])
    put("a3_v", [(0, 0, f("L3_attn_Wv").T)])
    n, k = np.arange(SEQ)[None, :], np.arange(P)[:, None]
    put("a3_mask", [(0, b * SEQ, np.where(n < k + b * P, 0, -1.0e10).astype(np.float32)) for b in range(2)])
    hl = f("L1_ffn_hl_w").reshape(C, C)
    put("f1_hl", [(0, 0, hl.T)])
    put("f1_hlb", [(0, 0, f("L1_ffn_hl_b").reshape(C, 1))])
    row("f1_hlbr", f("L1_ffn_hl_b").reshape(C))
    wq, wk, wv, gw = f("L1_ffn_wq"), f("L1_ffn_wk"), f("L1_ffn_wv"), f("L1_ffn_gate_w")
    put("f1_q", [(16 * n, e * P + 32 * n, wq[n, e].T) for n in range(4) for e in range(4)])
    put("f1_k", [(16 * n, 32 * n, wk[n].T) for n in range(4)])
    put("f1_v", [(16 * n, 16 * n, wv[n].T) for n in range(4)])
    put("f1_g", [(64 * (n % 2), 16 * (n // 2) + 4 * n, gw[n].T) for n in range(4)])
    row("f1_gb", f("L1_ffn_gate_b").reshape(16))
    for name, key in (("f1_lg", "ln_g"), ("f1_lb", "ln_b"), ("f1_2b", "fc2_b"), ("f1_ng", "fnorm_g"), ("f1_nb", "fnorm_b")):
        row(name, f("L1_ffn_" + key))
    put("f1_1", [(16 * n, 16 * n, f("L1_ffn_fc1_w").T) for n in range(4)])
    put("f1_2", [(16 * n, 16 * n, f("L1_ffn_fc2_w").T) for n in range(4)])
    put("f1_1b", [(16 * n, 0, f("L1_ffn_fc1_b").reshape(16, 1)) for n in range(4)])
    put("f1_fg", [(0, 0, f("L1_ffn_fgate_w").T)])
    image = np.concatenate([out[n] if n in out else np.zeros((P, c), np.float32) for n, c, _ in IMAGE], axis=1)
    m = np.zeros((P, 18, P), np.float32)
    q, k = np.arange(P)[:, None], np.arange(P)[None, :]
    m[:, 0] = np.eye(P)
    for n in range(4):
        m[:, 1 + n] = np.where(k >= q, MASKED, 0)
        m[:, 5 + n] = np.where(k > q, MASKED, 0)
    for n in range(2):
        odd0 = np.where(((k < q) & (k % 2 == 1)) | (k == q), 0, MASKED)
        m[:, 9 + n] = odd0
        m[:, 11 + 2 * n] = np.where((k % 2 == 1) & (q >= 0), 0, MASKED)
        m[:, 12 + 2 * n] = odd0
    ids = np.ascontiguousarray(np.asarray(a["x"]).astype(np.int32).reshape(TILES, P).T)
    return {"x": ids, "turns": f("L0_tok_turns"), "image": np.ascontiguousarray(image), "masks": m}


def kernel(**inputs):
    import concourse.bacc as bacc
    from concourse.bass_utils import run_bass_kernel_spmd
    arrays = lay_out(inputs)
    nc = bacc.Bacc("TRN2", target_bir_lowering=False, num_devices=1)
    args, feeds = {}, {}
    for name, v in arrays.items():
        feeds[f"in_{name}"] = v
        args[name] = nc.dram_tensor(f"in_{name}", v.shape, mybir.dt.from_np(v.dtype), kind="ExternalInput").ap()
    out = nc.dram_tensor("out", (SEQS, SEQ, C), F32, kind="ExternalOutput").ap()
    tower(nc, args["x"], args["turns"], args["image"], args["masks"], out)
    r = run_bass_kernel_spmd(nc, [feeds], core_ids=[0])
    return r.results[0]["out"]
```

```python
from contextlib import ExitStack

import numpy as np
import concourse.bass as bass
from concourse import mybir

F32 = mybir.dt.float32
BF16 = mybir.dt.bfloat16
I32 = mybir.dt.int32
U32 = mybir.dt.uint32
ALU = mybir.AluOpType
ACT = mybir.ActivationFunctionType
AX = mybir.AxisListType

P = 128
SEQS, SEQ, C = 64, 256, 64
TILES = SEQS * SEQ // P
GT = 4
GROUPS = TILES // GT
NTOK = GT * P
BIG = 3.0e38
MASKED = -1.0e30
VOCAB, TURNS, DEG = 50257, 4, 5
E0, F0 = 16, 128
E2, F2, F2C = 8, 170, 85
E3, F3 = 8, 256
CAP3 = -(-5 * SEQS * SEQ // (4 * E3))

IMAGE = [
    ("ident", P, 0), ("coef", 4 * C, 0), ("rank", 16, 0),
    ("a0_qk", 128, 0), ("a0_v", C, 0), ("a0_lnw", 2, 0), ("a0_qkb", 2, 0), ("a0_vb", C, 0), ("a0_bias", 4 * P, 0),
    ("a0_scale", 1, 0), ("a0_o", C, 0), ("a0_ob", C, 0), ("a0_g2", C, 0), ("a0_b2", C, 0),
    ("f0_gw", E0, 1), ("f0_gb", E0, 1), ("f0_w1", E0 // 2 * F0, 1), ("f0_b1", E0, 1), ("f0_w2", E0 * C, 1),
    ("f0_b2", GT * C, 1), ("f0_g", C, 1), ("f0_b", C, 1),
    ("a1_q", 512, 2), ("a1_k", 512, 2), ("a1_v", 512, 2), ("a1_o", 4 * C, 2), ("a1_qb", 4, 2), ("a1_kb", 4, 2),
    ("a1_vb", 512, 2), ("a1_ob", C, 2), ("row0", 2, 2),
    ("f1_hl", C, 3), ("f1_hlb", 1, 3), ("f1_hlbr", C, 3), ("f1_q", 4 * P, 3), ("f1_k", P, 3), ("f1_v", C, 3),
    ("f1_g", 32, 3), ("f1_gb", 16, 3), ("f1_lg", 16, 3), ("f1_lb", 16, 3), ("f1_1", C, 3), ("f1_1b", 1, 3),
    ("f1_2", C, 3), ("f1_2b", 16, 3), ("f1_ng", 16, 3), ("f1_nb", 16, 3), ("f1_fg", 4, 3),
    ("a2_q", 256, 4), ("a2_k", 256, 4), ("a2_v", 256, 4), ("a2_qb", 2, 4), ("a2_kb", 2, 4), ("a2_vb", 256, 4),
    ("a2_o", 2 * C, 4), ("a2_ob", C, 4),
    ("r2_ln", 1, 5), ("r2_q", P, 5), ("r2_qp", P, 5), ("r2_k", P, 5), ("r2_kp", P, 5), ("r2_v", 32, 5), ("r2_o", C, 5),
    ("r2_cq", SEQ, 5), ("r2_sq", SEQ, 5), ("r2_ck", SEQ, 5), ("r2_sk", SEQ, 5),
    ("f2_ln", 1, 6), ("f2_gw", E2, 6), ("f2_w1", E2 * F2C, 6), ("f2_w3", E2 * F2C, 6), ("f2_w2", 2 * E2 * C, 6),
    ("a3_q", C, 7), ("a3_k", C, 7), ("a3_v", C, 7), ("a3_mask", 4 * P, 7),
    ("f3_gw", E3, 8), ("f3_gb", E3, 8), ("f3_w1", E3 * P, 8), ("f3_b1", 2 * E3, 8), ("f3_w2", 2 * E3 * C, 8),
    ("f3_b2", GT * C, 8), ("tri", P, 8), ("ones", P, 8),
]
LOADS = 9


LATE = (4, 5, 8)


def image_offsets():
    at, out, starts, dram = 0, {}, {}, {}
    size = [sum(c for _, c, g in IMAGE if g == k) for k in range(LOADS)]
    for k in [k for k in range(LOADS) if k not in LATE] + list(LATE):
        if k == LATE[0]:
            total, at = at, out["a0_qk"][0]
        starts[k] = (at, sum(size[:k]), size[k])
        for name, cols, group in IMAGE:
            if group == k:
                out[name] = (at, cols)
                at += cols
    assert at <= starts[3][0]
    return out, total, starts


class Count:

    def __init__(self, sem):
        self.sem, self.base, self.per, self.credit = sem, 0, 0, 0

    def stage(self, per, credit=0):
        self.per, self.credit = per, credit

    def after(self, i, n=0):
        return i * self.per + (self.base + self.credit + n)

    def close(self, groups, extra=0):
        self.base += self.credit + groups * self.per + extra
        self.per = self.credit = 0


def rows(ap, n, inner):
    return ap.rearrange("p (a c) -> p a c", a=1).to_broadcast([P, n, inner])


class Core:

    def __init__(self, nc, ctx):
        self.nc, self.ctx = nc, ctx
        self.off, total, self.starts = image_offsets()
        self.h = ctx.enter_context(nc.sbuf_tensor("h", [P, TILES + 2 * GT, C], F32))
        self.w = ctx.enter_context(nc.sbuf_tensor("weights", [P, total], F32))
        self.wb = ctx.enter_context(nc.sbuf_tensor("masks", [P, 15, P], BF16))
        self.xn = ctx.enter_context(nc.sbuf_tensor("xn", [P, GT, 2, C], F32))
        self.xU = ctx.enter_context(nc.sbuf_tensor("xT_upper", [P, NTOK], F32))
        self.xL = ctx.enter_context(nc.sbuf_tensor("xT_lower", [P, NTOK], F32))
        self.bnst = ctx.enter_context(nc.sbuf_tensor("bnst", [P, GT, 6], F32))
        self.mv = ctx.enter_context(nc.sbuf_tensor("mv", [P, GT, 2], F32))
        self.rstd = ctx.enter_context(nc.sbuf_tensor("rstd", [P, GT], F32))
        self.rwork = ctx.enter_context(nc.sbuf_tensor("rwork", [P, 4, 16], F32))
        self.half = ctx.enter_context(nc.sbuf_tensor("minus_half", [P, 16], F32))
        self.bank = [ctx.enter_context(nc.psum_tensor(f"bank{b}", [P, 512], F32)) for b in range(8)]
        self.counts = {}
        self.carrier = ctx.enter_context(nc.semaphore("wait_carrier"))
        self.loaded = [ctx.enter_context(nc.semaphore(f"loaded{k}")) for k in range(LOADS)]

    def count(self, name):
        if name not in self.counts:
            self.counts[name] = Count(self.ctx.enter_context(self.nc.semaphore(name)))
        return self.counts[name]

    def W(self, name, p0=0, p1=P):
        at, cols = self.off[name]
        return self.w[p0:p1, at:at + cols]

    def settle(self, eng):
        eng.sem_inc(self.carrier, 1)

    def hgroup(self, i):
        return self.h[:, bass.ds(i * GT, GT), :]


def link(eng, cnt, i, step, K=None):
    def then(ins, wait=True, settle=False):
        step[0] += 1
        ins.then_inc(cnt.sem, 1)
        if wait:
            eng.wait_ge(cnt.sem, cnt.after(i, step[0]))
        if settle:
            K.settle(eng)
    return then


class Front:

    def __init__(self, K, kind, eps, dup=False, scale=None, bias=None, src=None, kept=None):
        self.K, self.kind, self.eps, self.dup = K, kind, eps, dup
        self.scale, self.bias, self.src, self.kept = scale, bias, K.h if src is None else src, kept
        self.vec, self.stats, self.rs = K.count("front_vec"), K.count("stats_ready"), K.count("rstd_ready")
        self.pool, self.xn_r = K.count("front_pool"), K.count("xn_ready")
        self.xt_ps, self.xt_r = K.count("xT_in_psum"), K.count("xT_ready")
        self.passes = len(eps)
        self.vec.stage({"ln": 1, "lnln": 3, "rms": 2, "lnrms": 4}[kind])
        self.stats.stage(self.passes)
        self.rs.stage(self.passes)
        self.pool.stage(self.passes)
        self.xn_r.stage(1)
        self.xt_ps.stage(1, 1)
        self.xt_r.stage(1)

    def close(self, ahead=0):
        for c in (self.vec, self.stats, self.rs, self.pool, self.xn_r):
            c.close(GROUPS + 1 + ahead)
        for c in (self.xt_ps, self.xt_r):
            c.close(GROUPS + 1)

    def open_pe(self, pe):
        pe.sem_inc(self.xt_ps.sem, 1)

    def mean_var(self, v, src, lk):
        K = self.K
        for j in range(GT):
            ins = v.bn_stats(K.bnst[:, j, :], src(j))
        lk(ins, settle=True)
        for j in range(GT):
            ins = v.bn_aggr(K.mv[:, j, :], K.bnst[:, j, :])
        ins.then_inc(self.stats.sem, 1)

    def mean_square(self, v, src, lk):
        K = self.K
        lk(v.tensor_tensor(K.xn[:, :, 0, :], src, src, ALU.mult))
        lk(v.tensor_reduce(K.mv[:, :, 0], K.xn[:, :, 0, :], AX.X, ALU.add))
        v.tensor_scalar(K.mv[:, :, 1], K.mv[:, :, 0], 1.0 / C, None, ALU.mult).then_inc(self.stats.sem, 1)

    def statistics(self, v, i):
        self.lk = link(v, self.vec, i, [0], self.K)
        if self.kind == "rms":
            v.wait_ge(self.xt_ps.sem, self.xt_ps.after(i, 0))
            self.mean_square(v, self.src[:, bass.ds(i * GT, GT), :], self.lk)
        else:
            self.mean_var(v, lambda j: self.src[:, bass.ds(i * GT + j, 1), :], self.lk)

    def rstds(self, g, i, norms=(0, 1)):
        K = self.K
        for n, eps in [(n, eps) for n, eps in enumerate(self.eps) if n in norms]:
            g.wait_ge(self.stats.sem, self.stats.after(i, n + 1))
            K.settle(g)
            g.tensor_scalar(K.rwork[:, 0, 0:GT], K.mv[:, :, 1], eps, None, ALU.add).then_inc(self.pool.sem, 1)
            g.wait_ge(self.pool.sem, self.pool.after(i, n + 1))
            g.tensor_tensor(K.rstd[:, :], K.rwork[:, 0, 0:GT], K.half[:, 0:GT], ALU.pow).then_inc(self.rs.sem, 1)

    def normalise(self, v, i, part=None):
        K = self.K
        if part == 0 and self.passes == 1:
            return
        if part == 1 and self.passes == 2:
            self.finish(v, i)
            return
        v.wait_ge(self.rs.sem, self.rs.after(i, 1))
        v.wait_ge(self.xt_ps.sem, self.xt_ps.after(i, 0))
        centred = (lambda dst, src, j: v.tensor_scalar(dst, src, K.mv[:, j, 0:1], K.rstd[:, j:j + 1], ALU.subtract, ALU.mult))
        scaled = (lambda dst, src, j: v.tensor_scalar(dst, src, K.rstd[:, j:j + 1], None, ALU.mult))
        tile = (lambda j: self.src[:, bass.ds(i * GT + j, 1), :])
        self.tile, self.last = tile, centred
        if self.kind == "lnln":
            for j in range(GT):
                ins = centred(K.xn[:, j, 0, :], tile(j), j)
            self.lk(ins)
            self.mean_var(v, lambda j: K.xn[:, j, 0, :], self.lk)
            self.tile = (lambda j: K.xn[:, j, 0, :])
        elif self.kind == "lnrms":
            for j in range(GT):
                ins = centred(self.kept[:, bass.ds(i * GT + j, 1), :], tile(j), j)
            self.lk(ins)
            self.mean_square(v, self.kept[:, bass.ds(i * GT, GT), :], self.lk)
            self.tile = (lambda j: self.kept[:, bass.ds(i * GT + j, 1), :])
        if "rms" in self.kind:
            self.last = scaled
        if part != 0:
            self.finish(v, i)

    def finish(self, v, i):
        K = self.K
        if self.passes == 2:
            v.wait_ge(self.rs.sem, self.rs.after(i, 2))
        for j in range(GT):
            for d in range(2 if self.dup else 1):
                ins = self.last(K.xn[:, j, d, :], self.tile(j), j)
        ins.then_inc(self.xn_r.sem, 1)

    def transpose(self, pe, i, bank):
        K = self.K
        pe.wait_ge(self.xn_r.sem, self.xn_r.after(i, 1))
        K.settle(pe)
        for j in range(GT):
            if self.dup:
                ins = pe.transpose(K.bank[bank][:, j * P:(j + 1) * P], K.xn[:, j, :, :].rearrange("p a c -> p (a c)"), K.W("ident"))
            else:
                ins = pe.transpose(K.bank[bank][0:C, j * P:(j + 1) * P], K.xn[:, j, 0, :], K.W("ident"))
        ins.then_inc(self.xt_ps.sem, 1)

    def move(self, a, i, bank, to=None):
        K = self.K
        a.wait_ge(self.xt_ps.sem, self.xt_ps.after(i, 1))
        for dst, p0 in zip(to or (K.xU, K.xL), (0, C) if self.dup else (0,)):
            r = slice(p0, p0 + C)
            if self.scale is None:
                ins = a.activation(dst[r, :], K.bank[bank][r, :], ACT.Copy)
            elif self.bias is None:
                ins = a.activation(dst[r, :], K.bank[bank][r, :], ACT.Copy, scale=self.scale[r, :])
            else:
                ins = a.activation(dst[r, :], K.bank[bank][r, :], ACT.Identity, scale=self.scale[r, :], bias=self.bias[r, :])
        ins.then_inc(self.xt_r.sem, 1)


def embed_stage(K, x, turns, image, masks):
    nc = K.nc
    HALF = 4
    CT = TILES // HALF
    feat_r, ft_ps, ft_sb, emb_ps, emb_r = (K.count(n) for n in ("features_ready", "featT_in_psum", "featT_ready",
                                                                "emb_in_psum", "emb_ready"))
    with ExitStack() as ctx:
        def sb(n, s, d=F32):
            return ctx.enter_context(nc.sbuf_tensor(n, s, d))
        ids = sb("ids", [P, TILES], I32)
        rowsT = sb("turn_rows", [P, TILES * TURNS])
        absT = sb("turn_abs", [P, TILES * TURNS])
        intT = sb("turn_int", [P, TILES * TURNS], I32)
        feat = sb("features", [P, TILES, 32])
        fstage = sb("feature_stage", [P, 2, P])
        featT = sb("featT", [P, 2, P])
        masks_in = sb("masks_in", [P, 15, P])
        masks_loaded = K.count("masks_loaded")
        ids_in, gathered = K.count("ids_in"), [K.count(f"gathered{c}") for c in range(HALF)]
        vec, zeroed, staged = K.count("embed_vec"), K.count("zeroed"), K.count("feature_staged")
        for c in (feat_r, ft_ps, ft_sb, emb_ps, emb_r, staged):
            c.stage(1)
        block = ctx.enter_context(nc.Block())

        @block.sync
        def _(sp):
            sp.dma_start(ids[:, :], x).then_inc(ids_in.sem, 16)
            sp.dma_start(masks_in[:, :, :], masks).then_inc(masks_loaded.sem, 16)
            for k in [k for k in range(LOADS) if k not in LATE]:
                at, src, cols = K.starts[k]
                sp.dma_start(K.w[:, at:at + cols], image[:, src:src + cols]).then_inc(K.loaded[k], 16)

        @block.gpsimd
        def _(g):
            g.memset(K.half[:, :], -0.5)
            g.memset(K.h[:, TILES:TILES + 2 * GT, :], 0.0)
            g.memset(feat[:, :, TURNS * DEG:32], 0.0)
            g.memset(feat[:, :, 0:TURNS], 1.0).then_inc(zeroed.sem, 1)
            g.wait_ge(ids_in.sem, 16)
            for c in range(HALF):
                for j in range(c * CT, (c + 1) * CT):
                    g.indirect_dma_start(rowsT[:, j * TURNS:(j + 1) * TURNS], None, turns,
                                         bass.IndirectOffsetOnAxis(ids[:, j:j + 1].bitcast(U32), 0)).then_inc(gathered[c].sem, 16)

        per_chunk = GROUPS // HALF

        @block.scalar
        def _(a):
            a.preload_act_table(ACT.Exp)
            for c in range(HALF):
                a.wait_ge(feat_r.sem, c + 1)
                with a.Fori(c * per_chunk // 2, (c + 1) * per_chunk // 2) as i0:
                    for u in range(2):
                        i = i0 * 2 + u
                        a.wait_ge(emb_ps.sem, i + 1)
                        a.activation(fstage[:, u, :], feat[:, bass.ds(i * GT, GT), :], ACT.Copy).then_inc(staged.sem, 1)
                        a.wait_ge(ft_ps.sem, i + 1)
                        a.activation(featT[:, u, :], K.bank[u][:, 0:P], ACT.Copy).then_inc(ft_sb.sem, 1)

        @block.tensor
        def _(pe):
            pe.wait_ge(K.loaded[0], 16)
            pe.sem_inc(emb_ps.sem, 1)
            with pe.Fori(0, GROUPS // 2) as i0:
                for u in range(2):
                    i = i0 * 2 + u
                    pe.wait_ge(staged.sem, i + 1)
                    pe.transpose(K.bank[u][:, 0:P], fstage[:, u, :], K.W("ident")).then_inc(ft_ps.sem, 1)
                    pe.wait_ge(ft_sb.sem, i + 1)
                    pe.wait_ge(emb_r.sem, i0 * 2 + 1)
                    pe.matmul(K.bank[2 + u][:, 0:GT * C], featT[:, u, :], K.W("coef"), start=True, stop=True)\
                        .then_inc(emb_ps.sem, 1)

        @block.vector
        def _(v):
            n = 0
            v.memset(K.xU[C:P, :], 0.0)
            v.memset(K.xL[0:C, :], 0.0)
            v.wait_ge(masks_loaded.sem, 16)
            v.tensor_copy(K.wb[:, :, :], masks_in[:, :, :])
            v.wait_ge(zeroed.sem, 1)

            def lk(ins):
                nonlocal n
                n += 1
                ins.then_inc(vec.sem, 1)
                v.wait_ge(vec.sem, n)
            for c in range(HALF):
                v.wait_ge(gathered[c].sem, 16 * CT)
                s = slice(c * CT * TURNS, (c + 1) * CT * TURNS)
                t, a, k = rowsT[:, s], absT[:, s], intT[:, s]
                lk(v.scalar_tensor_tensor(a, t, -1.0, t, ALU.mult, ALU.max))
                lk(v.tensor_copy(k, a))
                f1 = feat[:, c * CT:(c + 1) * CT, TURNS:2 * TURNS]
                a3 = a.rearrange("p (j d) -> p j d", d=TURNS)
                t3 = t.rearrange("p (j d) -> p j d", d=TURNS)
                lk(v.tensor_copy(f1, k.rearrange("p (j d) -> p j d", d=TURNS)))
                lk(v.tensor_tensor(a3, f1, a3, ALU.is_gt))
                lk(v.tensor_tensor(f1, f1, a3, ALU.subtract))
                lk(v.tensor_scalar(a, t, 0.0, 2.0, ALU.is_ge, ALU.mult))
                lk(v.tensor_scalar(a, a, -1.0, None, ALU.add))
                lk(v.tensor_tensor(f1, f1, a3, ALU.mult))
                for d in range(2, DEG):
                    prev = feat[:, c * CT:(c + 1) * CT, (d - 1) * TURNS:d * TURNS]
                    cur = feat[:, c * CT:(c + 1) * CT, d * TURNS:(d + 1) * TURNS]
                    ins = v.tensor_tensor(cur, prev, f1, ALU.mult)
                    if d < DEG - 1:
                        lk(ins)
                ins.then_inc(feat_r.sem, 1)
            v.sem_inc(emb_r.sem, 1)
            with v.Fori(0, GROUPS // 2) as i0:
                for u in range(2):
                    i = i0 * 2 + u
                    v.wait_ge(emb_ps.sem, i + 2)
                    v.tensor_copy(K.hgroup(i), K.bank[2 + u][:, 0:GT * C].rearrange("p (j c) -> p j c", j=GT))\
                        .then_inc(emb_r.sem, 1)


def late_weights(K, image):
    with K.nc.Block() as block:
        @block.sync
        def _(sp):
            for k in LATE:
                at, src, cols = K.starts[k]
                sp.dma_start(K.w[:, at:at + cols], image[:, src:src + cols]).then_inc(K.loaded[k], 16)


def store_stage(K, out):
    nc = K.nc
    done = K.count("stored")
    with nc.Block() as block:
        @block.sync
        def _(sp):
            o = out.rearrange("b (a p) c -> p (b a) c", p=P)
            for k in range(8):
                n = TILES // 8
                sp.dma_start(o[:, k * n:(k + 1) * n, :], K.h[:, k * n:(k + 1) * n, :]).then_inc(done.sem, 16)
            sp.wait_ge(done.sem, 128)


class Unit:

    def __init__(self, scores, masks, softs, outs, vw, dest):
        self.scores, self.masks, self.softs, self.outs, self.vw, self.dest = scores, masks, softs, outs, vw, dest
        self.cols = max(c + r * w for c, r, w in softs)
        self.rows = sum(r for _, r, _ in softs)


TB = (3, 4)
OB = (5, 6)
JB = (2, 7)


class Units:

    def __init__(self, K, ctx, units, bias=None, rownorm=None, piped=False):
        nc = K.nc
        self.K, self.sets, self.bias, self.rownorm, self.piped = K, units, bias, rownorm, piped
        self.N = len(units[0])
        self.SB, self.RP = ((0, 1), 2) if piped else ((0, 1, 2), 3)
        self.p = ctx.enter_context(nc.sbuf_tensor(f"probs_{nc.next_id()}", [P, self.RP, 512], F32))
        self.pT = ctx.enter_context(nc.sbuf_tensor(f"probsT_{nc.next_id()}", [P, 2, 512], F32))
        self.nm = ctx.enter_context(nc.sbuf_tensor(f"negmax_{nc.next_id()}", [P, 4, 4], F32))
        self.rd = ctx.enter_context(nc.sbuf_tensor(f"rden_{nc.next_id()}", [P, 2, 4], F32))
        if bias is not None:
            self.sb = ctx.enter_context(nc.sbuf_tensor(f"biased_{nc.next_id()}", [P, 4, 512], F32))
        names = ("scores_ready", "max_ready", "probs_ready", "probsT_in_psum", "probsT_ready", "values_summed", "normalised")
        self.sc, self.mx, self.ex, self.tp, self.tr, self.pv, self.no = (K.count(n) for n in names)
        self.vec = K.count("unit_vec")
        for c, credit in ((self.sc, 0), (self.mx, 0), (self.ex, 4), (self.tp, self.RP), (self.tr, 2), (self.pv, 2), (self.no, 2)):
            c.stage(self.N, credit)
        self.links = 1 + (bias is not None) + (rownorm is not None)
        self.vec.stage(self.N * self.links)

    def close(self, steps=0):
        for c, behind in ((self.sc, 0), (self.mx, 0), (self.ex, 0), (self.tp, 2), (self.tr, 2), (self.pv, 3), (self.no, 4)):
            c.close(GROUPS, max(0, steps - behind))
        self.vec.close(GROUPS)

    def open_pe(self, pe):
        pe.sem_inc(self.tp.sem, self.RP)
        pe.sem_inc(self.pv.sem, 2)

    def open_act(self, a):
        a.sem_inc(self.ex.sem, 4)
        a.sem_inc(self.tr.sem, 2)

    def open_vec(self, v):
        v.sem_inc(self.no.sem, 2)

    def unit(self, u, t):
        return self.sets[u % len(self.sets)][t] if t >= 0 else self.sets[(u + 1) % len(self.sets)][t]

    def pe_scores(self, pe, i, u, s):
        K, unit, nb = self.K, self.unit(u, s), len(self.SB)
        b = K.bank[self.SB[s % nb]]
        pe.wait_ge(self.ex.sem, self.ex.after(i, s - nb + 1))
        for n, (c, w, lhsT, rhs) in enumerate(unit.scores):
            ins = pe.matmul(b[:, c:c + w], lhsT, rhs, start=n == 0 or not unit.masks, stop=not unit.masks, skip_group_check=True)
        for n, (c, w, m) in enumerate(unit.masks):
            ins = pe.matmul(b[:, c:c + w], K.wb[:, 0, :], m, start=False, stop=True, skip_group_check=True)
        ins.then_inc(self.sc.sem, 1)

    def pe_turn(self, pe, i, u, t):
        K = self.K
        pe.wait_ge(self.ex.sem, self.ex.after(i, t + 1))
        pe.wait_ge(self.tr.sem, self.tr.after(i, t - 1))
        for c in range(0, self.unit(u, t).cols, P):
            ins = pe.transpose(K.bank[TB[t % 2]][:, c:c + P], self.p[:, t % self.RP, c:c + P], K.W("ident"))
        ins.then_inc(self.tp.sem, 1)

    def pe_values(self, pe, i, u, t):
        K, unit = self.K, self.unit(u, t)
        pe.wait_ge(self.tr.sem, self.tr.after(i, t + 1))
        pe.wait_ge(self.no.sem, self.no.after(i, t - 1))
        for n, terms in enumerate(unit.outs):
            for m, (blk, val) in enumerate(terms):
                ins = pe.matmul(K.bank[OB[t % 2]][:, n * unit.vw:(n + 1) * unit.vw], self.pT[:, t % 2, blk * P:(blk + 1) * P], val,
                                start=m == 0, stop=m == len(terms) - 1, skip_group_check=True)
        ins.then_inc(self.pv.sem, 1)

    def vec_max(self, v, i, u, s, lk):
        K, unit = self.K, self.unit(u, s)
        b = K.bank[self.SB[s % len(self.SB)]]
        v.wait_ge(self.sc.sem, self.sc.after(i, s + 1))
        v.wait_ge(self.ex.sem, self.ex.after(i, s - 3))
        src = b
        if self.bias is not None:
            lk(v.tensor_tensor(self.sb[:, s % 4, :], b[:, :], self.bias, ALU.add))
            src = self.sb[:, s % 4, :]
        r = 0
        for n, (c, k, w) in enumerate(unit.softs):
            ins = v.tensor_reduce(self.nm[:, s % 4, r:r + k], src[:, c:c + k * w].rearrange("p (a b) -> p a b", a=k),
                                  AX.X, ALU.max, negate=True)
            r += k
        ins.then_inc(self.mx.sem, 1)

    def vec_norm(self, v, i, u, t, lk):
        K, unit = self.K, self.unit(u, t)
        n = len(unit.outs)
        o = K.bank[OB[t % 2]][:, 0:n * unit.vw].rearrange("p (a c) -> p a c", c=unit.vw)
        v.wait_ge(self.pv.sem, self.pv.after(i, t + 1))
        lk(v.reciprocal(self.rd[:, t % 2, 0:n].rearrange("p (a c) -> p a c", c=1), o[:, :, unit.vw - 1:unit.vw]))
        if self.rownorm is not None:
            lk(v.tensor_tensor(self.rd[:, t % 2, 0:n], self.rd[:, t % 2, 0:n], self.rownorm(t % self.N, n), ALU.mult))
        v.tensor_tensor(unit.dest, o[:, :, 0:unit.vw - 1],
                        self.rd[:, t % 2, 0:n].rearrange("p (a c) -> p a c", c=1).to_broadcast([P, n, unit.vw - 1]), ALU.mult)\
            .then_inc(self.no.sem, 1)

    def act_exp(self, a, i, u, s):
        unit = self.unit(u, s)
        a.wait_ge(self.mx.sem, self.mx.after(i, s + 1))
        a.wait_ge(self.tp.sem, self.tp.after(i, s - self.RP + 1))
        src = self.K.bank[self.SB[s % len(self.SB)]] if self.bias is None else self.sb[:, s % 4, :]
        r = 0
        for c, k, w in unit.softs:
            for m in range(k):
                ins = a.activation(self.p[:, s % self.RP, c + m * w:c + (m + 1) * w], src[:, c + m * w:c + (m + 1) * w],
                                   ACT.Exp, bias=self.nm[:, s % 4, r:r + 1])
                r += 1
        ins.then_inc(self.ex.sem, 1)

    def act_move(self, a, i, u, t):
        a.wait_ge(self.tp.sem, self.tp.after(i, t + 1))
        a.wait_ge(self.pv.sem, self.pv.after(i, t - 1))
        n = self.unit(u, t).cols
        a.activation(self.pT[:, t % 2, 0:n], self.K.bank[TB[t % 2]][:, 0:n], ACT.Copy).then_inc(self.tr.sem, 1)

    def tensor(self, pe, i, splice):
        for s in range(self.N + 3):
            if s < self.N:
                self.pe_scores(pe, i, 0, s)
            if s in splice:
                splice[s](pe)
            if 0 <= s - 2 < self.N:
                self.pe_turn(pe, i, 0, s - 2)
            if 0 <= s - 3:
                self.pe_values(pe, i, 0, s - 3)

    def vector(self, v, i, splice):
        lk = link(v, self.vec, i, [0], self.K)
        for s in range(self.N + 4):
            if s < self.N:
                self.vec_max(v, i, 0, s, lk)
            if s in splice:
                splice[s](v)
            if s >= 4:
                self.vec_norm(v, i, 0, s - 4, lk)

    def scalar(self, a, i, splice):
        for s in range(self.N + 2):
            if s < self.N:
                self.act_exp(a, i, 0, s)
            if s in splice:
                splice[s](a)
            if s >= 2:
                self.act_move(a, i, 0, s - 2)


class Jobs:

    def __init__(self, K, front, proj, tail):
        self.K, self.front, self.np, self.nt = K, front, len(proj[0]), len(tail[0])
        self.jobs = [proj[u] + tail[u] for u in range(2)]
        self.ready = K.count("projection_ready")
        self.by = {"act": K.count("projection_moved_act"), "vec": K.count("projection_moved_vec")}
        who = [w for w, *_ in self.jobs[0]]
        self.who = who
        self.idx = [who[:k + 1].count(w) for k, w in enumerate(who)]
        self.early = {w: who[self.np:].count(w) for w in self.by}
        self.ready.stage(len(who), len(who))
        for w in self.by:
            self.by[w].stage(who.count(w), who.count(w))

    def close(self):
        for c in (self.ready, *self.by.values()):
            c.close(GROUPS)

    def value(self, cnt, b, n, early):
        return cnt.base + early + n if isinstance(b, int) else cnt.after(b, n)

    def open(self, eng, who):
        cnt, n = (self.ready, self.nt) if who == "pe" else (self.by[who], self.early[who])
        if n:
            eng.sem_inc(cnt.sem, n)

    def wait_moved(self, eng, b, k):
        w = self.who[k]
        eng.wait_ge(self.by[w].sem, self.value(self.by[w], b, self.idx[k], self.early[w]))

    def wait_proj(self, eng, b):
        for w in self.by:
            n = self.who[:self.np].count(w)
            if n:
                eng.wait_ge(self.by[w].sem, self.value(self.by[w], b, n, self.early[w]))

    def bank(self, k):
        return JB[(k + 1) % 2]

    def free(self, pe, b, k):
        nj = len(self.who)
        prev = k - 2
        if prev == -1:
            return
        if prev >= 0:
            self.wait_moved(pe, b, prev)
            return
        if isinstance(b, int):
            return
        last = [j for j in range(-1, nj) if self.bank(j) == self.bank(k)][-1]
        w = self.who[last]
        pe.wait_ge(self.by[w].sem, self.by[w].after(b, self.idx[last] - self.by[w].per))

    def tensor(self, pe, b, u, k):
        if k == -1:
            self.free(pe, b, k)
            self.front.transpose(pe, b + 1, self.bank(k))
            return
        if k == 0:
            pe.wait_ge(self.front.xt_r.sem, self.front.xt_r.after(b + 1, 1))
        self.free(pe, b, k)
        self.K.settle(pe)
        g, u = (b + 1, 1 - u) if k < self.np else (b, u)
        self.jobs[u][k][1](pe, self.K.bank[self.bank(k)], g).then_inc(self.ready.sem, 1)

    def move(self, eng, who, b, u, k):
        if k == -1:
            if who == "act":
                self.front.move(eng, b + 1, self.bank(k))
            return
        if self.who[k] == who:
            eng.wait_ge(self.ready.sem, self.value(self.ready, b, k + 1, self.nt))
            g, u = (b + 1, 1 - u) if k < self.np else (b, u)
            self.jobs[u][k][2](eng, self.K.bank[self.bank(k)], g).then_inc(self.by[who].sem, 1)


def piped_stage(K, load, front, r, make):
    nc = K.nc
    with ExitStack() as ctx:
        units, jobs, tail = make(ctx)
        N = units.N
        links = (r - 4) * units.links
        units.vec.stage(N * units.links, links)
        place = {}
        slots = [(s, n) for s in range(r, N) for n in range(3)][2:]
        place[(r, 0)] = [-1]
        spread = max(jobs.np, len(slots) - 3)
        for k in range(jobs.np):
            place.setdefault(slots[min(k * spread // jobs.np, len(slots) - 1)], []).append(k)
        for k in range(jobs.nt):
            n = k + 1 + tail.late + (k == jobs.nt - 1 and jobs.nt > 2)
            assert 4 + n // 3 < r
            place[(4 + n // 3, n % 3)] = [jobs.np + k]

        def body(step, b, u):
            for s in range(r, N):
                step(b, u, s, b, u)
            for s in range(r):
                step(b + 1, 1 - u, s, b, u)

        def run(eng, step, begin):
            begin()
            for s in range(r):
                step(0, 0, s, None, None)
            with eng.Fori(0, GROUPS // 2) as i0:
                body(step, i0 * 2, 0)
                body(step, i0 * 2 + 1, 1)

        block = ctx.enter_context(nc.Block())

        @block.tensor
        def _(pe):
            def job(b, u, s, n):
                for k in place.get((s, n), ()) if b is not None else ():
                    jobs.tensor(pe, b, u, k)

            def step(g, u, s, b, bu):
                if s == 0:
                    jobs.wait_proj(pe, -1 if b is None else b)
                units.pe_scores(pe, g, u, s)
                job(b, bu, s, 0)
                if b is not None or s >= 2:
                    units.pe_turn(pe, g, u, s - 2)
                job(b, bu, s, 1)
                if b is not None or s >= 3:
                    units.pe_values(pe, g, u, s - 3)
                job(b, bu, s, 2)

            def begin():
                pe.wait_ge(K.loaded[load], 16)
                front.open_pe(pe)
                units.open_pe(pe)
                jobs.open(pe, "pe")
                for k in range(-1, jobs.np):
                    jobs.tensor(pe, -1, 1, k)
            run(pe, step, begin)

        @block.vector
        def _(v):
            lk = [None]

            def step(g, u, s, b, bu):
                if b is None:
                    if s == 0:
                        lk[0] = link(v, units.vec, 0, [-links], K)
                elif s == r:
                    lk[0] = link(v, units.vec, b, [0], K)
                if s < r:
                    if s == 0:
                        front.statistics(v, g + 1)
                    if s == 1:
                        front.normalise(v, g + 1, 0)
                    if s == 2:
                        front.normalise(v, g + 1, 1)
                units.vec_max(v, g, u, s, lk[0])
                if b is not None and s < r and s in tail.vec_hooks:
                    tail.vec_hooks[s](v, b, bu)
                for n in range(3):
                    for k in place.get((s, n), ()) if b is not None else ():
                        jobs.move(v, "vec", b, bu, k)
                    if n == 0 and (b is not None or s >= 4):
                        units.vec_norm(v, g, u, s - 4, lk[0])

            def begin():
                v.wait_ge(K.loaded[load], 16)
                units.open_vec(v)
                jobs.open(v, "vec")
                front.statistics(v, 0)
                front.normalise(v, 0)
                for k in range(jobs.np):
                    jobs.move(v, "vec", -1, 1, k)
            run(v, step, begin)

        @block.scalar
        def _(a):
            def step(g, u, s, b, bu):
                if b is not None and s < r and s in tail.act_hooks:
                    tail.act_hooks[s](a, b, bu)
                units.act_exp(a, g, u, s)
                for n in range(3):
                    for k in place.get((s, n), ()) if b is not None else ():
                        jobs.move(a, "act", b, bu, k)
                    if n == 0 and (b is not None or s >= 2):
                        units.act_move(a, g, u, s - 2)

            def begin():
                a.wait_ge(K.loaded[load], 16)
                units.open_act(a)
                jobs.open(a, "act")
                for k in range(-1, jobs.np):
                    jobs.move(a, "act", -1, 1, k)
            run(a, step, begin)

        @block.gpsimd
        def _(g):
            front.rstds(g, 0)
            front.rstds(g, 1)
            with g.Fori(0, GROUPS) as i:
                front.rstds(g, i + 2)
        units.close(r)
        jobs.close()
        front.close(ahead=1)
        for c, per in tail.counts:
            c.close(GROUPS + per)


class PipedTail:
    late = 0
    """The heads' outputs of a group, projected and added to h, as jobs: transposes, 128 columns each; the product."""

    def __init__(self, K, ctx, osb, wo, bias, units, onto=None):
        nc = K.nc
        self.K, self.osb, self.wo, self.bias, self.units = K, osb, wo, bias, units
        self.onto = K.h if onto is None else onto
        self.width = osb[0].shape[2]
        self.nch, self.k = -(-self.width // P), min(P, self.width)
        self.oT = ctx.enter_context(nc.sbuf_tensor(f"outT_{nc.next_id()}", [P, self.nch, NTOK], F32))
        self.y = ctx.enter_context(nc.sbuf_tensor(f"out_{nc.next_id()}", [P, GT, C], F32)) if bias is not None else None
        self.vec = K.count("tail_vec")
        self.vec.stage(1 if bias is not None else 0)
        self.counts = [(self.vec, 0)]
        self.vec_hooks, self.act_hooks = {}, {}
        self.jobs = None

    def heads_ready(self, pe, g):
        pe.wait_ge(self.units.no.sem, self.units.no.after(g, self.units.N))

    def cols(self, j, width):
        return slice(j * width, (j + 1) * width)

    def list(self, u, width=C):
        def turn(c):
            def mm(pe, b, g):
                if c == 0:
                    self.heads_ready(pe, g)
                    self.K.settle(pe)
                for j in range(GT):
                    ins = pe.transpose(b[0:self.k, j * P:(j + 1) * P], self.osb[u][:, j, c * P:c * P + self.k], self.K.W("ident"))
                return ins
            return ("act", mm, lambda a, b, g: a.activation(self.oT[0:self.k, c, :], b[0:self.k, :], ACT.Copy))

        def product(pe, b, g):
            self.jobs.wait_moved(pe, g, self.jobs.np + self.nch - 1)
            self.K.settle(pe)
            for j in range(GT):
                for c in range(self.nch):
                    ins = pe.matmul(b[:, self.cols(j, width)], self.oT[0:self.k, c, j * P:(j + 1) * P],
                                    self.wo[0:self.k, c * width:(c + 1) * width], start=c == 0, stop=c == self.nch - 1, skip_group_check=True)
            return ins
        return [turn(c) for c in range(self.nch)] + [("vec", product, self.add)]

    def add(self, v, b, g):
        dest = self.onto[:, bass.ds(g * GT, GT), :]
        o = b[:, 0:GT * C].rearrange("p (j c) -> p j c", j=GT)
        if self.bias is None:
            return v.tensor_tensor(dest, dest, o, ALU.add)
        v.tensor_tensor(self.y[:, :, :], o, rows(self.bias, GT, C), ALU.add).then_inc(self.vec.sem, 1)
        v.wait_ge(self.vec.sem, self.vec.after(g, 1))
        self.K.settle(v)
        return v.tensor_tensor(dest, dest, self.y[:, :, :], ALU.add)


PB = (0, 1, 2, 7)


class Projections:

    def __init__(self, K, jobs):
        self.K, self.jobs = K, jobs
        self.ready, self.by = K.count("projection_ready"), {"act": K.count("projection_moved_act"), "vec": K.count("projection_moved_vec")}
        self.ready.stage(len(jobs))
        self.idx = []
        seen = {"act": 0, "vec": 0}
        for who, *_ in jobs:
            seen[who] += 1
            self.idx.append(seen[who])
        for who in seen:
            self.by[who].stage(seen[who])
        self.seen = seen

    def close(self):
        for c in (self.ready, *self.by.values()):
            c.close(GROUPS + 1)

    def tensor(self, pe, i):
        for j, (who, mm, _) in enumerate(self.jobs):
            if j >= len(PB):
                w = self.jobs[j - len(PB)][0]
                pe.wait_ge(self.by[w].sem, self.by[w].after(i, self.idx[j - len(PB)]))
            elif j == 0:
                for w, n in self.seen.items():
                    if n:
                        pe.wait_ge(self.by[w].sem, self.by[w].after(i, 0))
            self.K.settle(pe)
            mm(pe, self.K.bank[PB[j % 4]], i).then_inc(self.ready.sem, 1)

    def move(self, eng, who, i):
        for j, (w, _, mv) in enumerate(self.jobs):
            if w == who:
                eng.wait_ge(self.ready.sem, self.ready.after(i, j + 1))
                mv(eng, self.K.bank[PB[j % 4]], i).then_inc(self.by[who].sem, 1)

    def wait_moved(self, pe, i):
        for w, n in self.seen.items():
            if n:
                pe.wait_ge(self.by[w].sem, self.by[w].after(i, n))


def attention_stage(K, name, load, front, make):
    nc = K.nc
    with ExitStack() as ctx:
        units, proj, tail = make(ctx)
        block = ctx.enter_context(nc.Block())
        tail.stage()
        A0, A1, A2 = 0, min(2, units.N), min(4, units.N + 1)

        @block.tensor
        def _(pe):
            pe.wait_ge(K.loaded[load], 16)
            front.open_pe(pe)
            units.open_pe(pe)
            front.transpose(pe, 0, 7)
            pe.wait_ge(front.xt_r.sem, front.xt_r.after(0, 1))
            proj.tensor(pe, 0)
            with pe.Fori(0, GROUPS) as i:
                proj.wait_moved(pe, i)
                units.tensor(pe, i, {1: lambda e: tail.wait_free(e, i), A1: lambda e: front.transpose(e, i + 1, 7)})
                pe.wait_ge(front.xt_r.sem, front.xt_r.after(i + 1, 1))
                proj.tensor(pe, i + 1)
                tail.tensor(pe, i)

        @block.vector
        def _(v):
            v.wait_ge(K.loaded[load], 16)
            units.open_vec(v)
            tail.open_vec(v)
            front.statistics(v, 0)
            front.normalise(v, 0)
            proj.move(v, "vec", 0)
            front.statistics(v, 1)
            front.normalise(v, 1)
            with v.Fori(0, GROUPS) as i:
                units.vector(v, i, {A0: lambda e: front.statistics(e, i + 2), 1: lambda e: tail.early(e, i),
                                   A2: lambda e: front.normalise(e, i + 2)})
                proj.move(v, "vec", i + 1)
                tail.vector(v, i)

        @block.scalar
        def _(a):
            a.wait_ge(K.loaded[load], 16)
            units.open_act(a)
            front.move(a, 0, 7)
            proj.move(a, "act", 0)
            with a.Fori(0, GROUPS) as i:
                def move(e):
                    e.wait_ge(proj.ready.sem, proj.ready.after(i, len(proj.jobs)))
                    front.move(e, i + 1, 7)
                units.scalar(a, i, {A1 + 1: move})
                proj.move(a, "act", i + 1)
                tail.scalar(a, i)

        @block.gpsimd
        def _(g):
            front.rstds(g, 0)
            front.rstds(g, 1)
            with g.Fori(0, GROUPS) as i:
                front.rstds(g, i + 2)
                tail.gpsimd(g, i)
        units.close()
        proj.close()
        front.close(ahead=1)
        tail.close()


def late_tail_stage(K, load, front, make):
    nc = K.nc
    with ExitStack() as ctx:
        units, proj, tail = make(ctx)
        block = ctx.enter_context(nc.Block())
        tail.stage()

        @block.tensor
        def _(pe):
            def body(i, last):
                proj.wait_moved(pe, i)
                units.pe_scores(pe, i, 0, 0)
                units.pe_scores(pe, i, 0, 1)
                front.transpose(pe, i + 1, 7)
                if last is not None:
                    tail.tensor(pe, last)
                for t in range(2):
                    units.pe_turn(pe, i, 0, t)
                for t in range(2):
                    units.pe_values(pe, i, 0, t)
                pe.wait_ge(tail.mvd.sem, tail.mvd.after(i, 0))
                pe.wait_ge(front.xt_r.sem, front.xt_r.after(i + 1, 1))
                proj.tensor(pe, i + 1)
            pe.wait_ge(K.loaded[load], 16)
            front.open_pe(pe)
            units.open_pe(pe)
            front.transpose(pe, 0, 7)
            pe.wait_ge(front.xt_r.sem, front.xt_r.after(0, 1))
            proj.tensor(pe, 0)
            body(0, None)
            with pe.Fori(0, GROUPS - 1) as last:
                body(last + 1, last)
            proj.wait_moved(pe, GROUPS)
            tail.tensor(pe, GROUPS - 1)

        @block.vector
        def _(v):
            def body(i, last):
                lk = link(v, units.vec, i, [0], K)
                for s in range(2):
                    units.vec_max(v, i, 0, s, lk)
                front.statistics(v, i + 2)
                if last is not None:
                    tail.vector(v, last)
                front.normalise(v, i + 2)
                for t in range(2):
                    units.vec_norm(v, i, 0, t, lk)
                proj.move(v, "vec", i + 1)
            v.wait_ge(K.loaded[load], 16)
            units.open_vec(v)
            tail.open_vec(v)
            front.statistics(v, 0)
            front.normalise(v, 0)
            proj.move(v, "vec", 0)
            front.statistics(v, 1)
            front.normalise(v, 1)
            body(0, None)
            with v.Fori(0, GROUPS - 1) as last:
                body(last + 1, last)
            tail.vector(v, GROUPS - 1)

        @block.scalar
        def _(a):
            def body(i, last):
                a.wait_ge(proj.ready.sem, proj.ready.after(i, len(proj.jobs)))
                front.move(a, i + 1, 7)
                units.act_exp(a, i, 0, 0)
                if last is not None:
                    tail.scalar(a, last)
                units.act_exp(a, i, 0, 1)
                for t in range(2):
                    units.act_move(a, i, 0, t)
                proj.move(a, "act", i + 1)
            a.wait_ge(K.loaded[load], 16)
            units.open_act(a)
            front.move(a, 0, 7)
            proj.move(a, "act", 0)
            body(0, None)
            with a.Fori(0, GROUPS - 1) as last:
                body(last + 1, last)
            tail.scalar(a, GROUPS - 1)

        @block.gpsimd
        def _(g):
            for n in range(3):
                front.rstds(g, n)
            with g.Fori(0, GROUPS - 1) as last:
                front.rstds(g, last + 3, (0,))
                tail.gpsimd(g, last)
                front.rstds(g, last + 3, (1,))
            tail.gpsimd(g, GROUPS - 1)
        units.close()
        proj.close()
        front.close(ahead=1)
        tail.close()


class OutTail:

    def __init__(self, K, ctx, osb, wo, bias, post_norm=None, onto=None, bank=3):
        nc = K.nc
        self.onto = K.h if onto is None else onto
        self.bank = bank
        self.K, self.osb, self.wo, self.bias, self.post_norm = K, osb, wo, bias, post_norm
        self.width = osb.shape[2]
        self.nch = -(-self.width // P)
        self.k = min(P, self.width)
        self.oT = ctx.enter_context(nc.sbuf_tensor(f"outT_{nc.next_id()}", [P, self.nch, NTOK], F32))
        self.y = ctx.enter_context(nc.sbuf_tensor(f"out_{nc.next_id()}", [P, GT, C], F32))
        names = ("outT_in_psum", "outT_ready", "out_in_psum", "out_moved", "tail_vec", "tail_stats", "tail_pool", "tail_rstd")
        self.tps, self.tr, self.ops, self.mvd, self.vec, self.st, self.pool, self.rs = (K.count(n) for n in names)
        self.units, self.more = None, []

    def stage(self):
        for c, per in ((self.tps, self.nch), (self.tr, self.nch), (self.ops, 1), (self.mvd, 1),
                       (self.vec, 4 if self.post_norm else 0), (self.st, 1), (self.pool, 1), (self.rs, 1)):
            if self.post_norm or c not in (self.st, self.pool, self.rs):
                c.stage(per, int(c is self.mvd))

    def close(self):
        for c in (self.tps, self.tr, self.ops, self.mvd, self.vec, self.st, self.pool, self.rs):
            c.close(GROUPS)
        for c, groups in self.more:
            c.close(groups)

    def open_vec(self, v):
        v.sem_inc(self.mvd.sem, 1)

    def early(self, v, i):
        pass

    def wait_free(self, pe, i):
        pe.wait_ge(self.mvd.sem, self.mvd.after(i, 0))

    def tensor(self, pe, i):
        K = self.K
        pe.wait_ge(self.units.no.sem, self.units.no.after(i, self.units.N))
        K.settle(pe)
        for c in range(self.nch):
            for j in range(GT):
                ins = pe.transpose(K.bank[self.bank + c][0:self.k, j * P:(j + 1) * P], self.osb[:, j, c * P:c * P + self.k], K.W("ident"))
            ins.then_inc(self.tps.sem, 1)
        pe.wait_ge(self.tr.sem, self.tr.after(i, self.nch))
        K.settle(pe)
        for j in range(GT):
            for c in range(self.nch):
                ins = pe.matmul(K.bank[self.bank][:, j * C:(j + 1) * C], self.oT[0:self.k, c, j * P:(j + 1) * P],
                                self.wo[0:self.k, c * C:(c + 1) * C], start=c == 0, stop=c == self.nch - 1, skip_group_check=True)
        ins.then_inc(self.ops.sem, 1)

    def scalar(self, a, i):
        for c in range(self.nch):
            a.wait_ge(self.tps.sem, self.tps.after(i, c + 1))
            a.activation(self.oT[0:self.k, c, :], self.K.bank[self.bank + c][0:self.k, :], ACT.Copy).then_inc(self.tr.sem, 1)

    def vector(self, v, i):
        K, y = self.K, self.y
        lk = link(v, self.vec, i, [0], self.K)
        v.wait_ge(self.ops.sem, self.ops.after(i, 1))
        o = K.bank[self.bank][:, 0:GT * C].rearrange("p (j c) -> p j c", j=GT)
        dest = self.onto[:, bass.ds(i * GT, GT), :]
        if self.bias is None:
            v.tensor_tensor(dest, dest, o, ALU.add).then_inc(self.mvd.sem, 1)
            return
        v.tensor_tensor(y[:, :, :], o, rows(self.bias, GT, C), ALU.add).then_inc(self.mvd.sem, 1)
        v.wait_ge(self.mvd.sem, self.mvd.after(i, 1))
        if self.post_norm:
            eps, g, b, bnst, mv, rstd, _ = self.post_norm
            for j in range(GT):
                ins = v.bn_stats(bnst[:, j, :], y[:, j, :])
            lk(ins, settle=True)
            for j in range(GT):
                ins = v.bn_aggr(mv[:, j, :], bnst[:, j, :])
            ins.then_inc(self.st.sem, 1)
            v.wait_ge(self.rs.sem, self.rs.after(i, 1))
            for j in range(GT):
                ins = v.tensor_scalar(y[:, j, :], y[:, j, :], mv[:, j, 0:1], rstd[:, j:j + 1], ALU.subtract, ALU.mult)
            lk(ins)
            lk(v.tensor_tensor(y[:, :, :], y[:, :, :], rows(g, GT, C), ALU.mult))
            lk(v.tensor_tensor(y[:, :, :], y[:, :, :], rows(b, GT, C), ALU.add))
        v.tensor_tensor(dest, dest, y[:, :, :], ALU.add)

    def gpsimd(self, g, i):
        if self.post_norm:
            eps, _, _, _, mv, rstd, work = self.post_norm
            g.wait_ge(self.st.sem, self.st.after(i, 1))
            self.K.settle(g)
            g.tensor_scalar(work, mv[:, :, 1], eps, None, ALU.add).then_inc(self.pool.sem, 1)
            g.wait_ge(self.pool.sem, self.pool.after(i, 1))
            g.tensor_tensor(rstd, work, self.K.half[:, 0:GT], ALU.pow).then_inc(self.rs.sem, 1)


def values(ctx, nc, heads, d):
    return ctx.enter_context(nc.sbuf_tensor(f"values_{nc.next_id()}", [P, GT, heads, d + 1], F32))


def prepare(K, ones=(), zeros=()):
    with K.nc.Block() as block:
        @block.vector
        def _(v):
            for t in ones:
                v.memset(t, 1.0)
            for t in zeros:
                v.memset(t, 0.0)


def first_attention(K):
    nc = K.nc
    front = Front(K, "lnln", (1e-5, 1e-5), scale=K.W("a0_lnw")[:, 0:1], bias=K.W("a0_lnw")[:, 1:2])

    def make(ctx):
        qT = ctx.enter_context(nc.sbuf_tensor("a0_qT", [P, NTOK], F32))
        kT = ctx.enter_context(nc.sbuf_tensor("a0_kT", [P, NTOK], F32))
        vt = values(ctx, nc, 1, C)
        osb = ctx.enter_context(nc.sbuf_tensor("a0_o_sb", [P, GT, C], F32))
        post = (1e-5, K.W("a0_g2"), K.W("a0_b2"), ctx.enter_context(nc.sbuf_tensor("a0_bn", [P, GT, 6], F32)),
                ctx.enter_context(nc.sbuf_tensor("a0_mv", [P, GT, 2], F32)),
                ctx.enter_context(nc.sbuf_tensor("a0_rstd", [P, GT], F32))[:, :], 
                ctx.enter_context(nc.sbuf_tensor("a0_work", [P, GT], F32))[:, :])
        prepare(K, [vt[:, :, :, C:C + 1]], [qT[C:P, :], kT[C:P, :]])
        x = K.xU[:, :]
        jobs = [
            ("act", lambda pe, b, i: pe.matmul(b[0:C, :], K.W("a0_qk")[:, 0:C], x, start=True, stop=True),
             lambda a, b, i: a.activation(qT[0:C, :], b[0:C, :], ACT.Identity, bias=K.W("a0_qkb", 0, C)[:, 0:1])),
            ("vec", lambda pe, b, i: pe.matmul(b[0:C, :], K.W("a0_qk")[:, C:2 * C], x, start=True, stop=True),
             lambda v, b, i: v.tensor_scalar(kT[0:C, :], b[0:C, :], K.W("a0_qkb", 0, C)[:, 1:2], None, ALU.add)),
            ("vec", lambda pe, b, i: [pe.matmul(b[:, j * C:(j + 1) * C], K.xU[:, j * P:(j + 1) * P], K.W("a0_v"),
                                                start=True, stop=True) for j in range(GT)][-1],
             lambda v, b, i: v.tensor_tensor(vt[:, :, 0, 0:C], b[:, 0:GT * C].rearrange("p (j c) -> p j c", j=GT),
                                             rows(K.W("a0_vb"), GT, C), ALU.add)),
        ]
        us = []
        for s in range(2):
            us.append(Unit([(qb * SEQ, SEQ, qT[:, s * SEQ + qb * P:s * SEQ + (qb + 1) * P], kT[:, s * SEQ:(s + 1) * SEQ])
                            for qb in range(2)], [], [(0, 2, SEQ)],
                           [[(2 * qb + kb, vt[:, 2 * s + kb, 0, :]) for kb in range(2)] for qb in range(2)],
                           C + 1, osb[:, 2 * s:2 * s + 2, :]))
        units = Units(K, ctx, [us], bias=K.W("a0_bias"), rownorm=lambda t, n: K.W("a0_scale").to_broadcast([P, n]))
        tail = OutTail(K, ctx, osb, K.W("a0_o"), K.W("a0_ob"), post, bank=2)
        tail.units = units
        return units, Projections(K, jobs), tail
    late_tail_stage(K, 0, front, make)


def second_attention(K):
    nc = K.nc
    front = Front(K, "ln", (1e-5,))

    def make(ctx):
        H = 8
        qT = ctx.enter_context(nc.sbuf_tensor("a1_qT", [P, 4, NTOK], F32))
        kT = ctx.enter_context(nc.sbuf_tensor("a1_kT", [P, 2, 4, NTOK], F32))
        vt = values(ctx, nc, H, C)
        osb = ctx.enter_context(nc.sbuf_tensor("a1_o_sb", [P, GT, H * C], F32))
        prepare(K, [vt[:, :, :, C:C + 1]], [kT[C:P, 0, :, :], kT[0:C, 1, :, :]])
        x = K.xU[:, :]

        def qjob(c):
            return ("vec", lambda pe, b, i: pe.matmul(b[:, :], K.W("a1_q")[:, c * P:(c + 1) * P], x, start=True, stop=True),
                    lambda v, b, i: v.tensor_scalar(qT[:, c, :], b[:, :], K.W("a1_qb")[:, c:c + 1], 0.125, ALU.add, ALU.mult))

        def kjob(c):
            return ("act", lambda pe, b, i: pe.matmul(b[:, :], K.W("a1_k")[:, c * P:(c + 1) * P], x, start=True, stop=True),
                    lambda a, b, i: [a.activation(kT[r, p, c, :], b[r, :], ACT.Identity, bias=K.W("a1_kb")[r, c:c + 1])
                                     for p, r in enumerate((slice(0, C), slice(C, P)))][-1])

        def vjob(j):
            return ("vec", lambda pe, b, i: pe.matmul(b[:, :], K.xU[:, j * P:(j + 1) * P], K.W("a1_v"), start=True, stop=True),
                    lambda v, b, i: v.tensor_tensor(vt[:, j, :, 0:C], b[:, :].rearrange("p (h c) -> p h c", h=H),
                                                    K.W("a1_vb").rearrange("p (h c) -> p h c", h=H), ALU.add))
        jobs = [f(c) for c in range(4) for f in (qjob, kjob, vjob)]
        o5 = osb[:, :, :].rearrange("p j (m a c) -> p j m a c", m=4, a=2)
        us, q0 = [], []
        strict4 = K.wb[:, 1:5, :].rearrange("p a c -> p (a c)")
        strict = K.wb[:, 1, :]
        for s in range(2):
            t0 = s * SEQ
            for p in range(2):
                us.append(Unit([(P * m, P, qT[:, m, t0:t0 + P], kT[:, p, m, t0:t0 + P]) for m in range(4)], [(0, 512, strict4)],
                               [(0, 4, P)], [[(m, vt[:, 2 * s, 2 * m + p, :])] for m in range(4)], C + 1, o5[:, 2 * s, :, p, :]))
                q0.append(0)
                for mp in range(2):
                    us.append(Unit([(SEQ * a, SEQ, qT[:, 2 * mp + a, t0 + P:t0 + SEQ], kT[:, p, 2 * mp + a, t0:t0 + SEQ]) for a in range(2)],
                                   [(SEQ * a + P, P, strict) for a in range(2)], [(0, 2, SEQ)],
                                   [[(2 * a + kb, vt[:, 2 * s + kb, 2 * (2 * mp + a) + p, :]) for kb in range(2)] for a in range(2)],
                                   C + 1, o5[:, 2 * s + 1, 2 * mp:2 * mp + 2, p, :]))
                    q0.append(1)
        units = Units(K, ctx, [us], rownorm=lambda t, n: K.W("row0")[:, q0[t]:q0[t] + 1].to_broadcast([P, n]))
        tail = OutTail(K, ctx, osb, K.W("a1_o"), K.W("a1_ob"))
        tail.units = units
        return units, Projections(K, jobs), tail
    attention_stage(K, "a1", 2, front, make)


def second_routed_attention(K, x1):
    nc = K.nc
    front = Front(K, "lnrms", (1e-5, 1e-6), scale=K.W("r2_ln"), kept=x1)

    def make(ctx):
        H, HK, D = 4, 2, 16
        qT, kT, vt, osb = [], [], [], []
        for u in range(2):
            qT.append(ctx.enter_context(nc.sbuf_tensor(f"r2_qT{u}", [P, NTOK], F32)))
            kT.append(ctx.enter_context(nc.sbuf_tensor(f"r2_kT{u}", [P, 4, NTOK], F32)))
            vt.append(values(ctx, nc, HK, D))
            osb.append(ctx.enter_context(nc.sbuf_tensor(f"r2_o_sb{u}", [P, GT, C], F32)))
        t1 = ctx.enter_context(nc.sbuf_tensor("r2_t1", [P, 2, NTOK], F32))
        t2 = ctx.enter_context(nc.sbuf_tensor("r2_t2", [P, 2, NTOK], F32))
        prepare(K, [vt[u][:, :, :, D:D + 1] for u in range(2)], [kT[u][:, :, :] for u in range(2)])
        rope = K.count("rotary_part")
        rope.stage(2)

        def pair(ap):
            return ap.rearrange("p (s t) -> p s t", s=2)

        def table(name):
            return K.W(name).rearrange("p (s t) -> p s t", s=1).to_broadcast([P, 2, SEQ])

        def plain(w, tab, n):
            return ("vec", lambda pe, b, i: pe.matmul(b[:, :], K.W(w), K.xU[:, :], start=True, stop=True),
                    lambda v, b, i: v.tensor_tensor(pair(t1[:, n, :]), pair(b[:, :]), table(tab), ALU.mult))

        def turned(w, tab, dst, n):
            def mv(v, b, i):
                v.tensor_tensor(pair(t2[:, n, :]), pair(b[:, :]), table(tab), ALU.mult).then_inc(rope.sem, 1)
                v.wait_ge(rope.sem, rope.after(i, n + 1))
                for out, r in dst:
                    ins = v.tensor_tensor(out, t1[r, n, :], t2[r, n, :], ALU.add)
                return ins
            return ("vec", lambda pe, b, i: pe.matmul(b[:, :], K.W(w), K.xU[:, :], start=True, stop=True), mv)

        def proj(u):
            quads = [slice(32 * n, 32 * n + 32) for n in range(H)]
            return [plain("r2_k", "r2_ck", 0), turned("r2_kp", "r2_sk", [(kT[u][r, n, :], r) for n, r in enumerate(quads)], 0),
                    plain("r2_q", "r2_cq", 1), turned("r2_qp", "r2_sq", [(qT[u][:, :], slice(0, P))], 1),
                    ("act", lambda pe, b, i: [pe.matmul(b[:, j * 32:(j + 1) * 32], K.xU[:, j * P:(j + 1) * P], K.W("r2_v"),
                                                        start=True, stop=True) for j in range(GT)][-1],
                     lambda a, b, i: a.activation(vt[u][:, :, :, 0:D], b[:, 0:GT * 32].rearrange("p (j h c) -> p j h c", j=GT, h=HK),
                                                  ACT.Copy))]
        sets = [[], []]
        causal = K.wb[:, 5, :]
        for u in range(2):
            q, k, v = qT[u], kT[u], vt[u]
            for s in range(2):
                t0 = s * SEQ
                for n in range(H):
                    g = n // (H // HK)
                    sets[u].append(Unit([(0, P, q[:, t0:t0 + P], k[:, n, t0:t0 + P]), (P, SEQ, q[:, t0 + P:t0 + SEQ], k[:, n, t0:t0 + SEQ])],
                                        [(0, P, causal), (SEQ, P, causal)], [(0, 1, P), (P, 1, SEQ)],
                                        [[(0, v[:, 2 * s, g, :])], [(1, v[:, 2 * s, g, :]), (2, v[:, 2 * s + 1, g, :])]],
                                        D + 1, osb[u][:, 2 * s:2 * s + 2, n * D:(n + 1) * D]))
        units = Units(K, ctx, sets, piped=True)
        tail = PipedTail(K, ctx, osb, K.W("r2_o"), None, units, onto=x1)
        tail.counts.append((rope, 1))
        tail.jobs = Jobs(K, front, [proj(u) for u in range(2)], [tail.list(u) for u in range(2)])
        return units, tail.jobs, tail
    piped_stage(K, 5, front, 5, make)


class GateTail(PipedTail):
    late = 3

    def __init__(self, K, ctx, qo, sx, mixed, units):
        super().__init__(K, ctx, [q.rearrange("p j n e d -> p j (n e d)") for q in qo], K.W("f1_g"), None, units)
        nc = K.nc
        self.qo, self.sx, self.mixed = qo, sx, mixed
        self.padm = ctx.enter_context(nc.sbuf_tensor("f1_not_padded", [P, GT * C], F32))
        self.lg = ctx.enter_context(nc.sbuf_tensor("f1_gate", [P, GT * 16], F32))
        self.m = ctx.enter_context(nc.sbuf_tensor("f1_gate_work", [P, GT * 4], F32))
        self.masked, self.shifted, self.exps = K.count("pads_zeroed"), K.count("gate_shifted"), K.count("gate_exps")
        self.vec.stage(6)
        for c in (self.masked, self.shifted, self.exps):
            c.stage(1)
            self.counts.append((c, 0))
        self.vec_hooks = {4: self.mask, 7: self.shift, 8: self.gates, 9: self.weigh, 10: self.mix}
        self.act_hooks = {8: self.exp}

    def heads_ready(self, pe, g):
        pe.wait_ge(self.masked.sem, self.masked.after(g, 1))

    def link(self, v, g, done):
        return link(v, self.vec, g, [done], self.K)

    def over(self, t, e):
        return t.rearrange("p (a c) -> p a c", c=1).to_broadcast([P, t.shape[1], e])

    def four(self):
        return self.lg[:, :].rearrange("p (a c) -> p a c", c=4)

    def mask(self, v, g, u):
        lk = self.link(v, g, 0)
        self.jobs.wait_proj(v, g)
        v.wait_ge(self.units.no.sem, self.units.no.after(g, self.units.N))
        lk(v.tensor_scalar(self.padm[:, :].rearrange("p (j c) -> p j c", j=GT), self.sx[:, bass.ds(g * GT, GT), :], 0.0, None,
                           ALU.not_equal))
        q4 = self.qo[u][:, :, :, :, :].rearrange("p j n e d -> p (j n) e d")
        v.tensor_tensor(q4, q4, self.padm[:, :].rearrange("p (a b d) -> p a b d", b=1, d=16).to_broadcast([P, GT * 4, 4, 16]), ALU.mult)\
            .then_inc(self.masked.sem, 1)

    def add(self, v, b, g):
        return v.tensor_tensor(self.lg[:, :].rearrange("p (j c) -> p j c", j=GT), b[:, 0:GT * 16].rearrange("p (j c) -> p j c", j=GT),
                               rows(self.K.W("f1_gb"), GT, 16), ALU.add)

    def shift(self, v, g, u):
        lk = self.link(v, g, 1)
        self.jobs.wait_moved(v, g, self.jobs.np + self.nch)
        self.K.settle(v)
        lk(v.tensor_reduce(self.m[:, :], self.four(), AX.X, ALU.max))
        v.tensor_tensor(self.four(), self.four(), self.over(self.m[:, :], 4), ALU.subtract).then_inc(self.shifted.sem, 1)

    def exp(self, a, g, u):
        a.wait_ge(self.shifted.sem, self.shifted.after(g, 1))
        a.activation(self.lg[:, :], self.lg[:, :], ACT.Exp).then_inc(self.exps.sem, 1)

    def gates(self, v, g, u):
        lk = self.link(v, g, 2)
        v.wait_ge(self.exps.sem, self.exps.after(g, 1))
        self.K.settle(v)
        lk(v.tensor_reduce(self.m[:, :], self.four(), AX.X, ALU.add))
        lk(v.reciprocal(self.m[:, :], self.m[:, :]))
        lk(v.tensor_tensor(self.four(), self.four(), self.over(self.m[:, :], 4), ALU.mult))

    def weigh(self, v, g, u):
        lk = self.link(v, g, 5)
        qe = self.qo[u][:, :, :, :, :].rearrange("p j n e d -> p (j n e) d")
        lk(v.tensor_tensor(qe, qe, self.over(self.lg[:, :], 16), ALU.mult))

    def mix(self, v, g, u):
        v.tensor_reduce(self.mixed[:, bass.ds(g * GT, GT), :].rearrange("p j (n d) -> p (j n) d", n=4),
                        self.qo[u][:, :, :, :, :].rearrange("p j n e d -> p (j n) d e"), AX.X, ALU.add)


def expert_heads(K):
    nc = K.nc
    with ExitStack() as ctx:
        sx = ctx.enter_context(nc.sbuf_tensor("head_features", [P, TILES + GT, C], F32))
        mixed = ctx.enter_context(nc.sbuf_tensor("mixed", [P, TILES, C], F32))
        expert_attention(K, sx, mixed)
        head_feed_forward(K, sx, mixed)


def expert_attention(K, sx, mixed):
    nc = K.nc
    front = Front(K, "ln", (1e-5,))

    def make(ctx):
        H, D, E = 4, 16, 4
        sxT = ctx.enter_context(nc.sbuf_tensor("f1_sxT", [P, NTOK], F32))
        qT, kT, vt, qo = [], [], [], []
        for u in range(2):
            qT.append(ctx.enter_context(nc.sbuf_tensor(f"f1_qT{u}", [P, E, NTOK], F32)))
            kT.append(ctx.enter_context(nc.sbuf_tensor(f"f1_kT{u}", [P, H, NTOK], F32)))
            vt.append(values(ctx, nc, H, D))
            qo.append(ctx.enter_context(nc.sbuf_tensor(f"f1_qo{u}", [P, GT, H, E, D], F32)))
        prepare(K, [vt[u][:, :, :, D:D + 1] for u in range(2)], [sxT[C:P, :]] + [kT[u][:, :, :] for u in range(2)])
        jobs = [None]

        def heads(pe, i):
            jobs[0].wait_moved(pe, i - 1, 0)
            K.settle(pe)

        def qjob(u, e):
            def mm(pe, b, i):
                heads(pe, i)
                return pe.matmul(b[:, :], K.W("f1_q")[:, e * P:(e + 1) * P], sxT[:, :], start=True, stop=True)
            if e % 2:
                return ("act", mm, lambda a, b, i: a.activation(qT[u][:, e, :], b[:, :], ACT.Copy, scale=4.0))
            return ("vec", mm, lambda v, b, i: v.tensor_scalar(qT[u][:, e, :], b[:, :], 4.0, None, ALU.mult))

        def kproduct(pe, b, i):
            heads(pe, i)
            return pe.matmul(b[:, :], K.W("f1_k"), sxT[:, :], start=True, stop=True)

        def vproduct(pe, b, i):
            heads(pe, i)
            return [pe.matmul(b[:, j * C:(j + 1) * C], sxT[:, j * P:(j + 1) * P], K.W("f1_v"), start=True, stop=True) for j in range(GT)][-1]

        def proj(u):
            return [
                ("act", lambda pe, b, i: pe.matmul(b[0:C, :], K.W("f1_hl"), K.xU[:, :], start=True, stop=True),
                 lambda a, b, i: a.activation(sxT[0:C, :], b[0:C, :], ACT.Identity, bias=K.W("f1_hlb", 0, C))),
                ("vec", lambda pe, b, i: [pe.matmul(b[:, j * C:(j + 1) * C], K.xU[:, j * P:(j + 1) * P], K.W("f1_hl"),
                                                    start=True, stop=True) for j in range(GT)][-1],
                 lambda v, b, i: v.tensor_tensor(sx[:, bass.ds(i * GT, GT), :], b[:, 0:GT * C].rearrange("p (j c) -> p j c", j=GT),
                                                 rows(K.W("f1_hlbr"), GT, C), ALU.add)),
                *[qjob(u, e) for e in range(E)],
                ("act", kproduct, lambda a, b, i: [a.activation(kT[u][32 * n:32 * n + 32, n, :], b[32 * n:32 * n + 32, :], ACT.Copy)
                                                   for n in range(H)][-1]),
                ("vec", vproduct, lambda v, b, i: v.tensor_copy(vt[u][:, :, :, 0:D], b[:, 0:GT * C].rearrange("p (j h c) -> p j h c", j=GT, h=H))),
            ]
        causal4 = K.wb[:, 5:9, :].rearrange("p a c -> p (a c)")
        causal = K.wb[:, 5, :]
        sets = [[], []]
        for u in range(2):
            q, k, v = qT[u], kT[u], vt[u]
            for s in range(2):
                t0 = s * SEQ
                for n in range(H):
                    sets[u].append(Unit([(e * P, P, q[:, e, t0:t0 + P], k[:, n, t0:t0 + P]) for e in range(E)], [(0, 512, causal4)],
                                        [(0, E, P)], [[(e, v[:, 2 * s, n, :])] for e in range(E)], D + 1, qo[u][:, 2 * s, n, :, :]))
                    for p in range(2):
                        sets[u].append(Unit([(a * SEQ, SEQ, q[:, 2 * p + a, t0 + P:t0 + SEQ], k[:, n, t0:t0 + SEQ]) for a in range(2)],
                                            [(a * SEQ + P, P, causal) for a in range(2)], [(0, 2, SEQ)],
                                            [[(2 * a + kb, v[:, 2 * s + kb, n, :]) for kb in range(2)] for a in range(2)],
                                            D + 1, qo[u][:, 2 * s + 1, n, 2 * p:2 * p + 2, :]))
        units = Units(K, ctx, sets, piped=True)
        tail = GateTail(K, ctx, qo, sx, mixed, units)
        jobs[0] = tail.jobs = Jobs(K, front, [proj(u) for u in range(2)], [tail.list(u, 16) for u in range(2)])
        return units, tail.jobs, tail
    piped_stage(K, 3, front, 12, make)


def head_feed_forward(K, sx, mixed):
    nc = K.nc
    H, D, FT, U = 4, 16, 8, 2
    STEPS, N, R = TILES // (FT * U), FT * C, FT * 4
    streams = range(U)
    with ExitStack() as ctx:
        def sb(n, s):
            return [ctx.enter_context(nc.sbuf_tensor(f"ff_{n}{u}", s, F32)) for u in streams]
        fx, y, sq, npm = (sb(n, [P, N]) for n in ("fx", "y", "square", "not_zero"))
        fxT, h1, npmT = (sb(n, [P, FT * P]) for n in ("fxT", "hidden", "not_zeroT"))
        mean, var, work, rstd, fg, m = (sb(n, [P, R]) for n in ("mean", "var", "work", "rstd", "gate", "gate_work"))
        resid = ctx.enter_context(nc.sbuf_tensor("ff_resid", [P, 2, C], F32))
        half = ctx.enter_context(nc.sbuf_tensor("ff_minus_half", [P, R], F32))
        names = ("ff_vec", "norm_stats", "norm_pool", "norm_rstd", "fx_ready", "fxT_in_psum", "fxT_ready", "not_zeroT", "hidden1_in_psum",
                 "hidden1_moved", "hidden1_ready", "layers_in_psum", "fout_ready", "foutT_in_psum", "foutT_ready", "head_gate_in_psum",
                 "head_gate_shifted", "head_gate_exps")
        counts = [[K.count(n + str(u)) for u in streams] for n in names]
        (vec, st, pl, rs, fr, ftp, ftr, nzt, h1p, h1m, h1r, zp, fo, fop, fot, gp, gsh, gex) = counts
        hs = K.count("halves_set")
        VEC = 25
        for both, per in zip(counts, (VEC, 2, 2, 2, 1, 1, 1, 1, 2, 2, 1, 1, 1, 1, 1, 1, 1, 1)):
            for c in both:
                c.stage(per, 0)
        block = ctx.enter_context(nc.Block())
        r3 = (lambda t: t.rearrange("p (a d) -> p a d", d=D))
        over = (lambda t, n: t.rearrange("p (a c) -> p a c", c=1).to_broadcast([P, t.shape[1], n]))
        row16 = (lambda name: rows(K.W(name), R, D))

        @block.vector
        def _(v):
            v.wait_ge(hs.sem, hs.base + 1)
            for u in streams:
                v.memset(fxT[u][C:P, :], 0.0)
                v.memset(h1[u][C:P, :], 0.0)
            for n in range(H):
                ins = v.tensor_copy(resid[:, :, n * D:(n + 1) * D], sx[:, 2 * n:2 * n + 2, n * D:(n + 1) * D])
            ins.then_inc(hs.sem, 1)
            v.wait_ge(hs.sem, hs.base + 2)

            def stream(i, u):
                done = [0]

                def lk(ins):
                    done[0] += 1
                    ins.then_inc(vec[u].sem, 1)
                    yield
                    v.wait_ge(vec[u].sem, vec[u].after(i, done[0]))

                def norm(t, g, b, k):
                    yield from lk(v.tensor_reduce(mean[u][:, :], r3(t[:, :]), AX.X, ALU.add))
                    yield from lk(v.tensor_scalar(mean[u][:, :], mean[u][:, :], 1.0 / D, None, ALU.mult))
                    yield from lk(v.tensor_tensor(r3(t[:, :]), r3(t[:, :]), over(mean[u][:, :], D), ALU.subtract))
                    yield from lk(v.tensor_tensor(sq[u][:, :], t[:, :], t[:, :], ALU.mult))
                    yield from lk(v.tensor_reduce(var[u][:, :], r3(sq[u][:, :]), AX.X, ALU.add))
                    v.tensor_scalar(var[u][:, :], var[u][:, :], 1.0 / D, None, ALU.mult).then_inc(st[u].sem, 1)
                    yield
                    v.wait_ge(rs[u].sem, rs[u].after(i, k))
                    yield from lk(v.tensor_tensor(r3(t[:, :]), r3(t[:, :]), over(rstd[u][:, :], D), ALU.mult))
                    yield from lk(v.tensor_tensor(r3(t[:, :]), r3(t[:, :]), row16(g), ALU.mult))
                t0 = (i * U + u) * FT
                yield from lk(v.tensor_tensor(fx[u][:, :].rearrange("p (s t c) -> p s (t c)", t=2, c=C),
                                              mixed[:, bass.ds(t0, FT), :].rearrange("p (s t) c -> p s (t c)", t=2),
                                              resid[:, :, :].rearrange("p (s t) c -> p s (t c)", s=1).to_broadcast([P, FT // 2, 2 * C]),
                                              ALU.add))
                yield from norm(fx[u], "f1_lg", "f1_lb", 1)
                v.tensor_tensor(r3(fx[u][:, :]), r3(fx[u][:, :]), row16("f1_lb"), ALU.add).then_inc(fr[u].sem, 1)
                yield
                v.wait_ge(fr[u].sem, fr[u].after(i, 1))
                yield from lk(v.tensor_scalar(npm[u][:, :], fx[u][:, :], 0.0, None, ALU.not_equal))
                v.wait_ge(ftr[u].sem, ftr[u].after(i, 1))
                v.tensor_scalar(npmT[u][0:C, :], fxT[u][0:C, :], 0.0, None, ALU.not_equal).then_inc(nzt[u].sem, 1)
                yield
                v.wait_ge(nzt[u].sem, nzt[u].after(i, 1))
                v.wait_ge(h1m[u].sem, h1m[u].after(i, 2))
                v.tensor_tensor(h1[u][0:C, :], h1[u][0:C, :], npmT[u][0:C, :], ALU.mult).then_inc(h1r[u].sem, 1)
                yield
                v.wait_ge(zp[u].sem, zp[u].after(i, 1))
                yield from lk(v.tensor_tensor(r3(y[u][:, :]), r3(K.bank[4 * u][:, :]), row16("f1_2b"), ALU.add))
                yield from lk(v.tensor_tensor(y[u][:, :], y[u][:, :], npm[u][:, :], ALU.mult))
                yield from lk(v.tensor_tensor(y[u][:, :], y[u][:, :], fx[u][:, :], ALU.add))
                yield from norm(y[u], "f1_ng", "f1_nb", 2)
                v.tensor_tensor(r3(y[u][:, :]), r3(y[u][:, :]), row16("f1_nb"), ALU.add).then_inc(fo[u].sem, 1)
                yield
                v.wait_ge(gp[u].sem, gp[u].after(i, 1))
                logits = K.bank[4 * u + 1][:, 0:R].rearrange("p (a c) -> p a c", c=H)
                gate = fg[u][:, :].rearrange("p (a c) -> p a c", c=H)
                yield from lk(v.tensor_reduce(m[u][:, 0:FT], logits, AX.X, ALU.max))
                v.tensor_tensor(gate, logits, over(m[u][:, 0:FT], H), ALU.subtract).then_inc(gsh[u].sem, 1)
                yield
                v.wait_ge(gex[u].sem, gex[u].after(i, 1))
                K.settle(v)
                yield from lk(v.tensor_reduce(m[u][:, 0:FT], gate, AX.X, ALU.add))
                yield from lk(v.reciprocal(m[u][:, 0:FT], m[u][:, 0:FT]))
                yield from lk(v.tensor_tensor(gate, gate, over(m[u][:, 0:FT], H), ALU.mult))
                yield from lk(v.tensor_tensor(r3(y[u][:, :]), r3(y[u][:, :]), over(fg[u][:, :], D), ALU.mult))
                dest = K.h[:, bass.ds(t0, FT), :]
                yield from lk(v.tensor_tensor(dest, dest, y[u][:, :].rearrange("p (j c) -> p j c", j=FT), ALU.add))
                assert done[0] == VEC, done

            with v.Fori(0, STEPS) as i:
                alive = [stream(i, u) for u in streams]
                while alive:
                    alive = [s for s in alive if next(s, "end") != "end"]

        @block.gpsimd
        def _(g):
            g.memset(half[:, :], -0.5).then_inc(hs.sem, 1)
            with g.Fori(0, STEPS) as i:
                for k in range(2):
                    for u in streams:
                        g.wait_ge(st[u].sem, st[u].after(i, k + 1))
                        K.settle(g)
                        g.tensor_scalar(work[u][:, :], var[u][:, :], 1e-8, None, ALU.add).then_inc(pl[u].sem, 1)
                        g.wait_ge(pl[u].sem, pl[u].after(i, k + 1))
                        g.tensor_tensor(rstd[u][:, :], work[u][:, :], half[:, :], ALU.pow).then_inc(rs[u].sem, 1)

        @block.tensor
        def _(pe):
            with pe.Fori(0, STEPS) as i:
                def turn(src, ready, out, bank):
                    for u in streams:
                        pe.wait_ge(ready[u].sem, ready[u].after(i, 1))
                        K.settle(pe)
                        for j in range(FT):
                            ins = pe.transpose(K.bank[4 * u + bank + j // 4][0:C, (j % 4) * P:(j % 4 + 1) * P], src[u][:, j * C:(j + 1) * C],
                                               K.W("ident"))
                        ins.then_inc(out[u].sem, 1)

                def products(src, ready, weight, width, out, bank):
                    for u in streams:
                        pe.wait_ge(ready[u].sem, ready[u].after(i, 1))
                        K.settle(pe)
                        for j in range(FT):
                            ins = pe.matmul(K.bank[4 * u + bank][:, j * width:(j + 1) * width], src[u][:, j * P:(j + 1) * P], K.W(weight),
                                            start=True, stop=True, skip_group_check=True)
                        ins.then_inc(out[u].sem, 1)
                turn(fx, fr, ftp, 0)
                for u in streams:
                    pe.wait_ge(ftr[u].sem, ftr[u].after(i, 1))
                    K.settle(pe)
                    for b in range(2):
                        pe.matmul(K.bank[4 * u + 2 + b][0:C, :], K.W("f1_1"), fxT[u][:, b * NTOK:(b + 1) * NTOK], start=True, stop=True)\
                            .then_inc(h1p[u].sem, 1)
                products(h1, h1r, "f1_2", C, zp, 0)
                turn(y, fo, fop, 2)
                products(fxT, fot, "f1_fg", H, gp, 1)

        @block.scalar
        def _(a):
            with a.Fori(0, STEPS) as i:
                def out(ready, done, bank):
                    for u in streams:
                        a.wait_ge(ready[u].sem, ready[u].after(i, 1))
                        for b in range(2):
                            ins = a.activation(fxT[u][0:C, b * NTOK:(b + 1) * NTOK], K.bank[4 * u + bank + b][0:C, :], ACT.Copy)
                        ins.then_inc(done[u].sem, 1)
                out(ftp, ftr, 0)
                for u in streams:
                    for b in range(2):
                        a.wait_ge(h1p[u].sem, h1p[u].after(i, b + 1))
                        a.activation(h1[u][0:C, b * NTOK:(b + 1) * NTOK], K.bank[4 * u + 2 + b][0:C, :], ACT.Relu, bias=K.W("f1_1b", 0, C))\
                            .then_inc(h1m[u].sem, 1)
                out(fop, fot, 2)
                for u in streams:
                    a.wait_ge(gsh[u].sem, gsh[u].after(i, 1))
                    a.activation(fg[u][:, :], fg[u][:, :], ACT.Exp).then_inc(gex[u].sem, 1)
        for both in counts:
            for c in both:
                c.close(STEPS)


def third_attention(K):
    nc = K.nc
    front = Front(K, "ln", (1e-5,))

    def make(ctx):
        H, D = 8, 32
        scale = float(np.float32(1.0) / np.sqrt(np.float32(D)))
        qT, kT, vt, osb = [], [], [], []
        for u in range(2):
            qT.append(ctx.enter_context(nc.sbuf_tensor(f"a2_qT{u}", [P, 2, NTOK], F32)))
            kT.append(ctx.enter_context(nc.sbuf_tensor(f"a2_kT{u}", [P, 4, 2, NTOK], F32)))
            vt.append(values(ctx, nc, H, D))
            osb.append(ctx.enter_context(nc.sbuf_tensor(f"a2_o_sb{u}", [P, GT, H * D], F32)))
        prepare(K, [vt[u][:, :, :, D:D + 1] for u in range(2)], [kT[u][:, n, :, :] for u in range(2) for n in range(4)])
        x = K.xU[:, :]

        def qjob(u, c):
            return ("vec", lambda pe, b, i: pe.matmul(b[:, :], K.W("a2_q")[:, c * P:(c + 1) * P], x, start=True, stop=True),
                    lambda v, b, i: v.tensor_scalar(qT[u][:, c, :], b[:, :], K.W("a2_qb")[:, c:c + 1], scale, ALU.add, ALU.mult))

        def kjob(u, c):
            return ("act", lambda pe, b, i: pe.matmul(b[:, :], K.W("a2_k")[:, c * P:(c + 1) * P], x, start=True, stop=True),
                    lambda a, b, i: [a.activation(kT[u][r, n, c, :], b[r, :], ACT.Identity, bias=K.W("a2_kb")[r, c:c + 1])
                                     for n, r in enumerate(slice(32 * n, 32 * n + 32) for n in range(4))][-1])

        def vjob(u, c):
            def mm(pe, b, i):
                for n in range(2):
                    j = 2 * c + n
                    ins = pe.matmul(b[:, n * SEQ:(n + 1) * SEQ], K.xU[:, j * P:(j + 1) * P], K.W("a2_v"), start=True, stop=True)
                return ins
            return ("vec", mm, lambda v, b, i: v.tensor_tensor(
                vt[u][:, 2 * c:2 * c + 2, :, 0:D], b[:, :].rearrange("p (j h c) -> p j h c", j=2, h=H),
                K.W("a2_vb").rearrange("p (j h c) -> p j h c", j=1, h=H).to_broadcast([P, 2, H, D]), ALU.add))
        proj = [[f(u, c) for c in range(2) for f in (qjob, kjob, vjob)] for u in range(2)]
        sets = [[], []]
        m0 = K.wb[:, 9:11, :].rearrange("p a c -> p (a c)")
        m1 = K.wb[:, 11:15, :].rearrange("p a c -> p (a c)")
        for u in range(2):
            q, k, v = qT[u], kT[u], vt[u]
            o5 = osb[u][:, :, :].rearrange("p j (m n c) -> p j m n c", m=2, n=4)
            for s in range(2):
                t0 = s * SEQ
                for n in range(4):
                    sets[u].append(Unit([(P * m, P, q[:, m, t0:t0 + P], k[:, n, m, t0:t0 + P]) for m in range(2)], [(0, 2 * P, m0)],
                                        [(0, 2, P)], [[(m, v[:, 2 * s, 4 * m + n, :])] for m in range(2)], D + 1, o5[:, 2 * s, :, n, :]))
                    sets[u].append(Unit([(SEQ * m, SEQ, q[:, m, t0 + P:t0 + SEQ], k[:, n, m, t0:t0 + SEQ]) for m in range(2)], [(0, 512, m1)],
                                        [(0, 2, SEQ)], [[(2 * m + kb, v[:, 2 * s + kb, 4 * m + n, :]) for kb in range(2)] for m in range(2)],
                                        D + 1, o5[:, 2 * s + 1, :, n, :]))
        units = Units(K, ctx, sets, piped=True)
        tail = PipedTail(K, ctx, osb, K.W("a2_o"), K.W("a2_ob"), units)
        tail.jobs = Jobs(K, front, proj, [tail.list(u) for u in range(2)])
        return units, tail.jobs, tail
    piped_stage(K, 4, front, 6, make)


def pick_first_max(v, lk, src, top, eq, one):
    n, e = src.shape[1], src.shape[2]
    b = (lambda t: t.rearrange("p (a c) -> p a c", c=1).to_broadcast([P, n, e]))
    lk(v.tensor_reduce(top, src, AX.X, ALU.max))
    lk(v.tensor_tensor(eq, src, b(top), ALU.is_equal))
    lk(v.tensor_tensor(eq, eq, pick_first_max.rank(n, e), ALU.mult))
    lk(v.tensor_reduce(pick_first_max.work, eq, AX.X, ALU.max))
    lk(v.tensor_tensor(one, eq, b(pick_first_max.work), ALU.is_equal))


class Mixture:

    def __init__(self, K, kind, load, front, E, CH, M, w1, w2, b1=None, w3=None, gw=None, gb=None, b2=None, kept=None):
        self.K, self.kind, self.load, self.front, self.kept = K, kind, load, front, kept
        self.E, self.CH, self.M, self.w1, self.w2, self.b1, self.w3, self.gw, self.gb, self.b2 = E, CH, M, w1, w2, b1, w3, gw, gb, b2
        self.NC = E * CH

    def run(self):
        K, nc, E, CH, NC, M = self.K, self.K.nc, self.E, self.CH, self.NC, self.M
        kind, front, kept, biased = self.kind, self.front, self.kept, self.b2 is not None
        gated = self.w3 is not None
        R = 8
        lag = 4 if gated else 6
        at_turn, at_router, at_exp = {"f0": (10, 12, 14), "f2": (6, 8, 9), "f3": (10, 12, 14)}[kind]
        with ExitStack() as ctx:
            def sb(n, s, d=F32):
                return ctx.enter_context(nc.sbuf_tensor(f"{kind}_{n}", s, d))
            xs = [(K.xU, K.xL), (sb("xT_upper", [P, NTOK]), sb("xT_lower", [P, NTOK]))]
            hT = sb("hidden", [P, R, NTOK])
            ug = sb("gate_part", [P, 2, NTOK]) if gated else None
            prod = sb("weighted", [P, 2, GT * C])
            acc = sb("sum", [P, GT, C])
            bsum = sb("bias_sum", [P, GT, C])
            g = sb("weights", [P, 2, GT, 32])
            gT = sb("weightsT", [P, P])
            lg, ex, eq, o1, o2, l2 = (sb(n, [P, GT, E]) for n in ("logits", "exps", "equal", "first", "second", "rest"))
            m1, m2, wk, sm = (sb(n, [P, GT]) for n in ("top1", "top2", "work", "sums"))
            run = sb("run", [P, GT + 1, E])
            bnst, mv, rstd, wk4 = sb("bn", [P, GT, 6]), sb("mv", [P, GT, 2]), sb("rstd", [P, GT]), sb("wk4", [P, GT])
            mask = sb("mask", [P, GT * C], I32) if kind == "f3" else None
            limits = sb("limits", [P, 3, GT * C]) if kind == "f3" else None
            names = ("logits_ready", "choice_vec", "shifted", "exps_ready", "weights_ready", "counts_in_psum", "counted",
                     "weightsT_in_psum", "weightsT_ready", "bias_in_psum", "sum_started", "hidden_in_psum", "hidden_ready", "gate_ready",
                     "expert_out", "weighted_ready", "summed", "mixture_stats", "mixture_pool", "mixture_rstd", "cleared", "bias_moved",
                     "mixture_vec")
            counts = [K.count(n) for n in names]
            (lgr, vec, shf, exr, wr, cps, cntd, gtp, gtr, bps, acs, hps, hr, gtd, eo, pr, sd, mst, mpl, mrs, clr, bmv, fin) = counts
            choice_steps, final_steps = {"f0": (17, 6), "f2": (21, 1), "f3": (18, 8)}[kind]
            for c, per, cr in ((lgr, 1, 0), (vec, choice_steps, 0), (shf, 1, 0), (exr, 1, 0), (wr, 1, 0), (cps, kind == "f3", 0),
                               (cntd, kind == "f3", 0), (gtp, biased, 0), (gtr, biased, 0), (bps, biased, 0), (acs, 1, 0), (hps, NC, 0),
                               (hr, NC, R), (gtd, NC if gated else 0, 0), (eo, E, 2 * R), (pr, E, 2), (sd, E, 2), (mst, kind == "f0", 0),
                               (mpl, kind == "f0", 0), (mrs, kind == "f0", 0), (clr, 0, 2), (bmv, biased, biased), (fin, final_steps, 0)):
                c.stage(int(per), int(cr))
            block = ctx.enter_context(nc.Block())
            B6, B7 = K.bank[6], K.bank[7]
            flat = (lambda t: t.rearrange("p a c -> p (a c)"))
            b3 = (lambda t: t.rearrange("p (a c) -> p a c", c=1).to_broadcast([P, GT, E]))
            rank = K.W("rank")[:, 0:E].rearrange("p (a c) -> p a c", a=1).to_broadcast([P, GT, E])

            def hbank(c):
                return (K.bank[2 * (c % 2)], K.bank[2 * (c % 2) + 1]) if gated else (K.bank[c % 4], None)
            nbanks = 2 if gated else 4

            @block.tensor
            def _(pe):
                def router(n, u):
                    pe.wait_ge(front.xt_r.sem, front.xt_r.after(n, 1))
                    K.settle(pe)
                    for j in range(GT):
                        ins = pe.matmul(B6[:, j * E:(j + 1) * E], xs[u][0][:, j * P:(j + 1) * P], self.gw[:, :], start=True, stop=True,
                                        skip_group_check=True)
                    ins.then_inc(lgr.sem, 1)

                def places(n):
                    pe.wait_ge(cntd.sem, cntd.after(n, 1))
                    K.settle(pe)
                    pe.matmul(B6[:, 64:64 + GT * E], K.W("tri"), flat(o1[:, :, :]), start=True, stop=False, skip_group_check=True)
                    pe.matmul(B6[:, 64:64 + GT * E], K.W("ones"), flat(run[:, 0:GT, :]), start=False, stop=True,
                              skip_group_check=True).then_inc(cps.sem, 1)

                def outputs(i, e):
                    pe.wait_ge(hr.sem, hr.after(i, (e + 1) * CH))
                    pe.wait_ge(pr.sem, pr.after(i, e - 1))
                    for j in range(GT):
                        for n in range(CH):
                            c = e * CH + n
                            ins = pe.matmul(K.bank[4 + e % 2][:, j * C:(j + 1) * C], hT[0:M, c % R, j * P:(j + 1) * P],
                                            self.w2[0:M, c * C:(c + 1) * C], start=n == 0, stop=n == CH - 1, skip_group_check=True)
                    ins.then_inc(eo.sem, 1)
                pe.wait_ge(K.loaded[self.load], 16)
                pe.wait_ge(clr.sem, clr.base + 2)
                front.open_pe(pe)
                pe.sem_inc(eo.sem, 2 * R)
                front.transpose(pe, 0, 6)
                router(0, 0)
                if kind == "f3":
                    places(0)
                with pe.Fori(0, GROUPS // 2) as i0:
                    for u in range(2):
                        i, done = i0 * 2 + u, 0
                        for c in range(NC):
                            z, z3 = hbank(c)
                            x = xs[u][c % 2]
                            pe.wait_ge(hr.sem, hr.after(i, c - nbanks + 1))
                            ins = pe.matmul(z[0:M, :], self.w1[:, (c // 2) * M:(c // 2 + 1) * M], x[:, :], start=True, stop=True)
                            if gated:
                                ins = pe.matmul(z3[0:M, :], self.w3[:, (c // 2) * M:(c // 2 + 1) * M], x[:, :], start=True, stop=True)
                            ins.then_inc(hps.sem, 1)
                            if c == at_turn:
                                front.transpose(pe, i + 1, 6)
                            if c == at_router:
                                router(i + 1, 1 - u)
                            if biased and c == NC - 4:
                                pe.wait_ge(bmv.sem, bmv.after(i, 0))
                                pe.wait_ge(wr.sem, wr.after(i, 1))
                                K.settle(pe)
                                pe.transpose(B7[:, P:2 * P], flat(g[:, u, :, :]), K.W("ident")).then_inc(gtp.sem, 1)
                            if biased and c == NC - 2:
                                pe.wait_ge(gtr.sem, gtr.after(i, 1))
                                pe.matmul(B7[:, 2 * P:4 * P], gT[:, :], self.b2, start=True, stop=True, skip_group_check=True).then_inc(bps.sem, 1)
                            while (done + 1) * CH - 1 <= c - lag:
                                outputs(i, done)
                                done += 1
                        while done < E:
                            outputs(i, done)
                            done += 1
                        if kind == "f3":
                            places(i + 1)

            @block.scalar
            def _(a):
                def exps(n):
                    a.wait_ge(shf.sem, shf.after(n, 1))
                    a.activation(ex[:, :, :], ex[:, :, :], ACT.Exp).then_inc(exr.sem, 1)
                a.wait_ge(K.loaded[self.load], 16)
                if not gated:
                    a.sem_inc(hr.sem, R)
                front.move(a, 0, 6, xs[0])
                exps(0)
                with a.Fori(0, GROUPS // 2) as i0:
                    for u in range(2):
                        i = i0 * 2 + u
                        for c in range(NC):
                            z, _ = hbank(c)
                            a.wait_ge(hps.sem, hps.after(i, c + 1))
                            if gated:
                                a.wait_ge(hr.sem, hr.after(i, c - 1))
                                a.activation(ug[0:M, c % 2, :], z[0:M, :], ACT.Silu).then_inc(gtd.sem, 1)
                            else:
                                a.wait_ge(eo.sem, eo.after(i, (c - R) // CH + 1))
                                a.activation(hT[0:M, c % R, :], z[0:M, :], ACT.Relu, bias=self.b1[0:M, c:c + 1]).then_inc(hr.sem, 1)
                            if c == at_turn:
                                front.move(a, i + 1, 6, xs[1 - u])
                            if c == at_exp:
                                exps(i + 1)
                            if biased and c == NC - 4:
                                a.wait_ge(gtp.sem, gtp.after(i, 1))
                                a.activation(gT[:, :], B7[:, P:2 * P], ACT.Copy).then_inc(gtr.sem, 1)

            @block.gpsimd
            def _(p):
                if kind == "f3":
                    for n, x in enumerate((0.0, 1.0e4, -1.0e4)):
                        p.memset(limits[:, n, :], x)
                p.memset(run[:, :, :], 0.0)
                p.memset(g[:, :, :, :], 0.0).then_inc(clr.sem, 1)
                p.sem_inc(sd.sem, 2)
                front.rstds(p, 0)
                with p.Fori(0, GROUPS) as i:
                    front.rstds(p, i + 1)
                    for e in range(E):
                        p.wait_ge(pr.sem, pr.after(i, e + 1))
                        if e == 0:
                            p.wait_ge(acs.sem, acs.after(i, 1))
                        else:
                            p.wait_ge(sd.sem, sd.after(i, e))
                        p.tensor_tensor(flat(acc[:, :, :]), flat(acc[:, :, :]), prod[:, e % 2, :], ALU.add).then_inc(sd.sem, 1)
                    if kind == "f0":
                        p.wait_ge(mst.sem, mst.after(i, 1))
                        K.settle(p)
                        p.tensor_scalar(wk4[:, :], mv[:, :, 1], 1e-5, None, ALU.add).then_inc(mpl.sem, 1)
                        p.wait_ge(mpl.sem, mpl.after(i, 1))
                        p.tensor_tensor(rstd[:, :], wk4[:, :], K.half[:, 0:GT], ALU.pow).then_inc(mrs.sem, 1)

            @block.vector
            def _(v):
                work = []

                def fill():
                    if work:
                        work.pop(0)()

                def choose(n, u, every):
                    st = [0]

                    def lk(ins, settle=False):
                        st[0] += 1
                        ins.then_inc(vec.sem, 1)
                        if st[0] > 3 and st[0] % every == 0:
                            fill()
                        v.wait_ge(vec.sem, vec.after(n, st[0]))
                        if settle:
                            K.settle(v)

                    def pick(src, top, one):
                        lk(v.tensor_reduce(top[:, :], src[:, :, :], AX.X, ALU.max))
                        lk(v.tensor_tensor(eq[:, :, :], src[:, :, :], b3(top[:, :]), ALU.is_equal))
                        lk(v.tensor_tensor(eq[:, :, :], eq[:, :, :], rank, ALU.mult))
                        lk(v.tensor_reduce(wk[:, :], eq[:, :, :], AX.X, ALU.max))
                        lk(v.tensor_tensor(one[:, :, :], eq[:, :, :], b3(wk[:, :]), ALU.is_equal))

                    def both(src):
                        pick(src, m1, o1)
                        lk(v.scalar_tensor_tensor(flat(l2[:, :, :]), flat(o1[:, :, :]), -BIG, flat(src[:, :, :]), ALU.mult, ALU.add))
                        pick(l2, m2, o2)
                        lk(v.tensor_tensor(o1[:, :, :], o1[:, :, :], o2[:, :, :], ALU.add))
                    weights = g[:, u, :, 0:E]
                    src = B6[:, 0:GT * E].rearrange("p (j e) -> p j e", j=GT)
                    v.wait_ge(lgr.sem, lgr.after(n, 1))
                    if self.gb is not None:
                        lk(v.tensor_tensor(lg[:, :, :], src, rows(self.gb, GT, E), ALU.add))
                    else:
                        lk(v.tensor_copy(lg[:, :, :], src))
                    lk(v.tensor_reduce(m1[:, :], lg[:, :, :], AX.X, ALU.max))
                    v.tensor_tensor(ex[:, :, :], lg[:, :, :], b3(m1[:, :]), ALU.subtract).then_inc(shf.sem, 1)
                    v.wait_ge(shf.sem, shf.after(n, 1))
                    if kind == "f0":
                        both(lg)
                        v.wait_ge(exr.sem, exr.after(n, 1))
                        K.settle(v)
                        lk(v.tensor_tensor(o1[:, :, :], o1[:, :, :], ex[:, :, :], ALU.mult))
                        lk(v.tensor_reduce(sm[:, :], o1[:, :, :], AX.X, ALU.add))
                        lk(v.reciprocal(sm[:, :], sm[:, :]))
                        v.tensor_tensor(weights, o1[:, :, :], b3(sm[:, :]), ALU.mult).then_inc(wr.sem, 1)
                        assert st[0] == choice_steps
                        return
                    v.wait_ge(exr.sem, exr.after(n, 1))
                    K.settle(v)
                    lk(v.tensor_reduce(sm[:, :], ex[:, :, :], AX.X, ALU.add))
                    lk(v.reciprocal(sm[:, :], sm[:, :]))
                    lk(v.tensor_tensor(lg[:, :, :], ex[:, :, :], b3(sm[:, :]), ALU.mult))
                    if kind == "f2":
                        both(lg)
                        lk(v.tensor_tensor(o1[:, :, :], o1[:, :, :], lg[:, :, :], ALU.mult))
                        lk(v.tensor_reduce(sm[:, :], o1[:, :, :], AX.X, ALU.add))
                        lk(v.tensor_scalar(sm[:, :], sm[:, :], 1e-9, None, ALU.add))
                        lk(v.reciprocal(sm[:, :], sm[:, :]))
                        v.tensor_tensor(weights, o1[:, :, :], b3(sm[:, :]), ALU.mult).then_inc(wr.sem, 1)
                        assert st[0] == choice_steps
                        return
                    pick(lg, m1, o1)
                    for j in range(GT):
                        ins = v.tensor_tensor(run[:, j + 1, :], run[:, j, :], o1[:, j, :], ALU.add)
                        if j < GT - 1:
                            lk(ins)
                    ins.then_inc(cntd.sem, 1)
                    while work:
                        fill()
                    v.wait_ge(cps.sem, cps.after(n, 1))
                    K.settle(v)
                    lk(v.tensor_copy(run[:, 0, :], run[:, GT, :]))
                    lk(v.tensor_tensor(l2[:, :, :], B6[:, 64:64 + GT * E].rearrange("p (j e) -> p j e", j=GT), o1[:, :, :], ALU.mult))
                    lk(v.tensor_reduce(sm[:, :], l2[:, :, :], AX.X, ALU.add))
                    lk(v.tensor_scalar(sm[:, :], sm[:, :], float(CAP3), None, ALU.is_le))
                    lk(v.tensor_tensor(sm[:, :], sm[:, :], m1[:, :], ALU.mult))
                    v.tensor_tensor(weights, o1[:, :, :], b3(sm[:, :]), ALU.mult).then_inc(wr.sem, 1)
                    assert st[0] == choice_steps

                def weigh(i, u, e):
                    v.wait_ge(eo.sem, eo.after(i, e + 1))
                    v.wait_ge(sd.sem, sd.after(i, e - 1))
                    v.tensor_tensor(prod[:, e % 2, :].rearrange("p (j c) -> p j c", j=GT),
                                    K.bank[4 + e % 2][:, 0:GT * C].rearrange("p (j c) -> p j c", j=GT),
                                    g[:, u, :, e:e + 1].to_broadcast([P, GT, C]), ALU.mult).then_inc(pr.sem, 1)

                def gate(i, c):
                    v.wait_ge(gtd.sem, gtd.after(i, c + 1))
                    v.wait_ge(eo.sem, eo.after(i, (c - R) // CH + 1))
                    v.tensor_tensor(hT[0:M, c % R, :], ug[0:M, c % 2, :], hbank(c)[1][0:M, :], ALU.mult).then_inc(hr.sem, 1)

                def move_bias(i):
                    v.wait_ge(bps.sem, bps.after(i, 1))
                    v.tensor_copy(bsum[:, :, :], B7[:, 2 * P:4 * P].rearrange("p (j c) -> p j c", j=GT)).then_inc(bmv.sem, 1)

                def group(i, u):
                    if kind == "f0":
                        v.wait_ge(wr.sem, wr.after(i, 1))
                        v.tensor_copy(acc[:, :, :], K.xn[:, :, 0, :]).then_inc(acs.sem, 1)
                    elif kind == "f2":
                        K.settle(v)
                        v.tensor_copy(acc[:, :, :], kept[:, bass.ds(i * GT, GT), :]).then_inc(acs.sem, 1)
                    else:
                        v.memset(acc[:, :, :], 0.0).then_inc(acs.sem, 1)
                    v.wait_ge(wr.sem, wr.after(i, 1))
                    front.statistics(v, i + 1)
                    e = 0
                    if gated:
                        for c in range(NC):
                            work.append(lambda c=c: gate(i, c))
                            if c - lag >= 1 and (c - lag) % CH == CH - 1:
                                work.append(lambda e=e: weigh(i, u, e))
                                e += 1
                    for e in range(e, E):
                        work.append(lambda e=e: weigh(i, u, e))
                        if biased and e == E - 3:
                            work.append(lambda: move_bias(i))
                    before_norm, before_choice, every = {"f0": (2, 4, 2), "f2": (3, 8, 1), "f3": (1, 2, 3)}[kind]
                    for _ in range(before_norm):
                        fill()
                    front.normalise(v, i + 1)
                    for _ in range(before_choice):
                        fill()
                    choose(i + 1, 1 - u, every)
                    while work:
                        fill()
                    v.wait_ge(sd.sem, sd.after(i, E))
                    st = [0]
                    lk = link(v, fin, i, st, K)
                    if biased:
                        v.wait_ge(bmv.sem, bmv.after(i, 1))
                        lk(v.tensor_tensor(acc[:, :, :], acc[:, :, :], bsum[:, :, :], ALU.add))
                    if kind == "f0":
                        for j in range(GT):
                            ins = v.bn_stats(bnst[:, j, :], acc[:, j, :])
                        lk(ins, settle=True)
                        for j in range(GT):
                            ins = v.bn_aggr(mv[:, j, :], bnst[:, j, :])
                        ins.then_inc(mst.sem, 1)
                        v.wait_ge(mrs.sem, mrs.after(i, 1))
                        for j in range(GT):
                            ins = v.tensor_scalar(acc[:, j, :], acc[:, j, :], mv[:, j, 0:1], rstd[:, j:j + 1], ALU.subtract, ALU.mult)
                        lk(ins)
                        lk(v.tensor_tensor(acc[:, :, :], acc[:, :, :], rows(K.W("f0_g"), GT, C), ALU.mult))
                        lk(v.tensor_tensor(acc[:, :, :], acc[:, :, :], rows(K.W("f0_b"), GT, C), ALU.add))
                    if kind == "f3":
                        y = flat(acc[:, :, :])
                        lk(v.tensor_tensor(mask[:, :], y, y, ALU.not_equal), settle=True)
                        lk(v.copy_predicated(y, mask[:, :], limits[:, 0, :]))
                        lk(v.tensor_scalar(mask[:, :], y, 3.4028234e38, None, ALU.is_gt), settle=True)
                        lk(v.copy_predicated(y, mask[:, :], limits[:, 1, :]))
                        lk(v.tensor_scalar(mask[:, :], y, -3.4028234e38, None, ALU.is_lt), settle=True)
                        lk(v.copy_predicated(y, mask[:, :], limits[:, 2, :]))
                    lk(v.tensor_tensor(K.hgroup(i), K.hgroup(i), acc[:, :, :], ALU.add))
                    assert st[0] == final_steps, (kind, st[0])

                v.memset(xs[1][0][C:P, :], 0.0)
                v.memset(xs[1][1][0:C, :], 0.0).then_inc(clr.sem, 1)
                v.wait_ge(K.loaded[self.load], 16)
                v.wait_ge(clr.sem, clr.base + 2)
                v.sem_inc(pr.sem, 2)
                if biased:
                    v.sem_inc(bmv.sem, 1)
                if gated:
                    v.sem_inc(hr.sem, R)
                front.statistics(v, 0)
                front.normalise(v, 0)
                choose(0, 0, 1)
                with v.Fori(0, GROUPS // 2) as i0:
                    for u in range(2):
                        group(i0 * 2 + u, u)
            for c in counts:
                c.close(GROUPS + (c in (lgr, vec, shf, exr, wr, cps, cntd)))
            front.close()


def first_mixture(K):
    Mixture(K, "f0", 1, Front(K, "ln", (1e-5,), dup=True), E0, 1, F0, K.W("f0_w1"), K.W("f0_w2"), b1=K.W("f0_b1"),
            gw=K.W("f0_gw"), gb=K.W("f0_gb"), b2=K.W("f0_b2")).run()


def second_mixture(K, x1):
    Mixture(K, "f2", 6, Front(K, "rms", (1e-6,), dup=True, scale=K.W("f2_ln"), src=x1), E2, 2, F2C, K.W("f2_w1"), K.W("f2_w2"),
            w3=K.W("f2_w3"), gw=K.W("f2_gw"), kept=x1).run()


def third_mixture(K):
    Mixture(K, "f3", 8, Front(K, "ln", (1e-5,), dup=True), E3, 2, P, K.W("f3_w1"), K.W("f3_w2"), b1=K.W("f3_b1"),
            gw=K.W("f3_gw"), gb=K.W("f3_gb"), b2=K.W("f3_b2")).run()


def third_layer_block(K):
    with K.nc.sbuf_tensor("x1", [P, TILES + 2 * GT, C], F32) as x1:
        with K.nc.Block() as block:
            @block.vector
            def _(v):
                v.memset(x1[:, TILES:TILES + 2 * GT, :], 0.0)
        second_routed_attention(K, x1)
        second_mixture(K, x1)


class KeySoftmaxUnits:

    N = 2

    def __init__(self, K, ctx, qT, kT, vt, scale, mask):
        nc = K.nc
        self.K, self.qT, self.kT, self.vt, self.scale, self.mask = K, qT, kT, vt, scale, mask
        self.sb = ctx.enter_context(nc.sbuf_tensor("a3_masked", [P, 2, 2 * SEQ], F32))
        self.p = ctx.enter_context(nc.sbuf_tensor("a3_probs", [P, 2, 2 * SEQ], F32))
        self.vs = ctx.enter_context(nc.sbuf_tensor("a3_values_over_sum", [P, 2, 2, C], F32))
        self.nm = ctx.enter_context(nc.sbuf_tensor("a3_negmax", [P, 2, 4], F32))
        self.rd = ctx.enter_context(nc.sbuf_tensor("a3_rden", [P, 2, 2], F32))
        names = ("scores_ready", "max_ready", "probs_ready", "values_over_sum", "values_summed", "normalised", "unit_vec")
        self.sc, self.mx, self.ex, self.vo, self.pv, self.no, self.vec = self.all = [K.count(n) for n in names]
        for c, credit in ((self.sc, 0), (self.mx, 0), (self.ex, 2), (self.vo, 0), (self.pv, 2), (self.no, 2)):
            c.stage(2, credit)
        self.vec.stage(8)

    def close(self):
        for c in self.all:
            c.close(GROUPS)

    def open_pe(self, pe):
        pe.sem_inc(self.pv.sem, 2)

    def open_act(self, a):
        a.sem_inc(self.ex.sem, 2)

    def open_vec(self, v):
        v.sem_inc(self.no.sem, 2)

    def tensor(self, pe, i, splice):
        K = self.K
        for s in range(2):
            for m in range(2):
                k0 = s * SEQ + m * P
                ins = pe.matmul(K.bank[s][:, m * SEQ:(m + 1) * SEQ], self.kT[:, k0:k0 + P], self.qT[:, s * SEQ:(s + 1) * SEQ],
                                start=True, stop=True)
            ins.then_inc(self.sc.sem, 1)
        for k in sorted(splice):
            splice[k](pe)
        for s in range(2):
            pe.wait_ge(self.vo.sem, self.vo.after(i, s + 1))
            pe.wait_ge(self.no.sem, self.no.after(i, s - 1))
            for n in range(2):
                for m in range(2):
                    ins = pe.matmul(K.bank[OB[s]][:, n * C:(n + 1) * C], self.p[:, s, m * SEQ + n * P:m * SEQ + (n + 1) * P],
                                    self.vs[:, s, m, :], start=m == 0, stop=m == 1, skip_group_check=True)
            ins.then_inc(self.pv.sem, 1)

    def vector(self, v, i, splice):
        K = self.K
        lk = link(v, self.vec, i, [0], K)
        steps = [splice[k] for k in sorted(splice)]
        for s in range(2):
            v.wait_ge(self.sc.sem, self.sc.after(i, s + 1))
            v.wait_ge(self.ex.sem, self.ex.after(i, s - 1))
            lk(v.tensor_tensor(self.sb[:, s, :], K.bank[s][:, :], self.mask, ALU.add))
            lk(v.tensor_reduce(self.nm[:, s, 2:4], self.sb[:, s, :].rearrange("p (a b) -> p a b", a=2), AX.X, ALU.max, negate=True))
            v.tensor_scalar(self.nm[:, s, 0:2], self.nm[:, s, 2:4], self.scale, None, ALU.mult).then_inc(self.mx.sem, 1)
        steps[0](v)
        K.proj.wait_moved(v, i)
        for s in range(2):
            v.wait_ge(self.ex.sem, self.ex.after(i, s + 1))
            lk(v.tensor_reduce(self.rd[:, s, :], self.p[:, s, :].rearrange("p (a b) -> p a b", a=2), AX.X, ALU.add))
            lk(v.reciprocal(self.rd[:, s, :], self.rd[:, s, :]))
            v.wait_ge(self.pv.sem, self.pv.after(i, s - 1))
            v.tensor_tensor(self.vs[:, s, :, :], self.vt[:, 2 * s:2 * s + 2, :],
                            self.rd[:, s, :].rearrange("p (a c) -> p a c", c=1).to_broadcast([P, 2, C]), ALU.mult).then_inc(self.vo.sem, 1)
        for f in steps[1:]:
            f(v)
        for s in range(2):
            v.wait_ge(self.pv.sem, self.pv.after(i, s + 1))
            dest = K.h[:, bass.ds(i * GT + 2 * s, 2), :]
            v.tensor_tensor(dest, dest, K.bank[OB[s]][:, 0:2 * C].rearrange("p (j c) -> p j c", j=2), ALU.add).then_inc(self.no.sem, 1)

    def scalar(self, a, i, splice):
        K = self.K
        for s in range(2):
            a.wait_ge(self.mx.sem, self.mx.after(i, s + 1))
            a.wait_ge(self.pv.sem, self.pv.after(i, s - 1))
            for m in range(2):
                r = slice(m * SEQ, (m + 1) * SEQ)
                ins = a.activation(self.p[:, s, r], self.sb[:, s, r], ACT.Exp, bias=self.nm[:, s, m:m + 1], scale=self.scale)
            ins.then_inc(self.ex.sem, 1)
        for k in sorted(splice):
            splice[k](a)


class NoTail:

    def stage(self):
        pass

    close = stage

    def open_vec(self, v):
        pass

    def early(self, e, i):
        pass

    wait_free = tensor = vector = scalar = gpsimd = early


def last_attention(K):
    nc = K.nc
    front = Front(K, "ln", (1e-5,))

    def make(ctx):
        qT = ctx.enter_context(nc.sbuf_tensor("a3_qT", [P, NTOK], F32))
        kT = ctx.enter_context(nc.sbuf_tensor("a3_kT", [P, NTOK], F32))
        prepare(K, [], [qT[C:P, :], kT[C:P, :]])
        vt = ctx.enter_context(nc.sbuf_tensor("a3_v_sb", [P, GT, C], F32))
        x = K.xU[:, :]
        jobs = [
            ("act", lambda pe, b, i: pe.matmul(b[0:C, :], K.W("a3_q"), x, start=True, stop=True),
             lambda a, b, i: a.activation(qT[0:C, :], b[0:C, :], ACT.Copy)),
            ("vec", lambda pe, b, i: pe.matmul(b[0:C, :], K.W("a3_k"), x, start=True, stop=True),
             lambda v, b, i: v.tensor_copy(kT[0:C, :], b[0:C, :])),
            ("act", lambda pe, b, i: [pe.matmul(b[:, j * C:(j + 1) * C], K.xU[:, j * P:(j + 1) * P], K.W("a3_v"),
                                                start=True, stop=True) for j in range(GT)][-1],
             lambda a, b, i: a.activation(vt[:, :, :], b[:, 0:GT * C].rearrange("p (j c) -> p j c", j=GT), ACT.Copy)),
        ]
        units = KeySoftmaxUnits(K, ctx, qT, kT, vt, 0.125, K.W("a3_mask"))
        K.proj = Projections(K, jobs)
        return units, K.proj, NoTail()
    attention_stage(K, "a3", 7, front, make)


STAGES = [first_attention, first_mixture, second_attention, expert_heads, third_attention, third_layer_block, last_attention, third_mixture]


def tower(nc, x, turns, image, masks, out, stages=None, h_in=None):
    with ExitStack() as ctx:
        K = Core(nc, ctx)
        embed_stage(K, x, turns, image, masks)
        if h_in is not None:
            hin = K.count("h_in")
            with nc.Block() as block:
                @block.sync
                def _(sp):
                    sp.dma_start(K.h[:, 0:TILES, :], h_in.rearrange("b (a p) c -> p (b a) c", p=P)).then_inc(hin.sem, 16)
                    sp.wait_ge(hin.sem, 16)
        for k, st in enumerate(STAGES):
            if stages is None or k in stages:
                st(K)
            if k == 2:
                late_weights(K, image)
        store_stage(K, out)


def lay_out(a):
    out = {}
    f = lambda n: np.asarray(a[n], np.float32) if np.asarray(a[n]).dtype != np.float32 else np.asarray(a[n])

    def put(name, parts, cols=None):
        w = dict((n, c) for n, c, _ in IMAGE)[name]
        t = np.zeros((P, w), np.float32)
        for (r0, c0, m) in parts:
            m = np.atleast_2d(m)
            t[r0:r0 + m.shape[0], c0:c0 + m.shape[1]] = m
        out[name] = t

    def col(name, *vs):
        put(name, [(0, k, v.reshape(-1, 1)) for k, v in enumerate(vs)])

    def row(name, v):
        put(name, [(0, 0, np.broadcast_to(v.reshape(1, -1), (P, v.size)))])

    put("ident", [(0, 0, np.eye(P, dtype=np.float32))])
    co = f("L0_tok_poly_coeffs").transpose(1, 0, 2).reshape(TURNS * DEG, C)
    put("coef", [(32 * j, j * C, co) for j in range(GT)])
    qkv, qb = f("L0_attn_qkv_w"), f("L0_attn_qkv_b")
    put("a0_qk", [(0, 0, qkv[:, :128])])
    put("a0_v", [(0, 0, qkv[:, 128:])])
    col("a0_lnw", f("L0_attn_ln1_g"), f("L0_attn_ln1_b"))
    col("a0_qkb", qb[:C], qb[C:2 * C])
    row("a0_vb", qb[128:])
    t = f("L0_attn_bias_table")
    q, k = np.arange(SEQ)[:, None], np.arange(SEQ)[None, :]
    rel = t[k - q + SEQ - 1]
    put("a0_bias", [(0, SEQ * b, rel[b * P:(b + 1) * P]) for b in range(2)])
    row("a0_scale", f("L0_attn_scale").reshape(1))
    put("a0_o", [(0, 0, f("L0_attn_proj_w"))])
    row("a0_ob", f("L0_attn_proj_b"))
    row("a0_g2", f("L0_attn_ln2_g"))
    row("a0_b2", f("L0_attn_ln2_b"))
    put("a1_q", [(0, 0, f("L1_attn_Wq"))])
    put("a1_k", [(0, 0, f("L1_attn_Wk"))])
    put("a1_v", [(0, 0, f("L1_attn_Wv"))])
    put("a1_o", [(0, c * C, f("L1_attn_Wu")[c * P:(c + 1) * P]) for c in range(4)])
    put("a1_qb", [(0, 0, f("L1_attn_bq").reshape(4, P).T)])
    put("a1_kb", [(0, 0, f("L1_attn_bk").reshape(4, P).T)])
    row("a1_vb", f("L1_attn_bv"))
    row("a1_ob", f("L1_attn_bu"))
    r0 = np.ones((P, 2), np.float32)
    r0[0, 0] = 0
    put("row0", [(0, 0, r0)])

    put("rank", [(0, 0, np.broadcast_to(16.0 - np.arange(16, dtype=np.float32), (P, 16)))])

    def halves(w, m):
        return [(C * (c % 2), (c // 2) * m, w[c]) for c in range(len(w))]

    def block_bias(b2, e):
        t = np.zeros((P, GT * C), np.float32)
        for j in range(GT):
            t[32 * j:32 * j + e, j * C:(j + 1) * C] = b2
        return [(0, 0, t)]
    put("f0_gw", [(0, 0, f("L0_ffn_gate_w"))])
    row("f0_gb", f("L0_ffn_gate_b"))
    put("f0_w1", halves(f("L0_ffn_w1"), F0))
    put("f0_b1", [(0, 0, f("L0_ffn_b1").T)])
    put("f0_w2", [(0, e * C, f("L0_ffn_w2")[e]) for e in range(E0)])
    put("f0_b2", block_bias(f("L0_ffn_b2"), E0))
    row("f0_g", f("L0_ffn_gamma"))
    row("f0_b", f("L0_ffn_beta"))
    put("a2_q", [(0, 0, f("L2_attn_W_Q").transpose(1, 0, 2).reshape(C, 256))])
    put("a2_k", [(0, 0, f("L2_attn_W_K").transpose(1, 0, 2).reshape(C, 256))])
    put("a2_v", [(0, 0, f("L2_attn_W_V").transpose(1, 0, 2).reshape(C, 256))])
    put("a2_qb", [(0, 0, f("L2_attn_b_Q").reshape(2, P).T)])
    put("a2_kb", [(0, 0, f("L2_attn_b_K").reshape(2, P).T)])
    row("a2_vb", f("L2_attn_b_V"))
    put("a2_o", [(0, c * C, f("L2_attn_W_O").reshape(256, C)[c * P:(c + 1) * P]) for c in range(2)])
    row("a2_ob", f("L2_attn_b_O"))
    col("r2_ln", f("L2_ffn_ln1_w"))
    wq, wk = f("L2_ffn_wq"), f("L2_ffn_wk")
    turn = np.concatenate([np.arange(8, 16), np.arange(0, 8)])
    put("r2_q", [(0, 32 * n, wq[16 * n:16 * n + 16].T) for n in range(4)])
    put("r2_qp", [(0, 32 * n, wq[16 * n:16 * n + 16][turn].T) for n in range(4)])
    put("r2_k", [(0, 32 * n, wk[16 * (n // 2):16 * (n // 2) + 16].T) for n in range(4)])
    put("r2_kp", [(0, 32 * n, wk[16 * (n // 2):16 * (n // 2) + 16][turn].T) for n in range(4)])
    put("r2_v", [(0, 0, f("L2_ffn_wv").T)])
    put("r2_o", [(0, 0, f("L2_ffn_wo").T)])
    inv = 1.0 / 10000.0 ** (np.arange(0, 16, 2, dtype=np.float32) / 16)
    fr = np.outer(np.arange(SEQ, dtype=np.float32), inv)
    emb = np.concatenate([fr, fr], axis=-1).astype(np.float32)
    cos, sin = np.cos(emb).T, np.sin(emb).T.copy()
    sin[0:8] *= -1.0
    for name, tab, sc in (("r2_cq", cos, 0.25), ("r2_sq", sin, 0.25), ("r2_ck", cos, 1.0), ("r2_sk", sin, 1.0)):
        put(name, [(32 * n, 0, (tab * sc).astype(np.float32)) for n in range(4)])
    put("f2_ln", [(0, 0, np.concatenate([f("L2_ffn_ln2_w")] * 2).reshape(P, 1))])
    put("f2_gw", [(0, 0, f("L2_ffn_router_w").T)])
    put("f2_w1", halves(f("L2_ffn_w1").reshape(16, F2C, C).transpose(0, 2, 1), F2C))
    put("f2_w3", halves(f("L2_ffn_w3").reshape(16, F2C, C).transpose(0, 2, 1), F2C))
    w2 = f("L2_ffn_w2").transpose(0, 2, 1).reshape(16, F2C, C)
    put("f2_w2", [(0, c * C, w2[c]) for c in range(16)])
    put("f3_gw", [(0, 0, f("L3_ffn_gate_w"))])
    row("f3_gb", f("L3_ffn_gate_b"))
    w1 = f("L3_ffn_w1").reshape(E3, C, 2, P).transpose(0, 2, 1, 3).reshape(16, C, P)
    put("f3_w1", halves(w1, P))
    put("f3_b1", [(0, 0, f("L3_ffn_b1").reshape(16, P).T)])
    w2 = f("L3_ffn_w2").reshape(16, P, C)
    put("f3_w2", [(0, c * C, w2[c]) for c in range(16)])
    put("f3_b2", block_bias(f("L3_ffn_b2"), E3))
    put("tri", [(0, 0, np.triu(np.ones((P, P), np.float32)))])
    put("ones", [(0, 0, np.ones((P, P), np.float32))])
    put("a3_q", [(0, 0, f("L3_attn_Wq").T)])
    put("a3_k", [(0, 0, f("L3_attn_Wk").T)])
    put("a3_v", [(0, 0, f("L3_attn_Wv").T)])
    n, k = np.arange(SEQ)[None, :], np.arange(P)[:, None]
    put("a3_mask", [(0, b * SEQ, np.where(n < k + b * P, 0, -1.0e10).astype(np.float32)) for b in range(2)])
    hl = f("L1_ffn_hl_w").reshape(C, C)
    put("f1_hl", [(0, 0, hl.T)])
    put("f1_hlb", [(0, 0, f("L1_ffn_hl_b").reshape(C, 1))])
    row("f1_hlbr", f("L1_ffn_hl_b").reshape(C))
    wq, wk, wv, gw = f("L1_ffn_wq"), f("L1_ffn_wk"), f("L1_ffn_wv"), f("L1_ffn_gate_w")
    put("f1_q", [(16 * n, e * P + 32 * n, wq[n, e].T) for n in range(4) for e in range(4)])
    put("f1_k", [(16 * n, 32 * n, wk[n].T) for n in range(4)])
    put("f1_v", [(16 * n, 16 * n, wv[n].T) for n in range(4)])
    put("f1_g", [(64 * (n % 2), 16 * (n // 2) + 4 * n, gw[n].T) for n in range(4)])
    row("f1_gb", f("L1_ffn_gate_b").reshape(16))
    for name, key in (("f1_lg", "ln_g"), ("f1_lb", "ln_b"), ("f1_2b", "fc2_b"), ("f1_ng", "fnorm_g"), ("f1_nb", "fnorm_b")):
        row(name, f("L1_ffn_" + key))
    put("f1_1", [(16 * n, 16 * n, f("L1_ffn_fc1_w").T) for n in range(4)])
    put("f1_2", [(16 * n, 16 * n, f("L1_ffn_fc2_w").T) for n in range(4)])
    put("f1_1b", [(16 * n, 0, f("L1_ffn_fc1_b").reshape(16, 1)) for n in range(4)])
    put("f1_fg", [(0, 0, f("L1_ffn_fgate_w").T)])
    image = np.concatenate([out[n] if n in out else np.zeros((P, c), np.float32) for n, c, _ in IMAGE], axis=1)
    m = np.zeros((P, 15, P), np.float32)
    q, k = np.arange(P)[:, None], np.arange(P)[None, :]
    m[:, 0] = np.eye(P)
    for n in range(4):
        m[:, 1 + n] = np.where(k >= q, MASKED, 0)
        m[:, 5 + n] = np.where(k > q, MASKED, 0)
    for n in range(2):
        odd0 = np.where(((k < q) & (k % 2 == 1)) | (k == q), 0, MASKED)
        m[:, 9 + n] = odd0
        m[:, 11 + 2 * n] = np.where((k % 2 == 1) & (q >= 0), 0, MASKED)
        m[:, 12 + 2 * n] = odd0
    ids = np.ascontiguousarray(np.asarray(a["x"]).astype(np.int32).reshape(TILES, P).T)
    return {"x": ids, "turns": f("L0_tok_turns"), "image": np.ascontiguousarray(image), "masks": m}


def kernel(**inputs):
    import concourse.bacc as bacc
    from concourse.bass_utils import run_bass_kernel_spmd
    arrays = lay_out(inputs)
    nc = bacc.Bacc("TRN2", target_bir_lowering=False, num_devices=1)
    args, feeds = {}, {}
    for name, v in arrays.items():
        feeds[f"in_{name}"] = v
        args[name] = nc.dram_tensor(f"in_{name}", v.shape, mybir.dt.from_np(v.dtype), kind="ExternalInput").ap()
    out = nc.dram_tensor("out", (SEQS, SEQ, C), F32, kind="ExternalOutput").ap()
    tower(nc, args["x"], args["turns"], args["image"], args["masks"], out)
    r = run_bass_kernel_spmd(nc, [feeds], core_ids=[0])
    return r.results[0]["out"]
```
